# Optimizing a Trainium2 kernel written in Bass

```python
import numpy as np
import jax
import jax.numpy as jnp

def _softmax(x, axis=-1):
    return jax.nn.softmax(x, axis=axis)

def _gelu(x):
    return jax.nn.gelu(x, approximate=True)

def _silu(x):
    return jax.nn.silu(x)

def _sigmoid(x):
    return jax.nn.sigmoid(x)

def _layernorm(x, axis=-1, eps=1e-05):
    m = jnp.mean(x, axis=axis, keepdims=True)
    v = jnp.var(x, axis=axis, keepdims=True)
    return (x - m) / jnp.sqrt(v + eps)

def _scatter_add(tgt, idx, src, axis=0):
    return tgt.at[idx].add(src)

def _segment_sum(src, seg, n):
    return jax.ops.segment_sum(src, seg, n)
kernel_name = 'mk_audio_tower_d2_tok_audfeat512_r4_87a9f1'

def setup_inputs(seed: int=0):
    np.random.seed(seed)
    _w = jnp.asarray

    def _rec_inputs():
        import jax
        import jax.numpy as jnp
        _rk = jax.random.key(seed)
        x = -7.10856e-05 + 0.999911 * jax.random.normal(jax.random.fold_in(_rk, 1), (64, 256, 128), jnp.float32)
        return x
    x = _rec_inputs()

    def _L0_tok_setup():
        import jax, jax.numpy as jnp
        import numpy as np
        EPS = 1e-05

        def conv1d(x, w, b, stride=1, padding=0):
            out = jax.lax.conv_general_dilated(x, w, window_strides=(stride,), padding=[(padding, padding)], dimension_numbers=('NCH', 'OIH', 'NCH'))
            return out + b[None, :, None]

        def layer_norm(x, g, b):
            mu = jnp.mean(x, axis=-1, keepdims=True)
            var = jnp.mean(jnp.square(x - mu), axis=-1, keepdims=True)
            return (x - mu) * jax.lax.rsqrt(var + EPS) * g + b
        key = jax.random.key(seed)
        ks = jax.random.split(key, 16)
        B, T, H = (64, 512, 128)
        Bn = H // 2
        s = 0.02
        return {'x': jax.random.normal(ks[0], (B, T, H), dtype=jnp.float32), 'w_compress': jax.random.normal(ks[1], (Bn, H, 1), dtype=jnp.float32) * s, 'b_compress': jnp.zeros((Bn,), dtype=jnp.float32), 'w_main': jax.random.normal(ks[2], (Bn, Bn, 3), dtype=jnp.float32) * s, 'b_main': jnp.zeros((Bn,), dtype=jnp.float32), 'w_expand': jax.random.normal(ks[3], (H, Bn, 1), dtype=jnp.float32) * s, 'b_expand': jnp.zeros((H,), dtype=jnp.float32), 'g_conv_norm': jnp.ones((H,), dtype=jnp.float32), 'b_conv_norm': jnp.zeros((H,), dtype=jnp.float32), 'w_ff1': jax.random.normal(ks[4], (Bn, H), dtype=jnp.float32) * s, 'b_ff1': jnp.zeros((Bn,), dtype=jnp.float32), 'w_ff2': jax.random.normal(ks[5], (H, Bn), dtype=jnp.float32) * s, 'b_ff2': jnp.zeros((H,), dtype=jnp.float32), 'g_ff_norm': jnp.ones((H,), dtype=jnp.float32), 'b_ff_norm': jnp.zeros((H,), dtype=jnp.float32)}
    _L0_tok_all = _L0_tok_setup()
    _L0_tok_in = {k: v for k, v in _L0_tok_all.items() if k in ('w_compress', 'b_compress', 'w_main', 'b_main', 'w_expand', 'b_expand', 'g_conv_norm', 'b_conv_norm', 'w_ff1', 'b_ff1', 'w_ff2', 'b_ff2', 'g_ff_norm', 'b_ff_norm')}
    del _L0_tok_all

    def _L0_attn_setup():
        import jax, jax.numpy as jnp
        import numpy as np
        N_HEAD = 8
        D_HEAD = 64
        D_MODEL = 128
        SEQ = 512
        BATCH = 2
        key = jax.random.key(seed)
        k1, k2, k3, k4 = jax.random.split(key, 4)
        s = 0.02
        h = jax.random.normal(k1, (SEQ, BATCH, D_MODEL), dtype=jnp.float32)
        Wq = jax.random.normal(k2, (N_HEAD * D_HEAD, D_MODEL), dtype=jnp.float32) * s
        Wkv = jax.random.normal(k3, (2 * N_HEAD * D_HEAD, D_MODEL), dtype=jnp.float32) * s
        Wo = jax.random.normal(k4, (D_MODEL, N_HEAD * D_HEAD), dtype=jnp.float32) * s
        return {'h': h, 'Wq': Wq, 'Wkv': Wkv, 'Wo': Wo}
    _L0_attn_all = _L0_attn_setup()
    _L0_attn_in = {k: v for k, v in _L0_attn_all.items() if k in ('Wq', 'Wkv', 'Wo')}
    del _L0_attn_all

    def _L0_ffn_setup():
        import jax, jax.numpy as jnp
        import numpy as np
        EPS = 1e-05
        TOP_K = 2

        def _moe_forward(x, Wg, W1, b1, W2, b2, gamma, beta):
            B, S, D = x.shape
            xf = x.reshape(-1, D)
            logits = xf @ Wg
            topv, topi = jax.lax.top_k(logits, TOP_K)
            gate_w = jax.nn.softmax(topv, axis=-1)
            h = jax.nn.relu(jnp.einsum('td,edh->teh', xf, W1) + b1[None])
            y = jnp.einsum('teh,ehd->ted', h, W2) + b2[None]
            mu = jnp.mean(y, axis=-1, keepdims=True)
            var = jnp.mean((y - mu) ** 2, axis=-1, keepdims=True)
            y = (y - mu) / jnp.sqrt(var + EPS) * gamma[None] + beta[None]
            y_sel = jnp.take_along_axis(y, topi[:, :, None], axis=1)
            out = jnp.sum(gate_w[:, :, None] * y_sel, axis=1)
            return out.reshape(B, S, D)
        key = jax.random.key(seed)
        ks = jax.random.split(key, 8)
        B, S, D, H, E = (4, 512, 128, 128, 8)
        sd = lambda fan_in: 1.0 / np.sqrt(fan_in)
        x = jax.random.normal(ks[0], (B, S, D), dtype=jnp.float32)
        Wg = jax.random.uniform(ks[1], (D, E), jnp.float32, -sd(D), sd(D))
        W1 = jax.random.uniform(ks[2], (E, D, H), jnp.float32, -sd(D), sd(D))
        b1 = jax.random.uniform(ks[3], (E, H), jnp.float32, -sd(D), sd(D))
        W2 = jax.random.uniform(ks[4], (E, H, D), jnp.float32, -sd(H), sd(H))
        b2 = jax.random.uniform(ks[5], (E, D), jnp.float32, -sd(H), sd(H))
        gamma = jnp.ones((E, D), jnp.float32)
        beta = jnp.zeros((E, D), jnp.float32)
        return {'x': x, 'Wg': Wg, 'W1': W1, 'b1': b1, 'W2': W2, 'b2': b2, 'gamma': gamma, 'beta': beta}
    _L0_ffn_all = _L0_ffn_setup()
    _L0_ffn_in = {k: v for k, v in _L0_ffn_all.items() if k in ('Wg', 'W1', 'b1', 'W2', 'b2', 'gamma', 'beta')}
    del _L0_ffn_all

    def _L1_attn_setup():
        import jax, jax.numpy as jnp
        import numpy as np
        import math
        D_MODEL = 128
        NUM_HEADS = 8
        LN_EPS = 1e-05
        key = jax.random.key(seed)
        ks = jax.random.split(key, 8)
        B, L, D = (2, 512, D_MODEL)
        x = jax.random.normal(ks[0], (B, L, D), dtype=jnp.float32)
        s = 0.02
        return {'x': x, 'W_qkv': jax.random.normal(ks[1], (D, 3 * D), dtype=jnp.float32) * s, 'b_qkv': jnp.zeros((3 * D,), dtype=jnp.float32), 'W_out': jax.random.normal(ks[2], (D, D), dtype=jnp.float32) * s, 'b_out': jnp.zeros((D,), dtype=jnp.float32), 'decay_logits': jnp.zeros((NUM_HEADS,), dtype=jnp.float32), 'ln_g': jnp.ones((D,), dtype=jnp.float32), 'ln_b': jnp.zeros((D,), dtype=jnp.float32)}
    _L1_attn_all = _L1_attn_setup()
    _L1_attn_in = {k: v for k, v in _L1_attn_all.items() if k in ('W_qkv', 'b_qkv', 'W_out', 'b_out', 'decay_logits', 'ln_g', 'ln_b')}
    del _L1_attn_all

    def _L1_ffn_setup():
        import jax, jax.numpy as jnp
        import numpy as np
        EPS = 1e-05
        NUM_HEADS = 8
        TOP_K = 2
        CAP_FACTOR = 2

        def layernorm(x, g, b):
            m = jnp.mean(x, axis=-1, keepdims=True)
            v = jnp.var(x, axis=-1, keepdims=True)
            return (x - m) * jax.lax.rsqrt(v + EPS) * g + b
        key = jax.random.key(seed)
        ks = jax.random.split(key, 16)
        B, S, H, E, F = (2, 512, 128, 64, 512)
        s = 0.02
        return {'x': jax.random.normal(ks[0], (B, S, H), jnp.float32), 'ln1_g': jnp.ones((H,), jnp.float32), 'ln1_b': jnp.zeros((H,), jnp.float32), 'wq': jax.random.normal(ks[1], (H, H), jnp.float32) * s, 'wk': jax.random.normal(ks[2], (H, H), jnp.float32) * s, 'wv': jax.random.normal(ks[3], (H, H), jnp.float32) * s, 'wo': jax.random.normal(ks[4], (H, H), jnp.float32) * s, 'ln2_g': jnp.ones((H,), jnp.float32), 'ln2_b': jnp.zeros((H,), jnp.float32), 'wr': jax.random.normal(ks[5], (H, E), jnp.float32) * s, 'w1': jax.random.normal(ks[6], (E, H, F), jnp.float32) * s, 'b1': jnp.zeros((E, F), jnp.float32), 'w2': jax.random.normal(ks[7], (E, F, H), jnp.float32) * s, 'b2': jnp.zeros((E, H), jnp.float32)}
    _L1_ffn_all = _L1_ffn_setup()
    _L1_ffn_in = {k: v for k, v in _L1_ffn_all.items() if k in ('ln1_g', 'ln1_b', 'wq', 'wk', 'wv', 'wo', 'ln2_g', 'ln2_b', 'wr', 'w1', 'b1', 'w2', 'b2')}
    del _L1_ffn_all
    return {'x': x, 'L0_tok_w_compress': _L0_tok_in['w_compress'], 'L0_tok_b_compress': _L0_tok_in['b_compress'], 'L0_tok_w_main': _L0_tok_in['w_main'], 'L0_tok_b_main': _L0_tok_in['b_main'], 'L0_tok_w_expand': _L0_tok_in['w_expand'], 'L0_tok_b_expand': _L0_tok_in['b_expand'], 'L0_tok_g_conv_norm': _L0_tok_in['g_conv_norm'], 'L0_tok_b_conv_norm': _L0_tok_in['b_conv_norm'], 'L0_tok_w_ff1': _L0_tok_in['w_ff1'], 'L0_tok_b_ff1': _L0_tok_in['b_ff1'], 'L0_tok_w_ff2': _L0_tok_in['w_ff2'], 'L0_tok_b_ff2': _L0_tok_in['b_ff2'], 'L0_tok_g_ff_norm': _L0_tok_in['g_ff_norm'], 'L0_tok_b_ff_norm': _L0_tok_in['b_ff_norm'], 'L0_attn_Wq': _L0_attn_in['Wq'], 'L0_attn_Wkv': _L0_attn_in['Wkv'], 'L0_attn_Wo': _L0_attn_in['Wo'], 'L0_ffn_Wg': _L0_ffn_in['Wg'], 'L0_ffn_W1': _L0_ffn_in['W1'], 'L0_ffn_b1': _L0_ffn_in['b1'], 'L0_ffn_W2': _L0_ffn_in['W2'], 'L0_ffn_b2': _L0_ffn_in['b2'], 'L0_ffn_gamma': _L0_ffn_in['gamma'], 'L0_ffn_beta': _L0_ffn_in['beta'], 'L1_attn_W_qkv': _L1_attn_in['W_qkv'], 'L1_attn_b_qkv': _L1_attn_in['b_qkv'], 'L1_attn_W_out': _L1_attn_in['W_out'], 'L1_attn_b_out': _L1_attn_in['b_out'], 'L1_attn_decay_logits': _L1_attn_in['decay_logits'], 'L1_attn_ln_g': _L1_attn_in['ln_g'], 'L1_attn_ln_b': _L1_attn_in['ln_b'], 'L1_ffn_ln1_g': _L1_ffn_in['ln1_g'], 'L1_ffn_ln1_b': _L1_ffn_in['ln1_b'], 'L1_ffn_wq': _L1_ffn_in['wq'], 'L1_ffn_wk': _L1_ffn_in['wk'], 'L1_ffn_wv': _L1_ffn_in['wv'], 'L1_ffn_wo': _L1_ffn_in['wo'], 'L1_ffn_ln2_g': _L1_ffn_in['ln2_g'], 'L1_ffn_ln2_b': _L1_ffn_in['ln2_b'], 'L1_ffn_wr': _L1_ffn_in['wr'], 'L1_ffn_w1': _L1_ffn_in['w1'], 'L1_ffn_b1': _L1_ffn_in['b1'], 'L1_ffn_w2': _L1_ffn_in['w2'], 'L1_ffn_b2': _L1_ffn_in['b2']}

def reference(x, L0_tok_w_compress, L0_tok_b_compress, L0_tok_w_main, L0_tok_b_main, L0_tok_w_expand, L0_tok_b_expand, L0_tok_g_conv_norm, L0_tok_b_conv_norm, L0_tok_w_ff1, L0_tok_b_ff1, L0_tok_w_ff2, L0_tok_b_ff2, L0_tok_g_ff_norm, L0_tok_b_ff_norm, L0_attn_Wq, L0_attn_Wkv, L0_attn_Wo, L0_ffn_Wg, L0_ffn_W1, L0_ffn_b1, L0_ffn_W2, L0_ffn_b2, L0_ffn_gamma, L0_ffn_beta, L1_attn_W_qkv, L1_attn_b_qkv, L1_attn_W_out, L1_attn_b_out, L1_attn_decay_logits, L1_attn_ln_g, L1_attn_ln_b, L1_ffn_ln1_g, L1_ffn_ln1_b, L1_ffn_wq, L1_ffn_wk, L1_ffn_wv, L1_ffn_wo, L1_ffn_ln2_g, L1_ffn_ln2_b, L1_ffn_wr, L1_ffn_w1, L1_ffn_b1, L1_ffn_w2, L1_ffn_b2):
    import jax
    import jax.numpy as jnp

    def _L0_tok_ref(x, w_compress, b_compress, w_main, b_main, w_expand, b_expand, g_conv_norm, b_conv_norm, w_ff1, b_ff1, w_ff2, b_ff2, g_ff_norm, b_ff_norm):
        import jax, jax.numpy as jnp
        import numpy as np
        EPS = 1e-05

        def conv1d(x, w, b, stride=1, padding=0):
            out = jax.lax.conv_general_dilated(x, w, window_strides=(stride,), padding=[(padding, padding)], dimension_numbers=('NCH', 'OIH', 'NCH'))
            return out + b[None, :, None]

        def layer_norm(x, g, b):
            mu = jnp.mean(x, axis=-1, keepdims=True)
            var = jnp.mean(jnp.square(x - mu), axis=-1, keepdims=True)
            return (x - mu) * jax.lax.rsqrt(var + EPS) * g + b
        xt = jnp.transpose(x, (0, 2, 1))
        identity = xt
        h = jax.nn.silu(conv1d(xt, w_compress, b_compress))
        h = jax.nn.silu(conv1d(h, w_main, b_main, stride=1, padding=1))
        h = conv1d(h, w_expand, b_expand)
        h = jnp.transpose(h, (0, 2, 1))
        identity = jnp.transpose(identity, (0, 2, 1))
        y = layer_norm(h + identity, g_conv_norm, b_conv_norm)
        ff = jnp.einsum('bth,oh->bto', y, w_ff1) + b_ff1
        ff = jax.nn.gelu(ff, approximate=False)
        ff = jnp.einsum('bto,ho->bth', ff, w_ff2) + b_ff2
        y = layer_norm(ff + y, g_ff_norm, b_ff_norm)
        yt = jnp.transpose(y, (0, 2, 1))
        pooled = jax.lax.reduce_window(yt, -jnp.inf, jax.lax.max, (1, 1, 3), (1, 1, 1), 'VALID')
        return jnp.transpose(pooled, (0, 2, 1))

    def _L0_attn_ref(h, Wq, Wkv, Wo):
        import jax, jax.numpy as jnp
        import numpy as np
        N_HEAD = 8
        D_HEAD = 64
        D_MODEL = 128
        SEQ = 512
        BATCH = 2
        S, B, D = h.shape
        scale = 1.0 / D_HEAD ** 0.5
        q = (h @ Wq.T).reshape(S, B, N_HEAD, D_HEAD)
        kv = h @ Wkv.T
        k, v = jnp.split(kv, 2, axis=-1)
        k = k.reshape(S, B, N_HEAD, D_HEAD)
        v = v.reshape(S, B, N_HEAD, D_HEAD)
        scores = jnp.einsum('qbhd,kbhd->qkbh', q, k) * scale
        causal = jnp.triu(jnp.ones((S, S), dtype=bool), k=1)
        scores = jnp.where(causal[:, :, None, None], jnp.float32(-1000000.0), scores)
        prob = jax.nn.softmax(scores, axis=1)
        attn_vec = jnp.einsum('qkbh,kbhd->qbhd', prob, v).reshape(S, B, N_HEAD * D_HEAD)
        return attn_vec @ Wo.T

    def _L0_ffn_ref(x, Wg, W1, b1, W2, b2, gamma, beta):
        import jax, jax.numpy as jnp
        import numpy as np
        EPS = 1e-05
        TOP_K = 2

        def _moe_forward(x, Wg, W1, b1, W2, b2, gamma, beta):
            B, S, D = x.shape
            xf = x.reshape(-1, D)
            logits = xf @ Wg
            topv, topi = jax.lax.top_k(logits, TOP_K)
            gate_w = jax.nn.softmax(topv, axis=-1)
            h = jax.nn.relu(jnp.einsum('td,edh->teh', xf, W1) + b1[None])
            y = jnp.einsum('teh,ehd->ted', h, W2) + b2[None]
            mu = jnp.mean(y, axis=-1, keepdims=True)
            var = jnp.mean((y - mu) ** 2, axis=-1, keepdims=True)
            y = (y - mu) / jnp.sqrt(var + EPS) * gamma[None] + beta[None]
            y_sel = jnp.take_along_axis(y, topi[:, :, None], axis=1)
            out = jnp.sum(gate_w[:, :, None] * y_sel, axis=1)
            return out.reshape(B, S, D)
        return _moe_forward(x, Wg, W1, b1, W2, b2, gamma, beta)

    def _L1_attn_ref(x, W_qkv, b_qkv, W_out, b_out, decay_logits, ln_g, ln_b):
        import jax, jax.numpy as jnp
        import numpy as np
        import math
        D_MODEL = 128
        NUM_HEADS = 8
        LN_EPS = 1e-05
        B, L, D = x.shape
        H = NUM_HEADS
        E = D // H
        qkv = x @ W_qkv + b_qkv
        q, k, v = jnp.split(qkv, 3, axis=-1)
        q = q.reshape(B, L, H, E)
        k = k.reshape(B, L, H, E)
        v = v.reshape(B, L, H, E)
        q = (jax.nn.elu(q) + 1.0) / math.sqrt(E)
        k = jax.nn.elu(k) + 1.0
        lam = 0.99 + 0.01 * jax.nn.sigmoid(decay_logits)
        lam = lam.reshape(1, 1, H, 1)
        idx = jnp.arange(L, dtype=jnp.float32).reshape(1, L, 1, 1)
        decay_k = lam ** (-idx)
        decay_q = lam ** idx
        k_d = k * decay_k
        kv = jnp.einsum('blhe,blhf->blhef', k_d, v)
        mem = jnp.cumsum(kv, axis=1)
        k_sum = jnp.cumsum(k_d, axis=1)
        q_d = q * decay_q
        num = jnp.einsum('blhe,blhef->blhf', q_d, mem)
        den = jnp.einsum('blhe,blhe->blh', q_d, k_sum)[..., None] + 1e-06
        out = (num / den).reshape(B, L, D)
        out = out @ W_out + b_out
        mu = jnp.mean(out, axis=-1, keepdims=True)
        var = jnp.var(out, axis=-1, keepdims=True)
        return (out - mu) / jnp.sqrt(var + LN_EPS) * ln_g + ln_b

    def _L1_ffn_ref(x, ln1_g, ln1_b, wq, wk, wv, wo, ln2_g, ln2_b, wr, w1, b1, w2, b2):
        import jax, jax.numpy as jnp
        import numpy as np
        EPS = 1e-05
        NUM_HEADS = 8
        TOP_K = 2
        CAP_FACTOR = 2

        def layernorm(x, g, b):
            m = jnp.mean(x, axis=-1, keepdims=True)
            v = jnp.var(x, axis=-1, keepdims=True)
            return (x - m) * jax.lax.rsqrt(v + EPS) * g + b
        B, S, H = x.shape
        NH = NUM_HEADS
        dh = H // NH
        x1 = layernorm(x, ln1_g, ln1_b)
        q = (x1 @ wq).reshape(B, S, NH, dh)
        k = (x1 @ wk).reshape(B, S, NH, dh)
        v = (x1 @ wv).reshape(B, S, NH, dh)
        scores = jnp.einsum('bqhd,bkhd->bhqk', q, k) * dh ** (-0.5)
        p = jax.nn.softmax(scores, axis=-1)
        attn_out = jnp.einsum('bhqk,bkhd->bqhd', p, v).reshape(B, S, H) @ wo
        x = x + attn_out
        x2 = layernorm(x, ln2_g, ln2_b).reshape(B * S, H)
        T = B * S
        E = wr.shape[1]
        C = CAP_FACTOR * (T * TOP_K // E)
        probs = jax.nn.softmax(x2 @ wr, axis=-1)
        gate_v, gate_i = jax.lax.top_k(probs, TOP_K)
        gate_v = gate_v / jnp.sum(gate_v, axis=-1, keepdims=True)
        ef = gate_i.reshape(-1)
        gf = gate_v.reshape(-1)
        oh = jax.nn.one_hot(ef, E, dtype=x2.dtype)
        pos = jnp.sum((jnp.cumsum(oh, axis=0) - oh) * oh, axis=1).astype(jnp.int32)
        keep = (pos < C).astype(x2.dtype)
        posc = jnp.minimum(pos, C - 1)
        tok = jnp.repeat(x2, TOP_K, axis=0) * keep[:, None]
        buf = jnp.zeros((E, C, H), x2.dtype).at[ef, posc].add(tok)
        h = jax.nn.gelu(jnp.einsum('ech,ehf->ecf', buf, w1) + b1[:, None, :])
        y = jnp.einsum('ecf,efh->ech', h, w2) + b2[:, None, :]
        ys = y[ef, posc] * (gf * keep)[:, None]
        moe_out = ys.reshape(T, TOP_K, H).sum(axis=1).reshape(B, S, H)
        return x + moe_out
    h = _L0_tok_ref(x, L0_tok_w_compress, L0_tok_b_compress, L0_tok_w_main, L0_tok_b_main, L0_tok_w_expand, L0_tok_b_expand, L0_tok_g_conv_norm, L0_tok_b_conv_norm, L0_tok_w_ff1, L0_tok_b_ff1, L0_tok_w_ff2, L0_tok_b_ff2, L0_tok_g_ff_norm, L0_tok_b_ff_norm)
    h = h + _L0_attn_ref(_layernorm(h, axis=-1), L0_attn_Wq, L0_attn_Wkv, L0_attn_Wo)
    h = h + _L0_ffn_ref(_layernorm(h, axis=-1), L0_ffn_Wg, L0_ffn_W1, L0_ffn_b1, L0_ffn_W2, L0_ffn_b2, L0_ffn_gamma, L0_ffn_beta)
    h = h + _L1_attn_ref(_layernorm(h, axis=-1), L1_attn_W_qkv, L1_attn_b_qkv, L1_attn_W_out, L1_attn_b_out, L1_attn_decay_logits, L1_attn_ln_g, L1_attn_ln_b)
    h = h + _L1_ffn_ref(_layernorm(h, axis=-1), L1_ffn_ln1_g, L1_ffn_ln1_b, L1_ffn_wq, L1_ffn_wk, L1_ffn_wv, L1_ffn_wo, L1_ffn_ln2_g, L1_ffn_ln2_b, L1_ffn_wr, L1_ffn_w1, L1_ffn_b1, L1_ffn_w2, L1_ffn_b2)
    return h

_drawn_inputs = setup_inputs


def setup_inputs(seed=0):
    import zlib

    import numpy as np

    out = dict(_drawn_inputs(seed))
    spreads = {'L0_tok_b_compress': (0.0, 0.426),
     'L0_tok_b_main': (0.0, 0.1),
     'L0_tok_b_expand': (0.0, 0.1),
     'L0_tok_g_conv_norm': (1.0, 0.2),
     'L0_tok_b_conv_norm': (0.0, 0.1),
     'L0_tok_b_ff1': (0.0, 0.1),
     'L0_tok_b_ff2': (0.0, 0.1),
     'L0_tok_g_ff_norm': (1.0, 0.2),
     'L0_tok_b_ff_norm': (0.0, 0.1),
     'L0_ffn_gamma': (1.0, 0.2),
     'L0_ffn_beta': (0.0, 0.1),
     'L1_attn_b_qkv': (0.0, 0.1),
     'L1_attn_b_out': (0.0, 0.1),
     'L1_attn_decay_logits': (0.0, 0.8),
     'L1_attn_ln_g': (1.0, 0.2),
     'L1_attn_ln_b': (0.0, 0.1),
     'L1_ffn_ln1_g': (1.0, 0.6),
     'L1_ffn_ln1_b': (0.0, 0.8),
     'L1_ffn_ln2_g': (1.0, 0.6),
     'L1_ffn_ln2_b': (0.0, 0.618),
     'L1_ffn_b1': (0.0, 0.8),
     'L1_ffn_b2': (0.0, 0.445)}
    factors = {'L0_tok_w_compress': 2.736,
     'L0_attn_Wq': 4.267,
     'L1_ffn_wq': 8.0,
     'L1_ffn_wk': 8.0,
     'L1_ffn_wv': 3.431,
     'L1_ffn_wo': 3.307,
     'L1_ffn_w1': 5.662,
     'L1_ffn_w2': 5.071}
    for name, (base, spread) in spreads.items():
        noise = np.random.default_rng([zlib.crc32(name.encode()), seed]).standard_normal(out[name].shape)
        drawn = base * np.exp(spread * noise) if base else spread * noise
        out[name] = jnp.asarray(drawn.astype(out[name].dtype))
    for name, factor in factors.items():
        out[name] = (out[name] * factor).astype(out[name].dtype)
    return out
```

```python
from contextlib import ExitStack

import concourse.bass as bass
from concourse import mybir

F32 = mybir.dt.float32
U32 = mybir.dt.uint32
I32 = mybir.dt.int32
ACT = mybir.ActivationFunctionType
ALU = mybir.AluOpType
AX = mybir.AxisListType

P = 128
BATCH = 64
T_IN = 256
SEQ = 254
HALF = 127
D = 128
BN = 64
TOKENS = BATCH * SEQ
POS_PAD = 256
EPS = 1e-5

N_HEAD = 8
D_HEAD = 64
E_HEAD = 16

EXP0 = 8
EXP1 = 64
FF1 = 512
CAP = 1016
assert CAP == 2 * (TOKENS * 2 // EXP1) and CAP == 8 * HALF


def over(ap, n):
    p, f = ap.shape
    return ap.unsqueeze(1).to_broadcast([p, n, f])


def wide(ap, n):
    p, g = ap.shape
    return ap.unsqueeze(2).to_broadcast([p, g, n])


class Place:

    def __init__(self, nc, ctx, phase):
        self.nc, self.ctx, self.phase = nc, ctx, phase
        self.sems = []

    def sb(self, name, shape, dt=F32):
        return self.ctx.enter_context(self.nc.sbuf_tensor(f"{self.phase}_sb_{name}", shape, dt))

    def banks(self, name, n):
        return [self.ctx.enter_context(self.nc.psum_tensor(f"{self.phase}_bank_{name}{i}", [P, 512], F32))
                for i in range(n)]

    def sem(self, name):
        self.sems.append(self.nc.alloc_semaphore(f"{self.phase}_{name}"))
        return self.sems[-1]

    def close(self):
        self.nc.clear_and_free_semaphores(self.sems)
        self.nc.all_engine_barrier()


class Signal:

    AHEAD = 2

    def __init__(self, sem, per=1):
        self.sem, self.per = sem, per

    def opened(self, eng):
        eng.sem_inc(self.sem, self.AHEAD * self.per)

    def count(self, unit, k=None, back=0):
        k = self.per if k is None else k
        return unit * self.per + (self.AHEAD - back) * self.per + k


class Landed:

    def __init__(self, sem, dmas, ahead=1):
        self.sem, self.all, self.ahead = sem, 16 * dmas, ahead

    def opened(self, eng):
        eng.sem_inc(self.sem, self.ahead * self.all)

    def count(self, unit, parity, back=0):
        return (unit - parity) * (self.all // 2) + (1 + self.ahead - back) * self.all

    def final(self, units):
        return (units // 2 + self.ahead) * self.all


def in_lanes(eng, units, stages, body):
    lead = stages - 1 + (stages - 1) % 2
    turns = (units - lead) // 2

    def step(first, fixed):
        body([first - s if 0 <= fixed - s < units else None for s in range(stages)],
             [(fixed - s) % 2 for s in range(stages)])

    for n in range(lead):
        step(n, n)
    with eng.Fori(0, turns) as turn:
        for odd in range(2):
            step(turn * 2 + (lead + odd), lead + odd)
    for n in range(lead + 2 * turns, units + stages - 1):
        step(n, n)


def load_rows(eng, dst, h, unit, landed):
    for b in range(2):
        eng.dma_start(dst[:, 2 * b:2 * b + 2, :],
                      h[bass.ds(unit * 2 + b, 1), 0:SEQ, :].rearrange("b (c p) d -> p (b c) d", p=HALF)).then_inc(landed.sem, 16)


def store_rows(eng, h, src, unit, landed):
    for b in range(2):
        eng.dma_start(h[bass.ds(unit * 2 + b, 1), 0:SEQ, :].rearrange("b (c p) d -> p (b c) d", p=HALF),
                      src[:, 2 * b:2 * b + 2, :]).then_inc(landed.sem, 16)


class Norm:

    def __init__(self, pl, tiles, rows):
        self.tiles, self.rows = tiles, rows
        sb, sem = pl.sb, pl.sem
        self.x = [sb(f"norm_x{b}", [rows, tiles, D]) for b in range(2)]
        self.st = [sb(f"norm_st{b}", [rows, tiles, 6]) for b in range(2)]
        self.mv = [sb(f"norm_mv{b}", [rows, tiles, 2]) for b in range(2)]
        self.rstd = [sb(f"norm_rstd{b}", [rows, tiles]) for b in range(2)]
        self.y = [sb(f"norm_y{b}", [rows, tiles, D]) for b in range(2)]
        self.stats = Signal(sem("norm_stats"), tiles)
        self.moments = Signal(sem("norm_moments"), tiles)
        self.var_eps = Signal(sem("norm_var_eps"))
        self.rstd_ready = Signal(sem("norm_rstd_ready"))
        self.ready = Signal(sem("norm_ready"))


def norm_moments(nc, dve, nm, u, b, t, passed):
    nc.vector.bn_stats(nm.st[b][:, t, :], nm.x[b][:, t, :]).then_inc(nm.stats.sem, 1)
    dve.wait_ge(nm.stats.sem, nm.stats.count(u, t + 1))
    dve.sem_inc(passed, 1)
    nc.vector.bn_aggr(nm.mv[b][:, t, :], nm.st[b][:, t, :]).then_inc(nm.moments.sem, 1)


def norm_rows(nc, pool, nm, u, b, eps, minus_half, passed, read):
    n = nm.tiles
    pool.wait_ge(nm.moments.sem, nm.moments.count(u))
    nc.gpsimd.tensor_tensor(nm.rstd[b][:, :], nm.mv[b][:, :, 1], eps[0:nm.rows, 0:n], ALU.add).then_inc(nm.var_eps.sem, 1)
    pool.wait_ge(nm.var_eps.sem, nm.var_eps.count(u))
    nc.gpsimd.tensor_tensor(nm.rstd[b][:, :], nm.rstd[b][:, :], minus_half[0:nm.rows, 0:n], ALU.pow).then_inc(nm.rstd_ready.sem, 1)
    pool.wait_ge(nm.rstd_ready.sem, nm.rstd_ready.count(u))
    pool.wait_ge(read.sem, read.count(u, back=2))
    pool.sem_inc(passed, 1)
    for t in range(n):
        last = nc.gpsimd.tensor_scalar(nm.y[b][:, t, :], nm.x[b][:, t, :], nm.mv[b][:, t, 0:1], nm.rstd[b][:, t:t + 1],
                                       ALU.subtract, ALU.mult)
    last.then_inc(nm.ready.sem, 1)


def phase_token_mixer(nc, x, ident, w_compress, w_main, w_expand, w_ff1, w_ff2, b_compress, b_main, b_ff1,
                      g1_col, b1_col, g2_col, b2_col, b_expand, g1_row, b1_row, b_ff2, h_out, slots):
    UNITS = 2
    STEPS = BATCH // 2 // UNITS
    TILES = 4
    N = TILES * P
    with ExitStack() as ctx:
        pl = Place(nc, ctx, "tok")
        sb, sem = pl.sb, pl.sem
        idn = sb("ident", [P, P])
        wc = sb("wc", [D, BN])
        wm = sb("wm", [BN, 3, BN])
        we = sb("we", [BN, D])
        w1 = sb("w1", [D, BN])
        w2 = sb("w2", [BN, D])
        cols = sb("cols", [P, 7])
        rows = sb("rows", [P, 4, D])
        x_sb = [sb(f"x{u}", [P, TILES, D]) for u in range(UNITS)]
        x_be = [sb(f"xbe{u}", [P, TILES, D]) for u in range(UNITS)]
        xT = [sb(f"xT{u}", [D, N]) for u in range(UNITS)]
        h1 = [sb(f"h1{u}", [BN, 2, T_IN + 2]) for u in range(UNITS)]
        h2 = [sb(f"h2{u}", [BN, N]) for u in range(UNITS)]
        sum1 = [sb(f"sum1{u}", [P, TILES, D]) for u in range(UNITS)]
        st = [sb(f"st{u}", [P, TILES, 6]) for u in range(UNITS)]
        mv = [sb(f"mv{u}", [P, TILES, 2]) for u in range(UNITS)]
        rstd = [sb(f"rstd{u}", [P, TILES]) for u in range(UNITS)]
        eps = sb("eps", [P, TILES])
        minus_half = sb("minus_half", [P, TILES])
        n1 = [sb(f"n1{u}", [P, TILES, D]) for u in range(UNITS)]
        res1 = [sb(f"res1{u}", [P, TILES, D]) for u in range(UNITS)]
        yT = [sb(f"yT{u}", [D, N]) for u in range(UNITS)]
        gel = [sb(f"gel{u}", [BN, N]) for u in range(UNITS)]
        zT = [sb(f"zT{u}", [D, 2, T_IN]) for u in range(UNITS)]
        pair = [sb(f"pair{u}", [D, 2, T_IN - 1]) for u in range(UNITS)]
        pooled = [sb(f"pooled{u}", [D, 2, SEQ]) for u in range(UNITS)]
        h_sb = [sb(f"h{u}", [HALF, TILES, D]) for u in range(UNITS)]
        ps = [pl.banks(f"ps{u}_", 4) for u in range(UNITS)]

        ZERO_ROWS = EXP1 * CAP // STEPS
        ZERO_LINES = ZERO_ROWS // (P // 4)
        zeros = sb("zeros", [P, (P // 4) * D])
        zeros_set = sem("zeros_set")
        zeros_stored = sem("zeros_stored")

        weights_in = sem("weights_in")
        pe_passed, dve_passed = sem("pe_passed"), sem("dve_passed")
        x_in = [sem(f"x_in{u}") for u in range(UNITS)]
        x_free = sem("x_free")
        x_turned = sem("x_turned")
        xT_ready = sem("xT_ready")
        compress_done = sem("compress_done")
        pad_zero = sem("pad_zero")
        h1_ready = sem("h1_ready")
        main_done = sem("main_done")
        h2_ready = sem("h2_ready")
        expand_done = sem("expand_done")
        xbe_ready = sem("xbe_ready")
        sum_ready = sem("sum_ready")
        stats_ready = sem("stats_ready")
        moments_ready = sem("moments_ready")
        var_eps_ready = sem("var_eps_ready")
        constants_set = sem("constants_set")
        rstd_ready = sem("rstd_ready")
        norm_ready = sem("norm_ready")
        scaled_ready = sem("scaled_ready")
        res_ready = sem("res_ready")
        y_turned = sem("y_turned")
        yT_ready = sem("yT_ready")
        ff1_done = sem("ff1_done")
        gelu_ready = sem("gelu_ready")
        ff2_done = sem("ff2_done")
        z_turned = sem("z_turned")
        zT_ready = sem("zT_ready")
        pair_ready = sem("pair_ready")
        pooled_ready = sem("pooled_ready")
        pooled_turned = sem("pooled_turned")
        h_ready = sem("h_ready")
        h_stored = [sem(f"h_stored{u}") for u in range(UNITS)]
        ff_res_ready = sem("ff_res_ready")
        WEIGHTS = 17

        with nc.Block() as block:

            @block.sync
            def _(sp):
                for dst, src in ((idn[:, :], ident), (wc[:, :], w_compress), (wm[:, :, :], w_main),
                                 (we[:, :], w_expand), (w1[:, :], w_ff1), (w2[:, :], w_ff2),
                                 (cols[0:BN, 0:1], b_compress), (cols[0:BN, 1:2], b_main),
                                 (cols[0:BN, 2:3], b_ff1), (cols[:, 3:4], g1_col), (cols[:, 4:5], b1_col),
                                 (cols[:, 5:6], g2_col), (cols[:, 6:7], b2_col),
                                 (rows[:, 0, :], b_expand.partition_broadcast(P)),
                                 (rows[:, 1, :], g1_row.partition_broadcast(P)),
                                 (rows[:, 2, :], b1_row.partition_broadcast(P)),
                                 (rows[:, 3, :], b_ff2.partition_broadcast(P))):
                    sp.dma_start(dst, src).then_inc(weights_in, 16)
                def load(step):
                    for u in range(UNITS):
                        sp.wait_ge(x_free, step * UNITS + u + 1)
                        for b in range(2):
                            sp.dma_start(x_sb[u][:, 2 * b:2 * b + 2, :],
                                         x[bass.ds((step * UNITS + u) * 2 + b, 1), :, :].rearrange(
                                             "b (c p) d -> p (b c) d", p=P)).then_inc(x_in[u], 16)

                def store(step):
                    for u in range(UNITS):
                        sp.wait_ge(h_ready, step * UNITS + UNITS + u + 1)
                        for b in range(2):
                            sp.dma_start(h_out[0:SEQ, bass.ds((step * UNITS + u) * 2 + b, 1), :].rearrange(
                                "(c p) b d -> p (c b) d", p=HALF), h_sb[u][:, 2 * b:2 * b + 2, :]).then_inc(h_stored[u], 16)

                load(0)
                with sp.Fori(1, STEPS) as step:
                    load(step)
                    store(step - 1)
                store(STEPS - 1)
                for u in range(UNITS):
                    sp.wait_ge(h_stored[u], 32 * STEPS + 32)

            @block.tensor
            def _(pe):
                pe.wait_ge(weights_in, 16 * WEIGHTS)
                with pe.Fori(0, STEPS) as step:
                    turn = [step * UNITS + u + 1 for u in range(UNITS)]
                    for u in range(UNITS):
                        pe.wait_ge(x_in[u], step * 32 + 32)
                        pe.wait_ge(h_ready, turn[u])
                        for c in range(TILES):
                            last = nc.tensor.transpose(ps[u][0][:, c * P:(c + 1) * P], x_sb[u][:, c, :], idn[:, :])
                        last.then_inc(x_turned, 1)
                    for u in range(UNITS):
                        pe.wait_ge(xT_ready, turn[u])
                        nc.tensor.matmul(ps[u][1][0:BN, :], wc[:, :], xT[u][:, :], start=True, stop=True).then_inc(compress_done, 1)
                    for u in range(UNITS):
                        pe.wait_ge(h1_ready, turn[u])
                        pe.sem_inc(pe_passed, 1)
                        for tap in range(3):
                            last = nc.tensor.matmul(ps[u][2][0:BN, :].rearrange("p (b t) -> p b t", b=2), wm[:, tap, :],
                                                    h1[u][:, :, tap:tap + T_IN], start=tap == 0, stop=tap == 2)
                        last.then_inc(main_done, 1)
                    for u in range(UNITS):
                        pe.wait_ge(h2_ready, turn[u])
                        for c in range(TILES):
                            last = nc.tensor.matmul(ps[u][3][:, c * P:(c + 1) * P], h2[u][:, c * P:(c + 1) * P],
                                                    we[:, :], start=True, stop=True)
                        last.then_inc(expand_done, 1)
                    for u in range(UNITS):
                        pe.wait_ge(norm_ready, 2 * step * UNITS + u + 1)
                        for c in range(TILES):
                            last = nc.tensor.transpose(ps[u][0][:, c * P:(c + 1) * P], n1[u][:, c, :], idn[:, :])
                        last.then_inc(y_turned, 1)
                    for u in range(UNITS):
                        pe.wait_ge(yT_ready, turn[u])
                        nc.tensor.matmul(ps[u][1][0:BN, :], w1[:, :], yT[u][:, :], start=True, stop=True).then_inc(ff1_done, 1)
                    for u in range(UNITS):
                        pe.wait_ge(gelu_ready, turn[u])
                        for c in range(TILES):
                            last = nc.tensor.matmul(ps[u][2][:, c * P:(c + 1) * P], gel[u][:, c * P:(c + 1) * P],
                                                    w2[:, :], start=True, stop=True)
                        last.then_inc(ff2_done, 1)
                    for u in range(UNITS):
                        pe.wait_ge(norm_ready, 2 * step * UNITS + UNITS + u + 1)
                        for c in range(TILES):
                            last = nc.tensor.transpose(ps[u][3][:, c * P:(c + 1) * P], n1[u][:, c, :], idn[:, :])
                        last.then_inc(z_turned, 1)
                    for u in range(UNITS):
                        pe.wait_ge(pooled_ready, turn[u])
                        for c in range(TILES):
                            last = nc.tensor.transpose(ps[u][0][0:HALF, c * P:(c + 1) * P],
                                                       pooled[u][:, c // 2, (c % 2) * HALF:(c % 2 + 1) * HALF], idn[:, :])
                        last.then_inc(pooled_turned, 1)

            @block.scalar
            def _(act):
                act.sem_inc(h_ready, UNITS)
                act.wait_ge(pad_zero, 1)
                act.wait_ge(zeros_set, 1)
                act.dma_start(h_out[SEQ:POS_PAD, :, :].rearrange("p b d -> (p b) d"), zeros[:, 0:D]).then_inc(zeros_stored, 16)
                with act.Fori(0, STEPS) as step:
                    act.dma_start(slots[bass.ds(step * ZERO_ROWS, ZERO_ROWS), :].rearrange("(p t) d -> p (t d)", p=ZERO_LINES),
                                  zeros[0:ZERO_LINES, :]).then_inc(zeros_stored, 16)
                    turn = [step * UNITS + u + 1 for u in range(UNITS)]
                    for u in range(UNITS):
                        act.wait_ge(x_turned, turn[u])
                        nc.scalar.copy(xT[u][:, :], ps[u][0][:, :]).then_inc(xT_ready, 1)
                    for u in range(UNITS):
                        act.wait_ge(compress_done, turn[u])
                        nc.scalar.activation(h1[u][:, :, 1:T_IN + 1], ps[u][1][0:BN, :].rearrange("p (b t) -> p b t", b=2),
                                             ACT.Silu, bias=cols[0:BN, 0:1]).then_inc(h1_ready, 1)
                    for u in range(UNITS):
                        act.wait_ge(main_done, turn[u])
                        nc.scalar.activation(h2[u][:, :], ps[u][2][0:BN, :], ACT.Silu, bias=cols[0:BN, 1:2]).then_inc(h2_ready, 1)
                    for u in range(UNITS):
                        act.wait_ge(y_turned, turn[u])
                        nc.scalar.activation(yT[u][:, :], ps[u][0][:, :], ACT.Identity, bias=cols[:, 4:5],
                                             scale=cols[:, 3:4]).then_inc(yT_ready, 1)
                    for u in range(UNITS):
                        act.wait_ge(ff1_done, turn[u])
                        nc.scalar.activation(gel[u][:, :], ps[u][1][0:BN, :], ACT.Gelu, bias=cols[0:BN, 2:3]).then_inc(gelu_ready, 1)
                    for u in range(UNITS):
                        act.wait_ge(z_turned, turn[u])
                        nc.scalar.activation(zT[u][:, :, :].rearrange("p b t -> p (b t)"), ps[u][3][:, :], ACT.Identity,
                                             bias=cols[:, 6:7], scale=cols[:, 5:6]).then_inc(zT_ready, 1)
                    for u in range(UNITS):
                        act.wait_ge(pooled_turned, turn[u])
                        act.wait_ge(h_stored[u], step * 32 + 32)
                        nc.scalar.copy(h_sb[u][:, :, :].rearrange("p c d -> p (c d)"), ps[u][0][0:HALF, :]).then_inc(h_ready, 1)
                act.wait_ge(zeros_stored, 16 * (STEPS + 1))

            @block.vector
            def _(dve):
                nc.vector.memset(zeros[:, :], 0.0).then_inc(zeros_set, 1)
                for u in range(UNITS):
                    nc.vector.memset(h1[u][:, :, 0:1], 0.0)
                    last = nc.vector.memset(h1[u][:, :, T_IN + 1:T_IN + 2], 0.0)
                last.then_inc(pad_zero, 1)
                dve.sem_inc(x_free, UNITS)
                for u in range(UNITS):
                    dve.sem_inc(h_stored[u], 32)

                def norm(u, n):
                    dve.wait_ge(sum_ready, n)
                    for c in range(TILES):
                        last = nc.vector.bn_stats(st[u][:, c, :], sum1[u][:, c, :])
                    last.then_inc(stats_ready, 1)
                    dve.wait_ge(stats_ready, n)
                    dve.sem_inc(dve_passed, 1)
                    for c in range(TILES):
                        last = nc.vector.bn_aggr(mv[u][:, c, :], st[u][:, c, :])
                    last.then_inc(moments_ready, 1)

                def norm_end(u, n):
                    dve.wait_ge(rstd_ready, n)
                    for c in range(TILES):
                        last = nc.vector.tensor_scalar(n1[u][:, c, :], sum1[u][:, c, :], mv[u][:, c, 0:1], rstd[u][:, c:c + 1],
                                                       ALU.subtract, ALU.mult)
                    last.then_inc(norm_ready, 1)

                with dve.Fori(0, STEPS) as step:
                    turn = [step * UNITS + u + 1 for u in range(UNITS)]
                    nth = [2 * step * UNITS + u + 1 for u in range(2 * UNITS)]
                    for u in range(UNITS):
                        dve.wait_ge(expand_done, turn[u])
                        dve.wait_ge(xbe_ready, turn[u])
                        nc.vector.tensor_tensor(sum1[u][:, :, :].rearrange("p c d -> p (c d)"), ps[u][3][:, :],
                                                x_be[u][:, :, :].rearrange("p c d -> p (c d)"), ALU.add).then_inc(sum_ready, 1)
                    for u in range(UNITS):
                        norm(u, nth[u])
                    for u in range(UNITS):
                        norm_end(u, nth[u])
                    for u in range(UNITS):
                        dve.wait_ge(ff2_done, turn[u])
                        dve.wait_ge(res_ready, turn[u])
                        nc.vector.tensor_tensor(sum1[u][:, :, :].rearrange("p c d -> p (c d)"), ps[u][2][:, :],
                                                res1[u][:, :, :].rearrange("p c d -> p (c d)"), ALU.add).then_inc(sum_ready, 1)
                    for u in range(UNITS):
                        norm(u, nth[UNITS + u])
                    for u in range(UNITS):
                        norm_end(u, nth[UNITS + u])
                    for u in range(UNITS):
                        dve.wait_ge(zT_ready, turn[u])
                        nc.vector.tensor_tensor(pair[u][:, :, :], zT[u][:, :, 0:T_IN - 1], zT[u][:, :, 1:T_IN], ALU.max).then_inc(pair_ready, 1)
                        dve.wait_ge(pair_ready, turn[u])
                        nc.vector.tensor_tensor(pooled[u][:, :, :], pair[u][:, :, 0:SEQ], zT[u][:, :, 2:T_IN], ALU.max).then_inc(pooled_ready, 1)

            @block.gpsimd
            def _(pool):
                nc.gpsimd.memset(eps[:, :], EPS)
                nc.gpsimd.memset(minus_half[:, :], -0.5).then_inc(constants_set, 1)
                pool.wait_ge(constants_set, 1)
                pool.wait_ge(weights_in, 16 * WEIGHTS)
                nc.gpsimd.tensor_tensor(rows[:, 2, :], rows[:, 2, :], rows[:, 3, :], ALU.add).then_inc(ff_res_ready, 1)
                pool.wait_ge(ff_res_ready, 1)
                with pool.Fori(0, STEPS) as step:
                    turn = [step * UNITS + u + 1 for u in range(UNITS)]
                    nth = [2 * step * UNITS + u + 1 for u in range(2 * UNITS)]
                    for u in range(UNITS):
                        pool.wait_ge(x_in[u], step * 32 + 32)
                        nc.gpsimd.tensor_tensor(x_be[u][:, :, :], x_sb[u][:, :, :], over(rows[:, 0, :], TILES), ALU.add).then_inc(xbe_ready, 1)
                    for u in range(UNITS):
                        pool.wait_ge(moments_ready, nth[u])
                        nc.gpsimd.tensor_tensor(rstd[u][:, :], mv[u][:, :, 1], eps[:, :], ALU.add).then_inc(var_eps_ready, 1)
                        pool.wait_ge(var_eps_ready, nth[u])
                        nc.gpsimd.tensor_tensor(rstd[u][:, :], rstd[u][:, :], minus_half[:, :], ALU.pow).then_inc(rstd_ready, 1)
                    for u in range(UNITS):
                        pool.wait_ge(norm_ready, nth[u])
                        nc.gpsimd.tensor_tensor(res1[u][:, :, :], n1[u][:, :, :], over(rows[:, 1, :], TILES), ALU.mult).then_inc(scaled_ready, 1)
                        pool.wait_ge(x_turned, turn[u])
                        pool.sem_inc(x_free, 1)
                    for u in range(UNITS):
                        pool.wait_ge(scaled_ready, turn[u])
                        nc.gpsimd.tensor_tensor(res1[u][:, :, :], res1[u][:, :, :], over(rows[:, 2, :], TILES), ALU.add).then_inc(res_ready, 1)
                    for u in range(UNITS):
                        pool.wait_ge(moments_ready, nth[UNITS + u])
                        nc.gpsimd.tensor_tensor(rstd[u][:, :], mv[u][:, :, 1], eps[:, :], ALU.add).then_inc(var_eps_ready, 1)
                        pool.wait_ge(var_eps_ready, nth[UNITS + u])
                        nc.gpsimd.tensor_tensor(rstd[u][:, :], rstd[u][:, :], minus_half[:, :], ALU.pow).then_inc(rstd_ready, 1)

        pl.close()


def phase_batch_attention(nc, h_in, ident, mask, wq, wk, wv, wo, h_out):
    UNITS = POS_PAD // 8
    TILES = 4
    N = TILES * P
    PAIRS = N_HEAD // 2
    NORM, TURN, PROJ, SOFT, OUT = range(5)
    with ExitStack() as ctx:
        pl = Place(nc, ctx, "bat")
        sb, sem = pl.sb, pl.sem
        idn = sb("ident", [P, P])
        msk = sb("mask", [P, N])
        wq_sb = sb("wq", [D, PAIRS, P])
        wk_sb = sb("wk", [D, PAIRS, P])
        wv_sb = sb("wv", [D, N])
        wo_sb = sb("wo", [P, PAIRS, D])
        eps = sb("eps", [P, TILES])
        minus_half = sb("minus_half", [P, TILES])

        def two(name, shape):
            return [sb(f"{name}{b}", shape) for b in range(2)]

        h_sb = two("h", [P, TILES, D])
        st = two("st", [P, TILES, 6])
        mv = two("mv", [P, TILES, 2])
        rstd = two("rstd", [P, TILES])
        hn = two("hn", [P, TILES, D])
        hnT = two("hnT", [D, N])
        qT = two("qT", [P, PAIRS, N])
        kT = two("kT", [P, PAIRS, N])
        v = two("v", [P, TILES, N])
        sc = two("sc", [P, N])
        top = two("top", [P, 8])
        ex = two("ex", [P, N])
        total = two("total", [P, 8])
        inv = two("inv", [P, 8])
        prob = two("prob", [P, TILES, N])
        prT = two("prT", [P, N])
        oT = two("oT", [P, N])
        res = two("res", [P, TILES, D])
        out = two("out", [P, TILES, D])

        ps_turn, = pl.banks("turn", 1)
        ps_proj = pl.banks("proj", 2)
        ps_sc = pl.banks("sc", 2)
        ps_prT, = pl.banks("prT", 1)
        ps_oT = ctx.enter_context(nc.psum_tensor("bat_bank_oT", [P, 2, N], F32))

        def ps_out(t):
            return ps_oT[:, t // 2, 256 + (t % 2) * D:256 + (t % 2 + 1) * D]


        weights_in = sem("weights_in")
        WEIGHTS = 6
        pe_passed, dve_passed, pool_passed = (sem(f"{e}_passed") for e in ("pe", "dve", "pool"))
        constants_set = sem("constants_set")
        h_in_s = [Landed(sem(f"h_in_s{b}"), 2) for b in range(2)]
        res_in = [Landed(sem(f"res_in{b}"), 2) for b in range(2)]
        stored = [Landed(sem(f"stored{b}"), 2) for b in range(2)]
        stats = Signal(sem("stats"), TILES)
        moments = Signal(sem("moments"), TILES)
        var_eps = Signal(sem("var_eps"))
        rstd_ready = Signal(sem("rstd_ready"))
        normed = Signal(sem("normed"))
        turned = Signal(sem("turned"))
        hnT_ready = Signal(sem("hnT_ready"))
        q_done = Signal(sem("q_done"), TILES)
        k_done = Signal(sem("k_done"), TILES)
        v_done = Signal(sem("v_done"), TILES)
        q_ready = Signal(sem("q_ready"), TILES)
        k_ready = Signal(sem("k_ready"), TILES)
        v_ready = Signal(sem("v_ready"), TILES)
        sc_done = Signal(sem("sc_done"), TILES)
        sc_masked = Signal(sem("sc_masked"), TILES)
        top_ready = Signal(sem("top_ready"), TILES)
        sc_ready = Signal(sem("sc_ready"), TILES)
        ex_ready = Signal(sem("ex_ready"), TILES)
        total_ready = Signal(sem("total_ready"), TILES)
        inv_ready = Signal(sem("inv_ready"), TILES)
        prob_ready = Signal(sem("prob_ready"), TILES)
        prob_turned = Signal(sem("prob_turned"), TILES)
        prT_ready = Signal(sem("prT_ready"), TILES)
        oT_done = Signal(sem("oT_done"), TILES)
        oT_ready = Signal(sem("oT_ready"), TILES)
        out_done = Signal(sem("out_done"), TILES)
        out_ready = Signal(sem("out_ready"), TILES)

        with nc.Block() as block:

            @block.sync
            def _(sp):
                for dst, src in ((idn[:, :], ident), (msk[:, :], mask), (wq_sb[:, :, :].rearrange("p j m -> p (j m)"), wq),
                                 (wk_sb[:, :, :].rearrange("p j m -> p (j m)"), wk), (wv_sb[:, :], wv),
                                 (wo_sb[:, :, :], wo.rearrange("(j p) d -> p j d", p=P))):
                    sp.dma_start(dst, src).then_inc(weights_in, 16)
                for b in range(2):
                    h_in_s[b].opened(sp)
                    res_in[b].opened(sp)
                    stored[b].opened(sp)

                def body(n, par):
                    if n[NORM] is not None:
                        u, b = n[NORM], par[NORM]
                        sp.wait_ge(normed.sem, normed.count(u, back=2))
                        for odd in range(2):
                            sp.dma_start(h_sb[b][odd * BATCH:(odd + 1) * BATCH, :, :],
                                         h_in[bass.ds(u * 8, 8), :, :].rearrange("(t two) b d -> two b t d", two=2)[odd]
                                         ).then_inc(h_in_s[b].sem, 16)
                    if n[SOFT] is not None:
                        u, b = n[SOFT], par[SOFT]
                        sp.wait_ge(out_ready.sem, out_ready.count(u, back=2))
                        for odd in range(2):
                            sp.dma_start(res[b][odd * BATCH:(odd + 1) * BATCH, :, :],
                                         h_in[bass.ds(u * 8, 8), :, :].rearrange("(t two) b d -> two b t d", two=2)[odd]
                                         ).then_inc(res_in[b].sem, 16)
                    if n[OUT] is not None:
                        u, b = n[OUT], par[OUT]
                        sp.wait_ge(out_ready.sem, out_ready.count(u))
                        for odd in range(2):
                            sp.dma_start(h_out[:, bass.ds(u * 8, 8), :].rearrange("b (t two) d -> two b t d", two=2)[odd],
                                         out[b][odd * BATCH:(odd + 1) * BATCH, :, :]).then_inc(stored[b].sem, 16)

                in_lanes(sp, UNITS, 5, body)
                for b in range(2):
                    sp.wait_ge(stored[b].sem, stored[b].final(UNITS))

            @block.tensor
            def _(pe):
                for s in (turned, q_done, k_done, v_done, sc_done, prob_turned, oT_done, out_done):
                    s.opened(pe)
                pe.wait_ge(weights_in, 16 * WEIGHTS)

                def body(n, par):
                    for t in range(TILES):
                        if n[OUT] is not None:
                            u, b = n[OUT], par[OUT]
                            pe.wait_ge(prob_ready.sem, prob_ready.count(u, t + 1))
                            pe.wait_ge(prT_ready.sem, prT_ready.count(u, t))
                            for j in range(PAIRS):
                                last = nc.tensor.transpose(ps_prT[:, j * P:(j + 1) * P], prob[b][:, t, j * P:(j + 1) * P], idn[:, :])
                            last.then_inc(prob_turned.sem, 1)
                        if n[PROJ] is not None:
                            u, b = n[PROJ], par[PROJ]
                            pe.wait_ge(hnT_ready.sem, hnT_ready.count(u))
                            pe.wait_ge(v_ready.sem, v_ready.count(u, t))
                            nc.tensor.matmul(ps_proj[0][:, :], wq_sb[:, t, :], hnT[b][:, :], start=True, stop=True).then_inc(q_done.sem, 1)
                        if n[SOFT] is not None:
                            u, b = n[SOFT], par[SOFT]
                            for s in (q_ready, k_ready) if t == 0 else ():
                                pe.wait_ge(s.sem, s.count(u))
                            pe.wait_ge(sc_masked.sem, sc_masked.count(u, t - 1))
                            pe.sem_inc(pe_passed, 1)
                            for j in range(PAIRS):
                                for pos in range(2):
                                    for hh in range(2):
                                        half = slice(hh * 64, hh * 64 + 64)
                                        at = (2 * t + pos) * BATCH
                                        last = nc.tensor.matmul(
                                            ps_sc[t % 2][half, (2 * j + pos) * 64:(2 * j + pos + 1) * 64],
                                            qT[b][half, j, at:at + BATCH], kT[b][half, j, at:at + BATCH],
                                            start=True, stop=True)
                            last.then_inc(sc_done.sem, 1)
                        if n[OUT] is not None:
                            u, b = n[OUT], par[OUT]
                            pe.wait_ge(prT_ready.sem, prT_ready.count(u, t + 1))
                            pe.wait_ge(oT_ready.sem, oT_ready.count(u, t))
                            pe.sem_inc(pe_passed, 1)
                            for j in range(PAIRS):
                                for pos in range(2):
                                    for hh in range(2):
                                        rows = slice(pos * 64, pos * 64 + 64)
                                        last = nc.tensor.matmul(
                                            ps_oT[hh * 64:hh * 64 + 64, pos, j * 64:j * 64 + 64],
                                            v[b][rows, t, (2 * j + hh) * D_HEAD:(2 * j + hh + 1) * D_HEAD],
                                            prT[t % 2][rows, j * P + hh * 64:j * P + hh * 64 + 64],
                                            start=True, stop=True)
                            last.then_inc(oT_done.sem, 1)
                        if n[PROJ] is not None:
                            u, b = n[PROJ], par[PROJ]
                            pe.wait_ge(k_ready.sem, k_ready.count(u, t))
                            nc.tensor.matmul(ps_proj[1][:, :], wk_sb[:, t, :], hnT[b][:, :], start=True, stop=True).then_inc(k_done.sem, 1)
                            pe.wait_ge(q_ready.sem, q_ready.count(u, t + 1))
                            nc.tensor.matmul(ps_proj[0][:, :], hnT[b][:, t * P:(t + 1) * P], wv_sb[:, :],
                                             start=True, stop=True).then_inc(v_done.sem, 1)
                        if n[OUT] is not None:
                            u, b = n[OUT], par[OUT]
                            pe.wait_ge(oT_ready.sem, oT_ready.count(u, t + 1))
                            pe.wait_ge(out_ready.sem, out_ready.count(u, t + 1, back=1))
                            for j in range(PAIRS):
                                last = nc.tensor.matmul(ps_out(t), oT[t % 2][:, j * P:(j + 1) * P],
                                                        wo_sb[:, j, :], start=j == 0, stop=j == PAIRS - 1)
                            last.then_inc(out_done.sem, 1)
                    if n[TURN] is not None:
                        u, b = n[TURN], par[TURN]
                        pe.wait_ge(normed.sem, normed.count(u))
                        pe.wait_ge(hnT_ready.sem, hnT_ready.count(u, back=1))
                        for t in range(TILES):
                            last = nc.tensor.transpose(ps_turn[:, t * P:(t + 1) * P], hn[b][:, t, :], idn[:, :])
                        last.then_inc(turned.sem, 1)

                in_lanes(pe, UNITS, 5, body)

            @block.scalar
            def _(act):
                for s in (hnT_ready, q_ready, k_ready, v_ready, ex_ready, oT_ready):
                    s.opened(act)

                def body(n, par):
                    for t in range(TILES):
                        if n[PROJ] is not None:
                            u, b = n[PROJ], par[PROJ]
                            act.wait_ge(q_done.sem, q_done.count(u, t + 1))
                            act.wait_ge(sc_done.sem, sc_done.count(u, back=2))
                            nc.scalar.activation(qT[b][:, t, :], ps_proj[0][:, :], ACT.Copy, scale=D_HEAD ** -0.5).then_inc(q_ready.sem, 1)
                        if n[SOFT] is not None:
                            u, b = n[SOFT], par[SOFT]
                            act.wait_ge(sc_ready.sem, sc_ready.count(u, t + 1))
                            act.wait_ge(prob_ready.sem, prob_ready.count(u, t - 1))
                            nc.scalar.activation(ex[t % 2][:, :], sc[t % 2][:, :], ACT.Exp).then_inc(ex_ready.sem, 1)
                        if n[OUT] is not None:
                            u, b = n[OUT], par[OUT]
                            act.wait_ge(oT_done.sem, oT_done.count(u, t + 1))
                            act.wait_ge(out_done.sem, out_done.count(u, t - 1))
                            nc.scalar.copy(oT[t % 2][:, :].rearrange("p (j two q) -> p two j q", two=2, q=64),
                                           ps_oT[:, :, 0:256].rearrange("p two (j q) -> p two j q", q=64)).then_inc(oT_ready.sem, 1)
                        if n[PROJ] is not None:
                            u, b = n[PROJ], par[PROJ]
                            act.wait_ge(k_done.sem, k_done.count(u, t + 1))
                            nc.scalar.copy(kT[b][:, t, :], ps_proj[1][:, :]).then_inc(k_ready.sem, 1)
                            act.wait_ge(v_done.sem, v_done.count(u, t + 1))
                            act.wait_ge(oT_done.sem, oT_done.count(u, t + 1, back=2))
                            nc.scalar.copy(v[b][:, t, :], ps_proj[0][:, :]).then_inc(v_ready.sem, 1)
                    if n[TURN] is not None:
                        u, b = n[TURN], par[TURN]
                        act.wait_ge(turned.sem, turned.count(u))
                        act.wait_ge(v_done.sem, v_done.count(u, back=2))
                        nc.scalar.copy(hnT[b][:, :], ps_turn[:, :]).then_inc(hnT_ready.sem, 1)

                in_lanes(act, UNITS, 5, body)

            @block.vector
            def _(dve):
                for s in (stats, moments, sc_masked, top_ready, sc_ready, total_ready, inv_ready, prT_ready, out_ready):
                    s.opened(dve)
                dve.wait_ge(weights_in, 16 * WEIGHTS)

                def body(n, par):
                    for t in range(TILES):
                        if n[SOFT] is not None:
                            u, b = n[SOFT], t % 2
                            dve.wait_ge(sc_done.sem, sc_done.count(u, t + 1))
                            dve.wait_ge(ex_ready.sem, ex_ready.count(u, t - 1))
                            nc.vector.tensor_tensor(sc[b][:, :], ps_sc[b][:, :], msk[:, :], ALU.add).then_inc(sc_masked.sem, 1)
                            dve.wait_ge(sc_masked.sem, sc_masked.count(u, t + 1))
                            nc.vector.tensor_reduce(top[b][:, :], sc[b][:, :].rearrange("p (g k) -> p g k", k=64),
                                                    AX.X, ALU.max).then_inc(top_ready.sem, 1)
                        if n[OUT] is not None:
                            u, b = n[OUT], par[OUT]
                            dve.wait_ge(prob_turned.sem, prob_turned.count(u, t + 1))
                            dve.wait_ge(oT_done.sem, oT_done.count(u, t - 1))
                            nc.vector.tensor_copy(prT[t % 2][:, :], ps_prT[:, :]).then_inc(prT_ready.sem, 1)
                        if n[SOFT] is not None:
                            u, b = n[SOFT], t % 2
                            dve.wait_ge(top_ready.sem, top_ready.count(u, t + 1))
                            nc.vector.tensor_tensor(sc[b][:, :].rearrange("p (g k) -> p g k", k=64),
                                                    sc[b][:, :].rearrange("p (g k) -> p g k", k=64),
                                                    wide(top[b][:, :], 64), ALU.subtract).then_inc(sc_ready.sem, 1)
                        if n[NORM] is not None:
                            u, b = n[NORM], par[NORM]
                            if t == 0:
                                dve.wait_ge(h_in_s[b].sem, h_in_s[b].count(u, b))
                                dve.wait_ge(normed.sem, normed.count(u, back=2))
                            nc.vector.bn_stats(st[b][:, t, :], h_sb[b][:, t, :]).then_inc(stats.sem, 1)
                            dve.wait_ge(stats.sem, stats.count(u, t + 1))
                            dve.sem_inc(dve_passed, 1)
                            nc.vector.bn_aggr(mv[b][:, t, :], st[b][:, t, :]).then_inc(moments.sem, 1)
                        if n[SOFT] is not None:
                            u, b = n[SOFT], t % 2
                            dve.wait_ge(ex_ready.sem, ex_ready.count(u, t + 1))
                            nc.vector.tensor_reduce(total[b][:, :], ex[b][:, :].rearrange("p (g k) -> p g k", k=64),
                                                    AX.X, ALU.add).then_inc(total_ready.sem, 1)
                            dve.wait_ge(total_ready.sem, total_ready.count(u, t + 1))
                            dve.wait_ge(prob_ready.sem, prob_ready.count(u, t - 1))
                            nc.vector.reciprocal(inv[b][:, :], total[b][:, :]).then_inc(inv_ready.sem, 1)
                        if n[OUT] is not None:
                            u, b = n[OUT], par[OUT]
                            if t == 0:
                                dve.wait_ge(res_in[b].sem, res_in[b].count(u, b))
                                dve.wait_ge(stored[b].sem, stored[b].count(u, b, back=1))
                            dve.wait_ge(out_done.sem, out_done.count(u, t + 1))
                            nc.vector.tensor_tensor(out[b][:, t, :], ps_out(t), res[b][:, t, :],
                                                    ALU.add).then_inc(out_ready.sem, 1)

                in_lanes(dve, UNITS, 5, body)

            @block.gpsimd
            def _(pool):
                for s in (var_eps, rstd_ready, normed, prob_ready):
                    s.opened(pool)
                nc.gpsimd.memset(eps[:, :], EPS)
                nc.gpsimd.memset(minus_half[:, :], -0.5).then_inc(constants_set, 1)
                pool.wait_ge(constants_set, 1)

                def body(n, par):
                    for t in range(TILES):
                        if n[SOFT] is not None:
                            u, b = n[SOFT], par[SOFT]
                            pool.wait_ge(inv_ready.sem, inv_ready.count(u, t + 1))
                            pool.wait_ge(prob_turned.sem, prob_turned.count(u, t + 1, back=2))
                            nc.gpsimd.tensor_tensor(prob[b][:, t, :].rearrange("p (g k) -> p g k", k=64),
                                                    ex[t % 2][:, :].rearrange("p (g k) -> p g k", k=64),
                                                    wide(inv[t % 2][:, :], 64), ALU.mult).then_inc(prob_ready.sem, 1)
                    if n[NORM] is not None:
                        u, b = n[NORM], par[NORM]
                        pool.wait_ge(moments.sem, moments.count(u))
                        nc.gpsimd.tensor_tensor(rstd[b][:, :], mv[b][:, :, 1], eps[:, :], ALU.add).then_inc(var_eps.sem, 1)
                        pool.wait_ge(var_eps.sem, var_eps.count(u))
                        nc.gpsimd.tensor_tensor(rstd[b][:, :], rstd[b][:, :], minus_half[:, :], ALU.pow).then_inc(rstd_ready.sem, 1)
                        pool.wait_ge(rstd_ready.sem, rstd_ready.count(u))
                        pool.wait_ge(turned.sem, turned.count(u, back=2))
                        pool.sem_inc(pool_passed, 1)
                        for t in range(TILES):
                            last = nc.gpsimd.tensor_scalar(hn[b][:, t, :], h_sb[b][:, t, :], mv[b][:, t, 0:1], rstd[b][:, t:t + 1],
                                                           ALU.subtract, ALU.mult)
                        last.then_inc(normed.sem, 1)

                in_lanes(pool, UNITS, 5, body)

        pl.close()


def phase_experts8(nc, h_in, ident, iota8, wg, w1, b1, w2, b2, gamma, beta, h_out):
    UNITS = BATCH // 2
    TILES = 4
    N = TILES * HALF
    NORM, TURN, HID, OUT, SUM = range(5)
    H = EXP0 // 2
    with ExitStack() as ctx:
        pl = Place(nc, ctx, "ex8")
        sb, sem = pl.sb, pl.sem
        idn = sb("ident", [P, P])
        iota = sb("iota", [P, EXP0])
        wg_sb = sb("wg", [D, EXP0])
        w1_sb = sb("w1", [D, EXP0, P])
        w2_sb = sb("w2", [P, EXP0, D])
        b1_sb = sb("b1", [P, EXP0])
        b2_sb = sb("b2", [P, EXP0, D])
        gam = sb("gamma", [P, EXP0, D])
        beta_sb = sb("beta", [EXP0, D])
        means = sb("means", [P, 2, EXP0])
        eps = sb("eps", [P, EXP0])
        minus_half = sb("minus_half", [P, EXP0])

        def two(name, shape, dt=F32):
            return [sb(f"{name}{b}", shape, dt) for b in range(2)]

        nm = Norm(pl, TILES, HALF)
        hnT = two("hnT", [D, N])
        hid = two("hid", [P, EXP0, N])
        logit = two("logit", [HALF, TILES, EXP0])
        top = two("top", [HALF, TILES, EXP0])
        at = two("at", [HALF, TILES, EXP0], U32)
        atf = two("atf", [HALF, TILES, 2])
        gap = two("gap", [HALF, TILES])
        egap = two("egap", [HALF, TILES])
        den = two("den", [HALF, TILES])
        gate = two("gate", [HALF, 2, TILES])
        hot = two("hot", [HALF, 2, TILES, EXP0])
        w = two("gated", [HALF, TILES, EXP0])
        wT = two("wT", [EXP0, HALF])
        yb = two("yb", [HALF, EXP0, D])
        sq = two("sq", [HALF, EXP0, D])
        ss = two("ss", [HALF, EXP0])
        s = two("scale", [HALF, TILES, EXP0])
        yg = two("yg", [HALF, TILES, EXP0, D])
        res = two("res", [HALF, TILES, D])
        acc = two("acc", [HALF, TILES, D])

        ps_turn, ps_misc = pl.banks("turn", 2)
        ps_hid = pl.banks("hid", 2)
        ps_y = [ctx.enter_context(nc.psum_tensor(f"ex8_bank_y{b}", [P, 2, H * D], F32)) for b in range(2)]
        ps_beta, ps_logit, ps_wT = ps_misc[0:HALF, 0:D], ps_misc[0:HALF, 128:160], ps_misc[0:EXP0, 192:192 + HALF]

        weights_in = sem("weights_in")
        WEIGHTS = 9
        constants_set = sem("constants_set")
        means_ready = sem("means_ready")
        centred = sem("centred")
        pe_passed, dve_passed, pool_passed = (sem(f"{e}_passed") for e in ("pe", "dve", "pool"))
        x_in = [Landed(sem(f"x_in{b}"), 2) for b in range(2)]
        res_in = [Landed(sem(f"res_in{b}"), 2) for b in range(2)]
        stored = [Landed(sem(f"stored{b}"), 2) for b in range(2)]
        turned = Signal(sem("turned"))
        hnT_ready = Signal(sem("hnT_ready"))
        logit_done = Signal(sem("logit_done"))
        logit_ready = Signal(sem("logit_ready"))
        top_ready = Signal(sem("top_ready"))
        at_ready = Signal(sem("at_ready"))
        atf_ready = Signal(sem("atf_ready"))
        gap_ready = Signal(sem("gap_ready"))
        egap_ready = Signal(sem("egap_ready"))
        den_ready = Signal(sem("den_ready"))
        gate0_ready = Signal(sem("gate0_ready"))
        gates_ready = Signal(sem("gates_ready"))
        hot_ready = Signal(sem("hot_ready"))
        hot_scaled = Signal(sem("hot_scaled"))
        w_ready = Signal(sem("w_ready"))
        hid_done = Signal(sem("hid_done"), EXP0)
        hid_ready = Signal(sem("hid_ready"), EXP0)
        wT_done = Signal(sem("wT_done"), TILES)
        wT_ready = Signal(sem("wT_ready"), TILES)
        y_done = Signal(sem("y_done"), TILES)
        y_ready = Signal(sem("y_ready"), TILES)
        beta_done = Signal(sem("beta_done"), TILES)
        acc_begun = Signal(sem("acc_begun"), TILES)
        ss_ready = Signal(sem("ss_ready"), TILES)
        var_ready = Signal(sem("var_ready"), TILES)
        yrstd_ready = Signal(sem("yrstd_ready"), TILES)
        s_ready = Signal(sem("s_ready"), TILES)
        yg_ready = Signal(sem("yg_ready"), TILES)
        acc_steps = Signal(sem("acc_steps"), EXP0)

        with nc.Block() as block:

            @block.sync
            def _(sp):
                for dst, src in ((idn[:, :], ident), (iota[:, :], iota8), (wg_sb[:, :], wg),
                                 (w1_sb[:, :, :], w1.rearrange("e d h -> d e h")),
                                 (w2_sb[:, :, :], w2.rearrange("e h d -> h e d")),
                                 (b1_sb[:, :], b1), (beta_sb[:, :], beta),
                                 (b2_sb[:, :, :].rearrange("p e d -> p (e d)"), b2.partition_broadcast(P)),
                                 (gam[:, :, :].rearrange("p e d -> p (e d)"), gamma.partition_broadcast(P))):
                    sp.dma_start(dst, src).then_inc(weights_in, 16)
                for b in range(2):
                    x_in[b].opened(sp)
                    res_in[b].opened(sp)
                    stored[b].opened(sp)

                def body(n, par):
                    if n[NORM] is not None:
                        u, b = n[NORM], par[NORM]
                        sp.wait_ge(nm.ready.sem, nm.ready.count(u, back=2))
                        load_rows(sp, nm.x[b], h_in, u, x_in[b])
                    if n[OUT] is not None:
                        u, b = n[OUT], par[OUT]
                        sp.wait_ge(acc_begun.sem, acc_begun.count(u, back=2))
                        load_rows(sp, res[b], h_in, u, res_in[b])
                    if n[SUM] is not None:
                        u, b = n[SUM], par[SUM]
                        sp.wait_ge(acc_steps.sem, acc_steps.count(u))
                        store_rows(sp, h_out, acc[b], u, stored[b])

                in_lanes(sp, UNITS, 5, body)
                for b in range(2):
                    sp.wait_ge(stored[b].sem, stored[b].final(UNITS))

            @block.tensor
            def _(pe):
                for x in (turned, logit_done, hid_done, wT_done, y_done, beta_done):
                    x.opened(pe)
                pe.wait_ge(weights_in, 16 * WEIGHTS)
                pe.wait_ge(centred, 2)

                def body(n, par):
                    if n[HID] is not None:
                        u, b = n[HID], par[HID]
                        pe.wait_ge(hnT_ready.sem, hnT_ready.count(u))
                        pe.wait_ge(acc_begun.sem, acc_begun.count(u, back=2))
                        for t in range(TILES):
                            last = nc.tensor.matmul(ps_logit[:, t * EXP0:(t + 1) * EXP0], hnT[b][:, t * HALF:(t + 1) * HALF],
                                                    wg_sb[:, :], start=True, stop=True)
                        last.then_inc(logit_done.sem, 1)
                    for t in range(TILES):
                        if n[OUT] is not None:
                            u, b = n[OUT], par[OUT]
                            if t == 0:
                                pe.wait_ge(hid_ready.sem, hid_ready.count(u))
                                pe.wait_ge(w_ready.sem, w_ready.count(u))
                                if n[HID] is not None:
                                    pe.wait_ge(logit_ready.sem, logit_ready.count(n[HID]))
                            pe.wait_ge(acc_begun.sem, acc_begun.count(u, t))
                            nc.tensor.transpose(ps_wT, w[b][:, t, :], idn[0:HALF, 0:HALF]).then_inc(wT_done.sem, 1)
                            pe.wait_ge(y_ready.sem, y_ready.count(u, t - 1))
                            for e in range(EXP0):
                                last = nc.tensor.matmul(ps_y[t % 2][0:HALF, e // H, (e % H) * D:(e % H + 1) * D],
                                                        hid[b][:, e, t * HALF:(t + 1) * HALF], w2_sb[:, e, :],
                                                        start=True, stop=True)
                            last.then_inc(y_done.sem, 1)
                            pe.wait_ge(wT_ready.sem, wT_ready.count(u, t + 1))
                            nc.tensor.matmul(ps_beta, wT[t % 2][:, :], beta_sb[:, :], start=True, stop=True).then_inc(beta_done.sem, 1)
                        if n[HID] is not None:
                            u, b = n[HID], par[HID]
                            for e in (2 * t, 2 * t + 1):
                                pe.wait_ge(hid_ready.sem, hid_ready.count(u, e - 1))
                                nc.tensor.matmul(ps_hid[e % 2][:, 0:N], w1_sb[:, e, :], hnT[b][:, :],
                                                 start=True, stop=True).then_inc(hid_done.sem, 1)
                    if n[TURN] is not None:
                        u, b = n[TURN], par[TURN]
                        pe.wait_ge(nm.ready.sem, nm.ready.count(u))
                        pe.wait_ge(hnT_ready.sem, hnT_ready.count(u, back=1))
                        for t in range(TILES):
                            last = nc.tensor.transpose(ps_turn[:, t * HALF:(t + 1) * HALF], nm.y[b][:, t, :], idn[0:HALF, 0:HALF])
                        last.then_inc(turned.sem, 1)

                in_lanes(pe, UNITS, 5, body)

            @block.scalar
            def _(act):
                for x in (hnT_ready, logit_ready, egap_ready, hid_ready, wT_ready, ss_ready):
                    x.opened(act)
                act.wait_ge(weights_in, 16 * WEIGHTS)

                def body(n, par):
                    if n[HID] is not None:
                        u, b = n[HID], par[HID]
                        act.wait_ge(logit_done.sem, logit_done.count(u))
                        act.wait_ge(at_ready.sem, at_ready.count(u, back=2))
                        nc.scalar.copy(logit[b][:, :, :].rearrange("p t e -> p (t e)"), ps_logit).then_inc(logit_ready.sem, 1)
                    for t in range(TILES):
                        if n[OUT] is not None:
                            u, b = n[OUT], par[OUT]
                            act.wait_ge(wT_done.sem, wT_done.count(u, t + 1))
                            act.wait_ge(beta_done.sem, beta_done.count(u, t - 1))
                            nc.scalar.copy(wT[t % 2][:, :], ps_wT).then_inc(wT_ready.sem, 1)
                        if n[HID] is not None:
                            u, b = n[HID], par[HID]
                            for e in (2 * t, 2 * t + 1):
                                act.wait_ge(hid_done.sem, hid_done.count(u, e + 1))
                                act.wait_ge(y_done.sem, y_done.count(u, back=2))
                                nc.scalar.activation(hid[b][:, e, :], ps_hid[e % 2][:, 0:N], ACT.Relu,
                                                     bias=b1_sb[:, e:e + 1]).then_inc(hid_ready.sem, 1)
                            if t == 1:
                                act.wait_ge(gap_ready.sem, gap_ready.count(u))
                                act.wait_ge(gates_ready.sem, gates_ready.count(u, back=2))
                                nc.scalar.activation(egap[b][:, :], gap[b][:, :], ACT.Exp).then_inc(egap_ready.sem, 1)
                        if n[OUT] is not None:
                            u, b = n[OUT], par[OUT]
                            act.wait_ge(y_ready.sem, y_ready.count(u, t + 1))
                            act.wait_ge(var_ready.sem, var_ready.count(u, t - 1))
                            act.wait_ge(ss_ready.sem, ss_ready.count(u, t - 1))
                            for e in range(EXP0):
                                last = nc.scalar.activation(sq[t % 2][:, e, :], yb[t % 2][:, e, :], ACT.Square,
                                                            accum_out=ss[t % 2][:, e:e + 1])
                            last.then_inc(ss_ready.sem, 1)
                    if n[TURN] is not None:
                        u, b = n[TURN], par[TURN]
                        act.wait_ge(turned.sem, turned.count(u))
                        act.wait_ge(hid_done.sem, hid_done.count(u, back=2))
                        nc.scalar.copy(hnT[b][:, :], ps_turn[:, 0:N]).then_inc(hnT_ready.sem, 1)

                in_lanes(act, UNITS, 5, body)

            @block.vector
            def _(dve):
                for x in (nm.stats, nm.moments, top_ready, at_ready, atf_ready, gap_ready, den_ready, gate0_ready,
                          gates_ready, hot_ready, hot_scaled, w_ready, y_ready, acc_begun, acc_steps):
                    x.opened(dve)
                dve.wait_ge(weights_in, 16 * WEIGHTS)
                nc.vector.tensor_reduce(means[:, 0, :], w2_sb[:, :, :], AX.X, ALU.add)
                nc.vector.tensor_reduce(means[:, 1, :], b2_sb[:, :, :], AX.X, ALU.add).then_inc(means_ready, 1)
                dve.wait_ge(means_ready, 1)
                nc.vector.tensor_scalar(means[:, :, :], means[:, :, :], 1.0 / D, None, ALU.mult).then_inc(means_ready, 1)
                dve.wait_ge(means_ready, 2)
                for i, x in enumerate((w2_sb, b2_sb)):
                    nc.vector.tensor_tensor(x[:, :, :], x[:, :, :], wide(means[:, i, :], D), ALU.subtract).then_inc(centred, 1)
                dve.wait_ge(centred, 2)

                def body(n, par):
                    if n[HID] is not None:
                        u, b = n[HID], par[HID]
                        dve.wait_ge(logit_ready.sem, logit_ready.count(u))
                        dve.wait_ge(atf_ready.sem, atf_ready.count(u, back=2))
                        dve.sem_inc(dve_passed, 1)
                        for t in range(TILES):
                            last = nc.vector.max(top[b][:, t, :], logit[b][:, t, :])
                        last.then_inc(top_ready.sem, 1)
                        dve.wait_ge(top_ready.sem, top_ready.count(u))
                        nc.vector.tensor_tensor(gap[b][:, :], top[b][:, :, 1], top[b][:, :, 0], ALU.subtract).then_inc(gap_ready.sem, 1)
                        for t in range(TILES):
                            last = nc.vector.max_index(at[b][:, t, :], top[b][:, t, :], logit[b][:, t, :])
                        last.then_inc(at_ready.sem, 1)
                    for t in range(TILES):
                        if n[OUT] is not None:
                            u, b = n[OUT], par[OUT]
                            dve.wait_ge(y_done.sem, y_done.count(u, t + 1))
                            dve.wait_ge(ss_ready.sem, ss_ready.count(u, t - 1))
                            dve.wait_ge(yg_ready.sem, yg_ready.count(u, t - 1))
                            nc.vector.tensor_tensor(yb[t % 2][:, :, :].rearrange("p e d -> p (e d)"),
                                                    ps_y[t % 2][0:HALF, :, :].rearrange("p k x -> p (k x)"),
                                                    b2_sb[0:HALF, :, :].rearrange("p e d -> p (e d)"), ALU.add).then_inc(y_ready.sem, 1)
                            if t == 0:
                                dve.wait_ge(res_in[b].sem, res_in[b].count(u, b))
                                dve.wait_ge(stored[b].sem, stored[b].count(u, b, back=1))
                            dve.wait_ge(beta_done.sem, beta_done.count(u, t + 1))
                            nc.vector.tensor_tensor(acc[b][:, t, :], ps_beta, res[b][:, t, :], ALU.add).then_inc(acc_begun.sem, 1)
                        if n[HID] is not None:
                            u, b = n[HID], par[HID]
                            if t == 0:
                                dve.wait_ge(at_ready.sem, at_ready.count(u))
                                nc.vector.tensor_copy(atf[b][:, :, :], at[b][:, :, 0:2]).then_inc(atf_ready.sem, 1)
                            if t == 1:
                                dve.wait_ge(atf_ready.sem, atf_ready.count(u))
                                for k in range(2):
                                    last = nc.vector.tensor_tensor(hot[b][:, k, :, :], over(iota[0:HALF, :], TILES),
                                                                   wide(atf[b][:, :, k], EXP0), ALU.is_equal)
                                last.then_inc(hot_ready.sem, 1)
                            if t == 2:
                                dve.wait_ge(egap_ready.sem, egap_ready.count(u))
                                nc.vector.tensor_scalar(den[b][:, :], egap[b][:, :], 1.0, None, ALU.add).then_inc(den_ready.sem, 1)
                                dve.wait_ge(den_ready.sem, den_ready.count(u))
                                nc.vector.reciprocal(gate[b][:, 0, :], den[b][:, :]).then_inc(gate0_ready.sem, 1)
                                dve.wait_ge(gate0_ready.sem, gate0_ready.count(u))
                                nc.vector.tensor_tensor(gate[b][:, 1, :], gate[b][:, 0, :], egap[b][:, :], ALU.mult).then_inc(gates_ready.sem, 1)
                            if t == 3:
                                dve.wait_ge(gates_ready.sem, gates_ready.count(u))
                                dve.wait_ge(hot_ready.sem, hot_ready.count(u))
                                for k in range(2):
                                    last = nc.vector.tensor_tensor(hot[b][:, k, :, :], hot[b][:, k, :, :],
                                                                   wide(gate[b][:, k, :], EXP0), ALU.mult)
                                last.then_inc(hot_scaled.sem, 1)
                                dve.wait_ge(hot_scaled.sem, hot_scaled.count(u))
                                dve.wait_ge(s_ready.sem, s_ready.count(u, back=2))
                                dve.wait_ge(wT_done.sem, wT_done.count(u, back=2))
                                nc.vector.tensor_tensor(w[b][:, :, :], hot[b][:, 0, :, :], hot[b][:, 1, :, :], ALU.add).then_inc(w_ready.sem, 1)
                        if n[NORM] is not None:
                            u, b = n[NORM], par[NORM]
                            if t == 0:
                                dve.wait_ge(x_in[b].sem, x_in[b].count(u, b))
                                dve.wait_ge(nm.ready.sem, nm.ready.count(u, back=2))
                            norm_moments(nc, dve, nm, u, b, t, dve_passed)
                    if n[SUM] is not None:
                        u, b = n[SUM], par[SUM]
                        for e in range(EXP0):
                            if e == 0:
                                dve.wait_ge(yg_ready.sem, yg_ready.count(u))
                                dve.wait_ge(s_ready.sem, s_ready.count(u))
                                dve.wait_ge(acc_begun.sem, acc_begun.count(u))
                            else:
                                dve.wait_ge(acc_steps.sem, acc_steps.count(u, e))
                            for t in range(TILES):
                                last = nc.vector.scalar_tensor_tensor(acc[b][:, t, :], yg[b][:, t, e, :], s[b][:, t, e:e + 1],
                                                                      acc[b][:, t, :], ALU.mult, ALU.add)
                            last.then_inc(acc_steps.sem, 1)

                in_lanes(dve, UNITS, 5, body)

            @block.gpsimd
            def _(pool):
                for x in (nm.var_eps, nm.rstd_ready, nm.ready, var_ready, yrstd_ready, s_ready, yg_ready):
                    x.opened(pool)
                nc.gpsimd.memset(eps[:, :], EPS)
                nc.gpsimd.memset(minus_half[:, :], -0.5).then_inc(constants_set, 1)
                pool.wait_ge(constants_set, 1)
                pool.wait_ge(weights_in, 16 * WEIGHTS)

                def body(n, par):
                    for t in range(TILES):
                        if n[OUT] is not None:
                            u, b = n[OUT], par[OUT]
                            pool.wait_ge(y_ready.sem, y_ready.count(u, t + 1))
                            pool.wait_ge(acc_steps.sem, acc_steps.count(u, back=2))
                            nc.gpsimd.tensor_tensor(yg[b][:, t, :, :], yb[t % 2][:, :, :], gam[0:HALF, :, :], ALU.mult).then_inc(yg_ready.sem, 1)
                            pool.wait_ge(ss_ready.sem, ss_ready.count(u, t + 1))
                            pool.sem_inc(pool_passed, 1)
                            nc.gpsimd.tensor_scalar(s[b][:, t, :], ss[t % 2][:, :], 1.0 / D, EPS, ALU.mult, ALU.add).then_inc(var_ready.sem, 1)
                            pool.wait_ge(var_ready.sem, var_ready.count(u, t + 1))
                            nc.gpsimd.tensor_tensor(s[b][:, t, :], s[b][:, t, :], minus_half[0:HALF, :], ALU.pow).then_inc(yrstd_ready.sem, 1)
                            pool.wait_ge(yrstd_ready.sem, yrstd_ready.count(u, t + 1))
                            nc.gpsimd.tensor_tensor(s[b][:, t, :], s[b][:, t, :], w[b][:, t, :], ALU.mult).then_inc(s_ready.sem, 1)
                    if n[NORM] is not None:
                        norm_rows(nc, pool, nm, n[NORM], par[NORM], eps, minus_half, pool_passed, turned)

                in_lanes(pool, UNITS, 5, body)

        pl.close()


def phase_linear_attention(nc, h_in, ident, mask, index, live, wq, wk, wv, bqk, bv, decay, wo, bo, ln_g, ln_b, h_out):
    UNITS = BATCH // 2
    TILES = 4
    GROUPS = 2
    N = TILES * HALF
    V = E_HEAD + 1
    NORM, TURN, PROJ, PROD, VAL, OUT, FIN = range(7)
    STAGES = 7
    ROUNDS = 4
    with ExitStack() as ctx:
        pl = Place(nc, ctx, "lin")
        sb, sem = pl.sb, pl.sem
        idn = sb("ident", [P, P])
        msk = sb("mask", [HALF, 3 * HALF])
        wqk_sb = sb("wqk", [D, 2, GROUPS, P])
        wv_sb = sb("wv", [D, D])
        wo_sb = sb("wo", [D, D])
        bqk_sb = sb("bqk", [P, 2, GROUPS])
        rows = sb("rows", [P, 4, D])
        live_sb = sb("live", [P, 2])
        dl = sb("dl", [P, GROUPS])
        lam = sb("lam", [P, GROUPS])
        idx = sb("idx", [P, 2, SEQ])
        dec = sb("dec", [P, 2, GROUPS, SEQ])
        eps = sb("eps", [P, TILES])
        minus_half = sb("minus_half", [P, TILES])

        def two(name, shape, dt=F32):
            return [sb(f"{name}{b}", shape, dt) for b in range(2)]

        nm = Norm(pl, TILES, HALF)
        hnT = two("hnT", [D, N])
        ex = two("ex", [P, N])
        rel = two("rel", [P, N])
        qk = two("qk", [P, 2, GROUPS, N])
        v = two("v", [HALF, TILES, N_HEAD, V])
        prod = two("prod", [HALF, 2, N_HEAD, 3 * HALF])
        inv = two("inv", [HALF, 2, N_HEAD])
        o = two("o", [HALF, TILES, D])
        oT = two("oT", [D, HALF])
        z = two("z", [HALF, TILES, D])
        zst = two("zst", [HALF, TILES, 6])
        zmv = two("zmv", [HALF, TILES, 2])
        zrstd = two("zrstd", [HALF, TILES])
        zn = two("zn", [HALF, TILES, D])
        res = two("res", [HALF, TILES, D])
        out = two("out", [HALF, TILES, D])

        ps_turn, ps_proj, ps_num, ps_out = pl.banks("x", 4)
        ps_prod = pl.banks("prod", 4)
        num = ps_num[0:HALF, 0:2 * N_HEAD * V].rearrange("p (c h v) -> p c h v", c=2, v=V)

        weights_in = sem("weights_in")
        WEIGHTS = 14
        constants_set = sem("constants_set")
        setup = sem("setup")
        exp_decay = sem("exp_decay")
        decay_ready = sem("decay_ready")
        pe_passed, dve_passed, pool_passed = (sem(f"{e}_passed") for e in ("pe", "dve", "pool"))
        x_in = [Landed(sem(f"x_in{b}"), 2) for b in range(2)]
        res_in = [Landed(sem(f"res_in{b}"), 2) for b in range(2)]
        stored = [Landed(sem(f"stored{b}"), 2) for b in range(2)]
        turned = Signal(sem("turned"))
        hnT_ready = Signal(sem("hnT_ready"))
        proj_done = Signal(sem("proj_done"), ROUNDS)
        proj_read = Signal(sem("proj_read"), ROUNDS)
        feature_ready = Signal(sem("feature_ready"), ROUNDS)
        qk_ready = Signal(sem("qk_ready"), ROUNDS)
        v_done = Signal(sem("v_done"))
        v_ready = Signal(sem("v_ready"))
        prod_done = Signal(sem("prod_done"), 2 * N_HEAD)
        prod_ready = Signal(sem("prod_ready"), 2 * N_HEAD)
        val_done = Signal(sem("val_done"), ROUNDS)
        inv_ready = Signal(sem("inv_ready"), 4)
        o_ready = Signal(sem("o_ready"), 2)
        oT_done = Signal(sem("oT_done"), TILES)
        oT_ready = Signal(sem("oT_ready"), TILES)
        z_done = Signal(sem("z_done"), TILES)
        z_ready = Signal(sem("z_ready"), TILES)
        zstats = Signal(sem("zstats"), TILES)
        zmoments = Signal(sem("zmoments"), TILES)
        zvar_eps = Signal(sem("zvar_eps"))
        zrstd_ready = Signal(sem("zrstd_ready"))
        zn_ready = Signal(sem("zn_ready"))
        zg_ready = Signal(sem("zg_ready"))
        zb_ready = Signal(sem("zb_ready"))
        out_ready = Signal(sem("out_ready"))

        with nc.Block() as block:

            @block.sync
            def _(sp):
                for dst, src in ((idn[:, :], ident), (msk[:, :], mask), (wqk_sb[:, 0, :, :].rearrange("p g m -> p (g m)"), wq),
                                 (wqk_sb[:, 1, :, :].rearrange("p g m -> p (g m)"), wk), (wv_sb[:, :], wv), (wo_sb[:, :], wo),
                                 (bqk_sb[:, :, :].rearrange("p w g -> p (w g)"), bqk), (live_sb[:, :], live), (dl[:, :], decay),
                                 (idx[:, :, :].rearrange("p w n -> p (w n)"), index),
                                 (rows[:, 0, :], bv.partition_broadcast(P)), (rows[:, 1, :], bo.partition_broadcast(P)),
                                 (rows[:, 2, :], ln_g.partition_broadcast(P)), (rows[:, 3, :], ln_b.partition_broadcast(P))):
                    sp.dma_start(dst, src).then_inc(weights_in, 16)
                for b in range(2):
                    x_in[b].opened(sp)
                    res_in[b].opened(sp)
                    stored[b].opened(sp)

                def body(n, par):
                    if n[NORM] is not None:
                        u, b = n[NORM], par[NORM]
                        sp.wait_ge(nm.ready.sem, nm.ready.count(u, back=2))
                        load_rows(sp, nm.x[b], h_in, u, x_in[b])
                    if n[OUT] is not None:
                        u, b = n[OUT], par[OUT]
                        sp.wait_ge(out_ready.sem, out_ready.count(u, back=2))
                        load_rows(sp, res[b], h_in, u, res_in[b])
                    if n[FIN] is not None:
                        u, b = n[FIN], par[FIN]
                        sp.wait_ge(out_ready.sem, out_ready.count(u))
                        store_rows(sp, h_out, out[b], u, stored[b])

                in_lanes(sp, UNITS, STAGES, body)
                for b in range(2):
                    sp.wait_ge(stored[b].sem, stored[b].final(UNITS))

            @block.tensor
            def _(pe):
                for x in (turned, proj_done, v_done, prod_done, val_done, oT_done, z_done):
                    x.opened(pe)
                pe.wait_ge(weights_in, 16 * WEIGHTS)

                def body(n, par):
                    for r in range(ROUNDS):
                        seq, g = r // 2, r % 2
                        if n[VAL] is not None:
                            u, b = n[VAL], par[VAL]
                            if r == 0:
                                pe.wait_ge(prod_ready.sem, prod_ready.count(u))
                                pe.wait_ge(v_ready.sem, v_ready.count(u))
                            if g == 0:
                                pe.wait_ge(o_ready.sem, o_ready.count(u, seq))
                            for h in range(4 * g, 4 * g + 4):
                                a = prod[b][:, seq, h, :]
                                nc.tensor.matmul(num[:, 0, h, :], a[:, 0:HALF], v[b][:, 2 * seq, h, :], start=True, stop=True)
                                nc.tensor.matmul(num[:, 1, h, :], a[:, HALF:2 * HALF], v[b][:, 2 * seq, h, :], start=True, stop=False)
                                last = nc.tensor.matmul(num[:, 1, h, :], a[:, 2 * HALF:3 * HALF], v[b][:, 2 * seq + 1, h, :],
                                                        start=False, stop=True)
                            last.then_inc(val_done.sem, 1)
                        if n[OUT] is not None:
                            u, b, t = n[OUT], par[OUT], r
                            if t == 0:
                                pe.wait_ge(o_ready.sem, o_ready.count(u))
                            pe.wait_ge(z_ready.sem, z_ready.count(u, t))
                            nc.tensor.transpose(ps_out[:, 0:HALF], o[b][:, t, :], idn[0:HALF, 0:HALF]).then_inc(oT_done.sem, 1)
                        if n[PROJ] is not None:
                            u, b = n[PROJ], par[PROJ]
                            if r == 0:
                                pe.wait_ge(hnT_ready.sem, hnT_ready.count(u))
                                pe.wait_ge(v_ready.sem, v_ready.count(u, back=1))
                            else:
                                pe.wait_ge(proj_read.sem, proj_read.count(u, r))
                            nc.tensor.matmul(ps_proj[:, 0:N], wqk_sb[:, r % 2, r // 2, :], hnT[b][:, :],
                                             start=True, stop=True).then_inc(proj_done.sem, 1)
                        if n[PROD] is not None:
                            u, b = n[PROD], par[PROD]
                            if r == 0:
                                pe.wait_ge(qk_ready.sem, qk_ready.count(u))
                            for i in range(4):
                                pe.wait_ge(prod_ready.sem, prod_ready.count(u, 4 * r + i - 3))
                                pe.sem_inc(pe_passed, 1)
                                part = slice(32 * i, 32 * i + 32)
                                at = seq * SEQ
                                q, k = qk[b][part, 0, g, :], qk[b][part, 1, g, :]
                                nc.tensor.matmul(ps_prod[i][0:HALF, 0:SEQ], k[:, at:at + HALF], q[:, at:at + SEQ], start=True, stop=True)
                                nc.tensor.matmul(ps_prod[i][0:HALF, SEQ:SEQ + HALF], k[:, at + HALF:at + SEQ], q[:, at + HALF:at + SEQ],
                                                 start=True, stop=True).then_inc(prod_done.sem, 1)
                        if n[OUT] is not None:
                            u, b, t = n[OUT], par[OUT], r
                            pe.wait_ge(oT_ready.sem, oT_ready.count(u, t + 1))
                            nc.tensor.matmul(ps_out[0:HALF, 128:256], oT[t % 2][:, :], wo_sb[:, :], start=True, stop=True).then_inc(z_done.sem, 1)
                    if n[PROJ] is not None:
                        u, b = n[PROJ], par[PROJ]
                        pe.wait_ge(proj_read.sem, proj_read.count(u))
                        for t in range(TILES):
                            last = nc.tensor.matmul(ps_proj[0:HALF, t * D:(t + 1) * D], hnT[b][:, t * HALF:(t + 1) * HALF], wv_sb[:, :],
                                                    start=True, stop=True)
                        last.then_inc(v_done.sem, 1)
                    if n[TURN] is not None:
                        u, b = n[TURN], par[TURN]
                        pe.wait_ge(nm.ready.sem, nm.ready.count(u))
                        pe.wait_ge(hnT_ready.sem, hnT_ready.count(u, back=1))
                        for t in range(TILES):
                            last = nc.tensor.transpose(ps_turn[:, t * HALF:(t + 1) * HALF], nm.y[b][:, t, :], idn[0:HALF, 0:HALF])
                        last.then_inc(turned.sem, 1)

                in_lanes(pe, UNITS, STAGES, body)

            @block.scalar
            def _(act):
                for x in (hnT_ready, proj_read, oT_ready):
                    x.opened(act)
                act.wait_ge(weights_in, 16 * WEIGHTS)
                nc.scalar.activation(lam[:, :], dl[:, :], ACT.Exp, scale=-1.0).then_inc(exp_decay, 1)

                def body(n, par):
                    for r in range(ROUNDS):
                        if n[OUT] is not None:
                            u, t = n[OUT], r
                            act.wait_ge(oT_done.sem, oT_done.count(u, t + 1))
                            act.wait_ge(z_done.sem, z_done.count(u, t - 1))
                            nc.scalar.copy(oT[t % 2][:, :], ps_out[:, 0:HALF]).then_inc(oT_ready.sem, 1)
                        if n[PROJ] is not None:
                            u = n[PROJ]
                            act.wait_ge(proj_done.sem, proj_done.count(u, r + 1))
                            act.wait_ge(qk_ready.sem, qk_ready.count(u, r - 1))
                            bias = bqk_sb[:, r % 2, r // 2:r // 2 + 1]
                            nc.scalar.activation(ex[r % 2][:, :], ps_proj[:, 0:N], ACT.Exp, bias=bias)
                            nc.scalar.activation(rel[r % 2][:, :], ps_proj[:, 0:N], ACT.Relu, bias=bias).then_inc(proj_read.sem, 1)
                    if n[TURN] is not None:
                        u, b = n[TURN], par[TURN]
                        act.wait_ge(turned.sem, turned.count(u))
                        act.wait_ge(v_done.sem, v_done.count(u, back=2))
                        nc.scalar.copy(hnT[b][:, :], ps_turn[:, 0:N]).then_inc(hnT_ready.sem, 1)

                in_lanes(act, UNITS, STAGES, body)

            @block.vector
            def _(dve):
                for x in (nm.stats, nm.moments, feature_ready, v_ready, prod_ready, inv_ready, o_ready, z_ready, zstats,
                          zmoments, out_ready):
                    x.opened(dve)
                for b in range(2):
                    nc.vector.memset(v[b][:, :, :, E_HEAD:V], 1.0)
                dve.wait_ge(exp_decay, 1)
                nc.vector.tensor_scalar(lam[:, :], lam[:, :], 1.0, None, ALU.add).then_inc(setup, 1)
                dve.wait_ge(setup, 1)
                nc.vector.reciprocal(lam[:, :], lam[:, :]).then_inc(setup, 1)
                dve.wait_ge(setup, 2)
                nc.vector.tensor_scalar(lam[:, :], lam[:, :], 0.01, 0.99, ALU.mult, ALU.add).then_inc(setup, 1)
                dve.wait_ge(weights_in, 16 * WEIGHTS)

                def body(n, par):
                    for r in range(ROUNDS):
                        seq, g = r // 2, r % 2
                        if n[VAL] is not None and g == 1:
                            u, b = n[VAL], par[VAL]
                            dve.wait_ge(val_done.sem, val_done.count(u, r + 1))
                            dve.wait_ge(oT_done.sem, oT_done.count(u, back=2))
                            nc.vector.tensor_scalar(inv[b][:, :, :], num[:, :, :, E_HEAD], 1e-6, None, ALU.add).then_inc(inv_ready.sem, 1)
                            dve.wait_ge(inv_ready.sem, inv_ready.count(u, 2 * seq + 1))
                            nc.vector.reciprocal(inv[b][:, :, :], inv[b][:, :, :]).then_inc(inv_ready.sem, 1)
                            dve.wait_ge(inv_ready.sem, inv_ready.count(u, 2 * seq + 2))
                            for c in range(2):
                                last = nc.vector.tensor_tensor(o[b][:, 2 * seq + c, :].rearrange("p (h e) -> p h e", e=E_HEAD),
                                                               num[:, c, :, 0:E_HEAD], wide(inv[b][:, c, :], E_HEAD), ALU.mult)
                            last.then_inc(o_ready.sem, 1)
                        if n[PROD] is not None:
                            u, b = n[PROD], par[PROD]
                            for i in range(4):
                                dve.wait_ge(prod_done.sem, prod_done.count(u, 4 * r + i + 1))
                                dve.wait_ge(val_done.sem, val_done.count(u, back=2))
                                nc.vector.tensor_tensor(prod[b][:, seq, 4 * g + i, :], ps_prod[i][0:HALF, 0:3 * HALF], msk[:, :],
                                                        ALU.mult).then_inc(prod_ready.sem, 1)
                        if n[PROJ] is not None:
                            u = n[PROJ]
                            dve.wait_ge(proj_read.sem, proj_read.count(u, r + 1))
                            nc.vector.scalar_tensor_tensor(ex[r % 2][:, :], ex[r % 2][:, :], 1.0, rel[r % 2][:, :],
                                                           ALU.min, ALU.add).then_inc(feature_ready.sem, 1)
                        if n[NORM] is not None:
                            u, b, t = n[NORM], par[NORM], r
                            if t == 0:
                                dve.wait_ge(x_in[b].sem, x_in[b].count(u, b))
                                dve.wait_ge(nm.ready.sem, nm.ready.count(u, back=2))
                            norm_moments(nc, dve, nm, u, b, t, dve_passed)
                        if n[OUT] is not None:
                            u, b, t = n[OUT], par[OUT], r
                            dve.wait_ge(z_done.sem, z_done.count(u, t + 1))
                            dve.wait_ge(zn_ready.sem, zn_ready.count(u, back=2))
                            nc.vector.tensor_tensor(z[b][:, t, :], ps_out[0:HALF, 128:256], rows[0:HALF, 1, :], ALU.add).then_inc(z_ready.sem, 1)
                            dve.wait_ge(z_ready.sem, z_ready.count(u, t + 1))
                            nc.vector.bn_stats(zst[b][:, t, :], z[b][:, t, :]).then_inc(zstats.sem, 1)
                            dve.wait_ge(zstats.sem, zstats.count(u, t + 1))
                            dve.sem_inc(dve_passed, 1)
                            nc.vector.bn_aggr(zmv[b][:, t, :], zst[b][:, t, :]).then_inc(zmoments.sem, 1)
                    if n[PROJ] is not None:
                        u, b = n[PROJ], par[PROJ]
                        dve.wait_ge(v_done.sem, v_done.count(u))
                        dve.wait_ge(val_done.sem, val_done.count(u, back=2))
                        for t in range(TILES):
                            last = nc.vector.tensor_tensor(v[b][:, t, :, 0:E_HEAD], ps_proj[0:HALF, t * D:(t + 1) * D].rearrange("p (h e) -> p h e", e=E_HEAD),
                                                           rows[0:HALF, 0, :].rearrange("p (h e) -> p h e", e=E_HEAD), ALU.add)
                        last.then_inc(v_ready.sem, 1)
                    if n[FIN] is not None:
                        u, b = n[FIN], par[FIN]
                        dve.wait_ge(res_in[b].sem, res_in[b].count(u, b))
                        dve.wait_ge(zb_ready.sem, zb_ready.count(u))
                        dve.wait_ge(stored[b].sem, stored[b].count(u, b, back=1))
                        nc.vector.tensor_tensor(out[b][:, :, :], zn[b][:, :, :], res[b][:, :, :], ALU.add).then_inc(out_ready.sem, 1)

                in_lanes(dve, UNITS, STAGES, body)

            @block.gpsimd
            def _(pool):
                for x in (nm.var_eps, nm.rstd_ready, nm.ready, qk_ready, zvar_eps, zrstd_ready, zn_ready, zg_ready, zb_ready):
                    x.opened(pool)
                nc.gpsimd.memset(eps[:, :], EPS)
                nc.gpsimd.memset(minus_half[:, :], -0.5).then_inc(constants_set, 1)
                pool.wait_ge(constants_set, 1)
                pool.wait_ge(weights_in, 16 * WEIGHTS)
                pool.wait_ge(setup, 3)
                for what in range(2):
                    for g in range(GROUPS):
                        last = nc.gpsimd.tensor_tensor(dec[:, what, g, :], lam[:, g:g + 1].to_broadcast([P, SEQ]), idx[:, what, :], ALU.pow)
                last.then_inc(decay_ready, 1)
                pool.wait_ge(decay_ready, 1)
                pool.sem_inc(pool_passed, 1)
                for what in range(2):
                    last = nc.gpsimd.tensor_scalar(dec[:, what, :, :], dec[:, what, :, :], live_sb[:, 1 - what:2 - what], None, ALU.mult)
                last.then_inc(decay_ready, 1)
                pool.wait_ge(decay_ready, 2)

                def body(n, par):
                    for r in range(ROUNDS):
                        what, g = r % 2, r // 2
                        if n[PROJ] is not None:
                            u, b = n[PROJ], par[PROJ]
                            pool.wait_ge(feature_ready.sem, feature_ready.count(u, r + 1))
                            pool.wait_ge(prod_done.sem, prod_done.count(u, back=2))
                            nc.gpsimd.tensor_tensor(qk[b][:, what, g, :].rearrange("p (s n) -> p s n", s=2),
                                                    ex[r % 2][:, :].rearrange("p (s n) -> p s n", s=2),
                                                    over(dec[:, what, g, :], 2), ALU.mult).then_inc(qk_ready.sem, 1)
                        if n[FIN] is not None:
                            u, b = n[FIN], par[FIN]
                            if r == 0:
                                pool.wait_ge(zmoments.sem, zmoments.count(u))
                                nc.gpsimd.tensor_tensor(zrstd[b][:, :], zmv[b][:, :, 1], eps[0:HALF, :], ALU.add).then_inc(zvar_eps.sem, 1)
                                pool.wait_ge(zvar_eps.sem, zvar_eps.count(u))
                                nc.gpsimd.tensor_tensor(zrstd[b][:, :], zrstd[b][:, :], minus_half[0:HALF, :], ALU.pow).then_inc(zrstd_ready.sem, 1)
                            if r == 1:
                                pool.wait_ge(zrstd_ready.sem, zrstd_ready.count(u))
                                pool.wait_ge(out_ready.sem, out_ready.count(u, back=2))
                                pool.sem_inc(pool_passed, 1)
                                for t in range(TILES):
                                    last = nc.gpsimd.tensor_scalar(zn[b][:, t, :], z[b][:, t, :], zmv[b][:, t, 0:1], zrstd[b][:, t:t + 1],
                                                                   ALU.subtract, ALU.mult)
                                last.then_inc(zn_ready.sem, 1)
                            if r == 2:
                                pool.wait_ge(zn_ready.sem, zn_ready.count(u))
                                nc.gpsimd.tensor_tensor(zn[b][:, :, :], zn[b][:, :, :], over(rows[0:HALF, 2, :], TILES), ALU.mult).then_inc(zg_ready.sem, 1)
                            if r == 3:
                                pool.wait_ge(zg_ready.sem, zg_ready.count(u))
                                nc.gpsimd.tensor_tensor(zn[b][:, :, :], zn[b][:, :, :], over(rows[0:HALF, 3, :], TILES), ALU.add).then_inc(zb_ready.sem, 1)
                    if n[NORM] is not None:
                        norm_rows(nc, pool, nm, n[NORM], par[NORM], eps, minus_half, pool_passed, turned)

                in_lanes(pool, UNITS, STAGES, body)

        pl.close()


def phase_attention(nc, h_in, ident, ones_row, wq, wk, wv, wo, g_col, b_col, y_dram, h_out):
    UNITS = BATCH // 2
    TILES = 4
    GROUPS = 2
    N = TILES * HALF
    V = E_HEAD + 1
    NORM, TURN, PROJ, TOP, EXP, OUT = range(6)
    STAGES = 6
    ROUNDS = 4
    HEADS = 2 * N_HEAD
    with ExitStack() as ctx:
        pl = Place(nc, ctx, "att")
        sb, sem = pl.sb, pl.sem
        idn = sb("ident", [P, P])
        one = sb("one", [P, 1])
        wqk_sb = sb("wqk", [D, 2, GROUPS, P])
        wv_sb = sb("wv", [D, D])
        wo_sb = sb("wo", [D, D])
        gb = sb("gb", [P, 2])
        eps = sb("eps", [P, TILES])
        minus_half = sb("minus_half", [P, TILES])

        def two(name, shape, dt=F32):
            return [sb(f"{name}{b}", shape, dt) for b in range(2)]

        nm = Norm(pl, TILES, HALF)
        var2 = two("var2", [HALF, TILES])
        yn = two("yn", [HALF, TILES, D])
        hnT = two("hnT", [D, N])
        q = two("q", [P, GROUPS, N])
        k = two("k", [P, GROUPS, N])
        qtop = two("qtop", [P, GROUPS, N])
        top = two("top", [HALF, 2, P])
        v = two("v", [HALF, TILES, N_HEAD, V])
        ex = two("ex", [HALF, 4, 2, SEQ])
        inv = two("inv", [HALF, 2, N_HEAD])
        o = two("o", [HALF, TILES, D])
        oT = two("oT", [D, HALF])
        res = two("res", [HALF, TILES, D])
        out = two("out", [HALF, TILES, D])

        ps_turn, ps_proj, ps_num, ps_out = pl.banks("x", 4)
        ps_top, ps_sc = pl.banks("top", 2), pl.banks("sc", 2)
        num = ps_num[0:HALF, 0:2 * N_HEAD * V].rearrange("p (c h v) -> p c h v", c=2, v=V)

        weights_in = sem("weights_in")
        WEIGHTS = 8
        constants_set = sem("constants_set")
        ones_set = sem("ones_set")
        pool_set = sem("pool_set")
        pe_passed, dve_passed, pool_passed = (sem(f"{e}_passed") for e in ("pe", "dve", "pool"))
        x_in = [Landed(sem(f"x_in{b}"), 2) for b in range(2)]
        res_in = [Landed(sem(f"res_in{b}"), 2) for b in range(2)]
        stored = [Landed(sem(f"stored{b}"), 2) for b in range(2)]
        y_out = [Landed(sem(f"y_out{b}"), 2) for b in range(2)]
        square_ready = Signal(sem("square_ready"))
        var2_ready = Signal(sem("var2_ready"))
        var2_eps = Signal(sem("var2_eps"))
        rstd2_ready = Signal(sem("rstd2_ready"))
        yn_ready = Signal(sem("yn_ready"))
        turned = Signal(sem("turned"))
        hnT_ready = Signal(sem("hnT_ready"))
        proj_done = Signal(sem("proj_done"), ROUNDS)
        qk_ready = Signal(sem("qk_ready"), ROUNDS)
        v_done = Signal(sem("v_done"))
        v_ready = Signal(sem("v_ready"))
        top_done = Signal(sem("top_done"), HEADS)
        top_ready = Signal(sem("top_ready"), HEADS)
        top_turned = Signal(sem("top_turned"), ROUNDS)
        qtop_ready = Signal(sem("qtop_ready"), ROUNDS)
        sc_done = Signal(sem("sc_done"), HEADS)
        ex_ready = Signal(sem("ex_ready"), HEADS)
        val_done = Signal(sem("val_done"), ROUNDS)
        inv_ready = Signal(sem("inv_ready"), 2)
        o_ready = Signal(sem("o_ready"), 2)
        oT_done = Signal(sem("oT_done"), TILES)
        oT_ready = Signal(sem("oT_ready"), TILES)
        z_done = Signal(sem("z_done"), TILES)
        out_ready = Signal(sem("out_ready"), TILES)

        with nc.Block() as block:

            @block.sync
            def _(sp):
                for dst, src in ((idn[:, :], ident), (one[:, :], ones_row), (wqk_sb[:, 0, :, :].rearrange("p g m -> p (g m)"), wq),
                                 (wqk_sb[:, 1, :, :].rearrange("p g m -> p (g m)"), wk), (wv_sb[:, :], wv), (wo_sb[:, :], wo),
                                 (gb[:, 0:1], g_col), (gb[:, 1:2], b_col)):
                    sp.dma_start(dst, src).then_inc(weights_in, 16)
                for b in range(2):
                    x_in[b].opened(sp)
                    res_in[b].opened(sp)
                    stored[b].opened(sp)
                    y_out[b].opened(sp)

                def body(n, par):
                    if n[NORM] is not None:
                        u, b = n[NORM], par[NORM]
                        sp.wait_ge(nm.ready.sem, nm.ready.count(u, back=2))
                        load_rows(sp, nm.x[b], h_in, u, x_in[b])
                    if n[TURN] is not None:
                        u, b = n[TURN], par[TURN]
                        sp.wait_ge(nm.ready.sem, nm.ready.count(u))
                        store_rows(sp, y_dram, nm.y[b], u, y_out[b])
                    if n[EXP] is not None:
                        u, b = n[EXP], par[EXP]
                        sp.wait_ge(out_ready.sem, out_ready.count(u, back=2))
                        sp.wait_ge(y_out[b].sem, y_out[b].count(u, b))
                        load_rows(sp, res[b], y_dram, u, res_in[b])
                    if n[OUT] is not None:
                        u, b = n[OUT], par[OUT]
                        sp.wait_ge(out_ready.sem, out_ready.count(u))
                        store_rows(sp, h_out, out[b], u, stored[b])

                in_lanes(sp, UNITS, STAGES, body)
                for b in range(2):
                    sp.wait_ge(stored[b].sem, stored[b].final(UNITS))

            @block.tensor
            def _(pe):
                for x in (turned, proj_done, v_done, top_done, top_turned, sc_done, val_done, oT_done, z_done):
                    x.opened(pe)
                pe.wait_ge(weights_in, 16 * WEIGHTS)

                def values(u, b, r):
                    seq, g = r // 2, r % 2
                    pe.wait_ge(ex_ready.sem, ex_ready.count(u, 4 * r + 4))
                    if r == 0:
                        pe.wait_ge(v_ready.sem, v_ready.count(u))
                    if g == 0:
                        pe.wait_ge(o_ready.sem, o_ready.count(u, seq))
                    for i in range(4):
                        for c in range(2):
                            for half in range(2):
                                last = nc.tensor.matmul(num[:, c, 4 * g + i, :], ex[r % 2][:, i, half, c * HALF:(c + 1) * HALF],
                                                        v[b][:, 2 * seq + half, 4 * g + i, :], start=half == 0, stop=half == 1)
                    last.then_inc(val_done.sem, 1)

                def turn_top(u, r, turned_before):
                    pe.wait_ge(top_ready.sem, top_ready.count(u, 4 * r + 4))
                    if r == 0 and turned_before is not None:
                        pe.wait_ge(hnT_ready.sem, hnT_ready.count(turned_before))
                    if r > 0:
                        pe.wait_ge(qtop_ready.sem, qtop_ready.count(u, r))
                    for c in range(2):
                        last = nc.tensor.transpose(ps_turn[:, c * HALF:(c + 1) * HALF], top[r % 2][:, c, :], idn[0:HALF, 0:HALF])
                    last.then_inc(top_turned.sem, 1)

                def body(n, par):
                    for r in range(ROUNDS):
                        seq, g = r // 2, r % 2
                        at = seq * SEQ
                        for i in range(4):
                            part = slice(32 * i, 32 * i + 32)
                            if n[TOP] is not None:
                                u, b = n[TOP], par[TOP]
                                if r == 0 and i == 0:
                                    pe.wait_ge(qk_ready.sem, qk_ready.count(u))
                                pe.wait_ge(top_ready.sem, top_ready.count(u, 4 * r + i - 1))
                                pe.sem_inc(pe_passed, 1)
                                for c in range(2):
                                    last = nc.tensor.matmul(ps_top[i % 2][0:HALF, c * SEQ:(c + 1) * SEQ],
                                                            q[b][part, g, at + c * HALF:at + (c + 1) * HALF], k[b][part, g, at:at + SEQ],
                                                            start=True, stop=True)
                                last.then_inc(top_done.sem, 1)
                            if n[EXP] is not None:
                                u, b = n[EXP], par[EXP]
                                if r == 0 and i == 0:
                                    pe.wait_ge(qtop_ready.sem, qtop_ready.count(u))
                                pe.wait_ge(ex_ready.sem, ex_ready.count(u, 4 * r + i - 1))
                                pe.sem_inc(pe_passed, 1)
                                for c in range(2):
                                    last = nc.tensor.matmul(ps_sc[i % 2][0:HALF, c * SEQ:(c + 1) * SEQ],
                                                            k[b][part, g, at + c * HALF:at + (c + 1) * HALF], qtop[b][part, g, at:at + SEQ],
                                                            start=True, stop=True)
                                last.then_inc(sc_done.sem, 1)
                            if i == 1 and r > 0 and n[EXP] is not None:
                                values(n[EXP], par[EXP], r - 1)
                            if i == 1 and r > 0 and n[TOP] is not None:
                                turn_top(n[TOP], r - 1, n[PROJ])
                            if i == 0 and n[OUT] is not None:
                                u, b, t = n[OUT], par[OUT], r
                                pe.wait_ge(out_ready.sem, out_ready.count(u, t))
                                pe.wait_ge(o_ready.sem, o_ready.count(u))
                                nc.tensor.transpose(ps_out[:, 0:HALF], o[b][:, t, :], idn[0:HALF, 0:HALF]).then_inc(oT_done.sem, 1)
                            if i == 2 and n[OUT] is not None:
                                u, b, t = n[OUT], par[OUT], r
                                pe.wait_ge(oT_ready.sem, oT_ready.count(u, t + 1))
                                nc.tensor.matmul(ps_out[0:HALF, 128:256], oT[t % 2][:, :], wo_sb[:, :], start=True, stop=True).then_inc(z_done.sem, 1)
                    if n[PROJ] is not None:
                        u, b = n[PROJ], par[PROJ]
                        pe.wait_ge(hnT_ready.sem, hnT_ready.count(u))
                        pe.wait_ge(v_ready.sem, v_ready.count(u, back=1))
                        for p in range(ROUNDS):
                            if p > 0:
                                pe.wait_ge(qk_ready.sem, qk_ready.count(u, p))
                            nc.tensor.matmul(ps_proj[:, 0:N], wqk_sb[:, p % 2, p // 2, :], hnT[b][:, :],
                                             start=True, stop=True).then_inc(proj_done.sem, 1)
                            if p == 0 and n[EXP] is not None:
                                values(n[EXP], par[EXP], ROUNDS - 1)
                            if p == 1 and n[TOP] is not None:
                                turn_top(n[TOP], ROUNDS - 1, n[PROJ])
                        pe.wait_ge(qk_ready.sem, qk_ready.count(u))
                        for t in range(TILES):
                            last = nc.tensor.matmul(ps_proj[0:HALF, t * D:(t + 1) * D], hnT[b][:, t * HALF:(t + 1) * HALF], wv_sb[:, :],
                                                    start=True, stop=True)
                        last.then_inc(v_done.sem, 1)
                    else:
                        if n[EXP] is not None:
                            values(n[EXP], par[EXP], ROUNDS - 1)
                        if n[TOP] is not None:
                            turn_top(n[TOP], ROUNDS - 1, n[PROJ])
                    if n[TURN] is not None:
                        u, b = n[TURN], par[TURN]
                        pe.wait_ge(yn_ready.sem, yn_ready.count(u))
                        pe.wait_ge(qtop_ready.sem, qtop_ready.count(u, back=2))
                        pe.wait_ge(hnT_ready.sem, hnT_ready.count(u, back=1))
                        for t in range(TILES):
                            last = nc.tensor.transpose(ps_turn[:, t * HALF:(t + 1) * HALF], yn[b][:, t, :], idn[0:HALF, 0:HALF])
                        last.then_inc(turned.sem, 1)

                in_lanes(pe, UNITS, STAGES, body)

            @block.scalar
            def _(act):
                for x in (hnT_ready, qk_ready, ex_ready, oT_ready, v_ready):
                    x.opened(act)
                act.wait_ge(ones_set, 2)
                act.wait_ge(weights_in, 16 * WEIGHTS)

                def body(n, par):
                    for r in range(ROUNDS):
                        for i in range(4):
                            if n[EXP] is not None:
                                u = n[EXP]
                                act.wait_ge(sc_done.sem, sc_done.count(u, 4 * r + i + 1))
                                if i == 0:
                                    act.wait_ge(val_done.sem, val_done.count(u, r - 1))
                                nc.scalar.activation(ex[r % 2][:, i, :, :].rearrange("p c n -> p (c n)"), ps_sc[i % 2][0:HALF, 0:N],
                                                     ACT.Exp).then_inc(ex_ready.sem, 1)
                            if i == 1 and n[OUT] is not None:
                                u, t = n[OUT], r
                                act.wait_ge(oT_done.sem, oT_done.count(u, t + 1))
                                act.wait_ge(z_done.sem, z_done.count(u, t - 1))
                                nc.scalar.copy(oT[t % 2][:, :], ps_out[:, 0:HALF]).then_inc(oT_ready.sem, 1)
                    if n[PROJ] is not None:
                        u, b = n[PROJ], par[PROJ]
                        for p in range(ROUNDS):
                            what, g = p % 2, p // 2
                            act.wait_ge(proj_done.sem, proj_done.count(u, p + 1))
                            if what == 0:
                                act.wait_ge(qtop_ready.sem, qtop_ready.count(u, back=2))
                                nc.scalar.activation(q[b][:, g, :], ps_proj[:, 0:N], ACT.Copy, scale=E_HEAD ** -0.5).then_inc(qk_ready.sem, 1)
                            else:
                                act.wait_ge(sc_done.sem, sc_done.count(u, back=2))
                                nc.scalar.activation(k[b][:, g, :], ps_proj[:, 0:N], ACT.Identity, bias=one[:, :]).then_inc(qk_ready.sem, 1)
                        act.wait_ge(v_done.sem, v_done.count(u))
                        act.wait_ge(val_done.sem, val_done.count(u, back=2))
                        nc.scalar.copy(v[b][:, :, :, 0:E_HEAD], ps_proj[0:HALF, :].rearrange("p (t h e) -> p t h e", t=TILES, e=E_HEAD)).then_inc(v_ready.sem, 1)
                    if n[TURN] is not None:
                        u, b = n[TURN], par[TURN]
                        act.wait_ge(turned.sem, turned.count(u))
                        act.wait_ge(v_done.sem, v_done.count(u, back=2))
                        nc.scalar.activation(hnT[b][:, :], ps_turn[:, 0:N], ACT.Identity, bias=gb[:, 1:2], scale=gb[:, 0:1]).then_inc(hnT_ready.sem, 1)

                in_lanes(act, UNITS, STAGES, body)

            @block.vector
            def _(dve):
                for x in (nm.stats, nm.moments, yn_ready, top_ready, qtop_ready, inv_ready, o_ready, out_ready):
                    x.opened(dve)
                for b in range(2):
                    nc.vector.memset(v[b][:, :, :, E_HEAD:V], 1.0).then_inc(ones_set, 1)
                for r in range(2):
                    nc.vector.memset(top[r][:, :, :], 0.0).then_inc(constants_set, 1)
                dve.wait_ge(constants_set, 2)

                def sums(u, b, seq):
                    dve.wait_ge(val_done.sem, val_done.count(u, 2 * seq + 2))
                    nc.vector.reciprocal(inv[b][:, :, :], num[:, :, :, E_HEAD]).then_inc(inv_ready.sem, 1)
                    dve.wait_ge(oT_done.sem, oT_done.count(u, back=2))
                    dve.wait_ge(inv_ready.sem, inv_ready.count(u, seq + 1))
                    for c in range(2):
                        last = nc.vector.tensor_tensor(o[b][:, 2 * seq + c, :].rearrange("p (h e) -> p h e", e=E_HEAD),
                                                       num[:, c, :, 0:E_HEAD], wide(inv[b][:, c, :], E_HEAD), ALU.mult)
                    last.then_inc(o_ready.sem, 1)

                def join_top(u, b, r):
                    seq, g = r // 2, r % 2
                    dve.wait_ge(top_turned.sem, top_turned.count(u, r + 1))
                    dve.wait_ge(sc_done.sem, sc_done.count(u, back=2))
                    nc.vector.scalar_tensor_tensor(qtop[b][:, g, seq * SEQ:(seq + 1) * SEQ], ps_turn[:, 0:SEQ], -1.0,
                                                   q[b][:, g, seq * SEQ:(seq + 1) * SEQ], ALU.mult, ALU.add).then_inc(qtop_ready.sem, 1)

                def body(n, par):
                    for r in range(ROUNDS):
                        seq, g = r // 2, r % 2
                        for i in range(4):
                            if n[TOP] is not None:
                                u = n[TOP]
                                dve.wait_ge(top_done.sem, top_done.count(u, 4 * r + i + 1))
                                if i == 0:
                                    dve.wait_ge(top_turned.sem, top_turned.count(u, r - 1))
                                nc.vector.tensor_reduce(top[r % 2][:, :, 32 * i + E_HEAD], ps_top[i % 2][0:HALF, 0:N].rearrange("p (c n) -> p c n", c=2),
                                                        AX.X, ALU.max).then_inc(top_ready.sem, 1)
                            if i == 1 and r == 2 and n[EXP] is not None:
                                sums(n[EXP], par[EXP], 0)
                            if i == 1 and r > 0 and n[TOP] is not None:
                                join_top(n[TOP], par[TOP], r - 1)
                            if i == 0 and n[NORM] is not None:
                                u, b, t = n[NORM], par[NORM], r
                                if t == 0:
                                    dve.wait_ge(x_in[b].sem, x_in[b].count(u, b))
                                    dve.wait_ge(rstd2_ready.sem, rstd2_ready.count(u, back=2))
                                norm_moments(nc, dve, nm, u, b, t, dve_passed)
                            if i == 3 and n[OUT] is not None:
                                u, b, t = n[OUT], par[OUT], r
                                if t == 0:
                                    dve.wait_ge(res_in[b].sem, res_in[b].count(u, b))
                                    dve.wait_ge(stored[b].sem, stored[b].count(u, b, back=1))
                                dve.wait_ge(z_done.sem, z_done.count(u, t + 1))
                                nc.vector.tensor_tensor(out[b][:, t, :], ps_out[0:HALF, 128:256], res[b][:, t, :], ALU.add).then_inc(out_ready.sem, 1)
                    if n[NORM] is not None:
                        u, b = n[NORM], par[NORM]
                        dve.wait_ge(rstd2_ready.sem, rstd2_ready.count(u))
                        dve.wait_ge(turned.sem, turned.count(u, back=2))
                        for t in range(TILES):
                            last = nc.vector.tensor_scalar(yn[b][:, t, :], nm.y[b][:, t, :], var2[b][:, t:t + 1], None, ALU.mult)
                        last.then_inc(yn_ready.sem, 1)
                    if n[EXP] is not None:
                        sums(n[EXP], par[EXP], 1)
                    if n[TOP] is not None:
                        join_top(n[TOP], par[TOP], ROUNDS - 1)

                in_lanes(dve, UNITS, STAGES, body)

            @block.gpsimd
            def _(pool):
                for x in (nm.var_eps, nm.rstd_ready, nm.ready, square_ready, var2_ready, var2_eps, rstd2_ready):
                    x.opened(pool)
                nc.gpsimd.memset(eps[:, :], EPS)
                nc.gpsimd.memset(minus_half[:, :], -0.5).then_inc(pool_set, 1)
                pool.wait_ge(pool_set, 1)

                def body(n, par):
                    if n[NORM] is not None:
                        u, b = n[NORM], par[NORM]
                        pool.wait_ge(y_out[b].sem, y_out[b].count(u, b, back=1))
                        norm_rows(nc, pool, nm, u, b, eps, minus_half, pool_passed, yn_ready)
                        nc.gpsimd.tensor_tensor(var2[b][:, :], nm.rstd[b][:, :], nm.rstd[b][:, :], ALU.mult).then_inc(square_ready.sem, 1)
                        pool.wait_ge(square_ready.sem, square_ready.count(u))
                        nc.gpsimd.tensor_tensor(var2[b][:, :], var2[b][:, :], nm.mv[b][:, :, 1], ALU.mult).then_inc(var2_ready.sem, 1)
                        pool.wait_ge(var2_ready.sem, var2_ready.count(u))
                        nc.gpsimd.tensor_tensor(var2[b][:, :], var2[b][:, :], eps[0:HALF, :], ALU.add).then_inc(var2_eps.sem, 1)
                        pool.wait_ge(var2_eps.sem, var2_eps.count(u))
                        nc.gpsimd.tensor_tensor(var2[b][:, :], var2[b][:, :], minus_half[0:HALF, :], ALU.pow).then_inc(rstd2_ready.sem, 1)

                in_lanes(pool, UNITS, STAGES, body)

        pl.close()


def phase_router(nc, x_in_dram, ident, before, iota64, wr, g_col, b_col, slots, slot_dram, gate_dram):
    UNITS = BATCH // 2
    TILES = 4
    N = TILES * HALF
    E = EXP1
    FAR = 1 << 20
    NORM, TURN, SOFT, GATE, PLACE = range(5)
    STAGES = 5
    with ExitStack() as ctx:
        pl = Place(nc, ctx, "rou")
        sb, sem = pl.sb, pl.sem
        idn = sb("ident", [P, P])
        bef = sb("before", [HALF, HALF])
        ones = sb("ones", [HALF, HALF])
        iota = sb("iota", [P, E])
        wr_sb = sb("wr", [D, E])
        gb = sb("gb", [P, 2])
        eps = sb("eps", [P, TILES])
        minus_half = sb("minus_half", [P, TILES])

        def two(name, shape, dt=F32):
            return [sb(f"{name}{b}", shape, dt) for b in range(2)]

        nm = Norm(pl, TILES, HALF)
        kept = two("kept", [HALF, TILES, D])
        xT = two("xT", [D, N])
        best = two("best", [HALF, TILES])
        ex = two("ex", [HALF, TILES, E])
        total = two("total", [HALF, TILES])
        prob = two("prob", [HALF, TILES, E])
        top = two("top", [HALF, TILES, 8])
        at = two("at", [HALF, TILES, 8], U32)
        atf = two("atf", [HALF, 2, TILES])
        hot = two("hot", [HALF, 2, TILES, E])
        both = two("both", [HALF, TILES, E])
        count = two("count", [HALF, TILES, E])
        share = two("share", [HALF, TILES])
        gate = two("gate", [HALF, 2, TILES])
        mine = two("mine", [HALF, 2, TILES, E])
        pos = two("pos", [HALF, 2, TILES])
        late = two("late", [HALF, 2, TILES])
        base = two("base", [HALF, 2, TILES])
        near = two("near", [HALF, 2, TILES])
        row = two("row", [HALF, 2, TILES])
        row_u = two("row_u", [HALF, 2, TILES], U32)
        read_f = two("read_f", [HALF, 2, TILES])
        read_u = two("read_u", [HALF, 2, TILES], U32)
        gated = two("gated", [HALF, 2, TILES])

        ps_turn, ps_logit, ps_pos = pl.banks("x", 3)
        logit = ps_logit[0:HALF, 0:TILES * E].rearrange("p (t e) -> p t e", e=E)
        place = ps_pos[0:HALF, 0:TILES * E].rearrange("p (t e) -> p t e", e=E)

        weights_in = sem("weights_in")
        WEIGHTS = 6
        constants_set = sem("constants_set")
        counts_set = sem("counts_set")
        dve_passed, pool_passed = sem("dve_passed"), sem("pool_passed")
        x_in = [Landed(sem(f"x_in{b}"), 2) for b in range(2)]
        scattered = [Landed(sem(f"scattered{b}"), 2 * TILES, ahead=0) for b in range(2)]
        scatter_over = Signal(sem("scatter_over"))
        noted = [Landed(sem(f"noted{b}"), 2) for b in range(2)]
        turned = Signal(sem("turned"))
        xT_ready = Signal(sem("xT_ready"))
        kept_ready = Signal(sem("kept_ready"))
        logit_done = Signal(sem("logit_done"))
        best_ready = Signal(sem("best_ready"))
        shifted = Signal(sem("shifted"))
        ex_ready = Signal(sem("ex_ready"))
        total_ready = Signal(sem("total_ready"))
        inv_ready = Signal(sem("inv_ready"))
        prob_ready = Signal(sem("prob_ready"))
        top_ready = Signal(sem("top_ready"))
        at_ready = Signal(sem("at_ready"))
        atf_ready = Signal(sem("atf_ready"))
        hot_ready = Signal(sem("hot_ready"))
        both_ready = Signal(sem("both_ready"))
        share_ready = Signal(sem("share_ready"))
        share_inv = Signal(sem("share_inv"))
        gate_ready = Signal(sem("gate_ready"))
        count_ready = Signal(sem("count_ready"), TILES)
        place_done = Signal(sem("place_done"))
        mine_ready = Signal(sem("mine_ready"))
        pos_ready = Signal(sem("pos_ready"))
        late_ready = Signal(sem("late_ready"))
        row_ready = Signal(sem("row_ready"))
        row_u_ready = Signal(sem("row_u_ready"))
        notes_ready = Signal(sem("notes_ready"))

        with nc.Block() as block:

            @block.sync
            def _(sp):
                for dst, src in ((idn[:, :], ident), (bef[:, :], before), (iota[:, :], iota64), (wr_sb[:, :], wr),
                                 (gb[:, 0:1], g_col), (gb[:, 1:2], b_col)):
                    sp.dma_start(dst, src).then_inc(weights_in, 16)
                for b in range(2):
                    x_in[b].opened(sp)
                    noted[b].opened(sp)
                scatter_over.opened(sp)

                def body(n, par):
                    if n[NORM] is not None:
                        u, b = n[NORM], par[NORM]
                        sp.wait_ge(nm.ready.sem, nm.ready.count(u, back=2))
                        load_rows(sp, nm.x[b], x_in_dram, u, x_in[b])
                    if n[PLACE] is not None:
                        u, b = n[PLACE], par[PLACE]
                        sp.wait_ge(notes_ready.sem, notes_ready.count(u))
                        sp.dma_start(slot_dram[bass.ds(u, 1), :, :].rearrange("u p x -> (u p) x"),
                                     read_u[b][:, :, :].rearrange("p k t -> p (k t)")).then_inc(noted[b].sem, 16)
                        sp.dma_start(gate_dram[bass.ds(u, 1), :, :].rearrange("u p x -> (u p) x"),
                                     gated[b][:, :, :].rearrange("p k t -> p (k t)")).then_inc(noted[b].sem, 16)
                        sp.wait_ge(scattered[b].sem, scattered[b].count(u, b))
                        sp.sem_inc(scatter_over.sem, 1)

                in_lanes(sp, UNITS, STAGES, body)
                for b in range(2):
                    sp.wait_ge(noted[b].sem, noted[b].final(UNITS))
                    sp.wait_ge(scattered[b].sem, scattered[b].final(UNITS))

            @block.tensor
            def _(pe):
                for x in (turned, logit_done, place_done):
                    x.opened(pe)
                pe.wait_ge(weights_in, 16 * WEIGHTS)
                pe.wait_ge(counts_set, 3)

                def body(n, par):
                    if n[PLACE] is not None:
                        u, b = n[PLACE], par[PLACE]
                        pe.wait_ge(count_ready.sem, count_ready.count(u))
                        pe.wait_ge(mine_ready.sem, mine_ready.count(u, back=1))
                        for t in range(TILES):
                            nc.tensor.matmul(place[:, t, :], bef[:, :], both[b][:, t, :], start=True, stop=False)
                            last = nc.tensor.matmul(place[:, t, :], ones[:, :], count[b][:, t, :], start=False, stop=True)
                        last.then_inc(place_done.sem, 1)
                    if n[SOFT] is not None:
                        u, b = n[SOFT], par[SOFT]
                        pe.wait_ge(xT_ready.sem, xT_ready.count(u))
                        pe.wait_ge(shifted.sem, shifted.count(u, back=1))
                        for t in range(TILES):
                            last = nc.tensor.matmul(logit[:, t, :], xT[b][:, t * HALF:(t + 1) * HALF], wr_sb[:, :], start=True, stop=True)
                        last.then_inc(logit_done.sem, 1)
                    if n[TURN] is not None:
                        u, b = n[TURN], par[TURN]
                        pe.wait_ge(nm.ready.sem, nm.ready.count(u))
                        pe.wait_ge(xT_ready.sem, xT_ready.count(u, back=1))
                        for t in range(TILES):
                            last = nc.tensor.transpose(ps_turn[:, t * HALF:(t + 1) * HALF], nm.y[b][:, t, :], idn[0:HALF, 0:HALF])
                        last.then_inc(turned.sem, 1)

                in_lanes(pe, UNITS, STAGES, body)

            @block.scalar
            def _(act):
                for x in (xT_ready, kept_ready, ex_ready):
                    x.opened(act)
                act.wait_ge(weights_in, 16 * WEIGHTS)

                def body(n, par):
                    if n[SOFT] is not None:
                        u, b = n[SOFT], par[SOFT]
                        act.wait_ge(shifted.sem, shifted.count(u))
                        nc.scalar.activation(ex[b][:, :, :], ex[b][:, :, :], ACT.Exp).then_inc(ex_ready.sem, 1)
                    if n[TURN] is not None:
                        u, b = n[TURN], par[TURN]
                        act.wait_ge(turned.sem, turned.count(u))
                        act.wait_ge(logit_done.sem, logit_done.count(u, back=2))
                        nc.scalar.activation(xT[b][:, :], ps_turn[:, 0:N], ACT.Identity, bias=gb[:, 1:2], scale=gb[:, 0:1]).then_inc(xT_ready.sem, 1)
                    if n[SOFT] is not None:
                        u, b = n[SOFT], par[SOFT]
                        act.wait_ge(scatter_over.sem, scatter_over.count(u, back=2))
                        act.wait_ge(nm.ready.sem, nm.ready.count(u))
                        nc.scalar.copy(kept[b][:, :, :], nm.y[b][:, :, :]).then_inc(kept_ready.sem, 1)

                in_lanes(act, UNITS, STAGES, body)

            @block.vector
            def _(dve):
                for x in (nm.stats, nm.moments, best_ready, shifted, total_ready, inv_ready, prob_ready, top_ready, at_ready,
                          atf_ready, hot_ready, both_ready, share_ready, share_inv, gate_ready, count_ready, mine_ready,
                          pos_ready, late_ready, row_ready, row_u_ready, notes_ready):
                    x.opened(dve)
                nc.vector.memset(ones[:, :], 1.0).then_inc(counts_set, 1)
                nc.vector.memset(both[1][:, :, :], 0.0).then_inc(counts_set, 1)
                nc.vector.memset(count[1][:, :, :], 0.0).then_inc(counts_set, 1)
                dve.wait_ge(counts_set, 3)
                dve.wait_ge(weights_in, 16 * WEIGHTS)

                def body(n, par):
                    if n[PLACE] is not None:
                        u, b = n[PLACE], par[PLACE]
                        dve.wait_ge(both_ready.sem, both_ready.count(u))
                        dve.wait_ge(place_done.sem, place_done.count(u, back=2))
                        for t in range(TILES):
                            if t > 0:
                                dve.wait_ge(count_ready.sem, count_ready.count(u, t))
                                nc.vector.tensor_tensor(count[b][:, t, :], count[b][:, t - 1, :], both[b][:, t - 1, :], ALU.add).then_inc(count_ready.sem, 1)
                            else:
                                dve.wait_ge(count_ready.sem, count_ready.count(u, back=1))
                                nc.vector.tensor_tensor(count[b][:, 0, :], count[1 - b][:, TILES - 1, :], both[1 - b][:, TILES - 1, :],
                                                        ALU.add).then_inc(count_ready.sem, 1)
                    if n[NORM] is not None:
                        u, b = n[NORM], par[NORM]
                        dve.wait_ge(x_in[b].sem, x_in[b].count(u, b))
                        dve.wait_ge(nm.ready.sem, nm.ready.count(u, back=2))
                        for t in range(TILES):
                            norm_moments(nc, dve, nm, u, b, t, dve_passed)
                    if n[SOFT] is not None:
                        u, b = n[SOFT], par[SOFT]
                        dve.wait_ge(logit_done.sem, logit_done.count(u))
                        nc.vector.tensor_reduce(best[b][:, :], logit, AX.X, ALU.max).then_inc(best_ready.sem, 1)
                        dve.wait_ge(best_ready.sem, best_ready.count(u))
                        dve.wait_ge(prob_ready.sem, prob_ready.count(u, back=2))
                        nc.vector.tensor_tensor(ex[b][:, :, :], logit, wide(best[b][:, :], E), ALU.subtract).then_inc(shifted.sem, 1)
                    if n[GATE] is not None:
                        u, b = n[GATE], par[GATE]
                        dve.wait_ge(ex_ready.sem, ex_ready.count(u))
                        nc.vector.tensor_reduce(total[b][:, :], ex[b][:, :, :], AX.X, ALU.add).then_inc(total_ready.sem, 1)
                        dve.wait_ge(total_ready.sem, total_ready.count(u))
                        nc.vector.reciprocal(total[b][:, :], total[b][:, :]).then_inc(inv_ready.sem, 1)
                        dve.wait_ge(inv_ready.sem, inv_ready.count(u))
                        nc.vector.tensor_tensor(prob[b][:, :, :], ex[b][:, :, :], wide(total[b][:, :], E), ALU.mult).then_inc(prob_ready.sem, 1)
                        dve.wait_ge(prob_ready.sem, prob_ready.count(u))
                        dve.sem_inc(dve_passed, 1)
                        for t in range(TILES):
                            last = nc.vector.max(top[b][:, t, :], prob[b][:, t, :])
                        last.then_inc(top_ready.sem, 1)
                        dve.wait_ge(top_ready.sem, top_ready.count(u))
                        nc.vector.tensor_tensor(share[b][:, :], top[b][:, :, 0], top[b][:, :, 1], ALU.add).then_inc(share_ready.sem, 1)
                        for t in range(TILES):
                            last = nc.vector.max_index(at[b][:, t, :], top[b][:, t, :], prob[b][:, t, :])
                        last.then_inc(at_ready.sem, 1)
                        dve.wait_ge(share_ready.sem, share_ready.count(u))
                        nc.vector.reciprocal(share[b][:, :], share[b][:, :]).then_inc(share_inv.sem, 1)
                        dve.wait_ge(at_ready.sem, at_ready.count(u))
                        nc.vector.tensor_copy(atf[b][:, :, :], at[b][:, :, 0:2].rearrange("p t k -> p k t")).then_inc(atf_ready.sem, 1)
                        dve.wait_ge(share_inv.sem, share_inv.count(u))
                        nc.vector.tensor_tensor(gate[b][:, :, :], top[b][:, :, 0:2].rearrange("p t k -> p k t"), over(share[b][:, :], 2),
                                                ALU.mult).then_inc(gate_ready.sem, 1)
                        dve.wait_ge(atf_ready.sem, atf_ready.count(u))
                        for k in range(2):
                            last = nc.vector.tensor_tensor(hot[b][:, k, :, :], over(iota[0:HALF, :], TILES), wide(atf[b][:, k, :], E), ALU.is_equal)
                        last.then_inc(hot_ready.sem, 1)
                        dve.wait_ge(hot_ready.sem, hot_ready.count(u))
                        nc.vector.tensor_tensor(both[b][:, :, :], hot[b][:, 0, :, :], hot[b][:, 1, :, :], ALU.add).then_inc(both_ready.sem, 1)
                    if n[PLACE] is not None:
                        u, b = n[PLACE], par[PLACE]
                        dve.wait_ge(place_done.sem, place_done.count(u))
                        for k in range(2):
                            last = nc.vector.tensor_tensor(mine[b][:, k, :, :], hot[b][:, k, :, :], place, ALU.mult)
                        last.then_inc(mine_ready.sem, 1)
                        dve.wait_ge(mine_ready.sem, mine_ready.count(u))
                        nc.vector.tensor_reduce(pos[b][:, :, :], mine[b][:, :, :, :], AX.X, ALU.add).then_inc(pos_ready.sem, 1)
                        dve.wait_ge(pos_ready.sem, pos_ready.count(u))
                        dve.wait_ge(noted[b].sem, noted[b].count(u, b, back=1))
                        nc.vector.tensor_scalar(late[b][:, :, :], pos[b][:, :, :], float(CAP), float(FAR), ALU.is_ge, ALU.mult)
                        nc.vector.tensor_scalar(base[b][:, :, :], atf[b][:, :, :], float(CAP), None, ALU.mult)
                        nc.vector.tensor_scalar(near[b][:, :, :], pos[b][:, :, :], float(CAP - 1), None, ALU.min)
                        nc.vector.scalar_tensor_tensor(gated[b][:, :, :], pos[b][:, :, :], float(CAP), gate[b][:, :, :], ALU.is_lt, ALU.mult).then_inc(late_ready.sem, 1)
                        dve.wait_ge(late_ready.sem, late_ready.count(u))
                        nc.vector.tensor_tensor(row[b][:, :, :], base[b][:, :, :], pos[b][:, :, :], ALU.add)
                        nc.vector.tensor_tensor(read_f[b][:, :, :], base[b][:, :, :], near[b][:, :, :], ALU.add).then_inc(row_ready.sem, 1)
                        dve.wait_ge(row_ready.sem, row_ready.count(u))
                        dve.wait_ge(scatter_over.sem, scatter_over.count(u, back=2))
                        nc.vector.tensor_tensor(row_u[b][:, :, :], row[b][:, :, :], late[b][:, :, :], ALU.add).then_inc(row_u_ready.sem, 1)
                        nc.vector.tensor_copy(read_u[b][:, :, :], read_f[b][:, :, :]).then_inc(notes_ready.sem, 1)

                in_lanes(dve, UNITS, STAGES, body)

            @block.gpsimd
            def _(pool):
                for x in (nm.var_eps, nm.rstd_ready, nm.ready):
                    x.opened(pool)
                nc.gpsimd.memset(eps[:, :], EPS)
                nc.gpsimd.memset(minus_half[:, :], -0.5).then_inc(constants_set, 1)
                pool.wait_ge(constants_set, 1)

                def body(n, par):
                    if n[PLACE] is not None:
                        u, b = n[PLACE], par[PLACE]
                        pool.wait_ge(kept_ready.sem, kept_ready.count(u))
                        pool.wait_ge(row_u_ready.sem, row_u_ready.count(u))
                        pool.sem_inc(pool_passed, 1)
                        for k in range(2):
                            for t in range(TILES):
                                nc.gpsimd.indirect_dma_start(
                                    out=slots, out_offset=bass.IndirectOffsetOnAxis(ap=row_u[b][:, k, t:t + 1], axis=0),
                                    in_=kept[b][:, t, :], in_offset=None, bounds_check=EXP1 * CAP - 1,
                                    oob_is_err=False).then_inc(scattered[b].sem, 16)
                    if n[NORM] is not None:
                        u, b = n[NORM], par[NORM]
                        pool.wait_ge(kept_ready.sem, kept_ready.count(u, back=2))
                        norm_rows(nc, pool, nm, u, b, eps, minus_half, pool_passed, turned)

                in_lanes(pool, UNITS, STAGES, body)

        pl.close()


def phase_experts64(nc, slots, ident, g_col, b_col, w1, b1, w2, b2, y_dram):
    TILES = CAP // HALF
    N = CAP // 2
    CH = FF1 // P
    LOAD, TURN, HID, OUT = range(4)
    STAGES = 4
    with ExitStack() as ctx:
        pl = Place(nc, ctx, "exp")
        sb, sem = pl.sb, pl.sem
        idn = sb("ident", [P, P])
        gb = sb("gb", [P, 2])

        def two(name, shape, dt=F32):
            return [sb(f"{name}{b}", shape, dt) for b in range(2)]

        x = two("x", [HALF, TILES, D])
        w1_sb = two("w1", [D, FF1])
        b1_sb = two("b1", [P, CH])
        w2_sb = two("w2", [P, CH, D])
        b2_sb = two("b2", [P, D])
        xT = two("xT", [D, CAP])
        hid = two("hid", [P, CH, CAP])
        y = two("y", [HALF, TILES, D])
        ps_turn = pl.banks("turn", 2)
        ps_hid = pl.banks("hid", 2)
        ps_out = pl.banks("out", 2)

        weights_in = sem("weights_in")
        pe_passed, = (sem("pe_passed"),)
        x_in = [Landed(sem(f"x_in{b}"), 1) for b in range(2)]
        w1_in = [Landed(sem(f"w1_in{b}"), 2) for b in range(2)]
        w2_in = [Landed(sem(f"w2_in{b}"), 2) for b in range(2)]
        stored = [Landed(sem(f"stored{b}"), 1) for b in range(2)]
        turned = Signal(sem("turned"), 2)
        xT_ready = Signal(sem("xT_ready"), 2)
        hid_done = Signal(sem("hid_done"), 2 * CH)
        hid_ready = Signal(sem("hid_ready"), 2 * CH)
        out_done = Signal(sem("out_done"), TILES)
        y_ready = Signal(sem("y_ready"), TILES)

        with nc.Block() as block:

            @block.sync
            def _(sp):
                for dst, src in ((idn[:, :], ident), (gb[:, 0:1], g_col), (gb[:, 1:2], b_col)):
                    sp.dma_start(dst, src).then_inc(weights_in, 16)
                for s in x_in + w1_in + w2_in + stored:
                    s.opened(sp)

                def body(n, par):
                    if n[LOAD] is not None:
                        u, b = n[LOAD], par[LOAD]
                        sp.wait_ge(turned.sem, turned.count(u, back=2))
                        sp.dma_start(x[b][:, :, :], slots[bass.ds(u * CAP, CAP), :].rearrange("(p t) d -> p t d", t=TILES)).then_inc(x_in[b].sem, 16)
                    if n[TURN] is not None:
                        u, b = n[TURN], par[TURN]
                        sp.wait_ge(hid_ready.sem, hid_ready.count(u, back=2))
                        sp.dma_start(w1_sb[b][:, :], w1[bass.ds(u, 1), :, :].rearrange("e d f -> (e d) f")).then_inc(w1_in[b].sem, 16)
                        sp.dma_start(b1_sb[b][:, :], b1[bass.ds(u, 1), :, :].rearrange("e p c -> (e p) c")).then_inc(w1_in[b].sem, 16)
                    if n[HID] is not None:
                        u, b = n[HID], par[HID]
                        sp.wait_ge(y_ready.sem, y_ready.count(u, back=2))
                        sp.dma_start(w2_sb[b][:, :, :], w2[bass.ds(u, 1), :, :].rearrange("e (c p) d -> p (e c) d", p=P)).then_inc(w2_in[b].sem, 16)
                        sp.dma_start(b2_sb[b][:, :], b2[bass.ds(u, 1), :].to_broadcast([P, D])).then_inc(w2_in[b].sem, 16)
                    if n[OUT] is not None:
                        u, b = n[OUT], par[OUT]
                        sp.wait_ge(y_ready.sem, y_ready.count(u))
                        sp.dma_start(y_dram[bass.ds(u * CAP, CAP), :].rearrange("(p t) d -> p t d", t=TILES), y[b][:, :, :]).then_inc(stored[b].sem, 16)

                in_lanes(sp, EXP1, STAGES, body)
                for b in range(2):
                    sp.wait_ge(stored[b].sem, stored[b].final(EXP1))

            @block.tensor
            def _(pe):
                for s in (turned, hid_done, out_done):
                    s.opened(pe)
                pe.wait_ge(weights_in, 48)

                def body(n, par):
                    for r in range(TILES):
                        if n[HID] is not None:
                            u, b = n[HID], par[HID]
                            half, c = r // CH, r % CH
                            if r == 0:
                                pe.wait_ge(w1_in[b].sem, w1_in[b].count(u, b))
                                pe.wait_ge(xT_ready.sem, xT_ready.count(u))
                            pe.wait_ge(hid_ready.sem, hid_ready.count(u, r - 1))
                            nc.tensor.matmul(ps_hid[r % 2][:, 0:N], w1_sb[b][:, c * P:(c + 1) * P], xT[b][:, half * N:(half + 1) * N],
                                             start=True, stop=True).then_inc(hid_done.sem, 1)
                        if n[OUT] is not None:
                            u, b = n[OUT], par[OUT]
                            if r == 0:
                                pe.wait_ge(w2_in[b].sem, w2_in[b].count(u, b))
                                pe.wait_ge(hid_ready.sem, hid_ready.count(u))
                            pe.wait_ge(y_ready.sem, y_ready.count(u, r - 1))
                            for c in range(CH):
                                last = nc.tensor.matmul(ps_out[r % 2][0:HALF, 0:D], hid[b][:, c, r * HALF:(r + 1) * HALF], w2_sb[b][:, c, :],
                                                        start=c == 0, stop=c == CH - 1)
                            last.then_inc(out_done.sem, 1)
                    if n[TURN] is not None:
                        u, b = n[TURN], par[TURN]
                        pe.wait_ge(x_in[b].sem, x_in[b].count(u, b))
                        for half in range(2):
                            pe.wait_ge(xT_ready.sem, xT_ready.count(u, half + 1, back=1))
                            for t in range(TILES // 2):
                                last = nc.tensor.transpose(ps_turn[half][:, t * HALF:(t + 1) * HALF], x[b][:, half * TILES // 2 + t, :], idn[0:HALF, 0:HALF])
                            last.then_inc(turned.sem, 1)

                in_lanes(pe, EXP1, STAGES, body)

            @block.scalar
            def _(act):
                for s in (xT_ready, hid_ready):
                    s.opened(act)
                act.wait_ge(weights_in, 48)

                def body(n, par):
                    for r in range(TILES):
                        if n[HID] is not None:
                            u, b = n[HID], par[HID]
                            half, c = r // CH, r % CH
                            if r == 0:
                                act.wait_ge(w1_in[b].sem, w1_in[b].count(u, b))
                                act.wait_ge(out_done.sem, out_done.count(u, back=2))
                            act.wait_ge(hid_done.sem, hid_done.count(u, r + 1))
                            nc.scalar.activation(hid[b][:, c, half * N:(half + 1) * N], ps_hid[r % 2][:, 0:N], ACT.Gelu_apprx_tanh,
                                                 bias=b1_sb[b][:, c:c + 1]).then_inc(hid_ready.sem, 1)
                    if n[TURN] is not None:
                        u, b = n[TURN], par[TURN]
                        act.wait_ge(hid_done.sem, hid_done.count(u, back=2))
                        for half in range(2):
                            act.wait_ge(turned.sem, turned.count(u, half + 1))
                            nc.scalar.activation(xT[b][:, half * N:(half + 1) * N], ps_turn[half][:, 0:N], ACT.Identity,
                                                 bias=gb[:, 1:2], scale=gb[:, 0:1]).then_inc(xT_ready.sem, 1)

                in_lanes(act, EXP1, STAGES, body)

            @block.vector
            def _(dve):
                y_ready.opened(dve)

                def body(n, par):
                    for r in range(TILES):
                        if n[OUT] is not None:
                            u, b = n[OUT], par[OUT]
                            if r == 0:
                                dve.wait_ge(w2_in[b].sem, w2_in[b].count(u, b))
                                dve.wait_ge(stored[b].sem, stored[b].count(u, b, back=1))
                            dve.wait_ge(out_done.sem, out_done.count(u, r + 1))
                            nc.vector.tensor_tensor(y[b][:, r, :], ps_out[r % 2][0:HALF, 0:D], b2_sb[b][0:HALF, :], ALU.add).then_inc(y_ready.sem, 1)

                in_lanes(dve, EXP1, STAGES, body)

        pl.close()


def phase_combine(nc, h_dram, x_dram, y_dram, slot_dram, gate_dram, out_dram):
    UNITS = BATCH // 2
    TILES = 4
    LOAD, GATHER, SUM = range(3)
    STAGES = 3
    with ExitStack() as ctx:
        pl = Place(nc, ctx, "com")
        sb, sem = pl.sb, pl.sem

        def two(name, shape, dt=F32):
            return [sb(f"{name}{b}", shape, dt) for b in range(2)]

        slot = two("slot", [HALF, 2 * TILES], U32)
        gate = two("gate", [HALF, 2 * TILES])
        h = two("h", [HALF, TILES, D])
        x = two("x", [HALF, TILES, D])
        y = two("y", [HALF, 2, TILES, D])
        acc = two("acc", [HALF, TILES, D])
        pool_passed = sem("pool_passed")
        slot_in = [Landed(sem(f"slot_in{b}"), 2) for b in range(2)]
        rows_in = [Landed(sem(f"rows_in{b}"), 4) for b in range(2)]
        gathered = [Landed(sem(f"gathered{b}"), 2 * TILES, ahead=0) for b in range(2)]
        stored = [Landed(sem(f"stored{b}"), 2) for b in range(2)]
        base_ready = Signal(sem("base_ready"))
        acc_ready = Signal(sem("acc_ready"), 2)

        with nc.Block() as block:

            @block.sync
            def _(sp):
                for s in slot_in + rows_in + stored:
                    s.opened(sp)

                def body(n, par):
                    if n[LOAD] is not None:
                        u, b = n[LOAD], par[LOAD]
                        sp.wait_ge(acc_ready.sem, acc_ready.count(u, back=2))
                        sp.dma_start(slot[b][:, :], slot_dram[bass.ds(u, 1), :, :].rearrange("u p x -> (u p) x")).then_inc(slot_in[b].sem, 16)
                        sp.dma_start(gate[b][:, :], gate_dram[bass.ds(u, 1), :, :].rearrange("u p x -> (u p) x")).then_inc(slot_in[b].sem, 16)
                        load_rows(sp, h[b], h_dram, u, rows_in[b])
                        load_rows(sp, x[b], x_dram, u, rows_in[b])
                    if n[SUM] is not None:
                        u, b = n[SUM], par[SUM]
                        sp.wait_ge(acc_ready.sem, acc_ready.count(u))
                        store_rows(sp, out_dram, acc[b], u, stored[b])

                in_lanes(sp, UNITS, STAGES, body)
                for b in range(2):
                    sp.wait_ge(stored[b].sem, stored[b].final(UNITS))

            @block.gpsimd
            def _(pool):
                def body(n, par):
                    if n[GATHER] is not None:
                        u, b = n[GATHER], par[GATHER]
                        pool.wait_ge(acc_ready.sem, acc_ready.count(u, back=2))
                        pool.wait_ge(slot_in[b].sem, slot_in[b].count(u, b))
                        pool.sem_inc(pool_passed, 1)
                        for k in range(2):
                            for t in range(TILES):
                                nc.gpsimd.indirect_dma_start(
                                    out=y[b][:, k, t, :], out_offset=None, in_=y_dram,
                                    in_offset=bass.IndirectOffsetOnAxis(ap=slot[b][:, k * TILES + t:k * TILES + t + 1], axis=0),
                                    ).then_inc(gathered[b].sem, 16)

                in_lanes(pool, UNITS, STAGES, body)

            @block.vector
            def _(dve):
                for s in (base_ready, acc_ready):
                    s.opened(dve)

                def body(n, par):
                    if n[SUM] is not None:
                        u, b = n[SUM], par[SUM]
                        dve.wait_ge(rows_in[b].sem, rows_in[b].count(u, b))
                        dve.wait_ge(stored[b].sem, stored[b].count(u, b, back=1))
                        nc.vector.tensor_tensor(acc[b][:, :, :], h[b][:, :, :], x[b][:, :, :], ALU.add).then_inc(base_ready.sem, 1)
                        dve.wait_ge(base_ready.sem, base_ready.count(u))
                        dve.wait_ge(gathered[b].sem, gathered[b].count(u, b))
                        for k in range(2):
                            if k == 1:
                                dve.wait_ge(acc_ready.sem, acc_ready.count(u, 1))
                            for t in range(TILES):
                                last = nc.vector.scalar_tensor_tensor(acc[b][:, t, :], y[b][:, k, t, :], gate[b][:, k * TILES + t:k * TILES + t + 1],
                                                                      acc[b][:, t, :], ALU.mult, ALU.add)
                            last.then_inc(acc_ready.sem, 1)

                in_lanes(dve, UNITS, STAGES, body)

        pl.close()


def audio_tower(nc, a, out):
    def scratch(name, shape, dt=F32):
        return nc.dram_tensor(name, shape, dt, kind="Internal").ap()

    h0 = scratch("h0", [POS_PAD, BATCH, D])
    h1 = scratch("h1", [BATCH, POS_PAD, D])
    h2 = scratch("h2", [BATCH, SEQ, D])
    h3 = scratch("h3", [BATCH, SEQ, D])
    y4 = scratch("y4", [BATCH, SEQ, D])
    x5 = scratch("x5", [BATCH, SEQ, D])
    slots = scratch("slots", [EXP1 * CAP, D])
    y_slots = scratch("y_slots", [EXP1 * CAP, D])
    slot_of = scratch("slot_of", [BATCH // 2, HALF, 8], U32)
    gate_of = scratch("gate_of", [BATCH // 2, HALF, 8])

    phase_token_mixer(nc, a["x"], a["ident"], a["tok_w_compress"], a["tok_w_main"], a["tok_w_expand"], a["tok_w_ff1"],
                      a["tok_w_ff2"], a["tok_b_compress"], a["tok_b_main"], a["tok_b_ff1"], a["tok_g1_col"],
                      a["tok_b1_col"], a["tok_g2_col"], a["tok_b2_col"], a["tok_b_expand"], a["tok_g1_row"],
                      a["tok_b1_row"], a["tok_b_ff2"], h0, slots)
    phase_batch_attention(nc, h0, a["ident"], a["bat_mask"], a["bat_wq"], a["bat_wk"], a["bat_wv"], a["bat_wo"], h1)
    phase_experts8(nc, h1, a["ident"], a["mix_iota"], a["mix_wg"], a["mix_w1"], a["mix_b1"], a["mix_w2"], a["mix_b2"],
                   a["mix_gamma"], a["mix_beta"], h2)
    phase_linear_attention(nc, h2, a["ident"], a["lin_mask"], a["lin_index"], a["lin_live"], a["lin_wq"], a["lin_wk"],
                           a["lin_wv"], a["lin_bqk"], a["lin_bv"], a["lin_decay"], a["lin_wo"], a["lin_bo"], a["lin_g"],
                           a["lin_b"], h3)
    phase_attention(nc, h3, a["ident"], a["att_ones_row"], a["att_wq"], a["att_wk"], a["att_wv"], a["att_wo"],
                    a["att_g"], a["att_b"], y4, x5)
    phase_router(nc, x5, a["ident"], a["rou_before"], a["rou_iota"], a["rou_wr"], a["exp_g"], a["exp_b"], slots,
                 slot_of, gate_of)
    phase_experts64(nc, slots, a["ident"], a["exp_g"], a["exp_b"], a["exp_w1"], a["exp_b1"], a["exp_w2"], a["exp_b2"],
                    y_slots)
    phase_combine(nc, h3, x5, y_slots, slot_of, gate_of, out)


def layouts(inputs, np):
    tok = {n[7:]: w for n, w in inputs.items() if n.startswith("L0_tok_")}
    bat = {n[8:]: w for n, w in inputs.items() if n.startswith("L0_attn_")}
    mix = {n[7:]: w for n, w in inputs.items() if n.startswith("L0_ffn_")}
    lin = {n[8:]: w for n, w in inputs.items() if n.startswith("L1_attn_")}
    ffn = {n[7:]: w for n, w in inputs.items() if n.startswith("L1_ffn_")}

    def heads(w):
        w = w.reshape(w.shape[:-1] + (N_HEAD, E_HEAD))
        return np.concatenate([w, np.zeros_like(w)], -1).reshape(w.shape[:-2] + (2 * D,))

    f32 = np.float32
    at = np.arange(HALF)
    upto = (at[None, :] >= at[:, None]).astype(f32)
    row = np.arange(P) % 32
    live = (row < E_HEAD).astype(f32)
    pos = np.arange(SEQ, dtype=f32)
    width = N_HEAD * D_HEAD
    bqk = [heads(lin["b_qkv"][i * D:(i + 1) * D]).reshape(2, P) for i in range(2)]
    return {
        "x": inputs["x"],
        "ident": np.eye(P, dtype=f32),
        "tok_w_compress": tok["w_compress"][:, :, 0].T, "tok_w_main": tok["w_main"].transpose(1, 2, 0),
        "tok_w_expand": tok["w_expand"][:, :, 0].T, "tok_w_ff1": tok["w_ff1"].T, "tok_w_ff2": tok["w_ff2"].T,
        "tok_b_compress": tok["b_compress"][:, None], "tok_b_main": tok["b_main"][:, None],
        "tok_b_ff1": tok["b_ff1"][:, None], "tok_g1_col": tok["g_conv_norm"][:, None],
        "tok_b1_col": tok["b_conv_norm"][:, None], "tok_g2_col": tok["g_ff_norm"][:, None],
        "tok_b2_col": tok["b_ff_norm"][:, None], "tok_b_expand": tok["b_expand"], "tok_g1_row": tok["g_conv_norm"],
        "tok_b1_row": tok["b_conv_norm"], "tok_b_ff2": tok["b_ff2"],
        "bat_mask": np.where(np.arange(4 * P)[None, :] % BATCH > np.arange(P)[:, None] % BATCH, f32(-1e6), f32(0)),
        "bat_wq": bat["Wq"].T, "bat_wk": bat["Wkv"][:width].T, "bat_wv": bat["Wkv"][width:].T, "bat_wo": bat["Wo"].T,
        "mix_iota": np.tile(np.arange(EXP0, dtype=f32), (P, 1)), "mix_wg": mix["Wg"], "mix_w1": mix["W1"],
        "mix_b1": mix["b1"].T, "mix_w2": mix["W2"], "mix_b2": mix["b2"].reshape(-1),
        "mix_gamma": mix["gamma"].reshape(-1), "mix_beta": mix["beta"],
        "lin_mask": np.concatenate([upto, np.ones((HALF, HALF), f32), upto], 1),
        "lin_index": np.tile(np.concatenate([pos, -pos]), (P, 1)), "lin_live": np.stack([live, live / 4], 1),
        "lin_wq": heads(lin["W_qkv"][:, :D]), "lin_wk": heads(lin["W_qkv"][:, D:2 * D]), "lin_wv": lin["W_qkv"][:, 2 * D:],
        "lin_bqk": np.stack(bqk).transpose(2, 0, 1).reshape(P, 4), "lin_bv": lin["b_qkv"][2 * D:],
        "lin_decay": np.repeat(lin["decay_logits"].reshape(2, 4), 32, axis=1).T, "lin_wo": lin["W_out"],
        "lin_bo": lin["b_out"], "lin_g": lin["ln_g"], "lin_b": lin["ln_b"],
        "att_ones_row": (row == E_HEAD).astype(f32)[:, None], "att_wq": heads(ffn["wq"]), "att_wk": heads(ffn["wk"]),
        "att_wv": ffn["wv"], "att_wo": ffn["wo"], "att_g": ffn["ln1_g"][:, None], "att_b": ffn["ln1_b"][:, None],
        "rou_before": (at[:, None] < at[None, :]).astype(f32), "rou_iota": np.tile(np.arange(EXP1, dtype=f32), (P, 1)),
        "rou_wr": ffn["wr"], "exp_g": ffn["ln2_g"][:, None], "exp_b": ffn["ln2_b"][:, None], "exp_w1": ffn["w1"],
        "exp_b1": ffn["b1"].reshape(EXP1, 4, P).transpose(0, 2, 1), "exp_w2": ffn["w2"], "exp_b2": ffn["b2"],
    }


def kernel(**inputs):
    import numpy as np
    import concourse.bacc as bacc
    from concourse.bass_utils import run_bass_kernel_spmd

    nc = bacc.Bacc("TRN2", target_bir_lowering=False, num_devices=1)
    arrays = {n: np.ascontiguousarray(a) for n, a in layouts({n: np.asarray(a) for n, a in inputs.items()}, np).items()}
    args = {n: nc.dram_tensor(n, a.shape, mybir.dt.from_np(a.dtype), kind="ExternalInput").ap() for n, a in arrays.items()}
    out = nc.dram_tensor("out", [BATCH, SEQ, D], F32, kind="ExternalOutput").ap()
    audio_tower(nc, args, out)
    return run_bass_kernel_spmd(nc, [arrays], core_ids=[0]).results[0]["out"]
```

```python
from contextlib import ExitStack

import concourse.bass as bass
from concourse import mybir

F32 = mybir.dt.float32
U32 = mybir.dt.uint32
I32 = mybir.dt.int32
ACT = mybir.ActivationFunctionType
ALU = mybir.AluOpType
AX = mybir.AxisListType

P = 128
BATCH = 64
T_IN = 256
SEQ = 254
HALF = 127
D = 128
BN = 64
TOKENS = BATCH * SEQ
POS_PAD = 256
EPS = 1e-5

N_HEAD = 8
D_HEAD = 64
E_HEAD = 16

EXP0 = 8
EXP1 = 64
FF1 = 512
CAP = 1016
assert CAP == 2 * (TOKENS * 2 // EXP1) and CAP == 8 * HALF


def over(ap, n):
    p, f = ap.shape
    return ap.unsqueeze(1).to_broadcast([p, n, f])


def wide(ap, n):
    p, g = ap.shape
    return ap.unsqueeze(2).to_broadcast([p, g, n])


class Place:

    def __init__(self, nc, ctx, phase):
        self.nc, self.ctx, self.phase = nc, ctx, phase
        self.sems = []

    def sb(self, name, shape, dt=F32):
        return self.ctx.enter_context(self.nc.sbuf_tensor(f"{self.phase}_sb_{name}", shape, dt))

    def banks(self, name, n):
        return [self.ctx.enter_context(self.nc.psum_tensor(f"{self.phase}_bank_{name}{i}", [P, 512], F32))
                for i in range(n)]

    def sem(self, name):
        self.sems.append(self.nc.alloc_semaphore(f"{self.phase}_{name}"))
        return self.sems[-1]

    def close(self):
        self.nc.clear_and_free_semaphores(self.sems)
        self.nc.all_engine_barrier()


class Signal:

    AHEAD = 2

    def __init__(self, sem, per=1):
        self.sem, self.per = sem, per

    def opened(self, eng):
        eng.sem_inc(self.sem, self.AHEAD * self.per)

    def count(self, unit, k=None, back=0):
        k = self.per if k is None else k
        return unit * self.per + (self.AHEAD - back) * self.per + k


class Landed:

    def __init__(self, sem, dmas, ahead=1):
        self.sem, self.all, self.ahead = sem, 16 * dmas, ahead

    def opened(self, eng):
        eng.sem_inc(self.sem, self.ahead * self.all)

    def count(self, unit, parity, back=0):
        return (unit - parity) * (self.all // 2) + (1 + self.ahead - back) * self.all

    def final(self, units):
        return (units // 2 + self.ahead) * self.all


def in_lanes(eng, units, stages, body):
    lead = stages - 1 + (stages - 1) % 2
    turns = (units - lead) // 2

    def step(first, fixed):
        body([first - s if 0 <= fixed - s < units else None for s in range(stages)],
             [(fixed - s) % 2 for s in range(stages)])

    for n in range(lead):
        step(n, n)
    with eng.Fori(0, turns) as turn:
        for odd in range(2):
            step(turn * 2 + (lead + odd), lead + odd)
    for n in range(lead + 2 * turns, units + stages - 1):
        step(n, n)


def load_rows(eng, dst, h, unit, landed):
    for b in range(2):
        eng.dma_start(dst[:, 2 * b:2 * b + 2, :],
                      h[bass.ds(unit * 2 + b, 1), 0:SEQ, :].rearrange("b (c p) d -> p (b c) d", p=HALF)).then_inc(landed.sem, 16)


def store_rows(eng, h, src, unit, landed):
    for b in range(2):
        eng.dma_start(h[bass.ds(unit * 2 + b, 1), 0:SEQ, :].rearrange("b (c p) d -> p (b c) d", p=HALF),
                      src[:, 2 * b:2 * b + 2, :]).then_inc(landed.sem, 16)


class Norm:

    def __init__(self, pl, tiles, rows):
        self.tiles, self.rows = tiles, rows
        sb, sem = pl.sb, pl.sem
        self.x = [sb(f"norm_x{b}", [rows, tiles, D]) for b in range(2)]
        self.st = [sb(f"norm_st{b}", [rows, tiles, 6]) for b in range(2)]
        self.mv = [sb(f"norm_mv{b}", [rows, tiles, 2]) for b in range(2)]
        self.rstd = [sb(f"norm_rstd{b}", [rows, tiles]) for b in range(2)]
        self.y = [sb(f"norm_y{b}", [rows, tiles, D]) for b in range(2)]
        self.stats = Signal(sem("norm_stats"), tiles)
        self.moments = Signal(sem("norm_moments"), tiles)
        self.var_eps = Signal(sem("norm_var_eps"))
        self.rstd_ready = Signal(sem("norm_rstd_ready"))
        self.ready = Signal(sem("norm_ready"))


def norm_moments(nc, dve, nm, u, b, t, passed):
    nc.vector.bn_stats(nm.st[b][:, t, :], nm.x[b][:, t, :]).then_inc(nm.stats.sem, 1)
    dve.wait_ge(nm.stats.sem, nm.stats.count(u, t + 1))
    dve.sem_inc(passed, 1)
    nc.vector.bn_aggr(nm.mv[b][:, t, :], nm.st[b][:, t, :]).then_inc(nm.moments.sem, 1)


def norm_rows(nc, pool, nm, u, b, eps, minus_half, passed, read):
    n = nm.tiles
    pool.wait_ge(nm.moments.sem, nm.moments.count(u))
    nc.gpsimd.tensor_tensor(nm.rstd[b][:, :], nm.mv[b][:, :, 1], eps[0:nm.rows, 0:n], ALU.add).then_inc(nm.var_eps.sem, 1)
    pool.wait_ge(nm.var_eps.sem, nm.var_eps.count(u))
    nc.gpsimd.tensor_tensor(nm.rstd[b][:, :], nm.rstd[b][:, :], minus_half[0:nm.rows, 0:n], ALU.pow).then_inc(nm.rstd_ready.sem, 1)
    pool.wait_ge(nm.rstd_ready.sem, nm.rstd_ready.count(u))
    pool.wait_ge(read.sem, read.count(u, back=2))
    pool.sem_inc(passed, 1)
    for t in range(n):
        last = nc.gpsimd.tensor_scalar(nm.y[b][:, t, :], nm.x[b][:, t, :], nm.mv[b][:, t, 0:1], nm.rstd[b][:, t:t + 1],
                                       ALU.subtract, ALU.mult)
    last.then_inc(nm.ready.sem, 1)


def phase_token_mixer(nc, x, ident, w_compress, w_main, w_expand, w_ff1, w_ff2, b_compress, b_main, b_ff1,
                      g1_col, b1_col, g2_col, b2_col, b_expand, g1_row, b1_row, b_ff2, h_out, slots):
    UNITS = 2
    STEPS = BATCH // 2 // UNITS
    TILES = 4
    N = TILES * P
    with ExitStack() as ctx:
        pl = Place(nc, ctx, "tok")
        sb, sem = pl.sb, pl.sem
        idn = sb("ident", [P, P])
        wc = sb("wc", [D, BN])
        wm = sb("wm", [BN, 3, BN])
        we = sb("we", [BN, D])
        w1 = sb("w1", [D, BN])
        w2 = sb("w2", [BN, D])
        cols = sb("cols", [P, 7])
        rows = sb("rows", [P, 4, D])
        x_sb = [sb(f"x{u}", [P, TILES, D]) for u in range(UNITS)]
        x_be = [sb(f"xbe{u}", [P, TILES, D]) for u in range(UNITS)]
        xT = [sb(f"xT{u}", [D, N]) for u in range(UNITS)]
        h1 = [sb(f"h1{u}", [BN, 2, T_IN + 2]) for u in range(UNITS)]
        h2 = [sb(f"h2{u}", [BN, N]) for u in range(UNITS)]
        sum1 = [sb(f"sum1{u}", [P, TILES, D]) for u in range(UNITS)]
        st = [sb(f"st{u}", [P, TILES, 6]) for u in range(UNITS)]
        mv = [sb(f"mv{u}", [P, TILES, 2]) for u in range(UNITS)]
        rstd = [sb(f"rstd{u}", [P, TILES]) for u in range(UNITS)]
        eps = sb("eps", [P, TILES])
        minus_half = sb("minus_half", [P, TILES])
        n1 = [sb(f"n1{u}", [P, TILES, D]) for u in range(UNITS)]
        res1 = [sb(f"res1{u}", [P, TILES, D]) for u in range(UNITS)]
        yT = [sb(f"yT{u}", [D, N]) for u in range(UNITS)]
        gel = [sb(f"gel{u}", [BN, N]) for u in range(UNITS)]
        zT = [sb(f"zT{u}", [D, 2, T_IN]) for u in range(UNITS)]
        pair = [sb(f"pair{u}", [D, 2, T_IN - 1]) for u in range(UNITS)]
        pooled = [sb(f"pooled{u}", [D, 2, SEQ]) for u in range(UNITS)]
        h_sb = [sb(f"h{u}", [HALF, TILES, D]) for u in range(UNITS)]
        ps = [pl.banks(f"ps{u}_", 4) for u in range(UNITS)]

        ZERO_ROWS = EXP1 * CAP // STEPS
        ZERO_LINES = ZERO_ROWS // (P // 4)
        zeros = sb("zeros", [P, (P // 4) * D])
        zeros_set = sem("zeros_set")
        zeros_stored = sem("zeros_stored")

        weights_in = sem("weights_in")
        pe_passed, dve_passed = sem("pe_passed"), sem("dve_passed")
        x_in = [sem(f"x_in{u}") for u in range(UNITS)]
        x_free = sem("x_free")
        x_turned = sem("x_turned")
        xT_ready = sem("xT_ready")
        compress_done = sem("compress_done")
        pad_zero = sem("pad_zero")
        h1_ready = sem("h1_ready")
        main_done = sem("main_done")
        h2_ready = sem("h2_ready")
        expand_done = sem("expand_done")
        xbe_ready = sem("xbe_ready")
        sum_ready = sem("sum_ready")
        stats_ready = sem("stats_ready")
        moments_ready = sem("moments_ready")
        var_eps_ready = sem("var_eps_ready")
        constants_set = sem("constants_set")
        rstd_ready = sem("rstd_ready")
        norm_ready = sem("norm_ready")
        scaled_ready = sem("scaled_ready")
        res_ready = sem("res_ready")
        y_turned = sem("y_turned")
        yT_ready = sem("yT_ready")
        ff1_done = sem("ff1_done")
        gelu_ready = sem("gelu_ready")
        ff2_done = sem("ff2_done")
        z_turned = sem("z_turned")
        zT_ready = sem("zT_ready")
        pair_ready = sem("pair_ready")
        pooled_ready = sem("pooled_ready")
        pooled_turned = sem("pooled_turned")
        h_ready = sem("h_ready")
        h_stored = [sem(f"h_stored{u}") for u in range(UNITS)]
        ff_res_ready = sem("ff_res_ready")
        WEIGHTS = 17

        with nc.Block() as block:

            @block.sync
            def _(sp):
                for dst, src in ((idn[:, :], ident), (wc[:, :], w_compress), (wm[:, :, :], w_main),
                                 (we[:, :], w_expand), (w1[:, :], w_ff1), (w2[:, :], w_ff2),
                                 (cols[0:BN, 0:1], b_compress), (cols[0:BN, 1:2], b_main),
                                 (cols[0:BN, 2:3], b_ff1), (cols[:, 3:4], g1_col), (cols[:, 4:5], b1_col),
                                 (cols[:, 5:6], g2_col), (cols[:, 6:7], b2_col),
                                 (rows[:, 0, :], b_expand.partition_broadcast(P)),
                                 (rows[:, 1, :], g1_row.partition_broadcast(P)),
                                 (rows[:, 2, :], b1_row.partition_broadcast(P)),
                                 (rows[:, 3, :], b_ff2.partition_broadcast(P))):
                    sp.dma_start(dst, src).then_inc(weights_in, 16)
                def load(step):
                    for u in range(UNITS):
                        sp.wait_ge(x_free, step * UNITS + u + 1)
                        for b in range(2):
                            sp.dma_start(x_sb[u][:, 2 * b:2 * b + 2, :],
                                         x[bass.ds((step * UNITS + u) * 2 + b, 1), :, :].rearrange(
                                             "b (c p) d -> p (b c) d", p=P)).then_inc(x_in[u], 16)

                def store(step):
                    for u in range(UNITS):
                        sp.wait_ge(h_ready, step * UNITS + UNITS + u + 1)
                        for b in range(2):
                            sp.dma_start(h_out[0:SEQ, bass.ds((step * UNITS + u) * 2 + b, 1), :].rearrange(
                                "(c p) b d -> p (c b) d", p=HALF), h_sb[u][:, 2 * b:2 * b + 2, :]).then_inc(h_stored[u], 16)

                load(0)
                with sp.Fori(1, STEPS) as step:
                    load(step)
                    store(step - 1)
                store(STEPS - 1)
                for u in range(UNITS):
                    sp.wait_ge(h_stored[u], 32 * STEPS + 32)

            @block.tensor
            def _(pe):
                pe.wait_ge(weights_in, 16 * WEIGHTS)
                with pe.Fori(0, STEPS) as step:
                    turn = [step * UNITS + u + 1 for u in range(UNITS)]
                    for u in range(UNITS):
                        pe.wait_ge(x_in[u], step * 32 + 32)
                        pe.wait_ge(h_ready, turn[u])
                        for c in range(TILES):
                            last = nc.tensor.transpose(ps[u][0][:, c * P:(c + 1) * P], x_sb[u][:, c, :], idn[:, :])
                        last.then_inc(x_turned, 1)
                    for u in range(UNITS):
                        pe.wait_ge(xT_ready, turn[u])
                        nc.tensor.matmul(ps[u][1][0:BN, :], wc[:, :], xT[u][:, :], start=True, stop=True).then_inc(compress_done, 1)
                    for u in range(UNITS):
                        pe.wait_ge(h1_ready, turn[u])
                        pe.sem_inc(pe_passed, 1)
                        for tap in range(3):
                            last = nc.tensor.matmul(ps[u][2][0:BN, :].rearrange("p (b t) -> p b t", b=2), wm[:, tap, :],
                                                    h1[u][:, :, tap:tap + T_IN], start=tap == 0, stop=tap == 2)
                        last.then_inc(main_done, 1)
                    for u in range(UNITS):
                        pe.wait_ge(h2_ready, turn[u])
                        for c in range(TILES):
                            last = nc.tensor.matmul(ps[u][3][:, c * P:(c + 1) * P], h2[u][:, c * P:(c + 1) * P],
                                                    we[:, :], start=True, stop=True)
                        last.then_inc(expand_done, 1)
                    for u in range(UNITS):
                        pe.wait_ge(norm_ready, 2 * step * UNITS + u + 1)
                        for c in range(TILES):
                            last = nc.tensor.transpose(ps[u][0][:, c * P:(c + 1) * P], n1[u][:, c, :], idn[:, :])
                        last.then_inc(y_turned, 1)
                    for u in range(UNITS):
                        pe.wait_ge(yT_ready, turn[u])
                        nc.tensor.matmul(ps[u][1][0:BN, :], w1[:, :], yT[u][:, :], start=True, stop=True).then_inc(ff1_done, 1)
                    for u in range(UNITS):
                        pe.wait_ge(gelu_ready, turn[u])
                        for c in range(TILES):
                            last = nc.tensor.matmul(ps[u][2][:, c * P:(c + 1) * P], gel[u][:, c * P:(c + 1) * P],
                                                    w2[:, :], start=True, stop=True)
                        last.then_inc(ff2_done, 1)
                    for u in range(UNITS):
                        pe.wait_ge(norm_ready, 2 * step * UNITS + UNITS + u + 1)
                        for c in range(TILES):
                            last = nc.tensor.transpose(ps[u][3][:, c * P:(c + 1) * P], n1[u][:, c, :], idn[:, :])
                        last.then_inc(z_turned, 1)
                    for u in range(UNITS):
                        pe.wait_ge(pooled_ready, turn[u])
                        for c in range(TILES):
                            last = nc.tensor.transpose(ps[u][0][0:HALF, c * P:(c + 1) * P],
                                                       pooled[u][:, c // 2, (c % 2) * HALF:(c % 2 + 1) * HALF], idn[:, :])
                        last.then_inc(pooled_turned, 1)

            @block.scalar
            def _(act):
                act.sem_inc(h_ready, UNITS)
                act.wait_ge(pad_zero, 1)
                act.wait_ge(zeros_set, 1)
                act.dma_start(h_out[SEQ:POS_PAD, :, :].rearrange("p b d -> (p b) d"), zeros[:, 0:D]).then_inc(zeros_stored, 16)
                with act.Fori(0, STEPS) as step:
                    act.dma_start(slots[bass.ds(step * ZERO_ROWS, ZERO_ROWS), :].rearrange("(p t) d -> p (t d)", p=ZERO_LINES),
                                  zeros[0:ZERO_LINES, :]).then_inc(zeros_stored, 16)
                    turn = [step * UNITS + u + 1 for u in range(UNITS)]
                    for u in range(UNITS):
                        act.wait_ge(x_turned, turn[u])
                        nc.scalar.copy(xT[u][:, :], ps[u][0][:, :]).then_inc(xT_ready, 1)
                    for u in range(UNITS):
                        act.wait_ge(compress_done, turn[u])
                        nc.scalar.activation(h1[u][:, :, 1:T_IN + 1], ps[u][1][0:BN, :].rearrange("p (b t) -> p b t", b=2),
                                             ACT.Silu, bias=cols[0:BN, 0:1]).then_inc(h1_ready, 1)
                    for u in range(UNITS):
                        act.wait_ge(main_done, turn[u])
                        nc.scalar.activation(h2[u][:, :], ps[u][2][0:BN, :], ACT.Silu, bias=cols[0:BN, 1:2]).then_inc(h2_ready, 1)
                    for u in range(UNITS):
                        act.wait_ge(y_turned, turn[u])
                        nc.scalar.activation(yT[u][:, :], ps[u][0][:, :], ACT.Identity, bias=cols[:, 4:5],
                                             scale=cols[:, 3:4]).then_inc(yT_ready, 1)
                    for u in range(UNITS):
                        act.wait_ge(ff1_done, turn[u])
                        nc.scalar.activation(gel[u][:, :], ps[u][1][0:BN, :], ACT.Gelu, bias=cols[0:BN, 2:3]).then_inc(gelu_ready, 1)
                    for u in range(UNITS):
                        act.wait_ge(z_turned, turn[u])
                        nc.scalar.activation(zT[u][:, :, :].rearrange("p b t -> p (b t)"), ps[u][3][:, :], ACT.Identity,
                                             bias=cols[:, 6:7], scale=cols[:, 5:6]).then_inc(zT_ready, 1)
                    for u in range(UNITS):
                        act.wait_ge(pooled_turned, turn[u])
                        act.wait_ge(h_stored[u], step * 32 + 32)
                        nc.scalar.copy(h_sb[u][:, :, :].rearrange("p c d -> p (c d)"), ps[u][0][0:HALF, :]).then_inc(h_ready, 1)
                act.wait_ge(zeros_stored, 16 * (STEPS + 1))

            @block.vector
            def _(dve):
                nc.vector.memset(zeros[:, :], 0.0).then_inc(zeros_set, 1)
                for u in range(UNITS):
                    nc.vector.memset(h1[u][:, :, 0:1], 0.0)
                    last = nc.vector.memset(h1[u][:, :, T_IN + 1:T_IN + 2], 0.0)
                last.then_inc(pad_zero, 1)
                dve.sem_inc(x_free, UNITS)
                for u in range(UNITS):
                    dve.sem_inc(h_stored[u], 32)

                def norm(u, n):
                    dve.wait_ge(sum_ready, n)
                    for c in range(TILES):
                        last = nc.vector.bn_stats(st[u][:, c, :], sum1[u][:, c, :])
                    last.then_inc(stats_ready, 1)
                    dve.wait_ge(stats_ready, n)
                    dve.sem_inc(dve_passed, 1)
                    for c in range(TILES):
                        last = nc.vector.bn_aggr(mv[u][:, c, :], st[u][:, c, :])
                    last.then_inc(moments_ready, 1)

                def norm_end(u, n):
                    dve.wait_ge(rstd_ready, n)
                    for c in range(TILES):
                        last = nc.vector.tensor_scalar(n1[u][:, c, :], sum1[u][:, c, :], mv[u][:, c, 0:1], rstd[u][:, c:c + 1],
                                                       ALU.subtract, ALU.mult)
                    last.then_inc(norm_ready, 1)

                with dve.Fori(0, STEPS) as step:
                    turn = [step * UNITS + u + 1 for u in range(UNITS)]
                    nth = [2 * step * UNITS + u + 1 for u in range(2 * UNITS)]
                    for u in range(UNITS):
                        dve.wait_ge(expand_done, turn[u])
                        dve.wait_ge(xbe_ready, turn[u])
                        nc.vector.tensor_tensor(sum1[u][:, :, :].rearrange("p c d -> p (c d)"), ps[u][3][:, :],
                                                x_be[u][:, :, :].rearrange("p c d -> p (c d)"), ALU.add).then_inc(sum_ready, 1)
                    for u in range(UNITS):
                        norm(u, nth[u])
                    for u in range(UNITS):
                        norm_end(u, nth[u])
                    for u in range(UNITS):
                        dve.wait_ge(ff2_done, turn[u])
                        dve.wait_ge(res_ready, turn[u])
                        nc.vector.tensor_tensor(sum1[u][:, :, :].rearrange("p c d -> p (c d)"), ps[u][2][:, :],
                                                res1[u][:, :, :].rearrange("p c d -> p (c d)"), ALU.add).then_inc(sum_ready, 1)
                    for u in range(UNITS):
                        norm(u, nth[UNITS + u])
                    for u in range(UNITS):
                        norm_end(u, nth[UNITS + u])
                    for u in range(UNITS):
                        dve.wait_ge(zT_ready, turn[u])
                        nc.vector.tensor_tensor(pair[u][:, :, :], zT[u][:, :, 0:T_IN - 1], zT[u][:, :, 1:T_IN], ALU.max).then_inc(pair_ready, 1)
                        dve.wait_ge(pair_ready, turn[u])
                        nc.vector.tensor_tensor(pooled[u][:, :, :], pair[u][:, :, 0:SEQ], zT[u][:, :, 2:T_IN], ALU.max).then_inc(pooled_ready, 1)

            @block.gpsimd
            def _(pool):
                nc.gpsimd.memset(eps[:, :], EPS)
                nc.gpsimd.memset(minus_half[:, :], -0.5).then_inc(constants_set, 1)
                pool.wait_ge(constants_set, 1)
                pool.wait_ge(weights_in, 16 * WEIGHTS)
                nc.gpsimd.tensor_tensor(rows[:, 2, :], rows[:, 2, :], rows[:, 3, :], ALU.add).then_inc(ff_res_ready, 1)
                pool.wait_ge(ff_res_ready, 1)
                with pool.Fori(0, STEPS) as step:
                    turn = [step * UNITS + u + 1 for u in range(UNITS)]
                    nth = [2 * step * UNITS + u + 1 for u in range(2 * UNITS)]
                    for u in range(UNITS):
                        pool.wait_ge(x_in[u], step * 32 + 32)
                        nc.gpsimd.tensor_tensor(x_be[u][:, :, :], x_sb[u][:, :, :], over(rows[:, 0, :], TILES), ALU.add).then_inc(xbe_ready, 1)
                    for u in range(UNITS):
                        pool.wait_ge(moments_ready, nth[u])
                        nc.gpsimd.tensor_tensor(rstd[u][:, :], mv[u][:, :, 1], eps[:, :], ALU.add).then_inc(var_eps_ready, 1)
                        pool.wait_ge(var_eps_ready, nth[u])
                        nc.gpsimd.tensor_tensor(rstd[u][:, :], rstd[u][:, :], minus_half[:, :], ALU.pow).then_inc(rstd_ready, 1)
                    for u in range(UNITS):
                        pool.wait_ge(norm_ready, nth[u])
                        nc.gpsimd.tensor_tensor(res1[u][:, :, :], n1[u][:, :, :], over(rows[:, 1, :], TILES), ALU.mult).then_inc(scaled_ready, 1)
                        pool.wait_ge(x_turned, turn[u])
                        pool.sem_inc(x_free, 1)
                    for u in range(UNITS):
                        pool.wait_ge(scaled_ready, turn[u])
                        nc.gpsimd.tensor_tensor(res1[u][:, :, :], res1[u][:, :, :], over(rows[:, 2, :], TILES), ALU.add).then_inc(res_ready, 1)
                    for u in range(UNITS):
                        pool.wait_ge(moments_ready, nth[UNITS + u])
                        nc.gpsimd.tensor_tensor(rstd[u][:, :], mv[u][:, :, 1], eps[:, :], ALU.add).then_inc(var_eps_ready, 1)
                        pool.wait_ge(var_eps_ready, nth[UNITS + u])
                        nc.gpsimd.tensor_tensor(rstd[u][:, :], rstd[u][:, :], minus_half[:, :], ALU.pow).then_inc(rstd_ready, 1)

        pl.close()


def phase_batch_attention(nc, h_in, ident, mask, wq, wk, wv, wo, h_out):
    UNITS = POS_PAD // 8
    TILES = 4
    N = TILES * P
    PAIRS = N_HEAD // 2
    NORM, TURN, PROJ, SOFT, FLIP, WEIGH, OUT = range(7)
    STAGES = 7
    with ExitStack() as ctx:
        pl = Place(nc, ctx, "bat")
        sb, sem = pl.sb, pl.sem
        idn = sb("ident", [P, P])
        msk = sb("mask", [P, N])
        wq_sb = sb("wq", [D, PAIRS, P])
        wk_sb = sb("wk", [D, PAIRS, P])
        wv_sb = sb("wv", [D, N])
        wo_sb = sb("wo", [P, PAIRS, D])
        eps = sb("eps", [P, TILES])
        minus_half = sb("minus_half", [P, TILES])

        def two(name, shape):
            return [sb(f"{name}{b}", shape) for b in range(2)]

        h_sb = two("h", [P, TILES, D])
        st = two("st", [P, TILES, 6])
        mv = two("mv", [P, TILES, 2])
        rstd = two("rstd", [P, TILES])
        hn = two("hn", [P, TILES, D])
        hnT = two("hnT", [D, N])
        qT = two("qT", [P, PAIRS, N])
        kT = two("kT", [P, PAIRS, N])
        v = two("v", [P, TILES, N])
        sc = two("sc", [P, N])
        top = two("top", [P, 8])
        ex = two("ex", [P, N])
        total = two("total", [P, 8])
        inv = two("inv", [P, 8])
        prob = two("prob", [P, TILES, N])
        prT = sb("prT", [P, TILES, N])
        oT = sb("oT", [P, TILES, N])
        res = two("res", [P, TILES, D])
        out = two("out", [P, TILES, D])

        ps_qk, ps_v, ps_prT, ps_out = pl.banks("x", 4)
        ps_sc = pl.banks("sc", 2)
        ps_oT = ctx.enter_context(nc.psum_tensor("bat_bank_oT", [P, 2, N], F32))

        weights_in = sem("weights_in")
        WEIGHTS = 6
        pe_passed, dve_passed, pool_passed = (sem(f"{e}_passed") for e in ("pe", "dve", "pool"))
        constants_set = sem("constants_set")
        h_in_s = [Landed(sem(f"h_in_s{b}"), 2) for b in range(2)]
        res_in = [Landed(sem(f"res_in{b}"), 2) for b in range(2)]
        stored = [Landed(sem(f"stored{b}"), 2) for b in range(2)]
        stats = Signal(sem("stats"), TILES)
        moments = Signal(sem("moments"), TILES)
        var_eps = Signal(sem("var_eps"))
        rstd_ready = Signal(sem("rstd_ready"))
        normed = Signal(sem("normed"))
        turned = Signal(sem("turned"))
        hnT_ready = Signal(sem("hnT_ready"))
        q_done = Signal(sem("q_done"), TILES)
        k_done = Signal(sem("k_done"), TILES)
        v_done = Signal(sem("v_done"), TILES)
        q_ready = Signal(sem("q_ready"), TILES)
        k_ready = Signal(sem("k_ready"), TILES)
        v_ready = Signal(sem("v_ready"), TILES)
        sc_done = Signal(sem("sc_done"), TILES)
        sc_masked = Signal(sem("sc_masked"), TILES)
        top_ready = Signal(sem("top_ready"), TILES)
        sc_ready = Signal(sem("sc_ready"), TILES)
        ex_ready = Signal(sem("ex_ready"), TILES)
        total_ready = Signal(sem("total_ready"), TILES)
        inv_ready = Signal(sem("inv_ready"), TILES)
        prob_ready = Signal(sem("prob_ready"), TILES)
        prob_turned = Signal(sem("prob_turned"), TILES)
        prT_ready = Signal(sem("prT_ready"), TILES)
        oT_done = Signal(sem("oT_done"), TILES)
        oT_ready = Signal(sem("oT_ready"), TILES)
        out_done = Signal(sem("out_done"), TILES)
        out_ready = Signal(sem("out_ready"), TILES)

        with nc.Block() as block:

            @block.sync
            def _(sp):
                for dst, src in ((idn[:, :], ident), (msk[:, :], mask), (wq_sb[:, :, :].rearrange("p j m -> p (j m)"), wq),
                                 (wk_sb[:, :, :].rearrange("p j m -> p (j m)"), wk), (wv_sb[:, :], wv),
                                 (wo_sb[:, :, :], wo.rearrange("(j p) d -> p j d", p=P))):
                    sp.dma_start(dst, src).then_inc(weights_in, 16)
                for b in range(2):
                    h_in_s[b].opened(sp)
                    res_in[b].opened(sp)
                    stored[b].opened(sp)

                def body(n, par):
                    if n[NORM] is not None:
                        u, b = n[NORM], par[NORM]
                        sp.wait_ge(normed.sem, normed.count(u, back=2))
                        for odd in range(2):
                            sp.dma_start(h_sb[b][odd * BATCH:(odd + 1) * BATCH, :, :],
                                         h_in[bass.ds(u * 8, 8), :, :].rearrange("(t two) b d -> two b t d", two=2)[odd]
                                         ).then_inc(h_in_s[b].sem, 16)
                    if n[WEIGH] is not None:
                        u, b = n[WEIGH], par[WEIGH]
                        sp.wait_ge(out_ready.sem, out_ready.count(u, back=2))
                        for odd in range(2):
                            sp.dma_start(res[b][odd * BATCH:(odd + 1) * BATCH, :, :],
                                         h_in[bass.ds(u * 8, 8), :, :].rearrange("(t two) b d -> two b t d", two=2)[odd]
                                         ).then_inc(res_in[b].sem, 16)
                    if n[OUT] is not None:
                        u, b = n[OUT], par[OUT]
                        sp.wait_ge(out_ready.sem, out_ready.count(u))
                        for odd in range(2):
                            sp.dma_start(h_out[:, bass.ds(u * 8, 8), :].rearrange("b (t two) d -> two b t d", two=2)[odd],
                                         out[b][odd * BATCH:(odd + 1) * BATCH, :, :]).then_inc(stored[b].sem, 16)

                in_lanes(sp, UNITS, STAGES, body)
                for b in range(2):
                    sp.wait_ge(stored[b].sem, stored[b].final(UNITS))

            @block.tensor
            def _(pe):
                for s in (turned, q_done, k_done, v_done, sc_done, prob_turned, oT_done, out_done):
                    s.opened(pe)
                pe.wait_ge(weights_in, 16 * WEIGHTS)

                def flip(u, b, t):
                    pe.wait_ge(prob_ready.sem, prob_ready.count(u, t + 1))
                    pe.wait_ge(prT_ready.sem, prT_ready.count(u, t))
                    for j in range(PAIRS):
                        last = nc.tensor.transpose(ps_prT[:, j * P:(j + 1) * P], prob[b][:, t, j * P:(j + 1) * P], idn[:, :])
                    last.then_inc(prob_turned.sem, 1)

                def scores(u, b, t):
                    for s in (q_ready, k_ready) if t == 0 else ():
                        pe.wait_ge(s.sem, s.count(u))
                    pe.wait_ge(sc_masked.sem, sc_masked.count(u, t - 1))
                    pe.sem_inc(pe_passed, 1)
                    for j in range(PAIRS):
                        for pos in range(2):
                            for hh in range(2):
                                half = slice(hh * 64, hh * 64 + 64)
                                at = (2 * t + pos) * BATCH
                                last = nc.tensor.matmul(ps_sc[t % 2][half, (2 * j + pos) * 64:(2 * j + pos + 1) * 64],
                                                        qT[b][half, j, at:at + BATCH], kT[b][half, j, at:at + BATCH],
                                                        start=True, stop=True)
                    last.then_inc(sc_done.sem, 1)

                def weigh(u, b, t):
                    if t == 0:
                        pe.wait_ge(prT_ready.sem, prT_ready.count(u))
                        pe.wait_ge(v_ready.sem, v_ready.count(u))
                    pe.wait_ge(oT_ready.sem, oT_ready.count(u, t))
                    pe.sem_inc(pe_passed, 1)
                    for j in range(PAIRS):
                        for pos in range(2):
                            for hh in range(2):
                                rows = slice(pos * 64, pos * 64 + 64)
                                last = nc.tensor.matmul(ps_oT[hh * 64:hh * 64 + 64, pos, j * 64:j * 64 + 64],
                                                        v[b][rows, t, (2 * j + hh) * D_HEAD:(2 * j + hh + 1) * D_HEAD],
                                                        prT[rows, t, j * P + hh * 64:j * P + hh * 64 + 64],
                                                        start=True, stop=True)
                    last.then_inc(oT_done.sem, 1)

                def project_q(u, b, t):
                    if t == 0:
                        pe.wait_ge(hnT_ready.sem, hnT_ready.count(u))
                    pe.wait_ge(k_ready.sem, k_ready.count(u, t))
                    nc.tensor.matmul(ps_qk[:, :], wq_sb[:, t, :], hnT[b][:, :], start=True, stop=True).then_inc(q_done.sem, 1)

                def project_k(u, b, t):
                    pe.wait_ge(q_ready.sem, q_ready.count(u, t + 1))
                    nc.tensor.matmul(ps_qk[:, :], wk_sb[:, t, :], hnT[b][:, :], start=True, stop=True).then_inc(k_done.sem, 1)

                def project_v(u, b, t, turned_before):
                    if t == 0 and turned_before is not None:
                        pe.wait_ge(hnT_ready.sem, hnT_ready.count(turned_before))
                    pe.wait_ge(v_ready.sem, v_ready.count(u, t))
                    nc.tensor.matmul(ps_v[:, :], hnT[b][:, t * P:(t + 1) * P], wv_sb[:, :], start=True, stop=True).then_inc(v_done.sem, 1)

                def output(u, t):
                    if t == 0:
                        pe.wait_ge(oT_ready.sem, oT_ready.count(u))
                    pe.wait_ge(out_ready.sem, out_ready.count(u, t))
                    for j in range(PAIRS):
                        last = nc.tensor.matmul(ps_out[:, t * D:(t + 1) * D], oT[:, t, j * P:(j + 1) * P],
                                                wo_sb[:, j, :], start=j == 0, stop=j == PAIRS - 1)
                    last.then_inc(out_done.sem, 1)

                def turn(u, b, projected):
                    pe.wait_ge(normed.sem, normed.count(u))
                    if projected is not None:
                        pe.wait_ge(v_ready.sem, v_ready.count(projected))
                    for t in range(TILES):
                        last = nc.tensor.transpose(ps_v[:, t * P:(t + 1) * P], hn[b][:, t, :], idn[:, :])
                    last.then_inc(turned.sem, 1)

                def body(n, par):
                    for t in range(TILES):
                        if n[SOFT] is not None:
                            scores(n[SOFT], par[SOFT], t)
                        if n[OUT] is not None:
                            output(n[OUT], t)
                        if n[PROJ] is not None:
                            project_q(n[PROJ], par[PROJ], t)
                        if n[WEIGH] is not None:
                            weigh(n[WEIGH], par[WEIGH], t)
                        if n[SOFT] is not None:
                            project_v(n[SOFT], par[SOFT], t, n[PROJ])
                        if n[FLIP] is not None:
                            flip(n[FLIP], par[FLIP], t)
                        if n[PROJ] is not None:
                            project_k(n[PROJ], par[PROJ], t)
                    if n[TURN] is not None:
                        if n[PROJ] is None:
                            pe.wait_ge(hnT_ready.sem, hnT_ready.count(n[TURN], back=1))
                        turn(n[TURN], par[TURN], n[SOFT])

                in_lanes(pe, UNITS, STAGES, body)

            @block.scalar
            def _(act):
                for s in (hnT_ready, q_ready, k_ready, v_ready, ex_ready, oT_ready):
                    s.opened(act)

                def body(n, par):
                    for t in range(TILES):
                        if n[PROJ] is not None:
                            u, b = n[PROJ], par[PROJ]
                            act.wait_ge(q_done.sem, q_done.count(u, t + 1))
                            act.wait_ge(sc_done.sem, sc_done.count(u, back=2))
                            nc.scalar.activation(qT[b][:, t, :], ps_qk[:, :], ACT.Copy, scale=D_HEAD ** -0.5).then_inc(q_ready.sem, 1)
                        if n[WEIGH] is not None:
                            u = n[WEIGH]
                            act.wait_ge(oT_done.sem, oT_done.count(u, t + 1))
                            act.wait_ge(out_done.sem, out_done.count(u, t + 1, back=1))
                            nc.scalar.copy(oT[:, t, :].rearrange("p (j two q) -> p two j q", two=2, q=64),
                                           ps_oT[:, :, 0:256].rearrange("p two (j q) -> p two j q", q=64)).then_inc(oT_ready.sem, 1)
                        if n[SOFT] is not None:
                            u, b = n[SOFT], par[SOFT]
                            act.wait_ge(v_done.sem, v_done.count(u, t + 1))
                            act.wait_ge(oT_done.sem, oT_done.count(u, t + 1, back=2))
                            nc.scalar.copy(v[b][:, t, :], ps_v[:, :]).then_inc(v_ready.sem, 1)
                        if n[SOFT] is not None:
                            u, b = n[SOFT], par[SOFT]
                            act.wait_ge(sc_ready.sem, sc_ready.count(u, t + 1))
                            act.wait_ge(prob_ready.sem, prob_ready.count(u, t - 1))
                            nc.scalar.activation(ex[t % 2][:, :], sc[t % 2][:, :], ACT.Exp).then_inc(ex_ready.sem, 1)
                        if n[PROJ] is not None:
                            u, b = n[PROJ], par[PROJ]
                            act.wait_ge(k_done.sem, k_done.count(u, t + 1))
                            nc.scalar.copy(kT[b][:, t, :], ps_qk[:, :]).then_inc(k_ready.sem, 1)
                    if n[TURN] is not None:
                        u, b = n[TURN], par[TURN]
                        act.wait_ge(turned.sem, turned.count(u))
                        act.wait_ge(v_done.sem, v_done.count(u, back=2))
                        nc.scalar.copy(hnT[b][:, :], ps_v[:, :]).then_inc(hnT_ready.sem, 1)

                in_lanes(act, UNITS, STAGES, body)

            @block.vector
            def _(dve):
                for s in (stats, moments, sc_masked, top_ready, sc_ready, total_ready, inv_ready, prT_ready, out_ready):
                    s.opened(dve)
                dve.wait_ge(weights_in, 16 * WEIGHTS)

                def body(n, par):
                    for t in range(TILES):
                        if n[SOFT] is not None:
                            u, b = n[SOFT], t % 2
                            dve.wait_ge(sc_done.sem, sc_done.count(u, t + 1))
                            dve.wait_ge(ex_ready.sem, ex_ready.count(u, t - 1))
                            nc.vector.tensor_tensor(sc[b][:, :], ps_sc[b][:, :], msk[:, :], ALU.add).then_inc(sc_masked.sem, 1)
                            dve.wait_ge(sc_masked.sem, sc_masked.count(u, t + 1))
                            nc.vector.tensor_reduce(top[b][:, :], sc[b][:, :].rearrange("p (g k) -> p g k", k=64),
                                                    AX.X, ALU.max).then_inc(top_ready.sem, 1)
                        if n[SOFT] is not None:
                            u, b = n[SOFT], t % 2
                            dve.wait_ge(top_ready.sem, top_ready.count(u, t + 1))
                            nc.vector.tensor_tensor(sc[b][:, :].rearrange("p (g k) -> p g k", k=64),
                                                    sc[b][:, :].rearrange("p (g k) -> p g k", k=64),
                                                    wide(top[b][:, :], 64), ALU.subtract).then_inc(sc_ready.sem, 1)
                        if n[NORM] is not None:
                            u, b = n[NORM], par[NORM]
                            if t == 0:
                                dve.wait_ge(h_in_s[b].sem, h_in_s[b].count(u, b))
                                dve.wait_ge(normed.sem, normed.count(u, back=2))
                            nc.vector.bn_stats(st[b][:, t, :], h_sb[b][:, t, :]).then_inc(stats.sem, 1)
                            dve.wait_ge(stats.sem, stats.count(u, t + 1))
                            dve.sem_inc(dve_passed, 1)
                            nc.vector.bn_aggr(mv[b][:, t, :], st[b][:, t, :]).then_inc(moments.sem, 1)
                        if n[FLIP] is not None:
                            u = n[FLIP]
                            dve.wait_ge(prob_turned.sem, prob_turned.count(u, t + 1))
                            dve.wait_ge(oT_done.sem, oT_done.count(u, t + 1, back=1))
                            nc.vector.tensor_copy(prT[:, t, :], ps_prT[:, :]).then_inc(prT_ready.sem, 1)
                        if n[SOFT] is not None:
                            u, b = n[SOFT], t % 2
                            dve.wait_ge(ex_ready.sem, ex_ready.count(u, t + 1))
                            nc.vector.tensor_reduce(total[b][:, :], ex[b][:, :].rearrange("p (g k) -> p g k", k=64),
                                                    AX.X, ALU.add).then_inc(total_ready.sem, 1)
                            dve.wait_ge(total_ready.sem, total_ready.count(u, t + 1))
                            dve.wait_ge(prob_ready.sem, prob_ready.count(u, t - 1))
                            nc.vector.reciprocal(inv[b][:, :], total[b][:, :]).then_inc(inv_ready.sem, 1)
                        if n[OUT] is not None:
                            u, b = n[OUT], par[OUT]
                            if t == 0:
                                dve.wait_ge(res_in[b].sem, res_in[b].count(u, b))
                                dve.wait_ge(stored[b].sem, stored[b].count(u, b, back=1))
                            dve.wait_ge(out_done.sem, out_done.count(u, t + 1))
                            nc.vector.tensor_tensor(out[b][:, t, :], ps_out[:, t * D:(t + 1) * D], res[b][:, t, :],
                                                    ALU.add).then_inc(out_ready.sem, 1)

                in_lanes(dve, UNITS, STAGES, body)

            @block.gpsimd
            def _(pool):
                for s in (var_eps, rstd_ready, normed, prob_ready):
                    s.opened(pool)
                nc.gpsimd.memset(eps[:, :], EPS)
                nc.gpsimd.memset(minus_half[:, :], -0.5).then_inc(constants_set, 1)
                pool.wait_ge(constants_set, 1)

                def body(n, par):
                    for t in range(TILES):
                        if n[SOFT] is not None:
                            u, b = n[SOFT], par[SOFT]
                            pool.wait_ge(inv_ready.sem, inv_ready.count(u, t + 1))
                            pool.wait_ge(prob_turned.sem, prob_turned.count(u, t + 1, back=2))
                            nc.gpsimd.tensor_tensor(prob[b][:, t, :].rearrange("p (g k) -> p g k", k=64),
                                                    ex[t % 2][:, :].rearrange("p (g k) -> p g k", k=64),
                                                    wide(inv[t % 2][:, :], 64), ALU.mult).then_inc(prob_ready.sem, 1)
                    if n[NORM] is not None:
                        u, b = n[NORM], par[NORM]
                        pool.wait_ge(moments.sem, moments.count(u))
                        nc.gpsimd.tensor_tensor(rstd[b][:, :], mv[b][:, :, 1], eps[:, :], ALU.add).then_inc(var_eps.sem, 1)
                        pool.wait_ge(var_eps.sem, var_eps.count(u))
                        nc.gpsimd.tensor_tensor(rstd[b][:, :], rstd[b][:, :], minus_half[:, :], ALU.pow).then_inc(rstd_ready.sem, 1)
                        pool.wait_ge(rstd_ready.sem, rstd_ready.count(u))
                        pool.wait_ge(turned.sem, turned.count(u, back=2))
                        pool.sem_inc(pool_passed, 1)
                        for t in range(TILES):
                            last = nc.gpsimd.tensor_scalar(hn[b][:, t, :], h_sb[b][:, t, :], mv[b][:, t, 0:1], rstd[b][:, t:t + 1],
                                                           ALU.subtract, ALU.mult)
                        last.then_inc(normed.sem, 1)

                in_lanes(pool, UNITS, STAGES, body)

        pl.close()


def phase_experts8(nc, h_in, ident, iota8, wg, w1, b1, w2, b2, gamma, beta, h_out):
    UNITS = BATCH // 2
    TILES = 4
    N = TILES * HALF
    NORM, TURN, HID, OUT, SCALE, SUM = range(6)
    STAGES = 6
    H = EXP0 // 2
    with ExitStack() as ctx:
        pl = Place(nc, ctx, "ex8")
        sb, sem = pl.sb, pl.sem
        idn = sb("ident", [P, P])
        iota = sb("iota", [P, EXP0])
        wg_sb = sb("wg", [D, EXP0])
        w1_sb = sb("w1", [D, EXP0, P])
        w2_sb = sb("w2", [P, EXP0, D])
        b1_sb = sb("b1", [P, EXP0])
        b2_sb = sb("b2", [P, EXP0, D])
        gam = sb("gamma", [P, EXP0, D])
        beta_sb = sb("beta", [EXP0, D])
        means = sb("means", [P, 2, EXP0])
        eps = sb("eps", [P, TILES])
        minus_half = sb("minus_half", [P, TILES * EXP0])

        def two(name, shape, dt=F32):
            return [sb(f"{name}{b}", shape, dt) for b in range(2)]

        nm = Norm(pl, TILES, HALF)
        hnT = two("hnT", [D, N])
        hid = two("hid", [P, EXP0, N])
        logit = two("logit", [HALF, TILES, EXP0])
        top = two("top", [HALF, TILES, EXP0])
        at = two("at", [HALF, TILES, EXP0], U32)
        atf = two("atf", [HALF, TILES, 2])
        gap = two("gap", [HALF, TILES])
        egap = two("egap", [HALF, TILES])
        den = two("den", [HALF, TILES])
        gate = two("gate", [HALF, 2, TILES])
        hot = two("hot", [HALF, 2, TILES, EXP0])
        w = two("gated", [HALF, TILES, EXP0])
        wT = two("wT", [EXP0, HALF])
        yb = two("yb", [HALF, TILES, EXP0, D])
        sq = two("sq", [HALF, EXP0, D])
        ss = two("ss", [HALF, TILES, EXP0])
        s = two("scale", [HALF, TILES, EXP0])
        yg = two("yg", [HALF, TILES, EXP0, D])
        res = two("res", [HALF, TILES, D])
        acc = two("acc", [HALF, TILES, D])

        ps_turn, ps_misc = pl.banks("turn", 2)
        ps_hid = pl.banks("hid", 2)
        ps_y = [ctx.enter_context(nc.psum_tensor(f"ex8_bank_y{b}", [P, 2, H * D], F32)) for b in range(2)]
        ps_beta, ps_logit, ps_wT = ps_misc[0:HALF, 0:D], ps_misc[0:HALF, 128:160], ps_misc[0:EXP0, 192:192 + HALF]

        weights_in = sem("weights_in")
        WEIGHTS = 9
        constants_set = sem("constants_set")
        means_ready = sem("means_ready")
        centred = sem("centred")
        pe_passed, dve_passed, pool_passed = (sem(f"{e}_passed") for e in ("pe", "dve", "pool"))
        x_in = [Landed(sem(f"x_in{b}"), 2) for b in range(2)]
        res_in = [Landed(sem(f"res_in{b}"), 2) for b in range(2)]
        stored = [Landed(sem(f"stored{b}"), 2) for b in range(2)]
        turned = Signal(sem("turned"))
        hnT_ready = Signal(sem("hnT_ready"))
        logit_done = Signal(sem("logit_done"))
        logit_ready = Signal(sem("logit_ready"))
        top_ready = Signal(sem("top_ready"))
        at_ready = Signal(sem("at_ready"))
        atf_ready = Signal(sem("atf_ready"))
        gap_ready = Signal(sem("gap_ready"))
        egap_ready = Signal(sem("egap_ready"))
        den_ready = Signal(sem("den_ready"))
        gate0_ready = Signal(sem("gate0_ready"))
        gates_ready = Signal(sem("gates_ready"))
        hot_ready = Signal(sem("hot_ready"))
        hot_scaled = Signal(sem("hot_scaled"))
        w_ready = Signal(sem("w_ready"))
        hid_done = Signal(sem("hid_done"), EXP0)
        hid_ready = Signal(sem("hid_ready"), EXP0)
        wT_done = Signal(sem("wT_done"), TILES)
        wT_ready = Signal(sem("wT_ready"), TILES)
        y_done = Signal(sem("y_done"), TILES)
        y_ready = Signal(sem("y_ready"), TILES)
        beta_done = Signal(sem("beta_done"), TILES)
        acc_begun = Signal(sem("acc_begun"), TILES)
        ss_ready = Signal(sem("ss_ready"), TILES)
        var_ready = Signal(sem("var_ready"))
        yrstd_ready = Signal(sem("yrstd_ready"))
        s_ready = Signal(sem("s_ready"))
        yg_ready = Signal(sem("yg_ready"), TILES)
        acc_steps = Signal(sem("acc_steps"), EXP0)

        with nc.Block() as block:

            @block.sync
            def _(sp):
                for dst, src in ((idn[:, :], ident), (iota[:, :], iota8), (wg_sb[:, :], wg),
                                 (w1_sb[:, :, :], w1.rearrange("e d h -> d e h")),
                                 (w2_sb[:, :, :], w2.rearrange("e h d -> h e d")),
                                 (b1_sb[:, :], b1), (beta_sb[:, :], beta),
                                 (b2_sb[:, :, :].rearrange("p e d -> p (e d)"), b2.partition_broadcast(P)),
                                 (gam[:, :, :].rearrange("p e d -> p (e d)"), gamma.partition_broadcast(P))):
                    sp.dma_start(dst, src).then_inc(weights_in, 16)
                for b in range(2):
                    x_in[b].opened(sp)
                    res_in[b].opened(sp)
                    stored[b].opened(sp)

                def body(n, par):
                    if n[NORM] is not None:
                        u, b = n[NORM], par[NORM]
                        sp.wait_ge(nm.ready.sem, nm.ready.count(u, back=2))
                        load_rows(sp, nm.x[b], h_in, u, x_in[b])
                    if n[OUT] is not None:
                        u, b = n[OUT], par[OUT]
                        sp.wait_ge(acc_begun.sem, acc_begun.count(u, back=2))
                        load_rows(sp, res[b], h_in, u, res_in[b])
                    if n[SUM] is not None:
                        u, b = n[SUM], par[SUM]
                        sp.wait_ge(acc_steps.sem, acc_steps.count(u))
                        store_rows(sp, h_out, acc[b], u, stored[b])

                in_lanes(sp, UNITS, STAGES, body)
                for b in range(2):
                    sp.wait_ge(stored[b].sem, stored[b].final(UNITS))

            @block.tensor
            def _(pe):
                for x in (turned, logit_done, hid_done, wT_done, y_done, beta_done):
                    x.opened(pe)
                pe.wait_ge(weights_in, 16 * WEIGHTS)
                pe.wait_ge(centred, 2)

                def body(n, par):
                    if n[HID] is not None:
                        u, b = n[HID], par[HID]
                        pe.wait_ge(hnT_ready.sem, hnT_ready.count(u))
                        if n[SCALE] is not None:
                            pe.wait_ge(acc_begun.sem, acc_begun.count(n[SCALE], 0))
                        for t in range(TILES):
                            last = nc.tensor.matmul(ps_logit[:, t * EXP0:(t + 1) * EXP0], hnT[b][:, t * HALF:(t + 1) * HALF],
                                                    wg_sb[:, :], start=True, stop=True)
                        last.then_inc(logit_done.sem, 1)
                    for t in range(TILES):
                        if n[SCALE] is not None:
                            u, b = n[SCALE], par[SCALE]
                            if t == 0:
                                pe.wait_ge(w_ready.sem, w_ready.count(u))
                                if n[HID] is not None:
                                    pe.wait_ge(logit_ready.sem, logit_ready.count(n[HID]))
                            pe.wait_ge(acc_begun.sem, acc_begun.count(u, t))
                            nc.tensor.transpose(ps_wT, w[b][:, t, :], idn[0:HALF, 0:HALF]).then_inc(wT_done.sem, 1)
                        if n[OUT] is not None:
                            u, b = n[OUT], par[OUT]
                            if t == 0:
                                pe.wait_ge(hid_ready.sem, hid_ready.count(u))
                            pe.wait_ge(y_ready.sem, y_ready.count(u, t - 1))
                            for e in range(EXP0):
                                last = nc.tensor.matmul(ps_y[t % 2][0:HALF, e // H, (e % H) * D:(e % H + 1) * D],
                                                        hid[b][:, e, t * HALF:(t + 1) * HALF], w2_sb[:, e, :],
                                                        start=True, stop=True)
                            last.then_inc(y_done.sem, 1)
                        if n[SCALE] is not None:
                            u, b = n[SCALE], par[SCALE]
                            pe.wait_ge(wT_ready.sem, wT_ready.count(u, t + 1))
                            nc.tensor.matmul(ps_beta, wT[t % 2][:, :], beta_sb[:, :], start=True, stop=True).then_inc(beta_done.sem, 1)
                        if n[HID] is not None:
                            u, b = n[HID], par[HID]
                            for e in (2 * t, 2 * t + 1):
                                pe.wait_ge(hid_ready.sem, hid_ready.count(u, e - 1))
                                nc.tensor.matmul(ps_hid[e % 2][:, 0:N], w1_sb[:, e, :], hnT[b][:, :],
                                                 start=True, stop=True).then_inc(hid_done.sem, 1)
                    if n[TURN] is not None:
                        u, b = n[TURN], par[TURN]
                        pe.wait_ge(nm.ready.sem, nm.ready.count(u))
                        pe.wait_ge(hnT_ready.sem, hnT_ready.count(u, back=1))
                        for t in range(TILES):
                            last = nc.tensor.transpose(ps_turn[:, t * HALF:(t + 1) * HALF], nm.y[b][:, t, :], idn[0:HALF, 0:HALF])
                        last.then_inc(turned.sem, 1)

                in_lanes(pe, UNITS, STAGES, body)

            @block.scalar
            def _(act):
                for x in (hnT_ready, logit_ready, egap_ready, hid_ready, wT_ready, ss_ready):
                    x.opened(act)
                act.wait_ge(weights_in, 16 * WEIGHTS)

                def body(n, par):
                    if n[HID] is not None:
                        u, b = n[HID], par[HID]
                        act.wait_ge(logit_done.sem, logit_done.count(u))
                        act.wait_ge(at_ready.sem, at_ready.count(u, back=2))
                        nc.scalar.copy(logit[b][:, :, :].rearrange("p t e -> p (t e)"), ps_logit).then_inc(logit_ready.sem, 1)
                    for t in range(TILES):
                        if n[SCALE] is not None:
                            u, b = n[SCALE], par[SCALE]
                            act.wait_ge(wT_done.sem, wT_done.count(u, t + 1))
                            act.wait_ge(beta_done.sem, beta_done.count(u, t - 1))
                            nc.scalar.copy(wT[t % 2][:, :], ps_wT).then_inc(wT_ready.sem, 1)
                        if n[HID] is not None:
                            u, b = n[HID], par[HID]
                            for e in (2 * t, 2 * t + 1):
                                act.wait_ge(hid_done.sem, hid_done.count(u, e + 1))
                                act.wait_ge(y_done.sem, y_done.count(u, back=2))
                                nc.scalar.activation(hid[b][:, e, :], ps_hid[e % 2][:, 0:N], ACT.Relu,
                                                     bias=b1_sb[:, e:e + 1]).then_inc(hid_ready.sem, 1)
                            if t == 1:
                                act.wait_ge(gap_ready.sem, gap_ready.count(u))
                                act.wait_ge(gates_ready.sem, gates_ready.count(u, back=2))
                                nc.scalar.activation(egap[b][:, :], gap[b][:, :], ACT.Exp).then_inc(egap_ready.sem, 1)
                        if n[SCALE] is not None:
                            u, b = n[SCALE], par[SCALE]
                            act.wait_ge(y_ready.sem, y_ready.count(u, t + 1))
                            act.wait_ge(var_ready.sem, var_ready.count(u, back=2))
                            act.wait_ge(ss_ready.sem, ss_ready.count(u, t - 1))
                            for e in range(EXP0):
                                last = nc.scalar.activation(sq[t % 2][:, e, :], yb[b][:, t, e, :], ACT.Square,
                                                            accum_out=ss[b][:, t, e:e + 1])
                            last.then_inc(ss_ready.sem, 1)
                    if n[TURN] is not None:
                        u, b = n[TURN], par[TURN]
                        act.wait_ge(turned.sem, turned.count(u))
                        act.wait_ge(hid_done.sem, hid_done.count(u, back=2))
                        nc.scalar.copy(hnT[b][:, :], ps_turn[:, 0:N]).then_inc(hnT_ready.sem, 1)

                in_lanes(act, UNITS, STAGES, body)

            @block.vector
            def _(dve):
                for x in (nm.stats, nm.moments, top_ready, at_ready, atf_ready, gap_ready, den_ready, gate0_ready,
                          gates_ready, hot_ready, hot_scaled, w_ready, y_ready, acc_begun, acc_steps):
                    x.opened(dve)
                dve.wait_ge(weights_in, 16 * WEIGHTS)
                nc.vector.tensor_reduce(means[:, 0, :], w2_sb[:, :, :], AX.X, ALU.add)
                nc.vector.tensor_reduce(means[:, 1, :], b2_sb[:, :, :], AX.X, ALU.add).then_inc(means_ready, 1)
                dve.wait_ge(means_ready, 1)
                nc.vector.tensor_scalar(means[:, :, :], means[:, :, :], 1.0 / D, None, ALU.mult).then_inc(means_ready, 1)
                dve.wait_ge(means_ready, 2)
                for i, x in enumerate((w2_sb, b2_sb)):
                    nc.vector.tensor_tensor(x[:, :, :], x[:, :, :], wide(means[:, i, :], D), ALU.subtract).then_inc(centred, 1)
                dve.wait_ge(centred, 2)

                def add_experts(u, b, experts):
                    for e in experts:
                        if e == 0:
                            dve.wait_ge(yg_ready.sem, yg_ready.count(u))
                            dve.wait_ge(s_ready.sem, s_ready.count(u))
                            dve.wait_ge(acc_begun.sem, acc_begun.count(u))
                        else:
                            dve.wait_ge(acc_steps.sem, acc_steps.count(u, e))
                        for t in range(TILES):
                            last = nc.vector.scalar_tensor_tensor(acc[b][:, t, :], yg[b][:, t, e, :], s[b][:, t, e:e + 1],
                                                                  acc[b][:, t, :], ALU.mult, ALU.add)
                        last.then_inc(acc_steps.sem, 1)

                def body(n, par):
                    if n[HID] is not None:
                        u, b = n[HID], par[HID]
                        dve.wait_ge(logit_ready.sem, logit_ready.count(u))
                        dve.wait_ge(atf_ready.sem, atf_ready.count(u, back=2))
                        dve.sem_inc(dve_passed, 1)
                        for t in range(TILES):
                            last = nc.vector.max(top[b][:, t, :], logit[b][:, t, :])
                        last.then_inc(top_ready.sem, 1)
                        dve.wait_ge(top_ready.sem, top_ready.count(u))
                        nc.vector.tensor_tensor(gap[b][:, :], top[b][:, :, 1], top[b][:, :, 0], ALU.subtract).then_inc(gap_ready.sem, 1)
                        for t in range(TILES):
                            last = nc.vector.max_index(at[b][:, t, :], top[b][:, t, :], logit[b][:, t, :])
                        last.then_inc(at_ready.sem, 1)
                    for t in range(TILES):
                        if t == 1 and n[OUT] is not None:
                            u, b = n[OUT], par[OUT]
                            dve.wait_ge(hot_scaled.sem, hot_scaled.count(u))
                            dve.wait_ge(s_ready.sem, s_ready.count(u, back=2))
                            dve.wait_ge(wT_done.sem, wT_done.count(u, back=2))
                            nc.vector.tensor_tensor(w[b][:, :, :], hot[b][:, 0, :, :], hot[b][:, 1, :, :], ALU.add).then_inc(w_ready.sem, 1)
                        if n[OUT] is not None:
                            u, b = n[OUT], par[OUT]
                            dve.wait_ge(y_done.sem, y_done.count(u, t + 1))
                            dve.wait_ge(ss_ready.sem, ss_ready.count(u, back=2))
                            dve.wait_ge(yg_ready.sem, yg_ready.count(u, back=2))
                            nc.vector.tensor_tensor(yb[b][:, t, :, :].rearrange("p e d -> p (e d)"),
                                                    ps_y[t % 2][0:HALF, :, :].rearrange("p k x -> p (k x)"),
                                                    b2_sb[0:HALF, :, :].rearrange("p e d -> p (e d)"), ALU.add).then_inc(y_ready.sem, 1)
                        if n[SCALE] is not None:
                            u, b = n[SCALE], par[SCALE]
                            if t == 0:
                                dve.wait_ge(res_in[b].sem, res_in[b].count(u, b))
                                dve.wait_ge(stored[b].sem, stored[b].count(u, b, back=1))
                            dve.wait_ge(beta_done.sem, beta_done.count(u, t + 1))
                            nc.vector.tensor_tensor(acc[b][:, t, :], ps_beta, res[b][:, t, :], ALU.add).then_inc(acc_begun.sem, 1)
                        if n[HID] is not None:
                            u, b = n[HID], par[HID]
                            if t == 0:
                                dve.wait_ge(at_ready.sem, at_ready.count(u))
                                nc.vector.tensor_copy(atf[b][:, :, :], at[b][:, :, 0:2]).then_inc(atf_ready.sem, 1)
                            if t == 1:
                                dve.wait_ge(atf_ready.sem, atf_ready.count(u))
                                for k in range(2):
                                    last = nc.vector.tensor_tensor(hot[b][:, k, :, :], over(iota[0:HALF, :], TILES),
                                                                   wide(atf[b][:, :, k], EXP0), ALU.is_equal)
                                last.then_inc(hot_ready.sem, 1)
                            if t == 2:
                                dve.wait_ge(egap_ready.sem, egap_ready.count(u))
                                nc.vector.tensor_scalar(den[b][:, :], egap[b][:, :], 1.0, None, ALU.add).then_inc(den_ready.sem, 1)
                                dve.wait_ge(den_ready.sem, den_ready.count(u))
                                nc.vector.reciprocal(gate[b][:, 0, :], den[b][:, :]).then_inc(gate0_ready.sem, 1)
                                dve.wait_ge(gate0_ready.sem, gate0_ready.count(u))
                                nc.vector.tensor_tensor(gate[b][:, 1, :], gate[b][:, 0, :], egap[b][:, :], ALU.mult).then_inc(gates_ready.sem, 1)
                        if n[NORM] is not None:
                            u, b = n[NORM], par[NORM]
                            if t == 0:
                                dve.wait_ge(x_in[b].sem, x_in[b].count(u, b))
                                dve.wait_ge(nm.ready.sem, nm.ready.count(u, back=2))
                            norm_moments(nc, dve, nm, u, b, t, dve_passed)
                        if n[SUM] is not None:
                            add_experts(n[SUM], par[SUM], (2 * t, 2 * t + 1))
                    if n[HID] is not None:
                        u, b = n[HID], par[HID]
                        dve.wait_ge(gates_ready.sem, gates_ready.count(u))
                        dve.wait_ge(hot_ready.sem, hot_ready.count(u))
                        for k in range(2):
                            last = nc.vector.tensor_tensor(hot[b][:, k, :, :], hot[b][:, k, :, :],
                                                           wide(gate[b][:, k, :], EXP0), ALU.mult)
                        last.then_inc(hot_scaled.sem, 1)

                in_lanes(dve, UNITS, STAGES, body)

            @block.gpsimd
            def _(pool):
                for x in (nm.var_eps, nm.rstd_ready, nm.ready, var_ready, yrstd_ready, s_ready, yg_ready):
                    x.opened(pool)
                nc.gpsimd.memset(eps[:, :], EPS)
                nc.gpsimd.memset(minus_half[:, :], -0.5).then_inc(constants_set, 1)
                pool.wait_ge(constants_set, 1)
                pool.wait_ge(weights_in, 16 * WEIGHTS)

                def body(n, par):
                    for t in range(TILES):
                        if n[SCALE] is not None:
                            u, b = n[SCALE], par[SCALE]
                            pool.wait_ge(y_ready.sem, y_ready.count(u, t + 1))
                            pool.wait_ge(acc_steps.sem, acc_steps.count(u, back=2))
                            nc.gpsimd.tensor_tensor(yg[b][:, t, :, :], yb[b][:, t, :, :], gam[0:HALF, :, :], ALU.mult).then_inc(yg_ready.sem, 1)
                    if n[SCALE] is not None:
                        u, b = n[SCALE], par[SCALE]
                        pool.wait_ge(ss_ready.sem, ss_ready.count(u))
                        pool.wait_ge(acc_steps.sem, acc_steps.count(u, back=2))
                        pool.sem_inc(pool_passed, 1)
                        weights = s[b][:, :, :].rearrange("p t e -> p (t e)")
                        nc.gpsimd.tensor_scalar(weights, ss[b][:, :, :].rearrange("p t e -> p (t e)"), 1.0 / D, EPS,
                                                ALU.mult, ALU.add).then_inc(var_ready.sem, 1)
                        pool.wait_ge(var_ready.sem, var_ready.count(u))
                        nc.gpsimd.tensor_tensor(weights, weights, minus_half[0:HALF, :], ALU.pow).then_inc(yrstd_ready.sem, 1)
                        pool.wait_ge(yrstd_ready.sem, yrstd_ready.count(u))
                        nc.gpsimd.tensor_tensor(weights, weights, w[b][:, :, :].rearrange("p t e -> p (t e)"), ALU.mult).then_inc(s_ready.sem, 1)
                    if n[NORM] is not None:
                        norm_rows(nc, pool, nm, n[NORM], par[NORM], eps, minus_half, pool_passed, turned)

                in_lanes(pool, UNITS, STAGES, body)

        pl.close()


def phase_linear_attention(nc, h_in, ident, mask, blocks, head_mask, index, wq, wk, wv, bqk, bv, decay, wo, bo, ln_g, ln_b, h_out):
    UNITS = BATCH // 2
    TILES = 4
    N = TILES * HALF
    NORM, TURN, PROJ, PROD, VAL, OUT, FIN = range(7)
    STAGES = 7
    PAIRS = N_HEAD
    with ExitStack() as ctx:
        pl = Place(nc, ctx, "lin")
        sb, sem = pl.sb, pl.sem
        idn = sb("ident", [P, P])
        msk = sb("mask", [HALF, SEQ])
        blk = sb("blocks", [P, P])
        heads = sb("heads", [P, N_HEAD])
        wqk_sb = sb("wqk", [D, 2, D])
        wv_sb = sb("wv", [D, D])
        wo_sb = sb("wo", [D, D])
        bqk_sb = sb("bqk", [P, 2])
        rows = sb("rows", [P, 4, D])
        lam = sb("lam", [P, 1])
        idx = sb("idx", [P, P])
        powers = sb("powers", [P, P])
        dec = sb("dec", [P, 2, SEQ])
        eps = sb("eps", [P, TILES])
        minus_half = sb("minus_half", [P, TILES])

        def two(name, shape, dt=F32):
            return [sb(f"{name}{b}", shape, dt) for b in range(2)]

        nm = Norm(pl, TILES, HALF)
        hnT = two("hnT", [D, N])
        ex = two("ex", [P, N])
        rel = two("rel", [P, N])
        qk = [two("q", [P, N]), two("k", [P, N])]
        qh = sb("qh", [P, N_HEAD, N])
        kt = sb("kt", [HALF, TILES, D])
        sums = two("sums", [P, 2, D])
        qsum = sb("qsum", [P, N])
        inv = two("inv", [P, N])
        v = two("v", [HALF, TILES, N_HEAD, D + E_HEAD])
        prod = sb("prod", [HALF, PAIRS, 2, 2, HALF])
        oT = sb("oT", [D, N])
        z = two("z", [HALF, TILES, D])
        zst = two("zst", [HALF, TILES, 6])
        zmv = two("zmv", [HALF, TILES, 2])
        zrstd = two("zrstd", [HALF, TILES])
        zn = two("zn", [HALF, TILES, D])
        res = two("res", [HALF, TILES, D])
        out = two("out", [HALF, TILES, D])

        ps_proj, ps_kt, ps_den, ps_out = pl.banks("x", 4)
        ps_prod, ps_o = pl.banks("prod", 2), pl.banks("o", 2)

        weights_in = sem("weights_in")
        WEIGHTS = 15
        constants_set = sem("constants_set")
        zeros_set = sem("zeros_set")
        setup = sem("setup")
        exp_decay = sem("exp_decay")
        powers_ready = sem("powers_ready")
        dve_passed, pool_passed = (sem(f"{e}_passed") for e in ("dve", "pool"))
        x_in = [Landed(sem(f"x_in{b}"), 2) for b in range(2)]
        res_in = [Landed(sem(f"res_in{b}"), 2) for b in range(2)]
        stored = [Landed(sem(f"stored{b}"), 2) for b in range(2)]
        turned = Signal(sem("turned"))
        hnT_ready = Signal(sem("hnT_ready"))
        proj_done = Signal(sem("proj_done"), 2)
        proj_read = Signal(sem("proj_read"), 2)
        feature_ready = Signal(sem("feature_ready"), 2)
        qk_ready = Signal(sem("qk_ready"), 2)
        qh_ready = Signal(sem("qh_ready"))
        v_done = Signal(sem("v_done"))
        v_ready = Signal(sem("v_ready"))
        kt_done = Signal(sem("kt_done"))
        kt_ready = Signal(sem("kt_ready"))
        sums_done = Signal(sem("sums_done"))
        sums_ready = Signal(sem("sums_ready"))
        ksum_done = Signal(sem("ksum_done"))
        qsum_ready = Signal(sem("qsum_ready"))
        den_done = Signal(sem("den_done"))
        den_read = Signal(sem("den_read"))
        inv_ready = Signal(sem("inv_ready"))
        prod_done = Signal(sem("prod_done"), PAIRS)
        prod_ready = Signal(sem("prod_ready"), PAIRS)
        cross_done = Signal(sem("cross_done"))
        val_done = Signal(sem("val_done"), PAIRS)
        oT_ready = Signal(sem("oT_ready"))
        z_done = Signal(sem("z_done"))
        z_ready = Signal(sem("z_ready"))
        zstats = Signal(sem("zstats"), TILES)
        zmoments = Signal(sem("zmoments"), TILES)
        zvar_eps = Signal(sem("zvar_eps"))
        zrstd_ready = Signal(sem("zrstd_ready"))
        zn_ready = Signal(sem("zn_ready"))
        zg_ready = Signal(sem("zg_ready"))
        zb_ready = Signal(sem("zb_ready"))
        out_ready = Signal(sem("out_ready"))

        with nc.Block() as block:

            @block.sync
            def _(sp):
                for dst, src in ((idn[:, :], ident), (msk[:, :], mask), (blk[:, :], blocks), (heads[:, :], head_mask),
                                 (wqk_sb[:, 0, :], wq), (wqk_sb[:, 1, :], wk), (wv_sb[:, :], wv), (wo_sb[:, :], wo),
                                 (bqk_sb[:, :], bqk), (lam[:, :], decay), (idx[:, :], index),
                                 (rows[:, 0, :], bv.partition_broadcast(P)), (rows[:, 1, :], bo.partition_broadcast(P)),
                                 (rows[:, 2, :], ln_g.partition_broadcast(P)), (rows[:, 3, :], ln_b.partition_broadcast(P))):
                    sp.dma_start(dst, src).then_inc(weights_in, 16)
                for b in range(2):
                    x_in[b].opened(sp)
                    res_in[b].opened(sp)
                    stored[b].opened(sp)

                def body(n, par):
                    if n[NORM] is not None:
                        u, b = n[NORM], par[NORM]
                        sp.wait_ge(nm.ready.sem, nm.ready.count(u, back=2))
                        load_rows(sp, nm.x[b], h_in, u, x_in[b])
                    if n[OUT] is not None:
                        u, b = n[OUT], par[OUT]
                        sp.wait_ge(out_ready.sem, out_ready.count(u, back=2))
                        load_rows(sp, res[b], h_in, u, res_in[b])
                    if n[FIN] is not None:
                        u, b = n[FIN], par[FIN]
                        sp.wait_ge(out_ready.sem, out_ready.count(u))
                        store_rows(sp, h_out, out[b], u, stored[b])

                in_lanes(sp, UNITS, STAGES, body)
                for b in range(2):
                    sp.wait_ge(stored[b].sem, stored[b].final(UNITS))

            @block.tensor
            def _(pe):
                for x in (turned, proj_done, v_done, kt_done, sums_done, ksum_done, den_done, prod_done, cross_done, val_done, z_done):
                    x.opened(pe)
                pe.wait_ge(weights_in, 16 * WEIGHTS)

                def project(u, b, i):
                    if i == 0:
                        pe.wait_ge(hnT_ready.sem, hnT_ready.count(u))
                        pe.wait_ge(v_ready.sem, v_ready.count(u, back=1))
                    else:
                        pe.wait_ge(proj_read.sem, proj_read.count(u, 1))
                    nc.tensor.matmul(ps_proj[:, 0:N], wqk_sb[:, i, :], hnT[b][:, :], start=True, stop=True).then_inc(proj_done.sem, 1)

                def turn(u, b):
                    pe.wait_ge(nm.ready.sem, nm.ready.count(u))
                    pe.wait_ge(proj_read.sem, proj_read.count(u, back=1))
                    for t in range(TILES):
                        last = nc.tensor.transpose(ps_proj[:, t * HALF:(t + 1) * HALF], nm.y[b][:, t, :], idn[0:HALF, 0:HALF])
                    last.then_inc(turned.sem, 1)

                def project_v(u, b, turning):
                    pe.wait_ge(proj_read.sem, proj_read.count(u))
                    if turning is not None:
                        pe.wait_ge(hnT_ready.sem, hnT_ready.count(turning))
                    for t in range(TILES):
                        last = nc.tensor.matmul(ps_proj[0:HALF, t * D:(t + 1) * D], hnT[b][:, t * HALF:(t + 1) * HALF], wv_sb[:, :],
                                                start=True, stop=True)
                    last.then_inc(v_done.sem, 1)

                def turn_k(u, b):
                    pe.wait_ge(sums_ready.sem, sums_ready.count(u, back=1))
                    for t in range(TILES):
                        last = nc.tensor.transpose(ps_kt[0:HALF, t * D:(t + 1) * D], qk[1][b][:, t * HALF:(t + 1) * HALF], idn[:, :])
                    last.then_inc(kt_done.sem, 1)

                def running_k(u):
                    pe.wait_ge(kt_ready.sem, kt_ready.count(u))
                    pe.wait_ge(den_read.sem, den_read.count(u, back=1))
                    for seq in range(2):
                        at = seq * SEQ
                        nc.tensor.matmul(ps_den[:, at:at + SEQ], kt[:, 2 * seq, :], msk[:, :], start=True, stop=False)
                        last = nc.tensor.matmul(ps_den[:, at + HALF:at + SEQ], kt[:, 2 * seq + 1, :], msk[:, 0:HALF], start=False, stop=True)
                    last.then_inc(ksum_done.sem, 1)

                def sum_kv(u, b):
                    pe.wait_ge(v_ready.sem, v_ready.count(u))
                    for seq in range(2):
                        last = nc.tensor.matmul(ps_kt[:, seq * D:(seq + 1) * D].rearrange("p (h e) -> p h e", e=E_HEAD), kt[:, 2 * seq, :],
                                                v[b][:, 2 * seq, :, 0:E_HEAD], start=True, stop=True)
                    last.then_inc(sums_done.sem, 1)

                def denominators(u):
                    pe.wait_ge(qsum_ready.sem, qsum_ready.count(u))
                    nc.tensor.matmul(ps_den[:, 0:N], blk[:, :], qsum[:, :], start=True, stop=True).then_inc(den_done.sem, 1)

                def products(u, b, x):
                    seq = x // 4
                    if x == 0:
                        pe.wait_ge(qk_ready.sem, qk_ready.count(u))
                        pe.wait_ge(qh_ready.sem, qh_ready.count(u))
                    pe.wait_ge(prod_ready.sem, prod_ready.count(u, x - 1))
                    for i in range(2):
                        for c in range(2):
                            at = (2 * seq + c) * HALF
                            last = nc.tensor.matmul(ps_prod[x % 2][0:HALF, (2 * i + c) * HALF:(2 * i + c + 1) * HALF], qk[1][b][:, at:at + HALF],
                                                    qh[:, 2 * (x % 4) + i, at:at + HALF], start=True, stop=True)
                    last.then_inc(prod_done.sem, 1)

                def cross(u, b):
                    pe.wait_ge(sums_ready.sem, sums_ready.count(u))
                    pe.wait_ge(oT_ready.sem, oT_ready.count(u, back=2))
                    for seq in range(2):
                        at = seq * SEQ + HALF
                        last = nc.tensor.matmul(ps_o[b][:, at:at + HALF], sums[b][:, seq, :], qk[0][b][:, at:at + HALF], start=seq == 0, stop=False)
                    last.then_inc(cross_done.sem, 1)

                def values(u, b, x):
                    seq = x // 4
                    pe.wait_ge(prod_ready.sem, prod_ready.count(u, x + 1))
                    for i in range(2):
                        h = 2 * (x % 4) + i
                        for c in range(2):
                            at = (2 * seq + c) * HALF
                            by_head = v[b][:, 2 * seq + c, :, :].rearrange("p h x -> p (h x)")
                            last = nc.tensor.matmul(ps_o[b][:, at:at + HALF], by_head[:, h * D:(h + 1) * D], prod[:, x, i, c, :],
                                                    start=False, stop=x == PAIRS - 1 and i == 1 and c == 1)
                    last.then_inc(val_done.sem, 1)

                def output(u):
                    pe.wait_ge(oT_ready.sem, oT_ready.count(u))
                    pe.wait_ge(z_ready.sem, z_ready.count(u, back=1))
                    for t in range(TILES):
                        last = nc.tensor.matmul(ps_out[0:HALF, t * D:(t + 1) * D], oT[:, t * HALF:(t + 1) * HALF], wo_sb[:, :], start=True, stop=True)
                    last.then_inc(z_done.sem, 1)

                def body(n, par):
                    if n[VAL] is not None:
                        cross(n[VAL], par[VAL])
                    for x in range(PAIRS):
                        if n[PROD] is not None:
                            products(n[PROD], par[PROD], x)
                        if n[VAL] is not None:
                            values(n[VAL], par[VAL], x)
                        if n[PROJ] is not None and x < 2:
                            project(n[PROJ], par[PROJ], x)
                        if n[PROD] is not None:
                            if x == 0:
                                turn_k(n[PROD], par[PROD])
                            if x == 2:
                                running_k(n[PROD])
                                sum_kv(n[PROD], par[PROD])
                            if x == 5:
                                denominators(n[PROD])
                        if n[OUT] is not None and x == 1:
                            output(n[OUT])
                        if n[TURN] is not None and x == 4:
                            turn(n[TURN], par[TURN])
                    if n[PROJ] is not None:
                        project_v(n[PROJ], par[PROJ], n[TURN])

                in_lanes(pe, UNITS, STAGES, body)

            @block.scalar
            def _(act):
                for x in (hnT_ready, proj_read, kt_ready, qh_ready):
                    x.opened(act)
                act.wait_ge(weights_in, 16 * WEIGHTS)
                nc.scalar.activation(lam[:, :], lam[:, :], ACT.Exp, scale=-1.0).then_inc(exp_decay, 1)

                def body(n, par):
                    for x in range(PAIRS):
                        if n[PROJ] is not None and x < 2:
                            u = n[PROJ]
                            act.wait_ge(proj_done.sem, proj_done.count(u, x + 1))
                            act.wait_ge(qk_ready.sem, qk_ready.count(u, x + 1, back=1))
                            nc.scalar.activation(ex[x][:, :], ps_proj[:, 0:N], ACT.Exp, bias=bqk_sb[:, x:x + 1])
                            nc.scalar.activation(rel[x][:, :], ps_proj[:, 0:N], ACT.Relu, bias=bqk_sb[:, x:x + 1]).then_inc(proj_read.sem, 1)
                        if n[PROD] is not None and x == 1:
                            u = n[PROD]
                            act.wait_ge(kt_done.sem, kt_done.count(u))
                            act.wait_ge(sums_done.sem, sums_done.count(u, back=1))
                            nc.scalar.copy(kt[:, :, :].rearrange("p t d -> p (t d)"), ps_kt[0:HALF, :]).then_inc(kt_ready.sem, 1)
                        if n[TURN] is not None and x == 4:
                            u, b = n[TURN], par[TURN]
                            act.wait_ge(turned.sem, turned.count(u))
                            act.wait_ge(v_done.sem, v_done.count(u, back=2))
                            nc.scalar.copy(hnT[b][:, :], ps_proj[:, 0:N]).then_inc(hnT_ready.sem, 1)
                    if n[PROJ] is not None:
                        u, b = n[PROJ], par[PROJ]
                        act.wait_ge(qk_ready.sem, qk_ready.count(u, 1))
                        act.wait_ge(prod_done.sem, prod_done.count(u, back=1))
                        for h in range(N_HEAD):
                            last = nc.scalar.activation(qh[:, h, :], qk[0][b][:, :], ACT.Copy, scale=heads[:, h:h + 1])
                        last.then_inc(qh_ready.sem, 1)

                in_lanes(act, UNITS, STAGES, body)

            @block.vector
            def _(dve):
                for x in (nm.stats, nm.moments, feature_ready, v_ready, sums_ready, qsum_ready, den_read, inv_ready, prod_ready,
                          oT_ready, z_ready, zstats, zmoments, out_ready):
                    x.opened(dve)
                for b in range(2):
                    nc.vector.memset(v[b][:, :, :, :], 0.0).then_inc(zeros_set, 1)
                dve.wait_ge(exp_decay, 1)
                nc.vector.tensor_scalar(lam[:, :], lam[:, :], 1.0, None, ALU.add).then_inc(setup, 1)
                dve.wait_ge(setup, 1)
                nc.vector.reciprocal(lam[:, :], lam[:, :]).then_inc(setup, 1)
                dve.wait_ge(setup, 2)
                nc.vector.tensor_scalar(lam[:, :], lam[:, :], 0.01, 0.99, ALU.mult, ALU.add).then_inc(setup, 1)
                dve.wait_ge(powers_ready, 1)
                nc.vector.tensor_copy(dec[:, 0, 0:HALF], powers[:, 0:HALF])
                nc.vector.tensor_scalar(dec[:, 0, HALF:SEQ], powers[:, 0:HALF], powers[:, HALF:P], None, ALU.mult).then_inc(setup, 1)
                dve.wait_ge(setup, 4)
                nc.vector.reciprocal(dec[:, 1, :], dec[:, 0, :]).then_inc(setup, 1)
                dve.wait_ge(setup, 5)
                nc.vector.tensor_scalar(dec[:, 0, :], dec[:, 0, :], E_HEAD ** -0.5, None, ALU.mult).then_inc(setup, 1)
                dve.wait_ge(zeros_set, 2)
                dve.wait_ge(weights_in, 16 * WEIGHTS)

                def body(n, par):
                    for x in range(PAIRS):
                        if n[PROD] is not None:
                            u = n[PROD]
                            dve.wait_ge(prod_done.sem, prod_done.count(u, x + 1))
                            dve.wait_ge(val_done.sem, val_done.count(u, x + 1, back=1))
                            nc.vector.tensor_tensor(prod[:, x, :, :, :].rearrange("p i c n -> p (i c) n"),
                                                    ps_prod[x % 2][0:HALF, 0:N].rearrange("p (x n) -> p x n", n=HALF),
                                                    over(msk[:, 0:HALF], 4), ALU.mult).then_inc(prod_ready.sem, 1)
                        if n[OUT] is not None:
                            u, b = n[OUT], par[OUT]
                            if x == 0:
                                dve.wait_ge(val_done.sem, val_done.count(u))
                                dve.wait_ge(inv_ready.sem, inv_ready.count(u))
                                dve.wait_ge(z_done.sem, z_done.count(u, back=1))
                                nc.vector.tensor_tensor(oT[:, :], ps_o[b][:, 0:N], inv[b][:, :], ALU.mult).then_inc(oT_ready.sem, 1)
                            if x == 2:
                                dve.wait_ge(z_done.sem, z_done.count(u))
                                dve.wait_ge(zn_ready.sem, zn_ready.count(u, back=2))
                                nc.vector.tensor_tensor(z[b][:, :, :], ps_out[0:HALF, :].rearrange("p (t d) -> p t d", t=TILES),
                                                        over(rows[0:HALF, 1, :], TILES), ALU.add).then_inc(z_ready.sem, 1)
                            if x == 3:
                                dve.wait_ge(z_ready.sem, z_ready.count(u))
                                for t in range(TILES):
                                    nc.vector.bn_stats(zst[b][:, t, :], z[b][:, t, :]).then_inc(zstats.sem, 1)
                            if x == 4:
                                dve.wait_ge(zstats.sem, zstats.count(u))
                                dve.sem_inc(dve_passed, 1)
                                for t in range(TILES):
                                    nc.vector.bn_aggr(zmv[b][:, t, :], zst[b][:, t, :]).then_inc(zmoments.sem, 1)
                        if n[PROJ] is not None and x < 2:
                            u = n[PROJ]
                            dve.wait_ge(proj_read.sem, proj_read.count(u, x + 1))
                            nc.vector.scalar_tensor_tensor(ex[x][:, :], ex[x][:, :], 1.0, rel[x][:, :],
                                                           ALU.min, ALU.add).then_inc(feature_ready.sem, 1)
                        if n[PROD] is not None:
                            u, b = n[PROD], par[PROD]
                            if x == 3:
                                dve.wait_ge(ksum_done.sem, ksum_done.count(u))
                                dve.wait_ge(den_done.sem, den_done.count(u, back=1))
                                nc.vector.tensor_tensor(qsum[:, :], ps_den[:, 0:N], qk[0][b][:, :], ALU.mult).then_inc(qsum_ready.sem, 1)
                            if x == 4:
                                dve.wait_ge(sums_done.sem, sums_done.count(u))
                                dve.wait_ge(cross_done.sem, cross_done.count(u, back=2))
                                nc.vector.tensor_tensor(sums[b][:, :, :], ps_kt[:, 0:2 * D].rearrange("p (s d) -> p s d", s=2),
                                                        over(blk[:, :], 2), ALU.mult).then_inc(sums_ready.sem, 1)
                            if x == 6:
                                dve.wait_ge(den_done.sem, den_done.count(u))
                                dve.wait_ge(oT_ready.sem, oT_ready.count(u, back=2))
                                nc.vector.tensor_scalar(inv[b][:, :], ps_den[:, 0:N], 1e-6, None, ALU.add).then_inc(den_read.sem, 1)
                            if x == 7:
                                dve.wait_ge(den_read.sem, den_read.count(u))
                                nc.vector.reciprocal(inv[b][:, :], inv[b][:, :]).then_inc(inv_ready.sem, 1)
                        if n[NORM] is not None and x % 2 == 0:
                            u, b, t = n[NORM], par[NORM], x // 2
                            if t == 0:
                                dve.wait_ge(x_in[b].sem, x_in[b].count(u, b))
                                dve.wait_ge(nm.ready.sem, nm.ready.count(u, back=2))
                            norm_moments(nc, dve, nm, u, b, t, dve_passed)
                    if n[FIN] is not None:
                        u, b = n[FIN], par[FIN]
                        dve.wait_ge(res_in[b].sem, res_in[b].count(u, b))
                        dve.wait_ge(zb_ready.sem, zb_ready.count(u))
                        dve.wait_ge(stored[b].sem, stored[b].count(u, b, back=1))
                        nc.vector.tensor_tensor(out[b][:, :, :], zn[b][:, :, :], res[b][:, :, :], ALU.add).then_inc(out_ready.sem, 1)
                    if n[PROJ] is not None:
                        u, b = n[PROJ], par[PROJ]
                        dve.wait_ge(v_done.sem, v_done.count(u))
                        dve.wait_ge(val_done.sem, val_done.count(u, back=2))
                        for t in range(TILES):
                            last = nc.vector.tensor_tensor(v[b][:, t, :, 0:E_HEAD], ps_proj[0:HALF, t * D:(t + 1) * D].rearrange("p (h e) -> p h e", e=E_HEAD),
                                                           rows[0:HALF, 0, :].rearrange("p (h e) -> p h e", e=E_HEAD), ALU.add)
                        last.then_inc(v_ready.sem, 1)

                in_lanes(dve, UNITS, STAGES, body)

            @block.gpsimd
            def _(pool):
                for x in (nm.var_eps, nm.rstd_ready, nm.ready, qk_ready, zvar_eps, zrstd_ready, zn_ready, zg_ready, zb_ready):
                    x.opened(pool)
                nc.gpsimd.memset(eps[:, :], EPS)
                nc.gpsimd.memset(minus_half[:, :], -0.5).then_inc(constants_set, 1)
                pool.wait_ge(constants_set, 1)
                pool.wait_ge(weights_in, 16 * WEIGHTS)
                pool.wait_ge(setup, 3)
                nc.gpsimd.tensor_tensor(powers[:, :], lam[:, :].to_broadcast([P, P]), idx[:, :], ALU.pow).then_inc(powers_ready, 1)

                def body(n, par):
                    for x in range(4):
                        if n[PROJ] is not None and x < 2:
                            u, b = n[PROJ], par[PROJ]
                            pool.wait_ge(feature_ready.sem, feature_ready.count(u, x + 1))
                            pool.wait_ge(prod_done.sem, prod_done.count(u, back=2))
                            pool.wait_ge(cross_done.sem, cross_done.count(u, back=2))
                            nc.gpsimd.tensor_tensor(qk[x][b][:, :].rearrange("p (s n) -> p s n", s=2),
                                                    ex[x][:, :].rearrange("p (s n) -> p s n", s=2),
                                                    over(dec[:, x, :], 2), ALU.mult).then_inc(qk_ready.sem, 1)
                        if n[FIN] is not None:
                            u, b = n[FIN], par[FIN]
                            if x == 0:
                                pool.wait_ge(zmoments.sem, zmoments.count(u))
                                nc.gpsimd.tensor_tensor(zrstd[b][:, :], zmv[b][:, :, 1], eps[0:HALF, :], ALU.add).then_inc(zvar_eps.sem, 1)
                                pool.wait_ge(zvar_eps.sem, zvar_eps.count(u))
                                nc.gpsimd.tensor_tensor(zrstd[b][:, :], zrstd[b][:, :], minus_half[0:HALF, :], ALU.pow).then_inc(zrstd_ready.sem, 1)
                            if x == 1:
                                pool.wait_ge(zrstd_ready.sem, zrstd_ready.count(u))
                                pool.wait_ge(out_ready.sem, out_ready.count(u, back=2))
                                pool.sem_inc(pool_passed, 1)
                                for t in range(TILES):
                                    last = nc.gpsimd.tensor_scalar(zn[b][:, t, :], z[b][:, t, :], zmv[b][:, t, 0:1], zrstd[b][:, t:t + 1],
                                                                   ALU.subtract, ALU.mult)
                                last.then_inc(zn_ready.sem, 1)
                            if x == 2:
                                pool.wait_ge(zn_ready.sem, zn_ready.count(u))
                                nc.gpsimd.tensor_tensor(zn[b][:, :, :], zn[b][:, :, :], over(rows[0:HALF, 2, :], TILES), ALU.mult).then_inc(zg_ready.sem, 1)
                            if x == 3:
                                pool.wait_ge(zg_ready.sem, zg_ready.count(u))
                                nc.gpsimd.tensor_tensor(zn[b][:, :, :], zn[b][:, :, :], over(rows[0:HALF, 3, :], TILES), ALU.add).then_inc(zb_ready.sem, 1)
                    if n[NORM] is not None:
                        norm_rows(nc, pool, nm, n[NORM], par[NORM], eps, minus_half, pool_passed, turned)

                pool.wait_ge(setup, 6)
                in_lanes(pool, UNITS, STAGES, body)

        pl.close()


def phase_attention(nc, h_in, ident, head_mask, wq, wk, wv, wo, g_col, b_col, y_dram, h_out):
    UNITS = BATCH // 2
    TILES = 4
    N = TILES * HALF
    NORM, TURN, PROJ, SOFT, VAL, FIN = range(6)
    STAGES = 6
    HEADS = 2 * N_HEAD
    with ExitStack() as ctx:
        pl = Place(nc, ctx, "att")
        sb, sem = pl.sb, pl.sem
        idn = sb("ident", [P, P])
        heads = sb("heads", [P, N_HEAD])
        wqk_sb = sb("wqk", [D, 2, D])
        wv_sb = sb("wv", [D, D])
        wo_sb = sb("wo", [D, D])
        gb = sb("gb", [P, 2])
        eps = sb("eps", [P, TILES])
        minus_half = sb("minus_half", [P, TILES])

        def two(name, shape, dt=F32):
            return [sb(f"{name}{b}", shape, dt) for b in range(2)]

        nm = Norm(pl, TILES, HALF)
        var2 = two("var2", [HALF, TILES])
        yn = two("yn", [HALF, TILES, D])
        hnT = two("hnT", [D, N])
        q = two("q", [D, N])
        k = sb("k", [D, N])
        kh = two("kh", [D, N_HEAD, N])
        least = two("least", [HALF, HEADS, 2])
        ex = sb("ex", [HALF, HEADS, 2, SEQ])
        total = two("total", [HALF, HEADS, 2])
        inv = sb("inv", [HALF, HEADS, 2])
        inv_wide = sb("inv_wide", [HALF, TILES, N_HEAD, E_HEAD])
        invT = two("invT", [D, SEQ])
        exT = two("exT", [HALF, 2, SEQ])
        v = two("v", [HALF, TILES, N_HEAD, D + E_HEAD])
        oT = two("oT", [D, SEQ])
        res = two("res", [HALF, TILES, D])
        out = two("out", [HALF, TILES, D])

        ps_proj, ps_out = pl.banks("x", 2)
        ps_sc, ps_exT, ps_o = pl.banks("sc", 2), pl.banks("exT", 2), pl.banks("o", 2)

        weights_in = sem("weights_in")
        WEIGHTS = 8
        zeros_set = sem("zeros_set")
        pool_set = sem("pool_set")
        pe_passed, act_passed, dve_passed, pool_passed = (sem(f"{e}_passed") for e in ("pe", "act", "dve", "pool"))
        x_in = [Landed(sem(f"x_in{b}"), 2) for b in range(2)]
        res_in = [Landed(sem(f"res_in{b}"), 2) for b in range(2)]
        stored = [Landed(sem(f"stored{b}"), 2) for b in range(2)]
        y_out = [Landed(sem(f"y_out{b}"), 2) for b in range(2)]
        square_ready = Signal(sem("square_ready"))
        var2_ready = Signal(sem("var2_ready"))
        var2_eps = Signal(sem("var2_eps"))
        rstd2_ready = Signal(sem("rstd2_ready"))
        yn_ready = Signal(sem("yn_ready"))
        turned = Signal(sem("turned"))
        hnT_ready = Signal(sem("hnT_ready"))
        qk_done = Signal(sem("qk_done"), 2)
        qk_ready = Signal(sem("qk_ready"), 2)
        kh_ready = Signal(sem("kh_ready"))
        v_done = Signal(sem("v_done"))
        v_ready = Signal(sem("v_ready"))
        sc_done = Signal(sem("sc_done"), HEADS)
        least_ready = Signal(sem("least_ready"), HEADS)
        ex_ready = Signal(sem("ex_ready"), HEADS)
        ex_turned = Signal(sem("ex_turned"), HEADS)
        exT_ready = Signal(sem("exT_ready"), HEADS)
        val_done = Signal(sem("val_done"), HEADS)
        inv_ready = Signal(sem("inv_ready"))
        inv_wide_ready = Signal(sem("inv_wide_ready"))
        inv_turned = Signal(sem("inv_turned"), 2)
        invT_ready = Signal(sem("invT_ready"), 2)
        oT_ready = Signal(sem("oT_ready"), 2)
        z_done = Signal(sem("z_done"), 2)
        out_ready = Signal(sem("out_ready"), 2)

        with nc.Block() as block:

            @block.sync
            def _(sp):
                for dst, src in ((idn[:, :], ident), (heads[:, :], head_mask), (wqk_sb[:, 0, :], wq), (wqk_sb[:, 1, :], wk),
                                 (wv_sb[:, :], wv), (wo_sb[:, :], wo), (gb[:, 0:1], g_col), (gb[:, 1:2], b_col)):
                    sp.dma_start(dst, src).then_inc(weights_in, 16)
                for b in range(2):
                    x_in[b].opened(sp)
                    res_in[b].opened(sp)
                    stored[b].opened(sp)
                    y_out[b].opened(sp)

                def body(n, par):
                    if n[NORM] is not None:
                        u, b = n[NORM], par[NORM]
                        sp.wait_ge(nm.ready.sem, nm.ready.count(u, back=2))
                        load_rows(sp, nm.x[b], h_in, u, x_in[b])
                    if n[TURN] is not None:
                        u, b = n[TURN], par[TURN]
                        sp.wait_ge(nm.ready.sem, nm.ready.count(u))
                        store_rows(sp, y_dram, nm.y[b], u, y_out[b])
                    if n[VAL] is not None:
                        u, b = n[VAL], par[VAL]
                        sp.wait_ge(out_ready.sem, out_ready.count(u, back=2))
                        sp.wait_ge(y_out[b].sem, y_out[b].count(u, b))
                        load_rows(sp, res[b], y_dram, u, res_in[b])
                    if n[FIN] is not None:
                        u, b = n[FIN], par[FIN]
                        sp.wait_ge(out_ready.sem, out_ready.count(u))
                        store_rows(sp, h_out, out[b], u, stored[b])

                in_lanes(sp, UNITS, STAGES, body)
                for b in range(2):
                    sp.wait_ge(stored[b].sem, stored[b].final(UNITS))

            @block.tensor
            def _(pe):
                for x in (turned, qk_done, v_done, sc_done, ex_turned, val_done, inv_turned, z_done):
                    x.opened(pe)
                pe.wait_ge(weights_in, 16 * WEIGHTS)

                def project(u, b, i):
                    if i == 0:
                        pe.wait_ge(hnT_ready.sem, hnT_ready.count(u))
                        pe.wait_ge(v_ready.sem, v_ready.count(u, back=1))
                    else:
                        pe.wait_ge(qk_ready.sem, qk_ready.count(u, 1))
                    nc.tensor.matmul(ps_proj[:, 0:N], wqk_sb[:, i, :], hnT[b][:, :], start=True, stop=True).then_inc(qk_done.sem, 1)

                def turn(u, b):
                    pe.wait_ge(yn_ready.sem, yn_ready.count(u))
                    pe.wait_ge(qk_ready.sem, qk_ready.count(u, back=1))
                    for t in range(TILES):
                        last = nc.tensor.transpose(ps_proj[:, t * HALF:(t + 1) * HALF], yn[b][:, t, :], idn[0:HALF, 0:HALF])
                    last.then_inc(turned.sem, 1)

                def project_v(u, b, turning):
                    pe.wait_ge(qk_ready.sem, qk_ready.count(u))
                    if turning is not None:
                        pe.wait_ge(hnT_ready.sem, hnT_ready.count(turning))
                    for t in range(TILES):
                        last = nc.tensor.matmul(ps_proj[0:HALF, t * D:(t + 1) * D], hnT[b][:, t * HALF:(t + 1) * HALF], wv_sb[:, :],
                                                start=True, stop=True)
                    last.then_inc(v_done.sem, 1)

                def scores(u, b, x):
                    seq, h = x // N_HEAD, x % N_HEAD
                    if x == 0:
                        pe.wait_ge(kh_ready.sem, kh_ready.count(u))
                    pe.wait_ge(ex_ready.sem, ex_ready.count(u, x - 1))
                    for c in range(2):
                        at = seq * SEQ + c * HALF
                        last = nc.tensor.matmul(ps_sc[x % 2][0:HALF, c * SEQ:(c + 1) * SEQ], q[b][:, at:at + HALF],
                                                kh[b][:, h, seq * SEQ:(seq + 1) * SEQ], start=True, stop=True)
                    last.then_inc(sc_done.sem, 1)

                def turn_ex(u, x):
                    pe.wait_ge(ex_ready.sem, ex_ready.count(u, x + 1))
                    pe.wait_ge(exT_ready.sem, exT_ready.count(u, x - 1))
                    for half in range(2):
                        for c in range(2):
                            last = nc.tensor.transpose(ps_exT[x % 2][0:HALF, half * SEQ + c * HALF:half * SEQ + (c + 1) * HALF],
                                                       ex[:, x, c, half * HALF:(half + 1) * HALF], idn[0:HALF, 0:HALF])
                    last.then_inc(ex_turned.sem, 1)

                def values(u, b, x):
                    seq, h = x // N_HEAD, x % N_HEAD
                    pe.wait_ge(exT_ready.sem, exT_ready.count(u, x + 1))
                    if x == 0:
                        pe.wait_ge(v_ready.sem, v_ready.count(u))
                    if h == 0:
                        pe.wait_ge(oT_ready.sem, oT_ready.count(u, seq + 1, back=1))
                    for half in range(2):
                        by_head = v[b][:, 2 * seq + half, :, :].rearrange("p h x -> p (h x)")
                        last = nc.tensor.matmul(ps_o[seq][:, 0:SEQ], by_head[:, h * D:(h + 1) * D], exT[x % 2][:, half, :],
                                                start=h == 0 and half == 0, stop=h == N_HEAD - 1 and half == 1)
                    last.then_inc(val_done.sem, 1)

                def turn_inv(u, seq):
                    pe.wait_ge(inv_wide_ready.sem, inv_wide_ready.count(u))
                    pe.wait_ge(out_ready.sem, out_ready.count(u, seq))
                    for c in range(2):
                        last = nc.tensor.transpose(ps_out[:, c * HALF:(c + 1) * HALF],
                                                   inv_wide[:, 2 * seq + c, :, :].rearrange("p h e -> p (h e)"), idn[0:HALF, 0:HALF])
                    last.then_inc(inv_turned.sem, 1)

                def output(u, seq):
                    pe.wait_ge(oT_ready.sem, oT_ready.count(u, seq + 1))
                    for c in range(2):
                        last = nc.tensor.matmul(ps_out[0:HALF, 256 + c * D:256 + (c + 1) * D], oT[seq][:, c * HALF:(c + 1) * HALF],
                                                wo_sb[:, :], start=True, stop=True)
                    last.then_inc(z_done.sem, 1)

                def body(n, par):
                    for x in range(HEADS):
                        if n[SOFT] is not None:
                            scores(n[SOFT], par[SOFT], x)
                        if n[VAL] is not None:
                            turn_ex(n[VAL], x)
                        if x == 2 and n[FIN] is not None:
                            output(n[FIN], 1)
                        if x == 3 and n[PROJ] is not None:
                            project(n[PROJ], par[PROJ], 0)
                        if x == 6 and n[PROJ] is not None:
                            project(n[PROJ], par[PROJ], 1)
                        if x == 9 and n[TURN] is not None:
                            turn(n[TURN], par[TURN])
                        if n[VAL] is not None:
                            u = n[VAL]
                            if x > 0:
                                values(u, par[VAL], x - 1)
                            if x == 5:
                                turn_inv(u, 0)
                            if x == 10:
                                output(u, 0)
                            if x == 13:
                                turn_inv(u, 1)
                    if n[VAL] is not None:
                        values(n[VAL], par[VAL], HEADS - 1)
                    if n[PROJ] is not None:
                        project_v(n[PROJ], par[PROJ], n[TURN])

                in_lanes(pe, UNITS, STAGES, body)

            @block.scalar
            def _(act):
                for x in (hnT_ready, qk_ready, ex_ready, v_ready, invT_ready):
                    x.opened(act)
                act.wait_ge(zeros_set, 2)
                act.wait_ge(weights_in, 16 * WEIGHTS)

                def read_inv(u, seq):
                    act.wait_ge(inv_turned.sem, inv_turned.count(u, seq + 1))
                    act.wait_ge(oT_ready.sem, oT_ready.count(u, seq + 1, back=1))
                    nc.scalar.copy(invT[seq][:, :], ps_out[:, 0:SEQ]).then_inc(invT_ready.sem, 1)

                def body(n, par):
                    for x in range(HEADS):
                        if n[SOFT] is not None:
                            u, b = n[SOFT], par[SOFT]
                            act.wait_ge(least_ready.sem, least_ready.count(u, x + 1))
                            act.wait_ge(ex_turned.sem, ex_turned.count(u, x + 1, back=1))
                            if x == 0:
                                act.wait_ge(inv_ready.sem, inv_ready.count(u, back=2))
                            for c in range(2):
                                last = nc.scalar.activation(ex[:, x, c, :], ps_sc[x % 2][0:HALF, c * SEQ:(c + 1) * SEQ], ACT.Exp,
                                                            bias=least[b][:, x, c:c + 1], scale=-1.0,
                                                            accum_out=total[b][:, x, c:c + 1])
                            last.then_inc(ex_ready.sem, 1)
                        if x == 4 and n[PROJ] is not None:
                            u, b = n[PROJ], par[PROJ]
                            act.wait_ge(qk_done.sem, qk_done.count(u, 1))
                            act.wait_ge(sc_done.sem, sc_done.count(u, back=2))
                            nc.scalar.activation(q[b][:, :], ps_proj[:, 0:N], ACT.Copy, scale=-E_HEAD ** -0.5).then_inc(qk_ready.sem, 1)
                        if x == 6 and n[VAL] is not None:
                            read_inv(n[VAL], 0)
                        if x == 7 and n[PROJ] is not None:
                            u, b = n[PROJ], par[PROJ]
                            act.wait_ge(qk_done.sem, qk_done.count(u, 2))
                            act.wait_ge(kh_ready.sem, kh_ready.count(u, back=1))
                            nc.scalar.copy(k[:, :], ps_proj[:, 0:N]).then_inc(qk_ready.sem, 1)
                        if x == 10 and n[TURN] is not None:
                            u, b = n[TURN], par[TURN]
                            act.wait_ge(turned.sem, turned.count(u))
                            act.wait_ge(v_done.sem, v_done.count(u, back=2))
                            nc.scalar.activation(hnT[b][:, :], ps_proj[:, 0:N], ACT.Identity, bias=gb[:, 1:2], scale=gb[:, 0:1]).then_inc(hnT_ready.sem, 1)
                        if x == 14 and n[VAL] is not None:
                            read_inv(n[VAL], 1)
                    if n[PROJ] is not None:
                        u, b = n[PROJ], par[PROJ]
                        act.wait_ge(v_done.sem, v_done.count(u))
                        act.wait_ge(val_done.sem, val_done.count(u, back=2))
                        nc.scalar.copy(v[b][:, :, :, 0:E_HEAD], ps_proj[0:HALF, :].rearrange("p (t h e) -> p t h e", t=TILES, e=E_HEAD)).then_inc(v_ready.sem, 1)

                in_lanes(act, UNITS, STAGES, body)

            @block.vector
            def _(dve):
                for x in (nm.stats, nm.moments, yn_ready, least_ready, exT_ready, inv_ready, inv_wide_ready, oT_ready, out_ready):
                    x.opened(dve)
                for b in range(2):
                    nc.vector.memset(v[b][:, :, :, :], 0.0).then_inc(zeros_set, 1)

                def scale_sums(u, seq):
                    dve.wait_ge(val_done.sem, val_done.count(u, N_HEAD * (seq + 1)))
                    dve.wait_ge(invT_ready.sem, invT_ready.count(u, seq + 1))
                    dve.wait_ge(z_done.sem, z_done.count(u, seq + 1, back=1))
                    nc.vector.tensor_tensor(oT[seq][:, :], ps_o[seq][:, 0:SEQ], invT[seq][:, :], ALU.mult).then_inc(oT_ready.sem, 1)

                def add_residual(u, b, seq):
                    if seq == 0:
                        dve.wait_ge(res_in[b].sem, res_in[b].count(u, b))
                        dve.wait_ge(stored[b].sem, stored[b].count(u, b, back=1))
                    dve.wait_ge(z_done.sem, z_done.count(u, seq + 1))
                    nc.vector.tensor_tensor(out[b][:, 2 * seq:2 * seq + 2, :], ps_out[0:HALF, 256:512].rearrange("p (t d) -> p t d", t=2),
                                            res[b][:, 2 * seq:2 * seq + 2, :], ALU.add).then_inc(out_ready.sem, 1)

                def body(n, par):
                    for x in range(HEADS):
                        if n[SOFT] is not None:
                            u, b = n[SOFT], par[SOFT]
                            dve.wait_ge(sc_done.sem, sc_done.count(u, x + 1))
                            if x == 0:
                                dve.wait_ge(ex_ready.sem, ex_ready.count(u, back=2))
                            nc.vector.tensor_reduce(least[b][:, x, :], ps_sc[x % 2][0:HALF, 0:N].rearrange("p (c n) -> p c n", c=2),
                                                    AX.X, ALU.min).then_inc(least_ready.sem, 1)
                        if n[VAL] is not None:
                            u, b = n[VAL], par[VAL]
                            dve.wait_ge(ex_turned.sem, ex_turned.count(u, x + 1))
                            dve.wait_ge(val_done.sem, val_done.count(u, x - 1))
                            nc.vector.tensor_copy(exT[x % 2][:, :, :].rearrange("p c n -> p (c n)"), ps_exT[x % 2][0:HALF, 0:N]).then_inc(exT_ready.sem, 1)
                            if x == 1:
                                dve.wait_ge(inv_wide_ready.sem, inv_wide_ready.count(u, back=1))
                                dve.wait_ge(ex_ready.sem, ex_ready.count(u))
                                nc.vector.reciprocal(inv[:, :, :].rearrange("p h c -> p (h c)"), total[b][:, :, :].rearrange("p h c -> p (h c)")).then_inc(inv_ready.sem, 1)
                            if x == 2:
                                dve.wait_ge(inv_ready.sem, inv_ready.count(u))
                                dve.wait_ge(inv_turned.sem, inv_turned.count(u, back=1))
                                by_tile = inv[:, :, :].rearrange("p (s h) c -> p s c h", s=2)
                                for seq in range(2):
                                    for c in range(2):
                                        last = nc.vector.tensor_copy(inv_wide[:, 2 * seq + c, :, :], wide(by_tile[:, seq, c, :], E_HEAD))
                                last.then_inc(inv_wide_ready.sem, 1)
                            if x == 9:
                                scale_sums(u, 0)
                            if x == 11:
                                add_residual(u, b, 0)
                        if x == 0 and n[FIN] is not None:
                            scale_sums(n[FIN], 1)
                        if x == 3 and n[FIN] is not None:
                            add_residual(n[FIN], par[FIN], 1)
                        if n[NORM] is not None and x % 4 == 0:
                            u, b, t = n[NORM], par[NORM], x // 4
                            if t == 0:
                                dve.wait_ge(x_in[b].sem, x_in[b].count(u, b))
                                dve.wait_ge(rstd2_ready.sem, rstd2_ready.count(u, back=2))
                            norm_moments(nc, dve, nm, u, b, t, dve_passed)
                    if n[NORM] is not None:
                        u, b = n[NORM], par[NORM]
                        dve.wait_ge(rstd2_ready.sem, rstd2_ready.count(u))
                        dve.wait_ge(turned.sem, turned.count(u, back=2))
                        for t in range(TILES):
                            last = nc.vector.tensor_scalar(yn[b][:, t, :], nm.y[b][:, t, :], var2[b][:, t:t + 1], None, ALU.mult)
                        last.then_inc(yn_ready.sem, 1)

                in_lanes(dve, UNITS, STAGES, body)

            @block.gpsimd
            def _(pool):
                for x in (nm.var_eps, nm.rstd_ready, nm.ready, square_ready, var2_ready, var2_eps, rstd2_ready, kh_ready):
                    x.opened(pool)
                nc.gpsimd.memset(eps[:, :], EPS)
                nc.gpsimd.memset(minus_half[:, :], -0.5).then_inc(pool_set, 1)
                pool.wait_ge(pool_set, 1)
                pool.wait_ge(weights_in, 16 * WEIGHTS)

                def body(n, par):
                    if n[PROJ] is not None:
                        u, b = n[PROJ], par[PROJ]
                        pool.wait_ge(qk_ready.sem, qk_ready.count(u))
                        pool.wait_ge(sc_done.sem, sc_done.count(u, back=2))
                        pool.sem_inc(pool_passed, 1)
                        for h in range(N_HEAD):
                            last = nc.gpsimd.tensor_scalar(kh[b][:, h, :], k[:, :], heads[:, h:h + 1], None, ALU.mult)
                        last.then_inc(kh_ready.sem, 1)
                    if n[NORM] is not None:
                        u, b = n[NORM], par[NORM]
                        pool.wait_ge(y_out[b].sem, y_out[b].count(u, b, back=1))
                        norm_rows(nc, pool, nm, u, b, eps, minus_half, pool_passed, yn_ready)
                        nc.gpsimd.tensor_tensor(var2[b][:, :], nm.rstd[b][:, :], nm.rstd[b][:, :], ALU.mult).then_inc(square_ready.sem, 1)
                        pool.wait_ge(square_ready.sem, square_ready.count(u))
                        nc.gpsimd.tensor_tensor(var2[b][:, :], var2[b][:, :], nm.mv[b][:, :, 1], ALU.mult).then_inc(var2_ready.sem, 1)
                        pool.wait_ge(var2_ready.sem, var2_ready.count(u))
                        nc.gpsimd.tensor_tensor(var2[b][:, :], var2[b][:, :], eps[0:HALF, :], ALU.add).then_inc(var2_eps.sem, 1)
                        pool.wait_ge(var2_eps.sem, var2_eps.count(u))
                        nc.gpsimd.tensor_tensor(var2[b][:, :], var2[b][:, :], minus_half[0:HALF, :], ALU.pow).then_inc(rstd2_ready.sem, 1)

                in_lanes(pool, UNITS, STAGES, body)

        pl.close()


def phase_router(nc, x_in_dram, ident, before, iota64, wr, g_col, b_col, slots, slot_dram, gate_dram):
    UNITS = BATCH // 2
    TILES = 4
    N = TILES * HALF
    E = EXP1
    FAR = 1 << 20
    LOAD, NORM, TURN, SOFT, GATE, PLACE, SCATTER = range(7)
    STAGES = 7
    with ExitStack() as ctx:
        pl = Place(nc, ctx, "rou")
        sb, sem = pl.sb, pl.sem
        idn = sb("ident", [P, P])
        bef = sb("before", [HALF, HALF])
        ones = sb("ones", [HALF, HALF])
        iota = sb("iota", [P, E])
        wr_sb = sb("wr", [D, E])
        gb = sb("gb", [P, 2])
        eps = sb("eps", [P, TILES])
        minus_half = sb("minus_half", [P, TILES])

        def two(name, shape, dt=F32):
            return [sb(f"{name}{b}", shape, dt) for b in range(2)]

        nm = Norm(pl, TILES, HALF)
        kept = two("kept", [HALF, TILES, D])
        going = two("going", [HALF, TILES, D])
        xT = two("xT", [D, N])
        best = two("best", [HALF, TILES])
        ex = two("ex", [HALF, TILES, E])
        total = two("total", [HALF, TILES])
        prob = two("prob", [HALF, TILES, E])
        top = two("top", [HALF, TILES, 8])
        at = two("at", [HALF, TILES, 8], U32)
        atf = two("atf", [HALF, 2, TILES])
        hot = two("hot", [HALF, 2, TILES, E])
        both = two("both", [HALF, TILES, E])
        count = two("count", [HALF, TILES, E])
        share = two("share", [HALF, TILES])
        gate = two("gate", [HALF, 2, TILES])
        mine = two("mine", [HALF, 2, TILES, E])
        pos = two("pos", [HALF, 2, TILES])
        late = two("late", [HALF, 2, TILES])
        base = two("base", [HALF, 2, TILES])
        near = two("near", [HALF, 2, TILES])
        row = two("row", [HALF, 2, TILES])
        row_u = two("row_u", [HALF, 2, TILES], U32)
        read_f = two("read_f", [HALF, 2, TILES])
        read_u = two("read_u", [HALF, 2, TILES], U32)
        gated = two("gated", [HALF, 2, TILES])

        ps_turn, ps_logit, ps_pos = pl.banks("x", 3)
        logit = ps_logit[0:HALF, 0:TILES * E].rearrange("p (t e) -> p t e", e=E)
        place = ps_pos[0:HALF, 0:TILES * E].rearrange("p (t e) -> p t e", e=E)

        weights_in = sem("weights_in")
        WEIGHTS = 6
        constants_set = sem("constants_set")
        counts_set = sem("counts_set")
        dve_passed, pool_passed = sem("dve_passed"), sem("pool_passed")
        x_in = [Landed(sem(f"x_in{b}"), 2) for b in range(2)]
        scattered = [Landed(sem(f"scattered{b}"), 2 * TILES, ahead=0) for b in range(2)]
        scatter_over = Signal(sem("scatter_over"))
        noted = [Landed(sem(f"noted{b}"), 2) for b in range(2)]
        turned = Signal(sem("turned"))
        xT_ready = Signal(sem("xT_ready"))
        kept_ready = Signal(sem("kept_ready"))
        going_ready = Signal(sem("going_ready"))
        logit_done = Signal(sem("logit_done"))
        best_ready = Signal(sem("best_ready"))
        shifted = Signal(sem("shifted"))
        ex_ready = Signal(sem("ex_ready"))
        total_ready = Signal(sem("total_ready"))
        inv_ready = Signal(sem("inv_ready"))
        prob_ready = Signal(sem("prob_ready"))
        top_ready = Signal(sem("top_ready"))
        at_ready = Signal(sem("at_ready"))
        atf_ready = Signal(sem("atf_ready"))
        hot_ready = Signal(sem("hot_ready"))
        both_ready = Signal(sem("both_ready"))
        share_ready = Signal(sem("share_ready"))
        share_inv = Signal(sem("share_inv"))
        gate_ready = Signal(sem("gate_ready"))
        count_ready = Signal(sem("count_ready"), TILES)
        place_done = Signal(sem("place_done"))
        mine_ready = Signal(sem("mine_ready"))
        pos_ready = Signal(sem("pos_ready"))
        late_ready = Signal(sem("late_ready"))
        row_ready = Signal(sem("row_ready"))
        row_u_ready = Signal(sem("row_u_ready"))
        notes_ready = Signal(sem("notes_ready"))

        with nc.Block() as block:

            @block.sync
            def _(sp):
                for dst, src in ((idn[:, :], ident), (bef[:, :], before), (iota[:, :], iota64), (wr_sb[:, :], wr),
                                 (gb[:, 0:1], g_col), (gb[:, 1:2], b_col)):
                    sp.dma_start(dst, src).then_inc(weights_in, 16)
                for b in range(2):
                    x_in[b].opened(sp)
                    noted[b].opened(sp)
                scatter_over.opened(sp)

                def body(n, par):
                    if n[LOAD] is not None:
                        u, b = n[LOAD], par[LOAD]
                        sp.wait_ge(nm.ready.sem, nm.ready.count(u, back=2))
                        load_rows(sp, nm.x[b], x_in_dram, u, x_in[b])
                    if n[SCATTER] is not None:
                        u, b = n[SCATTER], par[SCATTER]
                        sp.wait_ge(scattered[b].sem, scattered[b].count(u, b))
                        sp.sem_inc(scatter_over.sem, 1)
                    if n[PLACE] is not None:
                        u, b = n[PLACE], par[PLACE]
                        sp.wait_ge(notes_ready.sem, notes_ready.count(u))
                        sp.dma_start(slot_dram[bass.ds(u, 1), :, :].rearrange("u p x -> (u p) x"),
                                     read_u[b][:, :, :].rearrange("p k t -> p (k t)")).then_inc(noted[b].sem, 16)
                        sp.dma_start(gate_dram[bass.ds(u, 1), :, :].rearrange("u p x -> (u p) x"),
                                     gated[b][:, :, :].rearrange("p k t -> p (k t)")).then_inc(noted[b].sem, 16)

                in_lanes(sp, UNITS, STAGES, body)
                for b in range(2):
                    sp.wait_ge(noted[b].sem, noted[b].final(UNITS))
                    sp.wait_ge(scattered[b].sem, scattered[b].final(UNITS))

            @block.tensor
            def _(pe):
                for x in (turned, logit_done, place_done):
                    x.opened(pe)
                pe.wait_ge(weights_in, 16 * WEIGHTS)
                pe.wait_ge(counts_set, 3)

                def body(n, par):
                    if n[PLACE] is not None:
                        u, b = n[PLACE], par[PLACE]
                        pe.wait_ge(count_ready.sem, count_ready.count(u))
                        pe.wait_ge(mine_ready.sem, mine_ready.count(u, back=1))
                        for t in range(TILES):
                            nc.tensor.matmul(place[:, t, :], bef[:, :], both[b][:, t, :], start=True, stop=False)
                            last = nc.tensor.matmul(place[:, t, :], ones[:, :], count[b][:, t, :], start=False, stop=True)
                        last.then_inc(place_done.sem, 1)
                    if n[SOFT] is not None:
                        u, b = n[SOFT], par[SOFT]
                        pe.wait_ge(xT_ready.sem, xT_ready.count(u))
                        pe.wait_ge(shifted.sem, shifted.count(u, back=1))
                        for t in range(TILES):
                            last = nc.tensor.matmul(logit[:, t, :], xT[b][:, t * HALF:(t + 1) * HALF], wr_sb[:, :], start=True, stop=True)
                        last.then_inc(logit_done.sem, 1)
                    if n[TURN] is not None:
                        u, b = n[TURN], par[TURN]
                        pe.wait_ge(nm.ready.sem, nm.ready.count(u))
                        pe.wait_ge(xT_ready.sem, xT_ready.count(u, back=1))
                        for t in range(TILES):
                            last = nc.tensor.transpose(ps_turn[:, t * HALF:(t + 1) * HALF], nm.y[b][:, t, :], idn[0:HALF, 0:HALF])
                        last.then_inc(turned.sem, 1)

                in_lanes(pe, UNITS, STAGES, body)

            @block.scalar
            def _(act):
                for x in (xT_ready, kept_ready, going_ready, ex_ready):
                    x.opened(act)
                act.wait_ge(weights_in, 16 * WEIGHTS)

                def body(n, par):
                    if n[PLACE] is not None:
                        u, b = n[PLACE], par[PLACE]
                        act.wait_ge(kept_ready.sem, kept_ready.count(u))
                        act.wait_ge(scatter_over.sem, scatter_over.count(u, back=2))
                        nc.scalar.copy(going[b][:, :, :], kept[b][:, :, :]).then_inc(going_ready.sem, 1)
                    if n[SOFT] is not None:
                        u, b = n[SOFT], par[SOFT]
                        act.wait_ge(going_ready.sem, going_ready.count(u, back=2))
                        act.wait_ge(nm.ready.sem, nm.ready.count(u))
                        nc.scalar.copy(kept[b][:, :, :], nm.y[b][:, :, :]).then_inc(kept_ready.sem, 1)
                    if n[SOFT] is not None:
                        u, b = n[SOFT], par[SOFT]
                        act.wait_ge(shifted.sem, shifted.count(u))
                        nc.scalar.activation(ex[b][:, :, :], ex[b][:, :, :], ACT.Exp).then_inc(ex_ready.sem, 1)
                    if n[TURN] is not None:
                        u, b = n[TURN], par[TURN]
                        act.wait_ge(turned.sem, turned.count(u))
                        act.wait_ge(logit_done.sem, logit_done.count(u, back=2))
                        nc.scalar.activation(xT[b][:, :], ps_turn[:, 0:N], ACT.Identity, bias=gb[:, 1:2], scale=gb[:, 0:1]).then_inc(xT_ready.sem, 1)

                in_lanes(act, UNITS, STAGES, body)

            @block.vector
            def _(dve):
                for x in (nm.stats, nm.moments, best_ready, shifted, total_ready, inv_ready, prob_ready, top_ready, at_ready,
                          atf_ready, hot_ready, both_ready, share_ready, share_inv, gate_ready, count_ready, mine_ready,
                          pos_ready, late_ready, row_ready, row_u_ready, notes_ready):
                    x.opened(dve)
                nc.vector.memset(ones[:, :], 1.0).then_inc(counts_set, 1)
                nc.vector.memset(both[1][:, :, :], 0.0).then_inc(counts_set, 1)
                nc.vector.memset(count[1][:, :, :], 0.0).then_inc(counts_set, 1)
                dve.wait_ge(counts_set, 3)
                dve.wait_ge(weights_in, 16 * WEIGHTS)

                def body(n, par):
                    if n[PLACE] is not None:
                        u, b = n[PLACE], par[PLACE]
                        dve.wait_ge(both_ready.sem, both_ready.count(u))
                        dve.wait_ge(place_done.sem, place_done.count(u, back=2))
                        for t in range(TILES):
                            if t > 0:
                                dve.wait_ge(count_ready.sem, count_ready.count(u, t))
                                nc.vector.tensor_tensor(count[b][:, t, :], count[b][:, t - 1, :], both[b][:, t - 1, :], ALU.add).then_inc(count_ready.sem, 1)
                            else:
                                dve.wait_ge(count_ready.sem, count_ready.count(u, back=1))
                                nc.vector.tensor_tensor(count[b][:, 0, :], count[1 - b][:, TILES - 1, :], both[1 - b][:, TILES - 1, :],
                                                        ALU.add).then_inc(count_ready.sem, 1)
                    if n[NORM] is not None:
                        u, b = n[NORM], par[NORM]
                        dve.wait_ge(x_in[b].sem, x_in[b].count(u, b))
                        dve.wait_ge(nm.ready.sem, nm.ready.count(u, back=2))
                        for t in range(TILES):
                            norm_moments(nc, dve, nm, u, b, t, dve_passed)
                    if n[SOFT] is not None:
                        u, b = n[SOFT], par[SOFT]
                        dve.wait_ge(logit_done.sem, logit_done.count(u))
                        nc.vector.tensor_reduce(best[b][:, :], logit, AX.X, ALU.max).then_inc(best_ready.sem, 1)
                        dve.wait_ge(best_ready.sem, best_ready.count(u))
                        dve.wait_ge(prob_ready.sem, prob_ready.count(u, back=2))
                        nc.vector.tensor_tensor(ex[b][:, :, :], logit, wide(best[b][:, :], E), ALU.subtract).then_inc(shifted.sem, 1)
                    if n[GATE] is not None:
                        u, b = n[GATE], par[GATE]
                        dve.wait_ge(ex_ready.sem, ex_ready.count(u))
                        nc.vector.tensor_reduce(total[b][:, :], ex[b][:, :, :], AX.X, ALU.add).then_inc(total_ready.sem, 1)
                        dve.wait_ge(total_ready.sem, total_ready.count(u))
                        nc.vector.reciprocal(total[b][:, :], total[b][:, :]).then_inc(inv_ready.sem, 1)
                        dve.wait_ge(inv_ready.sem, inv_ready.count(u))
                        nc.vector.tensor_tensor(prob[b][:, :, :], ex[b][:, :, :], wide(total[b][:, :], E), ALU.mult).then_inc(prob_ready.sem, 1)
                        dve.wait_ge(prob_ready.sem, prob_ready.count(u))
                        dve.sem_inc(dve_passed, 1)
                        for t in range(TILES):
                            last = nc.vector.max(top[b][:, t, :], prob[b][:, t, :])
                        last.then_inc(top_ready.sem, 1)
                        dve.wait_ge(top_ready.sem, top_ready.count(u))
                        nc.vector.tensor_tensor(share[b][:, :], top[b][:, :, 0], top[b][:, :, 1], ALU.add).then_inc(share_ready.sem, 1)
                        for t in range(TILES):
                            last = nc.vector.max_index(at[b][:, t, :], top[b][:, t, :], prob[b][:, t, :])
                        last.then_inc(at_ready.sem, 1)
                        dve.wait_ge(share_ready.sem, share_ready.count(u))
                        nc.vector.reciprocal(share[b][:, :], share[b][:, :]).then_inc(share_inv.sem, 1)
                        dve.wait_ge(at_ready.sem, at_ready.count(u))
                        nc.vector.tensor_copy(atf[b][:, :, :], at[b][:, :, 0:2].rearrange("p t k -> p k t")).then_inc(atf_ready.sem, 1)
                        dve.wait_ge(share_inv.sem, share_inv.count(u))
                        nc.vector.tensor_tensor(gate[b][:, :, :], top[b][:, :, 0:2].rearrange("p t k -> p k t"), over(share[b][:, :], 2),
                                                ALU.mult).then_inc(gate_ready.sem, 1)
                        dve.wait_ge(atf_ready.sem, atf_ready.count(u))
                        for k in range(2):
                            last = nc.vector.tensor_tensor(hot[b][:, k, :, :], over(iota[0:HALF, :], TILES), wide(atf[b][:, k, :], E), ALU.is_equal)
                        last.then_inc(hot_ready.sem, 1)
                        dve.wait_ge(hot_ready.sem, hot_ready.count(u))
                        nc.vector.tensor_tensor(both[b][:, :, :], hot[b][:, 0, :, :], hot[b][:, 1, :, :], ALU.add).then_inc(both_ready.sem, 1)
                    if n[PLACE] is not None:
                        u, b = n[PLACE], par[PLACE]
                        dve.wait_ge(place_done.sem, place_done.count(u))
                        for k in range(2):
                            last = nc.vector.tensor_tensor(mine[b][:, k, :, :], hot[b][:, k, :, :], place, ALU.mult)
                        last.then_inc(mine_ready.sem, 1)
                        dve.wait_ge(mine_ready.sem, mine_ready.count(u))
                        nc.vector.tensor_reduce(pos[b][:, :, :], mine[b][:, :, :, :], AX.X, ALU.add).then_inc(pos_ready.sem, 1)
                        dve.wait_ge(pos_ready.sem, pos_ready.count(u))
                        dve.wait_ge(noted[b].sem, noted[b].count(u, b, back=1))
                        nc.vector.tensor_scalar(late[b][:, :, :], pos[b][:, :, :], float(CAP), float(FAR), ALU.is_ge, ALU.mult)
                        nc.vector.tensor_scalar(base[b][:, :, :], atf[b][:, :, :], float(CAP), None, ALU.mult)
                        nc.vector.tensor_scalar(near[b][:, :, :], pos[b][:, :, :], float(CAP - 1), None, ALU.min)
                        nc.vector.scalar_tensor_tensor(gated[b][:, :, :], pos[b][:, :, :], float(CAP), gate[b][:, :, :], ALU.is_lt, ALU.mult).then_inc(late_ready.sem, 1)
                        dve.wait_ge(late_ready.sem, late_ready.count(u))
                        nc.vector.tensor_tensor(row[b][:, :, :], base[b][:, :, :], pos[b][:, :, :], ALU.add)
                        nc.vector.tensor_tensor(read_f[b][:, :, :], base[b][:, :, :], near[b][:, :, :], ALU.add).then_inc(row_ready.sem, 1)
                        dve.wait_ge(row_ready.sem, row_ready.count(u))
                        dve.wait_ge(scatter_over.sem, scatter_over.count(u, back=2))
                        nc.vector.tensor_tensor(row_u[b][:, :, :], row[b][:, :, :], late[b][:, :, :], ALU.add).then_inc(row_u_ready.sem, 1)
                        nc.vector.tensor_copy(read_u[b][:, :, :], read_f[b][:, :, :]).then_inc(notes_ready.sem, 1)

                in_lanes(dve, UNITS, STAGES, body)

            @block.gpsimd
            def _(pool):
                for x in (nm.var_eps, nm.rstd_ready, nm.ready):
                    x.opened(pool)
                nc.gpsimd.memset(eps[:, :], EPS)
                nc.gpsimd.memset(minus_half[:, :], -0.5).then_inc(constants_set, 1)
                pool.wait_ge(constants_set, 1)

                def body(n, par):
                    if n[SCATTER] is not None:
                        u, b = n[SCATTER], par[SCATTER]
                        pool.wait_ge(going_ready.sem, going_ready.count(u))
                        pool.wait_ge(row_u_ready.sem, row_u_ready.count(u))
                        pool.sem_inc(pool_passed, 1)
                        for k in range(2):
                            for t in range(TILES):
                                nc.gpsimd.indirect_dma_start(
                                    out=slots, out_offset=bass.IndirectOffsetOnAxis(ap=row_u[b][:, k, t:t + 1], axis=0),
                                    in_=going[b][:, t, :], in_offset=None, bounds_check=EXP1 * CAP - 1,
                                    oob_is_err=False).then_inc(scattered[b].sem, 16)
                    if n[NORM] is not None:
                        u, b = n[NORM], par[NORM]
                        pool.wait_ge(kept_ready.sem, kept_ready.count(u, back=2))
                        norm_rows(nc, pool, nm, u, b, eps, minus_half, pool_passed, turned)

                in_lanes(pool, UNITS, STAGES, body)

        pl.close()


def phase_experts64(nc, slots, ident, g_col, b_col, w1, b1, w2, b2, y_dram):
    TILES = CAP // HALF
    N = CAP // 2
    CH = FF1 // P
    LOAD, TURN, HID, OUT = range(4)
    STAGES = 4
    with ExitStack() as ctx:
        pl = Place(nc, ctx, "exp")
        sb, sem = pl.sb, pl.sem
        idn = sb("ident", [P, P])
        gb = sb("gb", [P, 2])

        def two(name, shape, dt=F32):
            return [sb(f"{name}{b}", shape, dt) for b in range(2)]

        x = two("x", [HALF, TILES, D])
        w1_sb = two("w1", [D, FF1])
        b1_sb = two("b1", [P, CH])
        w2_sb = two("w2", [P, CH, D])
        b2_sb = two("b2", [P, D])
        xT = two("xT", [D, CAP])
        hid = two("hid", [P, CH, CAP])
        y = two("y", [HALF, TILES, D])
        ps_turn = pl.banks("turn", 2)
        ps_hid = pl.banks("hid", 2)
        ps_out = pl.banks("out", 2)

        weights_in = sem("weights_in")
        pe_passed, = (sem("pe_passed"),)
        x_in = [Landed(sem(f"x_in{b}"), 1) for b in range(2)]
        w1_in = [Landed(sem(f"w1_in{b}"), 2) for b in range(2)]
        w2_in = [Landed(sem(f"w2_in{b}"), 2) for b in range(2)]
        stored = [Landed(sem(f"stored{b}"), 1) for b in range(2)]
        turned = Signal(sem("turned"), 2)
        xT_ready = Signal(sem("xT_ready"), 2)
        hid_done = Signal(sem("hid_done"), 2 * CH)
        hid_ready = Signal(sem("hid_ready"), 2 * CH)
        out_done = Signal(sem("out_done"), TILES)
        y_ready = Signal(sem("y_ready"), TILES)

        with nc.Block() as block:

            @block.sync
            def _(sp):
                for dst, src in ((idn[:, :], ident), (gb[:, 0:1], g_col), (gb[:, 1:2], b_col)):
                    sp.dma_start(dst, src).then_inc(weights_in, 16)
                for s in x_in + w1_in + w2_in + stored:
                    s.opened(sp)

                def body(n, par):
                    if n[LOAD] is not None:
                        u, b = n[LOAD], par[LOAD]
                        sp.wait_ge(turned.sem, turned.count(u, back=2))
                        sp.dma_start(x[b][:, :, :], slots[bass.ds(u * CAP, CAP), :].rearrange("(p t) d -> p t d", t=TILES)).then_inc(x_in[b].sem, 16)
                    if n[TURN] is not None:
                        u, b = n[TURN], par[TURN]
                        sp.wait_ge(hid_ready.sem, hid_ready.count(u, back=2))
                        sp.dma_start(w1_sb[b][:, :], w1[bass.ds(u, 1), :, :].rearrange("e d f -> (e d) f")).then_inc(w1_in[b].sem, 16)
                        sp.dma_start(b1_sb[b][:, :], b1[bass.ds(u, 1), :, :].rearrange("e p c -> (e p) c")).then_inc(w1_in[b].sem, 16)
                    if n[HID] is not None:
                        u, b = n[HID], par[HID]
                        sp.wait_ge(y_ready.sem, y_ready.count(u, back=2))
                        sp.dma_start(w2_sb[b][:, :, :], w2[bass.ds(u, 1), :, :].rearrange("e (c p) d -> p (e c) d", p=P)).then_inc(w2_in[b].sem, 16)
                        sp.dma_start(b2_sb[b][:, :], b2[bass.ds(u, 1), :].to_broadcast([P, D])).then_inc(w2_in[b].sem, 16)
                    if n[OUT] is not None:
                        u, b = n[OUT], par[OUT]
                        sp.wait_ge(y_ready.sem, y_ready.count(u))
                        sp.dma_start(y_dram[bass.ds(u * CAP, CAP), :].rearrange("(p t) d -> p t d", t=TILES), y[b][:, :, :]).then_inc(stored[b].sem, 16)

                in_lanes(sp, EXP1, STAGES, body)
                for b in range(2):
                    sp.wait_ge(stored[b].sem, stored[b].final(EXP1))

            @block.tensor
            def _(pe):
                for s in (turned, hid_done, out_done):
                    s.opened(pe)
                pe.wait_ge(weights_in, 48)

                def body(n, par):
                    for r in range(TILES):
                        if n[HID] is not None:
                            u, b = n[HID], par[HID]
                            half, c = r // CH, r % CH
                            if r == 0:
                                pe.wait_ge(w1_in[b].sem, w1_in[b].count(u, b))
                                pe.wait_ge(xT_ready.sem, xT_ready.count(u))
                            pe.wait_ge(hid_ready.sem, hid_ready.count(u, r - 1))
                            nc.tensor.matmul(ps_hid[r % 2][:, 0:N], w1_sb[b][:, c * P:(c + 1) * P], xT[b][:, half * N:(half + 1) * N],
                                             start=True, stop=True).then_inc(hid_done.sem, 1)
                        if n[OUT] is not None:
                            u, b = n[OUT], par[OUT]
                            if r == 0:
                                pe.wait_ge(w2_in[b].sem, w2_in[b].count(u, b))
                                pe.wait_ge(hid_ready.sem, hid_ready.count(u))
                            pe.wait_ge(y_ready.sem, y_ready.count(u, r - 1))
                            for c in range(CH):
                                last = nc.tensor.matmul(ps_out[r % 2][0:HALF, 0:D], hid[b][:, c, r * HALF:(r + 1) * HALF], w2_sb[b][:, c, :],
                                                        start=c == 0, stop=c == CH - 1)
                            last.then_inc(out_done.sem, 1)
                    if n[TURN] is not None:
                        u, b = n[TURN], par[TURN]
                        pe.wait_ge(x_in[b].sem, x_in[b].count(u, b))
                        for half in range(2):
                            pe.wait_ge(xT_ready.sem, xT_ready.count(u, half + 1, back=1))
                            for t in range(TILES // 2):
                                last = nc.tensor.transpose(ps_turn[half][:, t * HALF:(t + 1) * HALF], x[b][:, half * TILES // 2 + t, :], idn[0:HALF, 0:HALF])
                            last.then_inc(turned.sem, 1)

                in_lanes(pe, EXP1, STAGES, body)

            @block.scalar
            def _(act):
                for s in (xT_ready, hid_ready):
                    s.opened(act)
                act.wait_ge(weights_in, 48)

                def body(n, par):
                    for r in range(TILES):
                        if n[HID] is not None:
                            u, b = n[HID], par[HID]
                            half, c = r // CH, r % CH
                            if r == 0:
                                act.wait_ge(w1_in[b].sem, w1_in[b].count(u, b))
                                act.wait_ge(out_done.sem, out_done.count(u, back=2))
                            act.wait_ge(hid_done.sem, hid_done.count(u, r + 1))
                            nc.scalar.activation(hid[b][:, c, half * N:(half + 1) * N], ps_hid[r % 2][:, 0:N], ACT.Gelu_apprx_tanh,
                                                 bias=b1_sb[b][:, c:c + 1]).then_inc(hid_ready.sem, 1)
                    if n[TURN] is not None:
                        u, b = n[TURN], par[TURN]
                        act.wait_ge(hid_done.sem, hid_done.count(u, back=2))
                        for half in range(2):
                            act.wait_ge(turned.sem, turned.count(u, half + 1))
                            nc.scalar.activation(xT[b][:, half * N:(half + 1) * N], ps_turn[half][:, 0:N], ACT.Identity,
                                                 bias=gb[:, 1:2], scale=gb[:, 0:1]).then_inc(xT_ready.sem, 1)

                in_lanes(act, EXP1, STAGES, body)

            @block.vector
            def _(dve):
                y_ready.opened(dve)

                def body(n, par):
                    for r in range(TILES):
                        if n[OUT] is not None:
                            u, b = n[OUT], par[OUT]
                            if r == 0:
                                dve.wait_ge(w2_in[b].sem, w2_in[b].count(u, b))
                                dve.wait_ge(stored[b].sem, stored[b].count(u, b, back=1))
                            dve.wait_ge(out_done.sem, out_done.count(u, r + 1))
                            nc.vector.tensor_tensor(y[b][:, r, :], ps_out[r % 2][0:HALF, 0:D], b2_sb[b][0:HALF, :], ALU.add).then_inc(y_ready.sem, 1)

                in_lanes(dve, EXP1, STAGES, body)

        pl.close()


def phase_combine(nc, h_dram, x_dram, y_dram, slot_dram, gate_dram, out_dram):
    UNITS = BATCH // 2
    TILES = 4
    LOAD, GATHER, SUM = range(3)
    STAGES = 3
    with ExitStack() as ctx:
        pl = Place(nc, ctx, "com")
        sb, sem = pl.sb, pl.sem

        def two(name, shape, dt=F32):
            return [sb(f"{name}{b}", shape, dt) for b in range(2)]

        slot = two("slot", [HALF, 2 * TILES], U32)
        gate = two("gate", [HALF, 2 * TILES])
        h = two("h", [HALF, TILES, D])
        x = two("x", [HALF, TILES, D])
        y = two("y", [HALF, 2, TILES, D])
        acc = two("acc", [HALF, TILES, D])
        pool_passed = sem("pool_passed")
        slot_in = [Landed(sem(f"slot_in{b}"), 2) for b in range(2)]
        rows_in = [Landed(sem(f"rows_in{b}"), 4) for b in range(2)]
        gathered = [Landed(sem(f"gathered{b}"), 2 * TILES, ahead=0) for b in range(2)]
        stored = [Landed(sem(f"stored{b}"), 2) for b in range(2)]
        base_ready = Signal(sem("base_ready"))
        acc_ready = Signal(sem("acc_ready"), 2)

        with nc.Block() as block:

            @block.sync
            def _(sp):
                for s in slot_in + rows_in + stored:
                    s.opened(sp)

                def body(n, par):
                    if n[LOAD] is not None:
                        u, b = n[LOAD], par[LOAD]
                        sp.wait_ge(acc_ready.sem, acc_ready.count(u, back=2))
                        sp.dma_start(slot[b][:, :], slot_dram[bass.ds(u, 1), :, :].rearrange("u p x -> (u p) x")).then_inc(slot_in[b].sem, 16)
                        sp.dma_start(gate[b][:, :], gate_dram[bass.ds(u, 1), :, :].rearrange("u p x -> (u p) x")).then_inc(slot_in[b].sem, 16)
                        load_rows(sp, h[b], h_dram, u, rows_in[b])
                        load_rows(sp, x[b], x_dram, u, rows_in[b])
                    if n[SUM] is not None:
                        u, b = n[SUM], par[SUM]
                        sp.wait_ge(acc_ready.sem, acc_ready.count(u))
                        store_rows(sp, out_dram, acc[b], u, stored[b])

                in_lanes(sp, UNITS, STAGES, body)
                for b in range(2):
                    sp.wait_ge(stored[b].sem, stored[b].final(UNITS))

            @block.gpsimd
            def _(pool):
                def body(n, par):
                    if n[GATHER] is not None:
                        u, b = n[GATHER], par[GATHER]
                        pool.wait_ge(acc_ready.sem, acc_ready.count(u, back=2))
                        pool.wait_ge(slot_in[b].sem, slot_in[b].count(u, b))
                        pool.sem_inc(pool_passed, 1)
                        for k in range(2):
                            for t in range(TILES):
                                nc.gpsimd.indirect_dma_start(
                                    out=y[b][:, k, t, :], out_offset=None, in_=y_dram,
                                    in_offset=bass.IndirectOffsetOnAxis(ap=slot[b][:, k * TILES + t:k * TILES + t + 1], axis=0),
                                    ).then_inc(gathered[b].sem, 16)

                in_lanes(pool, UNITS, STAGES, body)

            @block.vector
            def _(dve):
                for s in (base_ready, acc_ready):
                    s.opened(dve)

                def body(n, par):
                    if n[SUM] is not None:
                        u, b = n[SUM], par[SUM]
                        dve.wait_ge(rows_in[b].sem, rows_in[b].count(u, b))
                        dve.wait_ge(stored[b].sem, stored[b].count(u, b, back=1))
                        nc.vector.tensor_tensor(acc[b][:, :, :], h[b][:, :, :], x[b][:, :, :], ALU.add).then_inc(base_ready.sem, 1)
                        dve.wait_ge(base_ready.sem, base_ready.count(u))
                        dve.wait_ge(gathered[b].sem, gathered[b].count(u, b))
                        for k in range(2):
                            if k == 1:
                                dve.wait_ge(acc_ready.sem, acc_ready.count(u, 1))
                            for t in range(TILES):
                                last = nc.vector.scalar_tensor_tensor(acc[b][:, t, :], y[b][:, k, t, :], gate[b][:, k * TILES + t:k * TILES + t + 1],
                                                                      acc[b][:, t, :], ALU.mult, ALU.add)
                            last.then_inc(acc_ready.sem, 1)

                in_lanes(dve, UNITS, STAGES, body)

        pl.close()


def audio_tower(nc, a, out):
    def scratch(name, shape, dt=F32):
        return nc.dram_tensor(name, shape, dt, kind="Internal").ap()

    h0 = scratch("h0", [POS_PAD, BATCH, D])
    h1 = scratch("h1", [BATCH, POS_PAD, D])
    h2 = scratch("h2", [BATCH, SEQ, D])
    h3 = scratch("h3", [BATCH, SEQ, D])
    y4 = scratch("y4", [BATCH, SEQ, D])
    x5 = scratch("x5", [BATCH, SEQ, D])
    slots = scratch("slots", [EXP1 * CAP, D])
    y_slots = scratch("y_slots", [EXP1 * CAP, D])
    slot_of = scratch("slot_of", [BATCH // 2, HALF, 8], U32)
    gate_of = scratch("gate_of", [BATCH // 2, HALF, 8])

    phase_token_mixer(nc, a["x"], a["ident"], a["tok_w_compress"], a["tok_w_main"], a["tok_w_expand"], a["tok_w_ff1"],
                      a["tok_w_ff2"], a["tok_b_compress"], a["tok_b_main"], a["tok_b_ff1"], a["tok_g1_col"],
                      a["tok_b1_col"], a["tok_g2_col"], a["tok_b2_col"], a["tok_b_expand"], a["tok_g1_row"],
                      a["tok_b1_row"], a["tok_b_ff2"], h0, slots)
    phase_batch_attention(nc, h0, a["ident"], a["bat_mask"], a["bat_wq"], a["bat_wk"], a["bat_wv"], a["bat_wo"], h1)
    phase_experts8(nc, h1, a["ident"], a["mix_iota"], a["mix_wg"], a["mix_w1"], a["mix_b1"], a["mix_w2"], a["mix_b2"],
                   a["mix_gamma"], a["mix_beta"], h2)
    phase_linear_attention(nc, h2, a["ident"], a["lin_mask"], a["lin_blocks"], a["head_mask"], a["lin_index"], a["lin_wq"], a["lin_wk"],
                           a["lin_wv"], a["lin_bqk"], a["lin_bv"], a["lin_decay"], a["lin_wo"], a["lin_bo"], a["lin_g"],
                           a["lin_b"], h3)
    phase_attention(nc, h3, a["ident"], a["head_mask"], a["att_wq"], a["att_wk"], a["att_wv"], a["att_wo"],
                    a["att_g"], a["att_b"], y4, x5)
    phase_router(nc, x5, a["ident"], a["rou_before"], a["rou_iota"], a["rou_wr"], a["exp_g"], a["exp_b"], slots,
                 slot_of, gate_of)
    phase_experts64(nc, slots, a["ident"], a["exp_g"], a["exp_b"], a["exp_w1"], a["exp_b1"], a["exp_w2"], a["exp_b2"],
                    y_slots)
    phase_combine(nc, h3, x5, y_slots, slot_of, gate_of, out)


def layouts(inputs, np):
    tok = {n[7:]: w for n, w in inputs.items() if n.startswith("L0_tok_")}
    bat = {n[8:]: w for n, w in inputs.items() if n.startswith("L0_attn_")}
    mix = {n[7:]: w for n, w in inputs.items() if n.startswith("L0_ffn_")}
    lin = {n[8:]: w for n, w in inputs.items() if n.startswith("L1_attn_")}
    ffn = {n[7:]: w for n, w in inputs.items() if n.startswith("L1_ffn_")}

    f32 = np.float32
    at = np.arange(HALF)
    upto = (at[None, :] >= at[:, None]).astype(f32)
    width = N_HEAD * D_HEAD
    return {
        "x": inputs["x"],
        "ident": np.eye(P, dtype=f32),
        "head_mask": np.repeat(np.eye(N_HEAD, dtype=f32), E_HEAD, axis=0),
        "tok_w_compress": tok["w_compress"][:, :, 0].T, "tok_w_main": tok["w_main"].transpose(1, 2, 0),
        "tok_w_expand": tok["w_expand"][:, :, 0].T, "tok_w_ff1": tok["w_ff1"].T, "tok_w_ff2": tok["w_ff2"].T,
        "tok_b_compress": tok["b_compress"][:, None], "tok_b_main": tok["b_main"][:, None],
        "tok_b_ff1": tok["b_ff1"][:, None], "tok_g1_col": tok["g_conv_norm"][:, None],
        "tok_b1_col": tok["b_conv_norm"][:, None], "tok_g2_col": tok["g_ff_norm"][:, None],
        "tok_b2_col": tok["b_ff_norm"][:, None], "tok_b_expand": tok["b_expand"], "tok_g1_row": tok["g_conv_norm"],
        "tok_b1_row": tok["b_conv_norm"], "tok_b_ff2": tok["b_ff2"],
        "bat_mask": np.where(np.arange(4 * P)[None, :] % BATCH > np.arange(P)[:, None] % BATCH, f32(-1e6), f32(0)),
        "bat_wq": bat["Wq"].T, "bat_wk": bat["Wkv"][:width].T, "bat_wv": bat["Wkv"][width:].T, "bat_wo": bat["Wo"].T,
        "mix_iota": np.tile(np.arange(EXP0, dtype=f32), (P, 1)), "mix_wg": mix["Wg"], "mix_w1": mix["W1"],
        "mix_b1": mix["b1"].T, "mix_w2": mix["W2"], "mix_b2": mix["b2"].reshape(-1),
        "mix_gamma": mix["gamma"].reshape(-1), "mix_beta": mix["beta"],
        "lin_mask": np.concatenate([upto, np.ones((HALF, HALF), f32)], 1),
        "lin_blocks": np.kron(np.eye(N_HEAD, dtype=f32), np.ones((E_HEAD, E_HEAD), f32)),
        "lin_index": np.tile(np.arange(P, dtype=f32), (P, 1)),
        "lin_wq": lin["W_qkv"][:, :D], "lin_wk": lin["W_qkv"][:, D:2 * D], "lin_wv": lin["W_qkv"][:, 2 * D:],
        "lin_bqk": lin["b_qkv"][:2 * D].reshape(2, D).T, "lin_bv": lin["b_qkv"][2 * D:],
        "lin_decay": np.repeat(lin["decay_logits"], E_HEAD)[:, None], "lin_wo": lin["W_out"],
        "lin_bo": lin["b_out"], "lin_g": lin["ln_g"], "lin_b": lin["ln_b"],
        "att_wq": ffn["wq"], "att_wk": ffn["wk"],
        "att_wv": ffn["wv"], "att_wo": ffn["wo"], "att_g": ffn["ln1_g"][:, None], "att_b": ffn["ln1_b"][:, None],
        "rou_before": (at[:, None] < at[None, :]).astype(f32), "rou_iota": np.tile(np.arange(EXP1, dtype=f32), (P, 1)),
        "rou_wr": ffn["wr"], "exp_g": ffn["ln2_g"][:, None], "exp_b": ffn["ln2_b"][:, None], "exp_w1": ffn["w1"],
        "exp_b1": ffn["b1"].reshape(EXP1, 4, P).transpose(0, 2, 1), "exp_w2": ffn["w2"], "exp_b2": ffn["b2"],
    }


def kernel(**inputs):
    import numpy as np
    import concourse.bacc as bacc
    from concourse.bass_utils import run_bass_kernel_spmd

    nc = bacc.Bacc("TRN2", target_bir_lowering=False, num_devices=1)
    arrays = {n: np.ascontiguousarray(a) for n, a in layouts({n: np.asarray(a) for n, a in inputs.items()}, np).items()}
    args = {n: nc.dram_tensor(n, a.shape, mybir.dt.from_np(a.dtype), kind="ExternalInput").ap() for n, a in arrays.items()}
    out = nc.dram_tensor("out", [BATCH, SEQ, D], F32, kind="ExternalOutput").ap()
    audio_tower(nc, args, out)
    return run_bass_kernel_spmd(nc, [arrays], core_ids=[0]).results[0]["out"]
```

```python
from contextlib import ExitStack

import concourse.bass as bass
from concourse import mybir

F32 = mybir.dt.float32
F32R = mybir.dt.float32r
U32 = mybir.dt.uint32
I32 = mybir.dt.int32
ACT = mybir.ActivationFunctionType
ALU = mybir.AluOpType
AX = mybir.AxisListType

P = 128
BATCH = 64
T_IN = 256
SEQ = 254
HALF = 127
D = 128
BN = 64
TOKENS = BATCH * SEQ
POS_PAD = 256
EPS = 1e-5

N_HEAD = 8
D_HEAD = 64
E_HEAD = 16

EXP0 = 8
EXP1 = 64
FF1 = 512
CAP = 1016
assert CAP == 2 * (TOKENS * 2 // EXP1) and CAP == 8 * HALF


def over(ap, n):
    p, f = ap.shape
    return ap.unsqueeze(1).to_broadcast([p, n, f])


def wide(ap, n):
    p, g = ap.shape
    return ap.unsqueeze(2).to_broadcast([p, g, n])


class Place:

    def __init__(self, nc, ctx, phase):
        self.nc, self.ctx, self.phase = nc, ctx, phase
        self.sems = []

    def sb(self, name, shape, dt=F32):
        return self.ctx.enter_context(self.nc.sbuf_tensor(f"{self.phase}_sb_{name}", shape, dt))

    def banks(self, name, n):
        return [self.ctx.enter_context(self.nc.psum_tensor(f"{self.phase}_bank_{name}{i}", [P, 512], F32))
                for i in range(n)]

    def sem(self, name):
        self.sems.append(self.nc.alloc_semaphore(f"{self.phase}_{name}"))
        return self.sems[-1]

    def close(self):
        self.nc.clear_and_free_semaphores(self.sems)
        self.nc.all_engine_barrier()


class Signal:

    AHEAD = 2

    def __init__(self, sem, per=1):
        self.sem, self.per = sem, per

    def opened(self, eng):
        eng.sem_inc(self.sem, self.AHEAD * self.per)

    def count(self, unit, k=None, back=0):
        k = self.per if k is None else k
        return unit * self.per + (self.AHEAD - back) * self.per + k


class Landed:

    def __init__(self, sem, dmas, ahead=1):
        self.sem, self.all, self.ahead = sem, 16 * dmas, ahead

    def opened(self, eng):
        eng.sem_inc(self.sem, self.ahead * self.all)

    def count(self, unit, parity, back=0):
        return (unit - parity) * (self.all // 2) + (1 + self.ahead - back) * self.all

    def final(self, units):
        return (units // 2 + self.ahead) * self.all


def in_lanes(eng, units, stages, body):
    lead = stages - 1 + (stages - 1) % 2
    turns = (units - lead) // 2

    def step(first, fixed):
        body([first - s if 0 <= fixed - s < units else None for s in range(stages)],
             [(fixed - s) % 2 for s in range(stages)])

    for n in range(lead):
        step(n, n)
    with eng.Fori(0, turns) as turn:
        for odd in range(2):
            step(turn * 2 + (lead + odd), lead + odd)
    for n in range(lead + 2 * turns, units + stages - 1):
        step(n, n)


def load_rows(eng, dst, h, unit, landed):
    for b in range(2):
        eng.dma_start(dst[:, 2 * b:2 * b + 2, :],
                      h[bass.ds(unit * 2 + b, 1), 0:SEQ, :].rearrange("b (c p) d -> p (b c) d", p=HALF)).then_inc(landed.sem, 16)


def store_rows(eng, h, src, unit, landed):
    for b in range(2):
        eng.dma_start(h[bass.ds(unit * 2 + b, 1), 0:SEQ, :].rearrange("b (c p) d -> p (b c) d", p=HALF),
                      src[:, 2 * b:2 * b + 2, :]).then_inc(landed.sem, 16)


class Norm:

    def __init__(self, pl, tiles, rows):
        self.tiles, self.rows = tiles, rows
        sb, sem = pl.sb, pl.sem
        self.x = [sb(f"norm_x{b}", [rows, tiles, D]) for b in range(2)]
        self.st = [sb(f"norm_st{b}", [rows, tiles, 6]) for b in range(2)]
        self.mv = [sb(f"norm_mv{b}", [rows, tiles, 2]) for b in range(2)]
        self.rstd = [sb(f"norm_rstd{b}", [rows, tiles]) for b in range(2)]
        self.y = [sb(f"norm_y{b}", [rows, tiles, D]) for b in range(2)]
        self.stats = Signal(sem("norm_stats"), tiles)
        self.moments = Signal(sem("norm_moments"), tiles)
        self.var_eps = Signal(sem("norm_var_eps"))
        self.rstd_ready = Signal(sem("norm_rstd_ready"))
        self.ready = Signal(sem("norm_ready"))


def norm_moments(nc, dve, nm, u, b, t, passed):
    nc.vector.bn_stats(nm.st[b][:, t, :], nm.x[b][:, t, :]).then_inc(nm.stats.sem, 1)
    dve.wait_ge(nm.stats.sem, nm.stats.count(u, t + 1))
    dve.sem_inc(passed, 1)
    nc.vector.bn_aggr(nm.mv[b][:, t, :], nm.st[b][:, t, :]).then_inc(nm.moments.sem, 1)


def norm_rows(nc, pool, nm, u, b, eps, minus_half, passed, read):
    n = nm.tiles
    pool.wait_ge(nm.moments.sem, nm.moments.count(u))
    nc.gpsimd.tensor_tensor(nm.rstd[b][:, :], nm.mv[b][:, :, 1], eps[0:nm.rows, 0:n], ALU.add).then_inc(nm.var_eps.sem, 1)
    pool.wait_ge(nm.var_eps.sem, nm.var_eps.count(u))
    nc.gpsimd.tensor_tensor(nm.rstd[b][:, :], nm.rstd[b][:, :], minus_half[0:nm.rows, 0:n], ALU.pow).then_inc(nm.rstd_ready.sem, 1)
    pool.wait_ge(nm.rstd_ready.sem, nm.rstd_ready.count(u))
    pool.wait_ge(read.sem, read.count(u, back=2))
    pool.sem_inc(passed, 1)
    for t in range(n):
        last = nc.gpsimd.tensor_scalar(nm.y[b][:, t, :], nm.x[b][:, t, :], nm.mv[b][:, t, 0:1], nm.rstd[b][:, t:t + 1],
                                       ALU.subtract, ALU.mult)
    last.then_inc(nm.ready.sem, 1)


def norm_scales(nc, pool, nm, sh, u, b, eps, minus_half, passed):
    n = nm.tiles
    pool.wait_ge(nm.moments.sem, nm.moments.count(u))
    pool.wait_ge(nm.ready.sem, nm.ready.count(u, back=2))
    nc.gpsimd.tensor_tensor(nm.rstd[b][:, :], nm.mv[b][:, :, 1], eps[0:nm.rows, 0:n], ALU.add).then_inc(nm.var_eps.sem, 1)
    pool.wait_ge(nm.var_eps.sem, nm.var_eps.count(u))
    nc.gpsimd.tensor_tensor(nm.rstd[b][:, :], nm.rstd[b][:, :], minus_half[0:nm.rows, 0:n], ALU.pow).then_inc(nm.rstd_ready.sem, 1)
    pool.wait_ge(nm.rstd_ready.sem, nm.rstd_ready.count(u))
    nc.gpsimd.tensor_tensor(sh.shift[b][:, :], nm.mv[b][:, :, 0], nm.rstd[b][:, :], ALU.mult).then_inc(sh.product.sem, 1)
    pool.wait_ge(sh.product.sem, sh.product.count(u))
    pool.sem_inc(passed, 1)
    nc.gpsimd.tensor_scalar(sh.shift[b][:, :], sh.shift[b][:, :], -1.0, None, ALU.mult).then_inc(sh.ready.sem, 1)


class Shift:

    def __init__(self, pl, tiles, rows):
        self.shift = [pl.sb(f"norm_shift{b}", [rows, tiles]) for b in range(2)]
        self.product = Signal(pl.sem("norm_product"))
        self.ready = Signal(pl.sem("norm_shift_ready"))


def norm_rows_scalar(nc, act, nm, sh, u, b, read):
    act.wait_ge(sh.ready.sem, sh.ready.count(u))
    act.wait_ge(read.sem, read.count(u, back=2))
    for t in range(nm.tiles):
        last = nc.scalar.activation(nm.y[b][:, t, :], nm.x[b][:, t, :], ACT.Identity, bias=sh.shift[b][:, t:t + 1],
                                    scale=nm.rstd[b][:, t:t + 1])
    last.then_inc(nm.ready.sem, 1)


def phase_token_mixer(nc, x, ident, w_compress, w_main, w_expand, w_ff1, w_ff2, b_compress, b_main, b_ff1,
                      g1_col, b1_col, g2_col, b2_col, b_expand, g1_row, b1_row, b_ff2, h_out, slots):
    UNITS = BATCH // 2
    TILES = 4
    N = TILES * P
    LOAD, CONV, NORM1, FF, NORM2, POOL = range(6)
    STAGES = 6
    ZERO_ROWS = EXP1 * CAP // UNITS
    ZERO_LINE = ZERO_ROWS // HALF
    with ExitStack() as ctx:
        pl = Place(nc, ctx, "tok")
        sb, sem = pl.sb, pl.sem

        def two(name, shape):
            return [sb(f"{name}{b}", shape) for b in range(2)]

        idn = sb("ident", [P, P])
        wc = sb("wc", [D, BN])
        wm = sb("wm", [BN, 3, BN])
        we = sb("we", [BN, D])
        w1 = sb("w1", [D, BN])
        w2 = sb("w2", [BN, D])
        cols = sb("cols", [P, 7])
        rows = sb("rows", [P, 4, D])
        eps = sb("eps", [P, TILES])
        minus_half = sb("minus_half", [P, TILES])
        zeros = sb("zeros", [P, ZERO_LINE * D])
        x_sb = two("x", [P, TILES, D])
        x_be = two("xbe", [P, TILES, D])
        xT = sb("xT", [D, N])
        h1 = sb("h1", [BN, 2, T_IN + 2])
        h2 = sb("h2", [BN, N])
        add = [two(f"add{i}", [P, TILES, D]) for i in (1, 2)]
        st = [two(f"st{i}", [P, TILES, 6]) for i in (1, 2)]
        mv = [two(f"mv{i}", [P, TILES, 2]) for i in (1, 2)]
        rstd = [two(f"rstd{i}", [P, TILES]) for i in (1, 2)]
        nrm = [two(f"nrm{i}", [P, TILES, D]) for i in (1, 2)]
        res = two("res", [P, TILES, D])
        yT = sb("yT", [D, N])
        gel = sb("gel", [BN, N])
        zT = sb("zT", [D, 2, T_IN])
        pair = sb("pair", [D, 2, T_IN - 1])
        pooled = sb("pooled", [D, 2, SEQ])
        h_sb = two("rows_out", [HALF, TILES, D])
        ps_x, ps_c, ps_m, ps_e, ps_y, ps_f1, ps_f2, ps_z = pl.banks("ps", 8)

        weights_in = sem("weights_in")
        WEIGHTS = 17
        zeros_set = sem("zeros_set")
        zeros_stored = sem("zeros_stored")
        pad_zero = sem("pad_zero")
        constants_set = sem("constants_set")
        ff_res_ready = sem("ff_res_ready")
        pe_passed, dve_passed = sem("pe_passed"), sem("dve_passed")
        x_in = [Landed(sem(f"x_in{b}"), 2) for b in range(2)]
        stored = [Landed(sem(f"stored{b}"), 2) for b in range(2)]
        x_turned = Signal(sem("x_turned"))
        xT_ready = Signal(sem("xT_ready"))
        xbe_ready = Signal(sem("xbe_ready"))
        compress_done = Signal(sem("compress_done"))
        h1_ready = Signal(sem("h1_ready"))
        main_done = Signal(sem("main_done"))
        h2_ready = Signal(sem("h2_ready"))
        expand_done = Signal(sem("expand_done"))
        add_ready = [Signal(sem(f"add_ready{i}")) for i in (1, 2)]
        stats = [Signal(sem(f"stats{i}")) for i in (1, 2)]
        moments = [Signal(sem(f"moments{i}")) for i in (1, 2)]
        var_eps = [Signal(sem(f"var_eps{i}")) for i in (1, 2)]
        rstd_ready = [Signal(sem(f"rstd_ready{i}")) for i in (1, 2)]
        nrm_ready = [Signal(sem(f"nrm_ready{i}")) for i in (1, 2)]
        scaled_ready = Signal(sem("scaled_ready"))
        res_ready = Signal(sem("res_ready"))
        y_turned = Signal(sem("y_turned"))
        yT_ready = Signal(sem("yT_ready"))
        ff1_done = Signal(sem("ff1_done"))
        gelu_ready = Signal(sem("gelu_ready"))
        ff2_done = Signal(sem("ff2_done"))
        z_turned = Signal(sem("z_turned"))
        zT_ready = Signal(sem("zT_ready"))
        pair_ready = Signal(sem("pair_ready"))
        pooled_ready = Signal(sem("pooled_ready"))
        pooled_turned = Signal(sem("pooled_turned"))
        h_ready = Signal(sem("h_ready"))

        with nc.Block() as block:

            @block.sync
            def _(sp):
                for dst, src in ((idn[:, :], ident), (wc[:, :], w_compress), (wm[:, :, :], w_main),
                                 (we[:, :], w_expand), (w1[:, :], w_ff1), (w2[:, :], w_ff2),
                                 (cols[0:BN, 0:1], b_compress), (cols[0:BN, 1:2], b_main),
                                 (cols[0:BN, 2:3], b_ff1), (cols[:, 3:4], g1_col), (cols[:, 4:5], b1_col),
                                 (cols[:, 5:6], g2_col), (cols[:, 6:7], b2_col),
                                 (rows[:, 0, :], b_expand.partition_broadcast(P)),
                                 (rows[:, 1, :], g1_row.partition_broadcast(P)),
                                 (rows[:, 2, :], b1_row.partition_broadcast(P)),
                                 (rows[:, 3, :], b_ff2.partition_broadcast(P))):
                    sp.dma_start(dst, src).then_inc(weights_in, 16)
                for s in x_in + stored:
                    s.opened(sp)

                def body(n, par):
                    if n[LOAD] is not None:
                        u, b = n[LOAD], par[LOAD]
                        sp.wait_ge(x_turned.sem, x_turned.count(u, back=2))
                        sp.wait_ge(xbe_ready.sem, xbe_ready.count(u, back=2))
                        for i in range(2):
                            sp.dma_start(x_sb[b][:, 2 * i:2 * i + 2, :],
                                         x[bass.ds(u * 2 + i, 1), :, :].rearrange("b (c p) d -> p (b c) d", p=P)).then_inc(x_in[b].sem, 16)
                    if n[POOL] is not None:
                        u, b = n[POOL], par[POOL]
                        sp.wait_ge(h_ready.sem, h_ready.count(u))
                        for i in range(2):
                            sp.dma_start(h_out[0:SEQ, bass.ds(u * 2 + i, 1), :].rearrange("(c p) b d -> p (c b) d", p=HALF),
                                         h_sb[b][:, 2 * i:2 * i + 2, :]).then_inc(stored[b].sem, 16)

                in_lanes(sp, UNITS, STAGES, body)
                for b in range(2):
                    sp.wait_ge(stored[b].sem, stored[b].final(UNITS))

            @block.tensor
            def _(pe):
                for s in (x_turned, compress_done, main_done, expand_done, y_turned, ff1_done, ff2_done, z_turned, pooled_turned):
                    s.opened(pe)
                pe.wait_ge(weights_in, 16 * WEIGHTS)

                def turn(bank, rows_of, signal):
                    for t in range(TILES):
                        last = nc.tensor.transpose(bank[:, t * P:(t + 1) * P], rows_of[:, t, :], idn[:, :])
                    last.then_inc(signal.sem, 1)

                def body(n, par):
                    conv, ff, pool = n[CONV], n[FF], n[POOL]
                    if conv is not None:
                        b = par[CONV]
                        pe.wait_ge(x_in[b].sem, x_in[b].count(conv, b))
                        pe.wait_ge(xT_ready.sem, xT_ready.count(conv, back=1))
                        turn(ps_x, x_sb[b], x_turned)
                    if ff is not None:
                        pe.wait_ge(nrm_ready[0].sem, nrm_ready[0].count(ff))
                        pe.wait_ge(yT_ready.sem, yT_ready.count(ff, back=1))
                        turn(ps_y, nrm[0][par[FF]], y_turned)
                    if pool is not None:
                        pe.wait_ge(nrm_ready[1].sem, nrm_ready[1].count(pool))
                        pe.wait_ge(h_ready.sem, h_ready.count(pool, back=1))
                        turn(ps_z, nrm[1][par[POOL]], z_turned)
                    if conv is not None:
                        pe.wait_ge(xT_ready.sem, xT_ready.count(conv))
                        pe.wait_ge(h1_ready.sem, h1_ready.count(conv, back=1))
                        nc.tensor.matmul(ps_c[0:BN, :], wc[:, :], xT[:, :], start=True, stop=True).then_inc(compress_done.sem, 1)
                    if ff is not None:
                        pe.wait_ge(yT_ready.sem, yT_ready.count(ff))
                        pe.wait_ge(gelu_ready.sem, gelu_ready.count(ff, back=1))
                        nc.tensor.matmul(ps_f1[0:BN, :], w1[:, :], yT[:, :], start=True, stop=True).then_inc(ff1_done.sem, 1)
                    if conv is not None:
                        pe.wait_ge(h1_ready.sem, h1_ready.count(conv))
                        pe.wait_ge(h2_ready.sem, h2_ready.count(conv, back=1))
                        pe.sem_inc(pe_passed, 1)
                        for tap in range(3):
                            last = nc.tensor.matmul(ps_m[0:BN, :].rearrange("p (b t) -> p b t", b=2), wm[:, tap, :],
                                                    h1[:, :, tap:tap + T_IN], start=tap == 0, stop=tap == 2)
                        last.then_inc(main_done.sem, 1)
                    if ff is not None:
                        pe.wait_ge(gelu_ready.sem, gelu_ready.count(ff))
                        pe.wait_ge(add_ready[1].sem, add_ready[1].count(ff, back=1))
                        for t in range(TILES):
                            last = nc.tensor.matmul(ps_f2[:, t * P:(t + 1) * P], gel[:, t * P:(t + 1) * P], w2[:, :], start=True, stop=True)
                        last.then_inc(ff2_done.sem, 1)
                    if pool is not None:
                        pe.wait_ge(pooled_ready.sem, pooled_ready.count(pool))
                        for t in range(TILES):
                            last = nc.tensor.transpose(ps_z[0:HALF, t * P:(t + 1) * P],
                                                       pooled[:, t // 2, (t % 2) * HALF:(t % 2 + 1) * HALF], idn[:, :])
                        last.then_inc(pooled_turned.sem, 1)
                    if conv is not None:
                        pe.wait_ge(h2_ready.sem, h2_ready.count(conv))
                        pe.wait_ge(add_ready[0].sem, add_ready[0].count(conv, back=1))
                        for t in range(TILES):
                            last = nc.tensor.matmul(ps_e[:, t * P:(t + 1) * P], h2[:, t * P:(t + 1) * P], we[:, :], start=True, stop=True)
                        last.then_inc(expand_done.sem, 1)

                in_lanes(pe, UNITS, STAGES, body)

            @block.scalar
            def _(act):
                for s in (xT_ready, h1_ready, h2_ready, yT_ready, gelu_ready, zT_ready, h_ready):
                    s.opened(act)
                act.wait_ge(weights_in, 16 * WEIGHTS)
                act.wait_ge(pad_zero, 1)
                act.wait_ge(zeros_set, 1)
                act.dma_start(h_out[SEQ:POS_PAD, :, :].rearrange("p b d -> (p b) d"), zeros[:, 0:D]).then_inc(zeros_stored, 16)

                def body(n, par):
                    conv, ff, pool = n[CONV], n[FF], n[POOL]
                    if n[LOAD] is not None:
                        act.dma_start(slots[bass.ds(n[LOAD] * ZERO_ROWS, ZERO_ROWS), :].rearrange("(p t) d -> p (t d)", p=HALF),
                                      zeros[0:HALF, :]).then_inc(zeros_stored, 16)
                    if conv is not None:
                        act.wait_ge(x_turned.sem, x_turned.count(conv))
                        act.wait_ge(compress_done.sem, compress_done.count(conv, back=1))
                        nc.scalar.copy(xT[:, :], ps_x[:, :]).then_inc(xT_ready.sem, 1)
                    if ff is not None:
                        act.wait_ge(y_turned.sem, y_turned.count(ff))
                        act.wait_ge(ff1_done.sem, ff1_done.count(ff, back=1))
                        nc.scalar.activation(yT[:, :], ps_y[:, :], ACT.Identity, bias=cols[:, 4:5], scale=cols[:, 3:4]).then_inc(yT_ready.sem, 1)
                    if pool is not None:
                        act.wait_ge(z_turned.sem, z_turned.count(pool))
                        act.wait_ge(pooled_ready.sem, pooled_ready.count(pool, back=1))
                        nc.scalar.activation(zT[:, :, :].rearrange("p b t -> p (b t)"), ps_z[:, :], ACT.Identity,
                                             bias=cols[:, 6:7], scale=cols[:, 5:6]).then_inc(zT_ready.sem, 1)
                    if conv is not None:
                        act.wait_ge(compress_done.sem, compress_done.count(conv))
                        act.wait_ge(main_done.sem, main_done.count(conv, back=1))
                        nc.scalar.activation(h1[:, :, 1:T_IN + 1], ps_c[0:BN, :].rearrange("p (b t) -> p b t", b=2),
                                             ACT.Silu, bias=cols[0:BN, 0:1]).then_inc(h1_ready.sem, 1)
                    if ff is not None:
                        act.wait_ge(ff1_done.sem, ff1_done.count(ff))
                        act.wait_ge(ff2_done.sem, ff2_done.count(ff, back=1))
                        nc.scalar.activation(gel[:, :], ps_f1[0:BN, :], ACT.Gelu, bias=cols[0:BN, 2:3]).then_inc(gelu_ready.sem, 1)
                    if conv is not None:
                        act.wait_ge(main_done.sem, main_done.count(conv))
                        act.wait_ge(expand_done.sem, expand_done.count(conv, back=1))
                        nc.scalar.activation(h2[:, :], ps_m[0:BN, :], ACT.Silu, bias=cols[0:BN, 1:2]).then_inc(h2_ready.sem, 1)
                    if pool is not None:
                        b = par[POOL]
                        act.wait_ge(pooled_turned.sem, pooled_turned.count(pool))
                        act.wait_ge(stored[b].sem, stored[b].count(pool, b, back=1))
                        nc.scalar.copy(h_sb[b][:, :, :].rearrange("p c d -> p (c d)"), ps_z[0:HALF, :]).then_inc(h_ready.sem, 1)

                in_lanes(act, UNITS, STAGES, body)
                act.wait_ge(zeros_stored, 16 * (UNITS + 1))

            @block.vector
            def _(dve):
                for s in add_ready + stats + moments + nrm_ready + [pair_ready, pooled_ready]:
                    s.opened(dve)
                nc.vector.memset(zeros[:, :], 0.0).then_inc(zeros_set, 1)
                nc.vector.memset(h1[:, :, 0:1], 0.0)
                nc.vector.memset(h1[:, :, T_IN + 1:T_IN + 2], 0.0).then_inc(pad_zero, 1)

                def norm_stats(i, u, b):
                    dve.wait_ge(add_ready[i].sem, add_ready[i].count(u))
                    dve.wait_ge(nrm_ready[i].sem, nrm_ready[i].count(u, back=2))
                    for t in range(TILES):
                        last = nc.vector.bn_stats(st[i][b][:, t, :], add[i][b][:, t, :])
                    last.then_inc(stats[i].sem, 1)

                def norm_aggregate(i, u, b):
                    dve.wait_ge(stats[i].sem, stats[i].count(u))
                    dve.sem_inc(dve_passed, 1)
                    for t in range(TILES):
                        last = nc.vector.bn_aggr(mv[i][b][:, t, :], st[i][b][:, t, :])
                    last.then_inc(moments[i].sem, 1)

                def norm_end(i, u, b):
                    dve.wait_ge(rstd_ready[i].sem, rstd_ready[i].count(u))
                    used = (y_turned, scaled_ready) if i == 0 else (z_turned,)
                    for s in used:
                        dve.wait_ge(s.sem, s.count(u, back=2))
                    for t in range(TILES):
                        last = nc.vector.tensor_scalar(nrm[i][b][:, t, :], add[i][b][:, t, :], mv[i][b][:, t, 0:1], rstd[i][b][:, t:t + 1],
                                                       ALU.subtract, ALU.mult)
                    last.then_inc(nrm_ready[i].sem, 1)

                def body(n, par):
                    lanes = [(i, n[s], par[s]) for i, s in ((0, NORM1), (1, NORM2)) if n[s] is not None]
                    for i, u, b in lanes:
                        norm_stats(i, u, b)
                    for i, u, b in lanes:
                        norm_aggregate(i, u, b)
                    if n[POOL] is not None:
                        u = n[POOL]
                        dve.wait_ge(zT_ready.sem, zT_ready.count(u))
                        nc.vector.tensor_tensor(pair[:, :, :], zT[:, :, 0:T_IN - 1], zT[:, :, 1:T_IN], ALU.max).then_inc(pair_ready.sem, 1)
                        dve.wait_ge(pair_ready.sem, pair_ready.count(u))
                        dve.wait_ge(pooled_turned.sem, pooled_turned.count(u, back=1))
                        nc.vector.tensor_tensor(pooled[:, :, :], pair[:, :, 0:SEQ], zT[:, :, 2:T_IN], ALU.max).then_inc(pooled_ready.sem, 1)
                    for i, u, b in lanes:
                        norm_end(i, u, b)
                    if n[FF] is not None:
                        u, b = n[FF], par[FF]
                        dve.wait_ge(ff2_done.sem, ff2_done.count(u))
                        dve.wait_ge(res_ready.sem, res_ready.count(u))
                        dve.wait_ge(nrm_ready[1].sem, nrm_ready[1].count(u, back=2))
                        nc.vector.tensor_tensor(add[1][b][:, :, :].rearrange("p c d -> p (c d)"), ps_f2[:, :],
                                                res[b][:, :, :].rearrange("p c d -> p (c d)"), ALU.add).then_inc(add_ready[1].sem, 1)
                    if n[CONV] is not None:
                        u, b = n[CONV], par[CONV]
                        dve.wait_ge(expand_done.sem, expand_done.count(u))
                        dve.wait_ge(xbe_ready.sem, xbe_ready.count(u))
                        dve.wait_ge(nrm_ready[0].sem, nrm_ready[0].count(u, back=2))
                        nc.vector.tensor_tensor(add[0][b][:, :, :].rearrange("p c d -> p (c d)"), ps_e[:, :],
                                                x_be[b][:, :, :].rearrange("p c d -> p (c d)"), ALU.add).then_inc(add_ready[0].sem, 1)

                in_lanes(dve, UNITS, STAGES, body)

            @block.gpsimd
            def _(pool):
                for s in var_eps + rstd_ready + [xbe_ready, scaled_ready, res_ready]:
                    s.opened(pool)
                nc.gpsimd.memset(eps[:, :], EPS)
                nc.gpsimd.memset(minus_half[:, :], -0.5).then_inc(constants_set, 1)
                pool.wait_ge(constants_set, 1)
                pool.wait_ge(weights_in, 16 * WEIGHTS)
                nc.gpsimd.tensor_tensor(rows[:, 2, :], rows[:, 2, :], rows[:, 3, :], ALU.add).then_inc(ff_res_ready, 1)
                pool.wait_ge(ff_res_ready, 1)

                def body(n, par):
                    if n[CONV] is not None:
                        u, b = n[CONV], par[CONV]
                        pool.wait_ge(x_in[b].sem, x_in[b].count(u, b))
                        pool.wait_ge(add_ready[0].sem, add_ready[0].count(u, back=2))
                        nc.gpsimd.tensor_tensor(x_be[b][:, :, :], x_sb[b][:, :, :], over(rows[:, 0, :], TILES), ALU.add).then_inc(xbe_ready.sem, 1)
                    for i, s in ((0, NORM1), (1, NORM2)):
                        if n[s] is not None:
                            u, b = n[s], par[s]
                            pool.wait_ge(moments[i].sem, moments[i].count(u))
                            nc.gpsimd.tensor_tensor(rstd[i][b][:, :], mv[i][b][:, :, 1], eps[:, :], ALU.add).then_inc(var_eps[i].sem, 1)
                            pool.wait_ge(var_eps[i].sem, var_eps[i].count(u))
                            nc.gpsimd.tensor_tensor(rstd[i][b][:, :], rstd[i][b][:, :], minus_half[:, :], ALU.pow).then_inc(rstd_ready[i].sem, 1)
                    if n[NORM1] is not None:
                        u, b = n[NORM1], par[NORM1]
                        pool.wait_ge(nrm_ready[0].sem, nrm_ready[0].count(u))
                        pool.wait_ge(add_ready[1].sem, add_ready[1].count(u, back=2))
                        nc.gpsimd.tensor_tensor(res[b][:, :, :], nrm[0][b][:, :, :], over(rows[:, 1, :], TILES), ALU.mult).then_inc(scaled_ready.sem, 1)
                        pool.wait_ge(scaled_ready.sem, scaled_ready.count(u))
                        nc.gpsimd.tensor_tensor(res[b][:, :, :], res[b][:, :, :], over(rows[:, 2, :], TILES), ALU.add).then_inc(res_ready.sem, 1)

                in_lanes(pool, UNITS, STAGES, body)

        pl.close()


def phase_batch_attention(nc, h_in, ident, mask, wq, wk, wv, wo, h_out):
    UNITS = POS_PAD // 8
    TILES = 4
    N = TILES * P
    PAIRS = N_HEAD // 2
    NORM, TURN, PROJ, SOFT, FLIP, WEIGH, OUT = range(7)
    STAGES = 7
    HIGH, LOW = range(2)
    PARTS = ((HIGH, LOW), (LOW, HIGH), (HIGH, HIGH))
    with ExitStack() as ctx:
        pl = Place(nc, ctx, "bat")
        sb, sem = pl.sb, pl.sem
        idn = sb("ident", [P, P])
        msk = sb("mask", [P, N])
        w_sb = [sb(f"w{x}", [D, N]) for x in "qkv"]
        ws = [[sb(f"w{x}_{part}", [D, N], F32R) for part in ("high", "low")] for x in "qkv"]
        wo_sb = sb("wo", [P, PAIRS, D])
        eps = sb("eps", [P, TILES])
        minus_half = sb("minus_half", [P, TILES])

        def two(name, shape):
            return [sb(f"{name}{b}", shape) for b in range(2)]

        h_sb = two("h", [P, TILES, D])
        st = two("st", [P, TILES, 6])
        mv = two("mv", [P, TILES, 2])
        rstd = two("rstd", [P, TILES])
        hn = two("hn", [P, TILES, D])
        hnT = [[sb(f"hnT_{part}{b}", [D, N], F32R) for part in ("high", "low")] for b in range(2)]
        qT = two("qT", [P, PAIRS, N])
        kT = two("kT", [P, PAIRS, N])
        v = two("v", [P, TILES, N])
        sc = two("sc", [P, N])
        top = two("top", [P, 8])
        ex = two("ex", [P, N])
        total = two("total", [P, 8])
        inv = two("inv", [P, 8])
        prob = two("prob", [P, TILES, N])
        prT = sb("prT", [P, TILES, N])
        oT = sb("oT", [P, TILES, N])
        res = two("res", [P, TILES, D])
        out = two("out", [P, TILES, D])

        ps_qk, ps_v, ps_prT, ps_out = pl.banks("x", 4)
        ps_sc = pl.banks("sc", 2)
        ps_oT = ctx.enter_context(nc.psum_tensor("bat_bank_oT", [P, 2, N], F32))

        weights_in = sem("weights_in")
        WEIGHTS = 6
        pe_passed, dve_passed, pool_passed = (sem(f"{e}_passed") for e in ("pe", "dve", "pool"))
        constants_set = sem("constants_set")
        h_in_s = [Landed(sem(f"h_in_s{b}"), 2) for b in range(2)]
        res_in = [Landed(sem(f"res_in{b}"), 2) for b in range(2)]
        stored = [Landed(sem(f"stored{b}"), 2) for b in range(2)]
        stats = Signal(sem("stats"), TILES)
        moments = Signal(sem("moments"), TILES)
        var_eps = Signal(sem("var_eps"))
        rstd_ready = Signal(sem("rstd_ready"))
        normed = Signal(sem("normed"))
        turned = Signal(sem("turned"))
        hnT_high = Signal(sem("hnT_high"))
        hnT_low = Signal(sem("hnT_low"))
        w_high = sem("w_high")
        w_low = sem("w_low")
        q_done = Signal(sem("q_done"), TILES)
        k_done = Signal(sem("k_done"), TILES)
        v_done = Signal(sem("v_done"), TILES)
        q_ready = Signal(sem("q_ready"), TILES)
        k_ready = Signal(sem("k_ready"), TILES)
        v_ready = Signal(sem("v_ready"), TILES)
        sc_done = Signal(sem("sc_done"), TILES)
        sc_masked = Signal(sem("sc_masked"), TILES)
        top_ready = Signal(sem("top_ready"), TILES)
        sc_ready = Signal(sem("sc_ready"), TILES)
        ex_ready = Signal(sem("ex_ready"), TILES)
        total_ready = Signal(sem("total_ready"), TILES)
        inv_ready = Signal(sem("inv_ready"), TILES)
        prob_ready = Signal(sem("prob_ready"), TILES)
        prob_turned = Signal(sem("prob_turned"), TILES)
        prT_ready = Signal(sem("prT_ready"), TILES)
        oT_done = Signal(sem("oT_done"), TILES)
        oT_ready = Signal(sem("oT_ready"), TILES)
        out_done = Signal(sem("out_done"), TILES)
        out_ready = Signal(sem("out_ready"), TILES)

        with nc.Block() as block:

            @block.sync
            def _(sp):
                for dst, src in ((idn[:, :], ident), (msk[:, :], mask), (w_sb[0][:, :], wq), (w_sb[1][:, :], wk), (w_sb[2][:, :], wv),
                                 (wo_sb[:, :, :], wo.rearrange("(j p) d -> p j d", p=P))):
                    sp.dma_start(dst, src).then_inc(weights_in, 16)
                for b in range(2):
                    h_in_s[b].opened(sp)
                    res_in[b].opened(sp)
                    stored[b].opened(sp)

                def body(n, par):
                    if n[NORM] is not None:
                        u, b = n[NORM], par[NORM]
                        sp.wait_ge(normed.sem, normed.count(u, back=2))
                        for odd in range(2):
                            sp.dma_start(h_sb[b][odd * BATCH:(odd + 1) * BATCH, :, :],
                                         h_in[bass.ds(u * 8, 8), :, :].rearrange("(t two) b d -> two b t d", two=2)[odd]
                                         ).then_inc(h_in_s[b].sem, 16)
                    if n[WEIGH] is not None:
                        u, b = n[WEIGH], par[WEIGH]
                        sp.wait_ge(out_ready.sem, out_ready.count(u, back=2))
                        for odd in range(2):
                            sp.dma_start(res[b][odd * BATCH:(odd + 1) * BATCH, :, :],
                                         h_in[bass.ds(u * 8, 8), :, :].rearrange("(t two) b d -> two b t d", two=2)[odd]
                                         ).then_inc(res_in[b].sem, 16)
                    if n[OUT] is not None:
                        u, b = n[OUT], par[OUT]
                        sp.wait_ge(out_ready.sem, out_ready.count(u))
                        for odd in range(2):
                            sp.dma_start(h_out[:, bass.ds(u * 8, 8), :].rearrange("b (t two) d -> two b t d", two=2)[odd],
                                         out[b][odd * BATCH:(odd + 1) * BATCH, :, :]).then_inc(stored[b].sem, 16)

                in_lanes(sp, UNITS, STAGES, body)
                for b in range(2):
                    sp.wait_ge(stored[b].sem, stored[b].final(UNITS))

            @block.tensor
            def _(pe):
                for s in (turned, q_done, k_done, v_done, sc_done, prob_turned, oT_done, out_done):
                    s.opened(pe)
                pe.wait_ge(weights_in, 16 * WEIGHTS)
                pe.wait_ge(w_low, 3)

                def parts_wait(u):
                    pe.wait_ge(hnT_low.sem, hnT_low.count(u))

                def flip(u, b, t):
                    pe.wait_ge(prob_ready.sem, prob_ready.count(u, t + 1))
                    pe.wait_ge(prT_ready.sem, prT_ready.count(u, t))
                    for j in range(PAIRS):
                        last = nc.tensor.transpose(ps_prT[:, j * P:(j + 1) * P], prob[b][:, t, j * P:(j + 1) * P], idn[:, :])
                    last.then_inc(prob_turned.sem, 1)

                def scores(u, b, t):
                    for s in (q_ready, k_ready) if t == 0 else ():
                        pe.wait_ge(s.sem, s.count(u))
                    pe.wait_ge(sc_masked.sem, sc_masked.count(u, t - 1))
                    pe.sem_inc(pe_passed, 1)
                    for j in range(PAIRS):
                        for pos in range(2):
                            for hh in range(2):
                                half = slice(hh * 64, hh * 64 + 64)
                                at = (2 * t + pos) * BATCH
                                last = nc.tensor.matmul(ps_sc[t % 2][half, (2 * j + pos) * 64:(2 * j + pos + 1) * 64],
                                                        qT[b][half, j, at:at + BATCH], kT[b][half, j, at:at + BATCH],
                                                        start=True, stop=True)
                    last.then_inc(sc_done.sem, 1)

                def weigh(u, b, t):
                    if t == 0:
                        pe.wait_ge(prT_ready.sem, prT_ready.count(u))
                        pe.wait_ge(v_ready.sem, v_ready.count(u))
                    pe.wait_ge(oT_ready.sem, oT_ready.count(u, t))
                    pe.sem_inc(pe_passed, 1)
                    for j in range(PAIRS):
                        for pos in range(2):
                            for hh in range(2):
                                rows = slice(pos * 64, pos * 64 + 64)
                                last = nc.tensor.matmul(ps_oT[hh * 64:hh * 64 + 64, pos, j * 64:j * 64 + 64],
                                                        v[b][rows, t, (2 * j + hh) * D_HEAD:(2 * j + hh + 1) * D_HEAD],
                                                        prT[rows, t, j * P + hh * 64:j * P + hh * 64 + 64],
                                                        start=True, stop=True)
                    last.then_inc(oT_done.sem, 1)

                def project(which, b, t):
                    for i, (wp, xp) in enumerate(PARTS):
                        last = nc.tensor.matmul(ps_qk[:, :], ws[which][wp][:, t * P:(t + 1) * P], hnT[b][xp][:, :], start=i == 0, stop=i == 2)
                    return last

                def project_q(u, b, t):
                    if t == 0:
                        parts_wait(u)
                    pe.wait_ge(k_ready.sem, k_ready.count(u, t))
                    project(0, b, t).then_inc(q_done.sem, 1)

                def project_k(u, b, t):
                    pe.wait_ge(q_ready.sem, q_ready.count(u, t + 1))
                    project(1, b, t).then_inc(k_done.sem, 1)

                def project_v(u, b, t, turned_before):
                    if t == 0 and turned_before is not None:
                        parts_wait(turned_before)
                    pe.wait_ge(v_ready.sem, v_ready.count(u, t))
                    for i, (xp, wp) in enumerate(PARTS):
                        last = nc.tensor.matmul(ps_v[:, :], hnT[b][xp][:, t * P:(t + 1) * P], ws[2][wp][:, :], start=i == 0, stop=i == 2)
                    last.then_inc(v_done.sem, 1)

                def output(u, t):
                    if t == 0:
                        pe.wait_ge(oT_ready.sem, oT_ready.count(u))
                    pe.wait_ge(out_ready.sem, out_ready.count(u, t))
                    for j in range(PAIRS):
                        last = nc.tensor.matmul(ps_out[:, t * D:(t + 1) * D], oT[:, t, j * P:(j + 1) * P],
                                                wo_sb[:, j, :], start=j == 0, stop=j == PAIRS - 1)
                    last.then_inc(out_done.sem, 1)

                def turn(u, b, projected):
                    pe.wait_ge(normed.sem, normed.count(u))
                    if projected is not None:
                        pe.wait_ge(v_ready.sem, v_ready.count(projected))
                    for t in range(TILES):
                        last = nc.tensor.transpose(ps_v[:, t * P:(t + 1) * P], hn[b][:, t, :], idn[:, :])
                    last.then_inc(turned.sem, 1)

                def body(n, par):
                    for t in range(TILES):
                        if n[SOFT] is not None:
                            scores(n[SOFT], par[SOFT], t)
                        if n[OUT] is not None:
                            output(n[OUT], t)
                        if n[PROJ] is not None:
                            project_q(n[PROJ], par[PROJ], t)
                        if n[WEIGH] is not None:
                            weigh(n[WEIGH], par[WEIGH], t)
                        if n[SOFT] is not None:
                            project_v(n[SOFT], par[SOFT], t, n[PROJ])
                        if n[FLIP] is not None:
                            flip(n[FLIP], par[FLIP], t)
                        if n[PROJ] is not None:
                            project_k(n[PROJ], par[PROJ], t)
                    if n[TURN] is not None:
                        if n[PROJ] is None:
                            pe.wait_ge(hnT_low.sem, hnT_low.count(n[TURN], back=1))
                        turn(n[TURN], par[TURN], n[SOFT])

                in_lanes(pe, UNITS, STAGES, body)

            @block.scalar
            def _(act):
                for s in (hnT_high, q_ready, k_ready, v_ready, ex_ready, oT_ready):
                    s.opened(act)

                def body(n, par):
                    for t in range(TILES):
                        if n[PROJ] is not None:
                            u, b = n[PROJ], par[PROJ]
                            act.wait_ge(q_done.sem, q_done.count(u, t + 1))
                            act.wait_ge(sc_done.sem, sc_done.count(u, back=2))
                            nc.scalar.activation(qT[b][:, t, :], ps_qk[:, :], ACT.Copy, scale=D_HEAD ** -0.5).then_inc(q_ready.sem, 1)
                        if n[WEIGH] is not None:
                            u = n[WEIGH]
                            act.wait_ge(oT_done.sem, oT_done.count(u, t + 1))
                            act.wait_ge(out_done.sem, out_done.count(u, t + 1, back=1))
                            nc.scalar.copy(oT[:, t, :].rearrange("p (j two q) -> p two j q", two=2, q=64),
                                           ps_oT[:, :, 0:256].rearrange("p two (j q) -> p two j q", q=64)).then_inc(oT_ready.sem, 1)
                        if n[SOFT] is not None:
                            u, b = n[SOFT], par[SOFT]
                            act.wait_ge(v_done.sem, v_done.count(u, t + 1))
                            act.wait_ge(oT_done.sem, oT_done.count(u, t + 1, back=2))
                            nc.scalar.copy(v[b][:, t, :], ps_v[:, :]).then_inc(v_ready.sem, 1)
                        if n[SOFT] is not None:
                            u, b = n[SOFT], par[SOFT]
                            act.wait_ge(sc_ready.sem, sc_ready.count(u, t + 1))
                            act.wait_ge(prob_ready.sem, prob_ready.count(u, t - 1))
                            nc.scalar.activation(ex[t % 2][:, :], sc[t % 2][:, :], ACT.Exp).then_inc(ex_ready.sem, 1)
                        if n[PROJ] is not None:
                            u, b = n[PROJ], par[PROJ]
                            act.wait_ge(k_done.sem, k_done.count(u, t + 1))
                            nc.scalar.copy(kT[b][:, t, :], ps_qk[:, :]).then_inc(k_ready.sem, 1)
                    if n[TURN] is not None:
                        u, b = n[TURN], par[TURN]
                        act.wait_ge(turned.sem, turned.count(u))
                        act.wait_ge(v_done.sem, v_done.count(u, back=2))
                        nc.scalar.copy(hnT[b][HIGH][:, :], ps_v[:, :]).then_inc(hnT_high.sem, 1)

                in_lanes(act, UNITS, STAGES, body)

            @block.vector
            def _(dve):
                for s in (stats, moments, sc_masked, top_ready, sc_ready, total_ready, inv_ready, prT_ready, out_ready, hnT_low):
                    s.opened(dve)
                dve.wait_ge(weights_in, 16 * WEIGHTS)
                for i in range(3):
                    nc.vector.tensor_copy(ws[i][HIGH][:, :], w_sb[i][:, :]).then_inc(w_high, 1)
                for i in range(3):
                    dve.wait_ge(w_high, i + 1)
                    nc.vector.tensor_tensor(ws[i][LOW][:, :], w_sb[i][:, :], ws[i][HIGH][:, :], ALU.subtract).then_inc(w_low, 1)

                def body(n, par):
                    for t in range(TILES):
                        if n[SOFT] is not None:
                            u, b = n[SOFT], t % 2
                            dve.wait_ge(sc_done.sem, sc_done.count(u, t + 1))
                            dve.wait_ge(ex_ready.sem, ex_ready.count(u, t - 1))
                            nc.vector.tensor_tensor(sc[b][:, :], ps_sc[b][:, :], msk[:, :], ALU.add).then_inc(sc_masked.sem, 1)
                            dve.wait_ge(sc_masked.sem, sc_masked.count(u, t + 1))
                            nc.vector.tensor_reduce(top[b][:, :], sc[b][:, :].rearrange("p (g k) -> p g k", k=64),
                                                    AX.X, ALU.max).then_inc(top_ready.sem, 1)
                        if n[SOFT] is not None:
                            u, b = n[SOFT], t % 2
                            dve.wait_ge(top_ready.sem, top_ready.count(u, t + 1))
                            nc.vector.tensor_tensor(sc[b][:, :].rearrange("p (g k) -> p g k", k=64),
                                                    sc[b][:, :].rearrange("p (g k) -> p g k", k=64),
                                                    wide(top[b][:, :], 64), ALU.subtract).then_inc(sc_ready.sem, 1)
                        if n[NORM] is not None:
                            u, b = n[NORM], par[NORM]
                            if t == 0:
                                dve.wait_ge(h_in_s[b].sem, h_in_s[b].count(u, b))
                                dve.wait_ge(normed.sem, normed.count(u, back=2))
                            nc.vector.bn_stats(st[b][:, t, :], h_sb[b][:, t, :]).then_inc(stats.sem, 1)
                            dve.wait_ge(stats.sem, stats.count(u, t + 1))
                            dve.sem_inc(dve_passed, 1)
                            nc.vector.bn_aggr(mv[b][:, t, :], st[b][:, t, :]).then_inc(moments.sem, 1)
                        if n[FLIP] is not None:
                            u = n[FLIP]
                            dve.wait_ge(prob_turned.sem, prob_turned.count(u, t + 1))
                            dve.wait_ge(oT_done.sem, oT_done.count(u, t + 1, back=1))
                            nc.vector.tensor_copy(prT[:, t, :], ps_prT[:, :]).then_inc(prT_ready.sem, 1)
                        if n[SOFT] is not None:
                            u, b = n[SOFT], t % 2
                            dve.wait_ge(ex_ready.sem, ex_ready.count(u, t + 1))
                            nc.vector.tensor_reduce(total[b][:, :], ex[b][:, :].rearrange("p (g k) -> p g k", k=64),
                                                    AX.X, ALU.add).then_inc(total_ready.sem, 1)
                            dve.wait_ge(total_ready.sem, total_ready.count(u, t + 1))
                            dve.wait_ge(prob_ready.sem, prob_ready.count(u, t - 1))
                            nc.vector.reciprocal(inv[b][:, :], total[b][:, :]).then_inc(inv_ready.sem, 1)
                        if n[OUT] is not None:
                            u, b = n[OUT], par[OUT]
                            if t == 0:
                                dve.wait_ge(res_in[b].sem, res_in[b].count(u, b))
                                dve.wait_ge(stored[b].sem, stored[b].count(u, b, back=1))
                            dve.wait_ge(out_done.sem, out_done.count(u, t + 1))
                            nc.vector.tensor_tensor(out[b][:, t, :], ps_out[:, t * D:(t + 1) * D], res[b][:, t, :],
                                                    ALU.add).then_inc(out_ready.sem, 1)
                    if n[TURN] is not None:
                        u, b = n[TURN], par[TURN]
                        dve.wait_ge(hnT_high.sem, hnT_high.count(u))
                        nc.vector.tensor_tensor(hnT[b][LOW][:, :], ps_v[:, :], hnT[b][HIGH][:, :], ALU.subtract).then_inc(hnT_low.sem, 1)

                in_lanes(dve, UNITS, STAGES, body)

            @block.gpsimd
            def _(pool):
                for s in (var_eps, rstd_ready, normed, prob_ready):
                    s.opened(pool)
                nc.gpsimd.memset(eps[:, :], EPS)
                nc.gpsimd.memset(minus_half[:, :], -0.5).then_inc(constants_set, 1)
                pool.wait_ge(constants_set, 1)

                def body(n, par):
                    for t in range(TILES):
                        if n[SOFT] is not None:
                            u, b = n[SOFT], par[SOFT]
                            pool.wait_ge(inv_ready.sem, inv_ready.count(u, t + 1))
                            pool.wait_ge(prob_turned.sem, prob_turned.count(u, t + 1, back=2))
                            nc.gpsimd.tensor_tensor(prob[b][:, t, :].rearrange("p (g k) -> p g k", k=64),
                                                    ex[t % 2][:, :].rearrange("p (g k) -> p g k", k=64),
                                                    wide(inv[t % 2][:, :], 64), ALU.mult).then_inc(prob_ready.sem, 1)
                    if n[NORM] is not None:
                        u, b = n[NORM], par[NORM]
                        pool.wait_ge(moments.sem, moments.count(u))
                        nc.gpsimd.tensor_tensor(rstd[b][:, :], mv[b][:, :, 1], eps[:, :], ALU.add).then_inc(var_eps.sem, 1)
                        pool.wait_ge(var_eps.sem, var_eps.count(u))
                        nc.gpsimd.tensor_tensor(rstd[b][:, :], rstd[b][:, :], minus_half[:, :], ALU.pow).then_inc(rstd_ready.sem, 1)
                        pool.wait_ge(rstd_ready.sem, rstd_ready.count(u))
                        pool.wait_ge(turned.sem, turned.count(u, back=2))
                        pool.sem_inc(pool_passed, 1)
                        for t in range(TILES):
                            last = nc.gpsimd.tensor_scalar(hn[b][:, t, :], h_sb[b][:, t, :], mv[b][:, t, 0:1], rstd[b][:, t:t + 1],
                                                           ALU.subtract, ALU.mult)
                        last.then_inc(normed.sem, 1)

                in_lanes(pool, UNITS, STAGES, body)

        pl.close()


def phase_experts8(nc, h_in, ident, iota8, wg, w1, b1, w2, b2, gamma, beta, h_out):
    UNITS = BATCH // 2
    TILES = 4
    N = TILES * HALF
    NORM, TURN, HID, OUT, SCALE, SUM = range(6)
    STAGES = 6
    H = EXP0 // 2
    with ExitStack() as ctx:
        pl = Place(nc, ctx, "ex8")
        sb, sem = pl.sb, pl.sem
        idn = sb("ident", [P, P])
        iota = sb("iota", [P, EXP0])
        wg_sb = sb("wg", [D, EXP0])
        w1_sb = sb("w1", [D, EXP0, P])
        w2_sb = sb("w2", [P, EXP0, D])
        b1_sb = sb("b1", [P, EXP0])
        b2_sb = sb("b2", [P, EXP0, D])
        gam = sb("gamma", [P, EXP0, D])
        beta_sb = sb("beta", [EXP0, D])
        means = sb("means", [P, 2, EXP0])
        eps = sb("eps", [P, TILES])
        minus_half = sb("minus_half", [P, TILES * EXP0])

        def two(name, shape, dt=F32):
            return [sb(f"{name}{b}", shape, dt) for b in range(2)]

        nm = Norm(pl, TILES, HALF)
        sh = Shift(pl, TILES, HALF)
        hnT = two("hnT", [D, N])
        hid = two("hid", [P, EXP0, N])
        logit = two("logit", [HALF, TILES, EXP0])
        top = two("top", [HALF, TILES, EXP0])
        at = two("at", [HALF, TILES, EXP0], U32)
        atf = two("atf", [HALF, TILES, 2])
        gap = two("gap", [HALF, TILES])
        egap = two("egap", [HALF, TILES])
        den = two("den", [HALF, TILES])
        gate = two("gate", [HALF, 2, TILES])
        hot = two("hot", [HALF, 2, TILES, EXP0])
        w = two("gated", [HALF, TILES, EXP0])
        wT = two("wT", [EXP0, HALF])
        yb = two("yb", [HALF, TILES, EXP0, D])
        sq = two("sq", [HALF, EXP0, D])
        own_sq = two("own_sq", [HALF, EXP0, D])
        ss = two("ss", [HALF, TILES, EXP0])
        s = two("scale", [HALF, TILES, EXP0])
        yg = two("yg", [HALF, TILES, EXP0, D])
        res = two("res", [HALF, TILES, D])
        acc = two("acc", [HALF, TILES, D])

        ps_turn, ps_misc = pl.banks("turn", 2)
        ps_hid = pl.banks("hid", 2)
        ps_y = [ctx.enter_context(nc.psum_tensor(f"ex8_bank_y{b}", [P, 2, H * D], F32)) for b in range(2)]
        ps_beta, ps_logit, ps_wT = ps_misc[0:HALF, 0:D], ps_misc[0:HALF, 128:160], ps_misc[0:EXP0, 192:192 + HALF]

        weights_in = sem("weights_in")
        WEIGHTS = 9
        constants_set = sem("constants_set")
        means_ready = sem("means_ready")
        centred = sem("centred")
        dve_passed, pool_passed = sem("dve_passed"), sem("pool_passed")
        x_in = [Landed(sem(f"x_in{b}"), 2) for b in range(2)]
        res_in = [Landed(sem(f"res_in{b}"), 2) for b in range(2)]
        stored = [Landed(sem(f"stored{b}"), 2) for b in range(2)]
        turned = Signal(sem("turned"))
        hnT_ready = Signal(sem("hnT_ready"))
        logit_done = Signal(sem("logit_done"))
        logit_ready = Signal(sem("logit_ready"))
        top_ready = Signal(sem("top_ready"))
        at_ready = Signal(sem("at_ready"))
        atf_ready = Signal(sem("atf_ready"))
        gap_ready = Signal(sem("gap_ready"))
        egap_ready = Signal(sem("egap_ready"))
        den_ready = Signal(sem("den_ready"))
        gate0_ready = Signal(sem("gate0_ready"))
        gates_ready = Signal(sem("gates_ready"))
        hot_ready = Signal(sem("hot_ready"))
        hot_scaled = Signal(sem("hot_scaled"))
        w_ready = Signal(sem("w_ready"))
        hid_done = Signal(sem("hid_done"), EXP0)
        hid_ready = Signal(sem("hid_ready"), EXP0)
        wT_done = Signal(sem("wT_done"), TILES)
        wT_ready = Signal(sem("wT_ready"), TILES)
        y_done = Signal(sem("y_done"), TILES)
        y_ready = Signal(sem("y_ready"), TILES)
        beta_done = Signal(sem("beta_done"), TILES)
        acc_begun = Signal(sem("acc_begun"), TILES)
        sq_ready = Signal(sem("sq_ready"), TILES - 2)
        ss_ready = Signal(sem("ss_ready"), TILES - 2)
        last_ss_ready = Signal(sem("last_ss_ready"), 2)
        var_ready = Signal(sem("var_ready"))
        yrstd_ready = Signal(sem("yrstd_ready"))
        s_ready = Signal(sem("s_ready"))
        yg_ready = Signal(sem("yg_ready"), TILES)
        acc_steps = Signal(sem("acc_steps"), EXP0)

        with nc.Block() as block:

            @block.sync
            def _(sp):
                for dst, src in ((idn[:, :], ident), (iota[:, :], iota8), (wg_sb[:, :], wg),
                                 (w1_sb[:, :, :], w1.rearrange("e d h -> d e h")),
                                 (w2_sb[:, :, :], w2.rearrange("e h d -> h e d")),
                                 (b1_sb[:, :], b1), (beta_sb[:, :], beta),
                                 (b2_sb[:, :, :].rearrange("p e d -> p (e d)"), b2.partition_broadcast(P)),
                                 (gam[:, :, :].rearrange("p e d -> p (e d)"), gamma.partition_broadcast(P))):
                    sp.dma_start(dst, src).then_inc(weights_in, 16)
                for b in range(2):
                    x_in[b].opened(sp)
                    res_in[b].opened(sp)
                    stored[b].opened(sp)

                def body(n, par):
                    if n[NORM] is not None:
                        u, b = n[NORM], par[NORM]
                        sp.wait_ge(nm.ready.sem, nm.ready.count(u, back=2))
                        load_rows(sp, nm.x[b], h_in, u, x_in[b])
                    if n[OUT] is not None:
                        u, b = n[OUT], par[OUT]
                        sp.wait_ge(acc_begun.sem, acc_begun.count(u, back=2))
                        load_rows(sp, res[b], h_in, u, res_in[b])
                    if n[SUM] is not None:
                        u, b = n[SUM], par[SUM]
                        sp.wait_ge(acc_steps.sem, acc_steps.count(u))
                        store_rows(sp, h_out, acc[b], u, stored[b])

                in_lanes(sp, UNITS, STAGES, body)
                for b in range(2):
                    sp.wait_ge(stored[b].sem, stored[b].final(UNITS))

            @block.tensor
            def _(pe):
                for x in (turned, logit_done, hid_done, wT_done, y_done, beta_done):
                    x.opened(pe)
                pe.wait_ge(weights_in, 16 * WEIGHTS)
                pe.wait_ge(centred, 2)

                def body(n, par):
                    if n[HID] is not None:
                        u, b = n[HID], par[HID]
                        pe.wait_ge(hnT_ready.sem, hnT_ready.count(u))
                        if n[SCALE] is not None:
                            pe.wait_ge(acc_begun.sem, acc_begun.count(n[SCALE], 0))
                        for t in range(TILES):
                            last = nc.tensor.matmul(ps_logit[:, t * EXP0:(t + 1) * EXP0], hnT[b][:, t * HALF:(t + 1) * HALF],
                                                    wg_sb[:, :], start=True, stop=True)
                        last.then_inc(logit_done.sem, 1)
                    for t in range(TILES):
                        if n[SCALE] is not None:
                            u, b = n[SCALE], par[SCALE]
                            if t == 0:
                                pe.wait_ge(w_ready.sem, w_ready.count(u))
                                if n[HID] is not None:
                                    pe.wait_ge(logit_ready.sem, logit_ready.count(n[HID]))
                            pe.wait_ge(acc_begun.sem, acc_begun.count(u, t))
                            nc.tensor.transpose(ps_wT, w[b][:, t, :], idn[0:HALF, 0:HALF]).then_inc(wT_done.sem, 1)
                        if n[OUT] is not None:
                            u, b = n[OUT], par[OUT]
                            if t == 0:
                                pe.wait_ge(hid_ready.sem, hid_ready.count(u))
                            pe.wait_ge(y_ready.sem, y_ready.count(u, t - 1))
                            for e in range(EXP0):
                                last = nc.tensor.matmul(ps_y[t % 2][0:HALF, e // H, (e % H) * D:(e % H + 1) * D],
                                                        hid[b][:, e, t * HALF:(t + 1) * HALF], w2_sb[:, e, :],
                                                        start=True, stop=True)
                            last.then_inc(y_done.sem, 1)
                        if n[SCALE] is not None:
                            u, b = n[SCALE], par[SCALE]
                            pe.wait_ge(wT_ready.sem, wT_ready.count(u, t + 1))
                            nc.tensor.matmul(ps_beta, wT[t % 2][:, :], beta_sb[:, :], start=True, stop=True).then_inc(beta_done.sem, 1)
                        if n[TURN] is not None and t == 1:
                            u, b = n[TURN], par[TURN]
                            pe.wait_ge(nm.ready.sem, nm.ready.count(u))
                            pe.wait_ge(hnT_ready.sem, hnT_ready.count(u, back=1))
                            for i in range(TILES):
                                last = nc.tensor.transpose(ps_turn[:, i * HALF:(i + 1) * HALF], nm.y[b][:, i, :], idn[0:HALF, 0:HALF])
                            last.then_inc(turned.sem, 1)
                        if n[HID] is not None:
                            u, b = n[HID], par[HID]
                            for e in (2 * t, 2 * t + 1):
                                pe.wait_ge(hid_ready.sem, hid_ready.count(u, e - 1))
                                nc.tensor.matmul(ps_hid[e % 2][:, 0:N], w1_sb[:, e, :], hnT[b][:, :],
                                                 start=True, stop=True).then_inc(hid_done.sem, 1)

                in_lanes(pe, UNITS, STAGES, body)

            @block.scalar
            def _(act):
                for x in (nm.ready, hnT_ready, logit_ready, egap_ready, hid_ready, wT_ready, sq_ready, last_ss_ready):
                    x.opened(act)
                act.wait_ge(weights_in, 16 * WEIGHTS)

                def body(n, par):
                    if n[HID] is not None:
                        u, b = n[HID], par[HID]
                        act.wait_ge(logit_done.sem, logit_done.count(u))
                        act.wait_ge(at_ready.sem, at_ready.count(u, back=2))
                        nc.scalar.copy(logit[b][:, :, :].rearrange("p t e -> p (t e)"), ps_logit).then_inc(logit_ready.sem, 1)
                    if n[TURN] is not None:
                        norm_rows_scalar(nc, act, nm, sh, n[TURN], par[TURN], turned)
                    for t in range(TILES):
                        if n[SCALE] is not None:
                            u, b = n[SCALE], par[SCALE]
                            act.wait_ge(wT_done.sem, wT_done.count(u, t + 1))
                            act.wait_ge(beta_done.sem, beta_done.count(u, t - 1))
                            nc.scalar.copy(wT[t % 2][:, :], ps_wT).then_inc(wT_ready.sem, 1)
                        if n[HID] is not None:
                            u, b = n[HID], par[HID]
                            for e in (2 * t, 2 * t + 1):
                                act.wait_ge(hid_done.sem, hid_done.count(u, e + 1))
                                act.wait_ge(y_done.sem, y_done.count(u, back=2))
                                nc.scalar.activation(hid[b][:, e, :], ps_hid[e % 2][:, 0:N], ACT.Relu,
                                                     bias=b1_sb[:, e:e + 1]).then_inc(hid_ready.sem, 1)
                            if t == 1:
                                act.wait_ge(gap_ready.sem, gap_ready.count(u))
                                act.wait_ge(gates_ready.sem, gates_ready.count(u, back=2))
                                nc.scalar.activation(egap[b][:, :], gap[b][:, :], ACT.Exp).then_inc(egap_ready.sem, 1)
                        if n[TURN] is not None and t == 1:
                            u, b = n[TURN], par[TURN]
                            act.wait_ge(turned.sem, turned.count(u))
                            act.wait_ge(hid_done.sem, hid_done.count(u, back=2))
                            nc.scalar.copy(hnT[b][:, :], ps_turn[:, 0:N]).then_inc(hnT_ready.sem, 1)
                        if n[SCALE] is not None:
                            u, b = n[SCALE], par[SCALE]
                            act.wait_ge(y_ready.sem, y_ready.count(u, t + 1))
                            if t < TILES - 2:
                                act.wait_ge(ss_ready.sem, ss_ready.count(u, 0))
                                nc.scalar.activation(sq[t % 2][:, :, :], yb[b][:, t, :, :], ACT.Square).then_inc(sq_ready.sem, 1)
                            else:
                                act.wait_ge(var_ready.sem, var_ready.count(u, back=2))
                                for e in range(EXP0):
                                    last = nc.scalar.activation(own_sq[t % 2][:, e, :], yb[b][:, t, e, :], ACT.Square,
                                                                accum_out=ss[b][:, t, e:e + 1])
                                last.then_inc(last_ss_ready.sem, 1)

                in_lanes(act, UNITS, STAGES, body)

            @block.vector
            def _(dve):
                for x in (nm.stats, nm.moments, top_ready, at_ready, atf_ready, gap_ready, den_ready, gate0_ready,
                          gates_ready, hot_ready, hot_scaled, w_ready, y_ready, ss_ready, acc_begun, acc_steps):
                    x.opened(dve)
                dve.wait_ge(weights_in, 16 * WEIGHTS)
                nc.vector.tensor_reduce(means[:, 0, :], w2_sb[:, :, :], AX.X, ALU.add)
                nc.vector.tensor_reduce(means[:, 1, :], b2_sb[:, :, :], AX.X, ALU.add).then_inc(means_ready, 1)
                dve.wait_ge(means_ready, 1)
                nc.vector.tensor_scalar(means[:, :, :], means[:, :, :], 1.0 / D, None, ALU.mult).then_inc(means_ready, 1)
                dve.wait_ge(means_ready, 2)
                for i, x in enumerate((w2_sb, b2_sb)):
                    nc.vector.tensor_tensor(x[:, :, :], x[:, :, :], wide(means[:, i, :], D), ALU.subtract).then_inc(centred, 1)
                dve.wait_ge(centred, 2)

                def sum_squares(u, b, t):
                    dve.wait_ge(sq_ready.sem, sq_ready.count(u, t + 1))
                    if t == 0:
                        dve.wait_ge(var_ready.sem, var_ready.count(u, back=2))
                    nc.vector.tensor_reduce(ss[b][:, t, :], sq[t % 2][:, :, :], AX.X, ALU.add).then_inc(ss_ready.sem, 1)

                def add_experts(u, b, experts):
                    for e in experts:
                        if e == 0:
                            dve.wait_ge(yg_ready.sem, yg_ready.count(u))
                            dve.wait_ge(s_ready.sem, s_ready.count(u))
                            dve.wait_ge(acc_begun.sem, acc_begun.count(u))
                        else:
                            dve.wait_ge(acc_steps.sem, acc_steps.count(u, e))
                        for t in range(TILES):
                            last = nc.vector.scalar_tensor_tensor(acc[b][:, t, :], yg[b][:, t, e, :], s[b][:, t, e:e + 1],
                                                                  acc[b][:, t, :], ALU.mult, ALU.add)
                        last.then_inc(acc_steps.sem, 1)

                def body(n, par):
                    if n[HID] is not None:
                        u, b = n[HID], par[HID]
                        dve.wait_ge(logit_ready.sem, logit_ready.count(u))
                        dve.wait_ge(atf_ready.sem, atf_ready.count(u, back=2))
                        dve.sem_inc(dve_passed, 1)
                        for t in range(TILES):
                            last = nc.vector.max(top[b][:, t, :], logit[b][:, t, :])
                        last.then_inc(top_ready.sem, 1)
                        dve.wait_ge(top_ready.sem, top_ready.count(u))
                        nc.vector.tensor_tensor(gap[b][:, :], top[b][:, :, 1], top[b][:, :, 0], ALU.subtract).then_inc(gap_ready.sem, 1)
                        for t in range(TILES):
                            last = nc.vector.max_index(at[b][:, t, :], top[b][:, t, :], logit[b][:, t, :])
                        last.then_inc(at_ready.sem, 1)
                    for t in range(TILES):
                        if t == 2 and n[OUT] is not None:
                            u, b = n[OUT], par[OUT]
                            dve.wait_ge(hot_scaled.sem, hot_scaled.count(u))
                            dve.wait_ge(s_ready.sem, s_ready.count(u, back=2))
                            dve.wait_ge(wT_done.sem, wT_done.count(u, back=2))
                            nc.vector.tensor_tensor(w[b][:, :, :], hot[b][:, 0, :, :], hot[b][:, 1, :, :], ALU.add).then_inc(w_ready.sem, 1)
                        if n[OUT] is not None:
                            u, b = n[OUT], par[OUT]
                            dve.wait_ge(y_done.sem, y_done.count(u, t + 1))
                            dve.wait_ge(ss_ready.sem, ss_ready.count(u, back=2))
                            dve.wait_ge(last_ss_ready.sem, last_ss_ready.count(u, back=2))
                            dve.wait_ge(yg_ready.sem, yg_ready.count(u, back=2))
                            nc.vector.tensor_tensor(yb[b][:, t, :, :].rearrange("p e d -> p (e d)"),
                                                    ps_y[t % 2][0:HALF, :, :].rearrange("p k x -> p (k x)"),
                                                    b2_sb[0:HALF, :, :].rearrange("p e d -> p (e d)"), ALU.add).then_inc(y_ready.sem, 1)
                        if n[SCALE] is not None:
                            u, b = n[SCALE], par[SCALE]
                            if t == 0:
                                dve.wait_ge(res_in[b].sem, res_in[b].count(u, b))
                                dve.wait_ge(stored[b].sem, stored[b].count(u, b, back=1))
                            dve.wait_ge(beta_done.sem, beta_done.count(u, t + 1))
                            nc.vector.tensor_tensor(acc[b][:, t, :], ps_beta, res[b][:, t, :], ALU.add).then_inc(acc_begun.sem, 1)
                        if n[HID] is not None:
                            u, b = n[HID], par[HID]
                            if t == 0:
                                dve.wait_ge(at_ready.sem, at_ready.count(u))
                                nc.vector.tensor_copy(atf[b][:, :, :], at[b][:, :, 0:2]).then_inc(atf_ready.sem, 1)
                            if t == 1:
                                dve.wait_ge(atf_ready.sem, atf_ready.count(u))
                                for k in range(2):
                                    last = nc.vector.tensor_tensor(hot[b][:, k, :, :], over(iota[0:HALF, :], TILES),
                                                                   wide(atf[b][:, :, k], EXP0), ALU.is_equal)
                                last.then_inc(hot_ready.sem, 1)
                            if t == 2:
                                dve.wait_ge(egap_ready.sem, egap_ready.count(u))
                                nc.vector.tensor_scalar(den[b][:, :], egap[b][:, :], 1.0, None, ALU.add).then_inc(den_ready.sem, 1)
                                dve.wait_ge(den_ready.sem, den_ready.count(u))
                                nc.vector.reciprocal(gate[b][:, 0, :], den[b][:, :]).then_inc(gate0_ready.sem, 1)
                                dve.wait_ge(gate0_ready.sem, gate0_ready.count(u))
                                nc.vector.tensor_tensor(gate[b][:, 1, :], gate[b][:, 0, :], egap[b][:, :], ALU.mult).then_inc(gates_ready.sem, 1)
                        if n[NORM] is not None and t < 2:
                            u, b = n[NORM], par[NORM]
                            if t == 0:
                                dve.wait_ge(x_in[b].sem, x_in[b].count(u, b))
                                dve.wait_ge(nm.ready.sem, nm.ready.count(u, back=2))
                            norm_moments(nc, dve, nm, u, b, 2 * t, dve_passed)
                            norm_moments(nc, dve, nm, u, b, 2 * t + 1, dve_passed)
                        if n[SUM] is not None:
                            add_experts(n[SUM], par[SUM], ((0,), (1,), (2, 3), (4, 5, 6, 7))[t])
                        if n[SCALE] is not None and t in (1, 2):
                            sum_squares(n[SCALE], par[SCALE], t - 1)
                    if n[HID] is not None:
                        u, b = n[HID], par[HID]
                        dve.wait_ge(gates_ready.sem, gates_ready.count(u))
                        dve.wait_ge(hot_ready.sem, hot_ready.count(u))
                        for k in range(2):
                            last = nc.vector.tensor_tensor(hot[b][:, k, :, :], hot[b][:, k, :, :],
                                                           wide(gate[b][:, k, :], EXP0), ALU.mult)
                        last.then_inc(hot_scaled.sem, 1)

                in_lanes(dve, UNITS, STAGES, body)

            @block.gpsimd
            def _(pool):
                for x in (nm.var_eps, nm.rstd_ready, sh.product, sh.ready, var_ready, yrstd_ready, s_ready, yg_ready):
                    x.opened(pool)
                nc.gpsimd.memset(eps[:, :], EPS)
                nc.gpsimd.memset(minus_half[:, :], -0.5).then_inc(constants_set, 1)
                pool.wait_ge(constants_set, 1)
                pool.wait_ge(weights_in, 16 * WEIGHTS)

                def body(n, par):
                    for t in range(TILES):
                        if n[SCALE] is not None:
                            u, b = n[SCALE], par[SCALE]
                            pool.wait_ge(y_ready.sem, y_ready.count(u, t + 1))
                            pool.wait_ge(acc_steps.sem, acc_steps.count(u, back=2))
                            nc.gpsimd.tensor_tensor(yg[b][:, t, :, :], yb[b][:, t, :, :], gam[0:HALF, :, :], ALU.mult).then_inc(yg_ready.sem, 1)
                    if n[NORM] is not None:
                        norm_scales(nc, pool, nm, sh, n[NORM], par[NORM], eps, minus_half, pool_passed)
                    if n[SCALE] is not None:
                        u, b = n[SCALE], par[SCALE]
                        pool.wait_ge(ss_ready.sem, ss_ready.count(u))
                        pool.wait_ge(last_ss_ready.sem, last_ss_ready.count(u))
                        pool.wait_ge(acc_steps.sem, acc_steps.count(u, back=2))
                        pool.sem_inc(pool_passed, 1)
                        weights = s[b][:, :, :].rearrange("p t e -> p (t e)")
                        nc.gpsimd.tensor_scalar(weights, ss[b][:, :, :].rearrange("p t e -> p (t e)"), 1.0 / D, EPS,
                                                ALU.mult, ALU.add).then_inc(var_ready.sem, 1)
                        pool.wait_ge(var_ready.sem, var_ready.count(u))
                        nc.gpsimd.tensor_tensor(weights, weights, minus_half[0:HALF, :], ALU.pow).then_inc(yrstd_ready.sem, 1)
                        pool.wait_ge(yrstd_ready.sem, yrstd_ready.count(u))
                        nc.gpsimd.tensor_tensor(weights, weights, w[b][:, :, :].rearrange("p t e -> p (t e)"), ALU.mult).then_inc(s_ready.sem, 1)

                in_lanes(pool, UNITS, STAGES, body)

        pl.close()


def phase_linear_attention(nc, h_in, ident, mask, blocks, head_mask, index, wq, wk, wv, bqk, bv, decay, wo, bo, ln_g, ln_b, h_out):
    UNITS = BATCH // 2
    TILES = 4
    N = TILES * HALF
    NORM, TURN, PROJ, PROD, VAL, OUT, FIN = range(7)
    STAGES = 7
    PAIRS = N_HEAD
    with ExitStack() as ctx:
        pl = Place(nc, ctx, "lin")
        sb, sem = pl.sb, pl.sem
        idn = sb("ident", [P, P])
        msk = sb("mask", [HALF, SEQ])
        blk = sb("blocks", [P, P])
        heads = sb("heads", [P, N_HEAD])
        wqk_sb = sb("wqk", [D, 2, D])
        wv_sb = sb("wv", [D, D])
        wo_sb = sb("wo", [D, D])
        bqk_sb = sb("bqk", [P, 2])
        rows = sb("rows", [P, 4, D])
        lam = sb("lam", [P, 1])
        idx = sb("idx", [P, P])
        powers = sb("powers", [P, P])
        dec = sb("dec", [P, 2, SEQ])
        eps = sb("eps", [P, TILES])
        minus_half = sb("minus_half", [P, TILES])

        def two(name, shape, dt=F32):
            return [sb(f"{name}{b}", shape, dt) for b in range(2)]

        nm = Norm(pl, TILES, HALF)
        hnT = two("hnT", [D, N])
        ex = two("ex", [P, N])
        rel = two("rel", [P, N])
        qk = [two("q", [P, N]), two("k", [P, N])]
        qh = sb("qh", [P, N_HEAD, N])
        kt = sb("kt", [HALF, TILES, D])
        sums = two("sums", [P, 2, D])
        qsum = sb("qsum", [P, N])
        inv = two("inv", [P, N])
        v = two("v", [HALF, TILES, N_HEAD, D + E_HEAD])
        prod = sb("prod", [HALF, PAIRS, 2, 2, HALF])
        oT = sb("oT", [D, N])
        z = two("z", [HALF, TILES, D])
        zst = two("zst", [HALF, TILES, 6])
        zmv = two("zmv", [HALF, TILES, 2])
        zrstd = two("zrstd", [HALF, TILES])
        zn = two("zn", [HALF, TILES, D])
        res = two("res", [HALF, TILES, D])
        out = two("out", [HALF, TILES, D])

        ps_proj, ps_kt, ps_den, ps_out = pl.banks("x", 4)
        ps_prod, ps_o = pl.banks("prod", 2), pl.banks("o", 2)

        weights_in = sem("weights_in")
        WEIGHTS = 15
        constants_set = sem("constants_set")
        zeros_set = sem("zeros_set")
        setup = sem("setup")
        exp_decay = sem("exp_decay")
        powers_ready = sem("powers_ready")
        dve_passed, pool_passed = (sem(f"{e}_passed") for e in ("dve", "pool"))
        x_in = [Landed(sem(f"x_in{b}"), 2) for b in range(2)]
        res_in = [Landed(sem(f"res_in{b}"), 2) for b in range(2)]
        stored = [Landed(sem(f"stored{b}"), 2) for b in range(2)]
        turned = Signal(sem("turned"))
        hnT_ready = Signal(sem("hnT_ready"))
        proj_done = Signal(sem("proj_done"), 2)
        proj_read = Signal(sem("proj_read"), 2)
        feature_ready = Signal(sem("feature_ready"), 2)
        qk_ready = Signal(sem("qk_ready"), 2)
        qh_ready = Signal(sem("qh_ready"), 4)
        v_done = Signal(sem("v_done"))
        v_ready = Signal(sem("v_ready"))
        kt_done = Signal(sem("kt_done"))
        kt_ready = Signal(sem("kt_ready"))
        sums_done = Signal(sem("sums_done"))
        sums_ready = Signal(sem("sums_ready"))
        ksum_done = Signal(sem("ksum_done"))
        qsum_ready = Signal(sem("qsum_ready"))
        den_done = Signal(sem("den_done"))
        den_read = Signal(sem("den_read"))
        inv_ready = Signal(sem("inv_ready"))
        prod_done = Signal(sem("prod_done"), PAIRS)
        prod_ready = Signal(sem("prod_ready"), PAIRS)
        cross_done = Signal(sem("cross_done"))
        val_done = Signal(sem("val_done"), PAIRS)
        oT_ready = Signal(sem("oT_ready"))
        z_done = Signal(sem("z_done"))
        z_ready = Signal(sem("z_ready"))
        zstats = Signal(sem("zstats"), TILES)
        zmoments = Signal(sem("zmoments"), TILES)
        zvar_eps = Signal(sem("zvar_eps"))
        zrstd_ready = Signal(sem("zrstd_ready"))
        zn_ready = Signal(sem("zn_ready"))
        zg_ready = Signal(sem("zg_ready"))
        zb_ready = Signal(sem("zb_ready"))
        out_ready = Signal(sem("out_ready"))

        with nc.Block() as block:

            @block.sync
            def _(sp):
                for dst, src in ((idn[:, :], ident), (msk[:, :], mask), (blk[:, :], blocks), (heads[:, :], head_mask),
                                 (wqk_sb[:, 0, :], wq), (wqk_sb[:, 1, :], wk), (wv_sb[:, :], wv), (wo_sb[:, :], wo),
                                 (bqk_sb[:, :], bqk), (lam[:, :], decay), (idx[:, :], index),
                                 (rows[:, 0, :], bv.partition_broadcast(P)), (rows[:, 1, :], bo.partition_broadcast(P)),
                                 (rows[:, 2, :], ln_g.partition_broadcast(P)), (rows[:, 3, :], ln_b.partition_broadcast(P))):
                    sp.dma_start(dst, src).then_inc(weights_in, 16)
                for b in range(2):
                    x_in[b].opened(sp)
                    res_in[b].opened(sp)
                    stored[b].opened(sp)

                def body(n, par):
                    if n[NORM] is not None:
                        u, b = n[NORM], par[NORM]
                        sp.wait_ge(nm.ready.sem, nm.ready.count(u, back=2))
                        load_rows(sp, nm.x[b], h_in, u, x_in[b])
                    if n[OUT] is not None:
                        u, b = n[OUT], par[OUT]
                        sp.wait_ge(out_ready.sem, out_ready.count(u, back=2))
                        load_rows(sp, res[b], h_in, u, res_in[b])
                    if n[FIN] is not None:
                        u, b = n[FIN], par[FIN]
                        sp.wait_ge(out_ready.sem, out_ready.count(u))
                        store_rows(sp, h_out, out[b], u, stored[b])

                in_lanes(sp, UNITS, STAGES, body)
                for b in range(2):
                    sp.wait_ge(stored[b].sem, stored[b].final(UNITS))

            @block.tensor
            def _(pe):
                for x in (turned, proj_done, v_done, kt_done, sums_done, ksum_done, den_done, prod_done, cross_done, val_done, z_done):
                    x.opened(pe)
                pe.wait_ge(weights_in, 16 * WEIGHTS)

                def project(u, b, i):
                    if i == 0:
                        pe.wait_ge(hnT_ready.sem, hnT_ready.count(u))
                        pe.wait_ge(v_ready.sem, v_ready.count(u, back=1))
                    else:
                        pe.wait_ge(proj_read.sem, proj_read.count(u, 1))
                    nc.tensor.matmul(ps_proj[:, 0:N], wqk_sb[:, i, :], hnT[b][:, :], start=True, stop=True).then_inc(proj_done.sem, 1)

                def turn(u, b):
                    pe.wait_ge(nm.ready.sem, nm.ready.count(u))
                    pe.wait_ge(proj_read.sem, proj_read.count(u, back=1))
                    for t in range(TILES):
                        last = nc.tensor.transpose(ps_proj[:, t * HALF:(t + 1) * HALF], nm.y[b][:, t, :], idn[0:HALF, 0:HALF])
                    last.then_inc(turned.sem, 1)

                def project_v(u, b, turning):
                    pe.wait_ge(proj_read.sem, proj_read.count(u))
                    if turning is not None:
                        pe.wait_ge(hnT_ready.sem, hnT_ready.count(turning))
                    for t in range(TILES):
                        last = nc.tensor.matmul(ps_proj[0:HALF, t * D:(t + 1) * D], hnT[b][:, t * HALF:(t + 1) * HALF], wv_sb[:, :],
                                                start=True, stop=True)
                    last.then_inc(v_done.sem, 1)

                def turn_k(u, b):
                    pe.wait_ge(sums_ready.sem, sums_ready.count(u, back=1))
                    for t in range(TILES):
                        last = nc.tensor.transpose(ps_kt[0:HALF, t * D:(t + 1) * D], qk[1][b][:, t * HALF:(t + 1) * HALF], idn[:, :])
                    last.then_inc(kt_done.sem, 1)

                def running_k(u):
                    pe.wait_ge(kt_ready.sem, kt_ready.count(u))
                    pe.wait_ge(den_read.sem, den_read.count(u, back=1))
                    for seq in range(2):
                        at = seq * SEQ
                        nc.tensor.matmul(ps_den[:, at:at + SEQ], kt[:, 2 * seq, :], msk[:, :], start=True, stop=False)
                        last = nc.tensor.matmul(ps_den[:, at + HALF:at + SEQ], kt[:, 2 * seq + 1, :], msk[:, 0:HALF], start=False, stop=True)
                    last.then_inc(ksum_done.sem, 1)

                def sum_kv(u, b):
                    pe.wait_ge(v_ready.sem, v_ready.count(u))
                    for seq in range(2):
                        last = nc.tensor.matmul(ps_kt[:, seq * D:(seq + 1) * D].rearrange("p (h e) -> p h e", e=E_HEAD), kt[:, 2 * seq, :],
                                                v[b][:, 2 * seq, :, 0:E_HEAD], start=True, stop=True)
                    last.then_inc(sums_done.sem, 1)

                def denominators(u):
                    pe.wait_ge(qsum_ready.sem, qsum_ready.count(u))
                    nc.tensor.matmul(ps_den[:, 0:N], blk[:, :], qsum[:, :], start=True, stop=True).then_inc(den_done.sem, 1)

                def products(u, b, x):
                    seq = x // 4
                    if x == 0:
                        pe.wait_ge(qk_ready.sem, qk_ready.count(u))
                    if x < 4:
                        pe.wait_ge(qh_ready.sem, qh_ready.count(u, x + 1))
                    pe.wait_ge(prod_ready.sem, prod_ready.count(u, x - 1))
                    for i in range(2):
                        for c in range(2):
                            at = (2 * seq + c) * HALF
                            last = nc.tensor.matmul(ps_prod[x % 2][0:HALF, (2 * i + c) * HALF:(2 * i + c + 1) * HALF], qk[1][b][:, at:at + HALF],
                                                    qh[:, 2 * (x % 4) + i, at:at + HALF], start=True, stop=True)
                    last.then_inc(prod_done.sem, 1)

                def cross(u, b):
                    pe.wait_ge(sums_ready.sem, sums_ready.count(u))
                    pe.wait_ge(oT_ready.sem, oT_ready.count(u, back=2))
                    for seq in range(2):
                        at = seq * SEQ + HALF
                        last = nc.tensor.matmul(ps_o[b][:, at:at + HALF], sums[b][:, seq, :], qk[0][b][:, at:at + HALF], start=seq == 0, stop=False)
                    last.then_inc(cross_done.sem, 1)

                def values(u, b, x):
                    seq = x // 4
                    pe.wait_ge(prod_ready.sem, prod_ready.count(u, x + 1))
                    for i in range(2):
                        h = 2 * (x % 4) + i
                        for c in range(2):
                            at = (2 * seq + c) * HALF
                            by_head = v[b][:, 2 * seq + c, :, :].rearrange("p h x -> p (h x)")
                            last = nc.tensor.matmul(ps_o[b][:, at:at + HALF], by_head[:, h * D:(h + 1) * D], prod[:, x, i, c, :],
                                                    start=False, stop=x == PAIRS - 1 and i == 1 and c == 1)
                    last.then_inc(val_done.sem, 1)

                def output(u):
                    pe.wait_ge(oT_ready.sem, oT_ready.count(u))
                    pe.wait_ge(z_ready.sem, z_ready.count(u, back=1))
                    for t in range(TILES):
                        last = nc.tensor.matmul(ps_out[0:HALF, t * D:(t + 1) * D], oT[:, t * HALF:(t + 1) * HALF], wo_sb[:, :], start=True, stop=True)
                    last.then_inc(z_done.sem, 1)

                def body(n, par):
                    if n[VAL] is not None:
                        cross(n[VAL], par[VAL])
                    for x in range(PAIRS):
                        if n[PROD] is not None:
                            products(n[PROD], par[PROD], x)
                        if n[VAL] is not None:
                            values(n[VAL], par[VAL], x)
                        if n[PROJ] is not None and x < 2:
                            project(n[PROJ], par[PROJ], x)
                        if n[PROD] is not None:
                            if x == 0:
                                turn_k(n[PROD], par[PROD])
                            if x == 2:
                                running_k(n[PROD])
                                sum_kv(n[PROD], par[PROD])
                            if x == 5:
                                denominators(n[PROD])
                        if n[OUT] is not None and x == 1:
                            output(n[OUT])
                        if n[TURN] is not None and x == 4:
                            turn(n[TURN], par[TURN])
                    if n[PROJ] is not None:
                        project_v(n[PROJ], par[PROJ], n[TURN])

                in_lanes(pe, UNITS, STAGES, body)

            @block.scalar
            def _(act):
                for x in (hnT_ready, proj_read, kt_ready, qh_ready):
                    x.opened(act)
                act.wait_ge(weights_in, 16 * WEIGHTS)
                nc.scalar.activation(lam[:, :], lam[:, :], ACT.Exp, scale=-1.0).then_inc(exp_decay, 1)

                def body(n, par):
                    for x in range(PAIRS):
                        if n[PROJ] is not None and x < 2:
                            u = n[PROJ]
                            act.wait_ge(proj_done.sem, proj_done.count(u, x + 1))
                            act.wait_ge(qk_ready.sem, qk_ready.count(u, x + 1, back=1))
                            nc.scalar.activation(ex[x][:, :], ps_proj[:, 0:N], ACT.Exp, bias=bqk_sb[:, x:x + 1])
                            nc.scalar.activation(rel[x][:, :], ps_proj[:, 0:N], ACT.Relu, bias=bqk_sb[:, x:x + 1]).then_inc(proj_read.sem, 1)
                        if n[PROD] is not None and x == 1:
                            u = n[PROD]
                            act.wait_ge(kt_done.sem, kt_done.count(u))
                            act.wait_ge(sums_done.sem, sums_done.count(u, back=1))
                            nc.scalar.copy(kt[:, :, :].rearrange("p t d -> p (t d)"), ps_kt[0:HALF, :]).then_inc(kt_ready.sem, 1)
                        if n[TURN] is not None and x == 4:
                            u, b = n[TURN], par[TURN]
                            act.wait_ge(turned.sem, turned.count(u))
                            act.wait_ge(v_done.sem, v_done.count(u, back=2))
                            nc.scalar.copy(hnT[b][:, :], ps_proj[:, 0:N]).then_inc(hnT_ready.sem, 1)
                        if n[PROJ] is not None and x >= 4:
                            u, b, pair = n[PROJ], par[PROJ], x - 4
                            if pair == 0:
                                act.wait_ge(qk_ready.sem, qk_ready.count(u, 1))
                            act.wait_ge(prod_done.sem, prod_done.count(u, x + 1, back=1))
                            for h in (2 * pair, 2 * pair + 1):
                                last = nc.scalar.activation(qh[:, h, :], qk[0][b][:, :], ACT.Copy, scale=heads[:, h:h + 1])
                            last.then_inc(qh_ready.sem, 1)

                in_lanes(act, UNITS, STAGES, body)

            @block.vector
            def _(dve):
                for x in (nm.stats, nm.moments, feature_ready, v_ready, sums_ready, qsum_ready, den_read, inv_ready, prod_ready,
                          oT_ready, z_ready, zstats, zmoments, out_ready):
                    x.opened(dve)
                for b in range(2):
                    nc.vector.memset(v[b][:, :, :, :], 0.0).then_inc(zeros_set, 1)
                dve.wait_ge(exp_decay, 1)
                nc.vector.tensor_scalar(lam[:, :], lam[:, :], 1.0, None, ALU.add).then_inc(setup, 1)
                dve.wait_ge(setup, 1)
                nc.vector.reciprocal(lam[:, :], lam[:, :]).then_inc(setup, 1)
                dve.wait_ge(setup, 2)
                nc.vector.tensor_scalar(lam[:, :], lam[:, :], 0.01, 0.99, ALU.mult, ALU.add).then_inc(setup, 1)
                dve.wait_ge(powers_ready, 1)
                nc.vector.tensor_copy(dec[:, 0, 0:HALF], powers[:, 0:HALF])
                nc.vector.tensor_scalar(dec[:, 0, HALF:SEQ], powers[:, 0:HALF], powers[:, HALF:P], None, ALU.mult).then_inc(setup, 1)
                dve.wait_ge(setup, 4)
                nc.vector.reciprocal(dec[:, 1, :], dec[:, 0, :]).then_inc(setup, 1)
                dve.wait_ge(setup, 5)
                nc.vector.tensor_scalar(dec[:, 0, :], dec[:, 0, :], E_HEAD ** -0.5, None, ALU.mult).then_inc(setup, 1)
                dve.wait_ge(zeros_set, 2)
                dve.wait_ge(weights_in, 16 * WEIGHTS)

                def body(n, par):
                    for x in range(PAIRS):
                        if n[PROD] is not None:
                            u = n[PROD]
                            dve.wait_ge(prod_done.sem, prod_done.count(u, x + 1))
                            dve.wait_ge(val_done.sem, val_done.count(u, x + 1, back=1))
                            nc.vector.tensor_tensor(prod[:, x, :, :, :].rearrange("p i c n -> p (i c) n"),
                                                    ps_prod[x % 2][0:HALF, 0:N].rearrange("p (x n) -> p x n", n=HALF),
                                                    over(msk[:, 0:HALF], 4), ALU.mult).then_inc(prod_ready.sem, 1)
                        if n[OUT] is not None:
                            u, b = n[OUT], par[OUT]
                            if x == 0:
                                dve.wait_ge(val_done.sem, val_done.count(u))
                                dve.wait_ge(inv_ready.sem, inv_ready.count(u))
                                dve.wait_ge(z_done.sem, z_done.count(u, back=1))
                                nc.vector.tensor_tensor(oT[:, :], ps_o[b][:, 0:N], inv[b][:, :], ALU.mult).then_inc(oT_ready.sem, 1)
                            if x == 2:
                                dve.wait_ge(z_done.sem, z_done.count(u))
                                dve.wait_ge(zn_ready.sem, zn_ready.count(u, back=2))
                                nc.vector.tensor_tensor(z[b][:, :, :], ps_out[0:HALF, :].rearrange("p (t d) -> p t d", t=TILES),
                                                        over(rows[0:HALF, 1, :], TILES), ALU.add).then_inc(z_ready.sem, 1)
                            if x == 3:
                                dve.wait_ge(z_ready.sem, z_ready.count(u))
                                for t in range(TILES):
                                    nc.vector.bn_stats(zst[b][:, t, :], z[b][:, t, :]).then_inc(zstats.sem, 1)
                            if x == 4:
                                dve.wait_ge(zstats.sem, zstats.count(u))
                                dve.sem_inc(dve_passed, 1)
                                for t in range(TILES):
                                    nc.vector.bn_aggr(zmv[b][:, t, :], zst[b][:, t, :]).then_inc(zmoments.sem, 1)
                        if n[PROJ] is not None and x < 2:
                            u = n[PROJ]
                            dve.wait_ge(proj_read.sem, proj_read.count(u, x + 1))
                            nc.vector.scalar_tensor_tensor(ex[x][:, :], ex[x][:, :], 1.0, rel[x][:, :],
                                                           ALU.min, ALU.add).then_inc(feature_ready.sem, 1)
                        if n[PROD] is not None:
                            u, b = n[PROD], par[PROD]
                            if x == 3:
                                dve.wait_ge(ksum_done.sem, ksum_done.count(u))
                                dve.wait_ge(den_done.sem, den_done.count(u, back=1))
                                nc.vector.tensor_tensor(qsum[:, :], ps_den[:, 0:N], qk[0][b][:, :], ALU.mult).then_inc(qsum_ready.sem, 1)
                            if x == 4:
                                dve.wait_ge(sums_done.sem, sums_done.count(u))
                                dve.wait_ge(cross_done.sem, cross_done.count(u, back=2))
                                nc.vector.tensor_tensor(sums[b][:, :, :], ps_kt[:, 0:2 * D].rearrange("p (s d) -> p s d", s=2),
                                                        over(blk[:, :], 2), ALU.mult).then_inc(sums_ready.sem, 1)
                            if x == 6:
                                dve.wait_ge(den_done.sem, den_done.count(u))
                                dve.wait_ge(oT_ready.sem, oT_ready.count(u, back=2))
                                nc.vector.tensor_scalar(inv[b][:, :], ps_den[:, 0:N], 1e-6, None, ALU.add).then_inc(den_read.sem, 1)
                        if n[VAL] is not None and x == 1:
                            u, b = n[VAL], par[VAL]
                            dve.wait_ge(den_read.sem, den_read.count(u))
                            nc.vector.reciprocal(inv[b][:, :], inv[b][:, :]).then_inc(inv_ready.sem, 1)
                        if n[NORM] is not None and x % 2 == 0:
                            u, b, t = n[NORM], par[NORM], x // 2
                            if t == 0:
                                dve.wait_ge(x_in[b].sem, x_in[b].count(u, b))
                                dve.wait_ge(nm.ready.sem, nm.ready.count(u, back=2))
                            norm_moments(nc, dve, nm, u, b, t, dve_passed)
                    if n[PROJ] is not None:
                        u, b = n[PROJ], par[PROJ]
                        dve.wait_ge(v_done.sem, v_done.count(u))
                        dve.wait_ge(val_done.sem, val_done.count(u, back=2))
                        for t in range(TILES):
                            last = nc.vector.tensor_tensor(v[b][:, t, :, 0:E_HEAD], ps_proj[0:HALF, t * D:(t + 1) * D].rearrange("p (h e) -> p h e", e=E_HEAD),
                                                           rows[0:HALF, 0, :].rearrange("p (h e) -> p h e", e=E_HEAD), ALU.add)
                        last.then_inc(v_ready.sem, 1)
                    if n[FIN] is not None:
                        u, b = n[FIN], par[FIN]
                        dve.wait_ge(res_in[b].sem, res_in[b].count(u, b))
                        dve.wait_ge(zb_ready.sem, zb_ready.count(u))
                        dve.wait_ge(stored[b].sem, stored[b].count(u, b, back=1))
                        nc.vector.tensor_tensor(out[b][:, :, :], zn[b][:, :, :], res[b][:, :, :], ALU.add).then_inc(out_ready.sem, 1)

                in_lanes(dve, UNITS, STAGES, body)

            @block.gpsimd
            def _(pool):
                for x in (nm.var_eps, nm.rstd_ready, nm.ready, qk_ready, zvar_eps, zrstd_ready, zn_ready, zg_ready, zb_ready):
                    x.opened(pool)
                nc.gpsimd.memset(eps[:, :], EPS)
                nc.gpsimd.memset(minus_half[:, :], -0.5).then_inc(constants_set, 1)
                pool.wait_ge(constants_set, 1)
                pool.wait_ge(weights_in, 16 * WEIGHTS)
                pool.wait_ge(setup, 3)
                nc.gpsimd.tensor_tensor(powers[:, :], lam[:, :].to_broadcast([P, P]), idx[:, :], ALU.pow).then_inc(powers_ready, 1)

                def body(n, par):
                    for x in range(4):
                        if n[PROJ] is not None and x < 2:
                            u, b = n[PROJ], par[PROJ]
                            pool.wait_ge(feature_ready.sem, feature_ready.count(u, x + 1))
                            pool.wait_ge(prod_done.sem, prod_done.count(u, back=2))
                            pool.wait_ge(cross_done.sem, cross_done.count(u, back=2))
                            nc.gpsimd.tensor_tensor(qk[x][b][:, :].rearrange("p (s n) -> p s n", s=2),
                                                    ex[x][:, :].rearrange("p (s n) -> p s n", s=2),
                                                    over(dec[:, x, :], 2), ALU.mult).then_inc(qk_ready.sem, 1)
                        if n[FIN] is not None:
                            u, b = n[FIN], par[FIN]
                            if x == 0:
                                pool.wait_ge(zmoments.sem, zmoments.count(u))
                                nc.gpsimd.tensor_tensor(zrstd[b][:, :], zmv[b][:, :, 1], eps[0:HALF, :], ALU.add).then_inc(zvar_eps.sem, 1)
                                pool.wait_ge(zvar_eps.sem, zvar_eps.count(u))
                                nc.gpsimd.tensor_tensor(zrstd[b][:, :], zrstd[b][:, :], minus_half[0:HALF, :], ALU.pow).then_inc(zrstd_ready.sem, 1)
                            if x == 1:
                                pool.wait_ge(zrstd_ready.sem, zrstd_ready.count(u))
                                pool.wait_ge(out_ready.sem, out_ready.count(u, back=2))
                                pool.sem_inc(pool_passed, 1)
                                for t in range(TILES):
                                    last = nc.gpsimd.tensor_scalar(zn[b][:, t, :], z[b][:, t, :], zmv[b][:, t, 0:1], zrstd[b][:, t:t + 1],
                                                                   ALU.subtract, ALU.mult)
                                last.then_inc(zn_ready.sem, 1)
                            if x == 2:
                                pool.wait_ge(zn_ready.sem, zn_ready.count(u))
                                nc.gpsimd.tensor_tensor(zn[b][:, :, :], zn[b][:, :, :], over(rows[0:HALF, 2, :], TILES), ALU.mult).then_inc(zg_ready.sem, 1)
                            if x == 3:
                                pool.wait_ge(zg_ready.sem, zg_ready.count(u))
                                nc.gpsimd.tensor_tensor(zn[b][:, :, :], zn[b][:, :, :], over(rows[0:HALF, 3, :], TILES), ALU.add).then_inc(zb_ready.sem, 1)
                    if n[NORM] is not None:
                        norm_rows(nc, pool, nm, n[NORM], par[NORM], eps, minus_half, pool_passed, turned)

                pool.wait_ge(setup, 6)
                in_lanes(pool, UNITS, STAGES, body)

        pl.close()


def phase_attention(nc, h_in, ident, head_mask, wq, wk, wv, wo, g_col, b_col, y_dram, h_out):
    UNITS = BATCH // 2
    TILES = 4
    N = TILES * HALF
    NORM, TURN, PROJ, SOFT, VAL, FIN = range(6)
    STAGES = 6
    HEADS = 2 * N_HEAD
    with ExitStack() as ctx:
        pl = Place(nc, ctx, "att")
        sb, sem = pl.sb, pl.sem
        idn = sb("ident", [P, P])
        heads = sb("heads", [P, N_HEAD])
        wqk_sb = sb("wqk", [D, 2, D])
        wv_sb = sb("wv", [D, D])
        wo_sb = sb("wo", [D, D])
        gb = sb("gb", [P, 2])
        eps = sb("eps", [P, TILES])
        minus_half = sb("minus_half", [P, TILES])

        def two(name, shape, dt=F32):
            return [sb(f"{name}{b}", shape, dt) for b in range(2)]

        nm = Norm(pl, TILES, HALF)
        var2 = two("var2", [HALF, TILES])
        yn = two("yn", [HALF, TILES, D])
        hnT = two("hnT", [D, N])
        q = two("q", [D, N])
        k = sb("k", [D, N])
        kh = two("kh", [D, N_HEAD, N])
        least = two("least", [HALF, HEADS, 2])
        ex = sb("ex", [HALF, HEADS, 2, SEQ])
        total = two("total", [HALF, HEADS, 2])
        inv = sb("inv", [HALF, HEADS, 2])
        inv_wide = sb("inv_wide", [HALF, TILES, N_HEAD, E_HEAD])
        invT = two("invT", [D, SEQ])
        exT = two("exT", [HALF, 2, SEQ])
        v = two("v", [HALF, TILES, N_HEAD, D + E_HEAD])
        oT = two("oT", [D, SEQ])
        res = two("res", [HALF, TILES, D])
        out = two("out", [HALF, TILES, D])

        ps_proj, ps_out = pl.banks("x", 2)
        ps_sc, ps_exT, ps_o = pl.banks("sc", 2), pl.banks("exT", 2), pl.banks("o", 2)

        weights_in = sem("weights_in")
        WEIGHTS = 8
        zeros_set = sem("zeros_set")
        pool_set = sem("pool_set")
        dve_passed, pool_passed = sem("dve_passed"), sem("pool_passed")
        x_in = [Landed(sem(f"x_in{b}"), 2) for b in range(2)]
        res_in = [Landed(sem(f"res_in{b}"), 2) for b in range(2)]
        stored = [Landed(sem(f"stored{b}"), 2) for b in range(2)]
        y_out = [Landed(sem(f"y_out{b}"), 2) for b in range(2)]
        square_ready = Signal(sem("square_ready"))
        var2_ready = Signal(sem("var2_ready"))
        var2_eps = Signal(sem("var2_eps"))
        rstd2_ready = Signal(sem("rstd2_ready"))
        yn_ready = Signal(sem("yn_ready"))
        turned = Signal(sem("turned"))
        hnT_ready = Signal(sem("hnT_ready"))
        qk_done = Signal(sem("qk_done"), 2)
        qk_ready = Signal(sem("qk_ready"), 2)
        kh_ready = Signal(sem("kh_ready"))
        v_done = Signal(sem("v_done"))
        v_ready = Signal(sem("v_ready"))
        sc_done = Signal(sem("sc_done"), HEADS)
        least_ready = Signal(sem("least_ready"), HEADS)
        ex_ready = Signal(sem("ex_ready"), HEADS)
        ex_turned = Signal(sem("ex_turned"), HEADS)
        exT_ready = Signal(sem("exT_ready"), HEADS)
        val_done = Signal(sem("val_done"), HEADS)
        inv_ready = Signal(sem("inv_ready"))
        inv_wide_ready = Signal(sem("inv_wide_ready"))
        inv_turned = Signal(sem("inv_turned"), 2)
        invT_ready = Signal(sem("invT_ready"), 2)
        oT_ready = Signal(sem("oT_ready"), 2)
        z_done = Signal(sem("z_done"), 2)
        out_ready = Signal(sem("out_ready"), 2)

        with nc.Block() as block:

            @block.sync
            def _(sp):
                for dst, src in ((idn[:, :], ident), (heads[:, :], head_mask), (wqk_sb[:, 0, :], wq), (wqk_sb[:, 1, :], wk),
                                 (wv_sb[:, :], wv), (wo_sb[:, :], wo), (gb[:, 0:1], g_col), (gb[:, 1:2], b_col)):
                    sp.dma_start(dst, src).then_inc(weights_in, 16)
                for b in range(2):
                    x_in[b].opened(sp)
                    res_in[b].opened(sp)
                    stored[b].opened(sp)
                    y_out[b].opened(sp)

                def body(n, par):
                    if n[NORM] is not None:
                        u, b = n[NORM], par[NORM]
                        sp.wait_ge(nm.ready.sem, nm.ready.count(u, back=2))
                        load_rows(sp, nm.x[b], h_in, u, x_in[b])
                    if n[TURN] is not None:
                        u, b = n[TURN], par[TURN]
                        sp.wait_ge(nm.ready.sem, nm.ready.count(u))
                        store_rows(sp, y_dram, nm.y[b], u, y_out[b])
                    if n[VAL] is not None:
                        u, b = n[VAL], par[VAL]
                        sp.wait_ge(out_ready.sem, out_ready.count(u, back=2))
                        sp.wait_ge(y_out[b].sem, y_out[b].count(u, b))
                        load_rows(sp, res[b], y_dram, u, res_in[b])
                    if n[FIN] is not None:
                        u, b = n[FIN], par[FIN]
                        sp.wait_ge(out_ready.sem, out_ready.count(u))
                        store_rows(sp, h_out, out[b], u, stored[b])

                in_lanes(sp, UNITS, STAGES, body)
                for b in range(2):
                    sp.wait_ge(stored[b].sem, stored[b].final(UNITS))

            @block.tensor
            def _(pe):
                for x in (turned, qk_done, v_done, sc_done, ex_turned, val_done, inv_turned, z_done):
                    x.opened(pe)
                pe.wait_ge(weights_in, 16 * WEIGHTS)

                def project(u, b, i):
                    if i == 0:
                        pe.wait_ge(hnT_ready.sem, hnT_ready.count(u))
                        pe.wait_ge(v_ready.sem, v_ready.count(u, back=1))
                    else:
                        pe.wait_ge(qk_ready.sem, qk_ready.count(u, 1))
                    nc.tensor.matmul(ps_proj[:, 0:N], wqk_sb[:, i, :], hnT[b][:, :], start=True, stop=True).then_inc(qk_done.sem, 1)

                def turn(u, b):
                    pe.wait_ge(yn_ready.sem, yn_ready.count(u))
                    pe.wait_ge(qk_ready.sem, qk_ready.count(u, back=1))
                    for t in range(TILES):
                        last = nc.tensor.transpose(ps_proj[:, t * HALF:(t + 1) * HALF], yn[b][:, t, :], idn[0:HALF, 0:HALF])
                    last.then_inc(turned.sem, 1)

                def project_v(u, b, turning):
                    pe.wait_ge(qk_ready.sem, qk_ready.count(u))
                    if turning is not None:
                        pe.wait_ge(hnT_ready.sem, hnT_ready.count(turning))
                    for t in range(TILES):
                        last = nc.tensor.matmul(ps_proj[0:HALF, t * D:(t + 1) * D], hnT[b][:, t * HALF:(t + 1) * HALF], wv_sb[:, :],
                                                start=True, stop=True)
                    last.then_inc(v_done.sem, 1)

                def scores(u, b, x):
                    seq, h = x // N_HEAD, x % N_HEAD
                    if x == 0:
                        pe.wait_ge(kh_ready.sem, kh_ready.count(u))
                    pe.wait_ge(ex_ready.sem, ex_ready.count(u, x - 1))
                    for c in range(2):
                        at = seq * SEQ + c * HALF
                        last = nc.tensor.matmul(ps_sc[x % 2][0:HALF, c * SEQ:(c + 1) * SEQ], q[b][:, at:at + HALF],
                                                kh[b][:, h, seq * SEQ:(seq + 1) * SEQ], start=True, stop=True)
                    last.then_inc(sc_done.sem, 1)

                def turn_ex(u, x):
                    pe.wait_ge(ex_ready.sem, ex_ready.count(u, x + 1))
                    pe.wait_ge(exT_ready.sem, exT_ready.count(u, x - 1))
                    for half in range(2):
                        for c in range(2):
                            last = nc.tensor.transpose(ps_exT[x % 2][0:HALF, half * SEQ + c * HALF:half * SEQ + (c + 1) * HALF],
                                                       ex[:, x, c, half * HALF:(half + 1) * HALF], idn[0:HALF, 0:HALF])
                    last.then_inc(ex_turned.sem, 1)

                def values(u, b, x):
                    seq, h = x // N_HEAD, x % N_HEAD
                    pe.wait_ge(exT_ready.sem, exT_ready.count(u, x + 1))
                    if x == 0:
                        pe.wait_ge(v_ready.sem, v_ready.count(u))
                    if h == 0:
                        pe.wait_ge(oT_ready.sem, oT_ready.count(u, seq + 1, back=1))
                    for half in range(2):
                        by_head = v[b][:, 2 * seq + half, :, :].rearrange("p h x -> p (h x)")
                        last = nc.tensor.matmul(ps_o[seq][:, 0:SEQ], by_head[:, h * D:(h + 1) * D], exT[x % 2][:, half, :],
                                                start=h == 0 and half == 0, stop=h == N_HEAD - 1 and half == 1)
                    last.then_inc(val_done.sem, 1)

                def turn_inv(u, seq):
                    pe.wait_ge(inv_wide_ready.sem, inv_wide_ready.count(u))
                    pe.wait_ge(out_ready.sem, out_ready.count(u, seq))
                    for c in range(2):
                        last = nc.tensor.transpose(ps_out[:, c * HALF:(c + 1) * HALF],
                                                   inv_wide[:, 2 * seq + c, :, :].rearrange("p h e -> p (h e)"), idn[0:HALF, 0:HALF])
                    last.then_inc(inv_turned.sem, 1)

                def output(u, seq):
                    pe.wait_ge(oT_ready.sem, oT_ready.count(u, seq + 1))
                    for c in range(2):
                        last = nc.tensor.matmul(ps_out[0:HALF, 256 + c * D:256 + (c + 1) * D], oT[seq][:, c * HALF:(c + 1) * HALF],
                                                wo_sb[:, :], start=True, stop=True)
                    last.then_inc(z_done.sem, 1)

                def body(n, par):
                    for x in range(HEADS):
                        if n[SOFT] is not None:
                            scores(n[SOFT], par[SOFT], x)
                        if n[VAL] is not None:
                            turn_ex(n[VAL], x)
                        if x == 2 and n[FIN] is not None:
                            output(n[FIN], 1)
                        if x == 3 and n[PROJ] is not None:
                            project(n[PROJ], par[PROJ], 0)
                        if x == 6 and n[PROJ] is not None:
                            project(n[PROJ], par[PROJ], 1)
                        if x == 9 and n[TURN] is not None:
                            turn(n[TURN], par[TURN])
                        if n[VAL] is not None:
                            u = n[VAL]
                            if x > 0:
                                values(u, par[VAL], x - 1)
                            if x == 5:
                                turn_inv(u, 0)
                            if x == 10:
                                output(u, 0)
                            if x == 13:
                                turn_inv(u, 1)
                    if n[VAL] is not None:
                        values(n[VAL], par[VAL], HEADS - 1)
                    if n[PROJ] is not None:
                        project_v(n[PROJ], par[PROJ], n[TURN])

                in_lanes(pe, UNITS, STAGES, body)

            @block.scalar
            def _(act):
                for x in (hnT_ready, qk_ready, ex_ready, v_ready, invT_ready):
                    x.opened(act)
                act.wait_ge(zeros_set, 2)
                act.wait_ge(weights_in, 16 * WEIGHTS)

                def read_inv(u, seq):
                    act.wait_ge(inv_turned.sem, inv_turned.count(u, seq + 1))
                    act.wait_ge(oT_ready.sem, oT_ready.count(u, seq + 1, back=1))
                    nc.scalar.copy(invT[seq][:, :], ps_out[:, 0:SEQ]).then_inc(invT_ready.sem, 1)

                def body(n, par):
                    for x in range(HEADS):
                        if n[SOFT] is not None:
                            u, b = n[SOFT], par[SOFT]
                            act.wait_ge(least_ready.sem, least_ready.count(u, x + 1))
                            act.wait_ge(ex_turned.sem, ex_turned.count(u, x + 1, back=1))
                            if x == 0:
                                act.wait_ge(inv_ready.sem, inv_ready.count(u, back=2))
                            for c in range(2):
                                last = nc.scalar.activation(ex[:, x, c, :], ps_sc[x % 2][0:HALF, c * SEQ:(c + 1) * SEQ], ACT.Exp,
                                                            bias=least[b][:, x, c:c + 1], scale=-1.0,
                                                            accum_out=total[b][:, x, c:c + 1])
                            last.then_inc(ex_ready.sem, 1)
                        if x == 4 and n[PROJ] is not None:
                            u, b = n[PROJ], par[PROJ]
                            act.wait_ge(qk_done.sem, qk_done.count(u, 1))
                            act.wait_ge(sc_done.sem, sc_done.count(u, back=2))
                            nc.scalar.activation(q[b][:, :], ps_proj[:, 0:N], ACT.Copy, scale=-E_HEAD ** -0.5).then_inc(qk_ready.sem, 1)
                        if x == 6 and n[VAL] is not None:
                            read_inv(n[VAL], 0)
                        if x == 7 and n[PROJ] is not None:
                            u, b = n[PROJ], par[PROJ]
                            act.wait_ge(qk_done.sem, qk_done.count(u, 2))
                            act.wait_ge(kh_ready.sem, kh_ready.count(u, back=1))
                            nc.scalar.copy(k[:, :], ps_proj[:, 0:N]).then_inc(qk_ready.sem, 1)
                        if x == 10 and n[TURN] is not None:
                            u, b = n[TURN], par[TURN]
                            act.wait_ge(turned.sem, turned.count(u))
                            act.wait_ge(v_done.sem, v_done.count(u, back=2))
                            nc.scalar.activation(hnT[b][:, :], ps_proj[:, 0:N], ACT.Identity, bias=gb[:, 1:2], scale=gb[:, 0:1]).then_inc(hnT_ready.sem, 1)
                        if x == 14 and n[VAL] is not None:
                            read_inv(n[VAL], 1)
                    if n[PROJ] is not None:
                        u, b = n[PROJ], par[PROJ]
                        act.wait_ge(v_done.sem, v_done.count(u))
                        act.wait_ge(val_done.sem, val_done.count(u, back=2))
                        nc.scalar.copy(v[b][:, :, :, 0:E_HEAD], ps_proj[0:HALF, :].rearrange("p (t h e) -> p t h e", t=TILES, e=E_HEAD)).then_inc(v_ready.sem, 1)

                in_lanes(act, UNITS, STAGES, body)

            @block.vector
            def _(dve):
                for x in (nm.stats, nm.moments, yn_ready, least_ready, exT_ready, inv_ready, inv_wide_ready, oT_ready, out_ready):
                    x.opened(dve)
                for b in range(2):
                    nc.vector.memset(v[b][:, :, :, :], 0.0).then_inc(zeros_set, 1)

                def scale_sums(u, seq):
                    dve.wait_ge(val_done.sem, val_done.count(u, N_HEAD * (seq + 1)))
                    dve.wait_ge(invT_ready.sem, invT_ready.count(u, seq + 1))
                    dve.wait_ge(z_done.sem, z_done.count(u, seq + 1, back=1))
                    nc.vector.tensor_tensor(oT[seq][:, :], ps_o[seq][:, 0:SEQ], invT[seq][:, :], ALU.mult).then_inc(oT_ready.sem, 1)

                def add_residual(u, b, seq):
                    if seq == 0:
                        dve.wait_ge(res_in[b].sem, res_in[b].count(u, b))
                        dve.wait_ge(stored[b].sem, stored[b].count(u, b, back=1))
                    dve.wait_ge(z_done.sem, z_done.count(u, seq + 1))
                    nc.vector.tensor_tensor(out[b][:, 2 * seq:2 * seq + 2, :], ps_out[0:HALF, 256:512].rearrange("p (t d) -> p t d", t=2),
                                            res[b][:, 2 * seq:2 * seq + 2, :], ALU.add).then_inc(out_ready.sem, 1)

                def body(n, par):
                    for x in range(HEADS):
                        if n[SOFT] is not None:
                            u, b = n[SOFT], par[SOFT]
                            dve.wait_ge(sc_done.sem, sc_done.count(u, x + 1))
                            if x == 0:
                                dve.wait_ge(ex_ready.sem, ex_ready.count(u, back=2))
                            nc.vector.tensor_reduce(least[b][:, x, :], ps_sc[x % 2][0:HALF, 0:N].rearrange("p (c n) -> p c n", c=2),
                                                    AX.X, ALU.min).then_inc(least_ready.sem, 1)
                        if n[VAL] is not None:
                            u, b = n[VAL], par[VAL]
                            dve.wait_ge(ex_turned.sem, ex_turned.count(u, x + 1))
                            dve.wait_ge(val_done.sem, val_done.count(u, x - 1))
                            nc.vector.tensor_copy(exT[x % 2][:, :, :].rearrange("p c n -> p (c n)"), ps_exT[x % 2][0:HALF, 0:N]).then_inc(exT_ready.sem, 1)
                            if x == 1:
                                dve.wait_ge(inv_wide_ready.sem, inv_wide_ready.count(u, back=1))
                                dve.wait_ge(ex_ready.sem, ex_ready.count(u))
                                nc.vector.reciprocal(inv[:, :, :].rearrange("p h c -> p (h c)"), total[b][:, :, :].rearrange("p h c -> p (h c)")).then_inc(inv_ready.sem, 1)
                            if x == 2:
                                dve.wait_ge(inv_ready.sem, inv_ready.count(u))
                                dve.wait_ge(inv_turned.sem, inv_turned.count(u, back=1))
                                by_tile = inv[:, :, :].rearrange("p (s h) c -> p s c h", s=2)
                                for seq in range(2):
                                    for c in range(2):
                                        last = nc.vector.tensor_copy(inv_wide[:, 2 * seq + c, :, :], wide(by_tile[:, seq, c, :], E_HEAD))
                                last.then_inc(inv_wide_ready.sem, 1)
                            if x == 9:
                                scale_sums(u, 0)
                            if x == 11:
                                add_residual(u, b, 0)
                        if x == 0 and n[FIN] is not None:
                            scale_sums(n[FIN], 1)
                        if x == 3 and n[FIN] is not None:
                            add_residual(n[FIN], par[FIN], 1)
                        if x == 5 and n[TURN] is not None:
                            u, b = n[TURN], par[TURN]
                            dve.wait_ge(rstd2_ready.sem, rstd2_ready.count(u))
                            dve.wait_ge(turned.sem, turned.count(u, back=2))
                            for t in range(TILES):
                                last = nc.vector.tensor_scalar(yn[b][:, t, :], nm.y[b][:, t, :], var2[b][:, t:t + 1], None, ALU.mult)
                            last.then_inc(yn_ready.sem, 1)
                        if n[NORM] is not None and x % 4 == 0:
                            u, b, t = n[NORM], par[NORM], x // 4
                            if t == 0:
                                dve.wait_ge(x_in[b].sem, x_in[b].count(u, b))
                                dve.wait_ge(rstd2_ready.sem, rstd2_ready.count(u, back=2))
                            norm_moments(nc, dve, nm, u, b, t, dve_passed)

                in_lanes(dve, UNITS, STAGES, body)

            @block.gpsimd
            def _(pool):
                for x in (nm.var_eps, nm.rstd_ready, nm.ready, square_ready, var2_ready, var2_eps, rstd2_ready, kh_ready):
                    x.opened(pool)
                nc.gpsimd.memset(eps[:, :], EPS)
                nc.gpsimd.memset(minus_half[:, :], -0.5).then_inc(pool_set, 1)
                pool.wait_ge(pool_set, 1)
                pool.wait_ge(weights_in, 16 * WEIGHTS)

                def body(n, par):
                    if n[PROJ] is not None:
                        u, b = n[PROJ], par[PROJ]
                        pool.wait_ge(qk_ready.sem, qk_ready.count(u))
                        pool.wait_ge(sc_done.sem, sc_done.count(u, back=2))
                        pool.sem_inc(pool_passed, 1)
                        for h in range(N_HEAD):
                            last = nc.gpsimd.tensor_scalar(kh[b][:, h, :], k[:, :], heads[:, h:h + 1], None, ALU.mult)
                        last.then_inc(kh_ready.sem, 1)
                    if n[NORM] is not None:
                        u, b = n[NORM], par[NORM]
                        pool.wait_ge(y_out[b].sem, y_out[b].count(u, b, back=1))
                        norm_rows(nc, pool, nm, u, b, eps, minus_half, pool_passed, yn_ready)
                        nc.gpsimd.tensor_tensor(var2[b][:, :], nm.rstd[b][:, :], nm.rstd[b][:, :], ALU.mult).then_inc(square_ready.sem, 1)
                        pool.wait_ge(square_ready.sem, square_ready.count(u))
                        nc.gpsimd.tensor_tensor(var2[b][:, :], var2[b][:, :], nm.mv[b][:, :, 1], ALU.mult).then_inc(var2_ready.sem, 1)
                        pool.wait_ge(var2_ready.sem, var2_ready.count(u))
                        nc.gpsimd.tensor_tensor(var2[b][:, :], var2[b][:, :], eps[0:HALF, :], ALU.add).then_inc(var2_eps.sem, 1)
                        pool.wait_ge(var2_eps.sem, var2_eps.count(u))
                        nc.gpsimd.tensor_tensor(var2[b][:, :], var2[b][:, :], minus_half[0:HALF, :], ALU.pow).then_inc(rstd2_ready.sem, 1)

                in_lanes(pool, UNITS, STAGES, body)

        pl.close()


def phase_router(nc, x_in_dram, ident, before, iota64, wr, g_col, b_col, slots, slot_dram, gate_dram):
    UNITS = BATCH // 2
    TILES = 4
    N = TILES * HALF
    E = EXP1
    FAR = 1 << 20
    LOAD, NORM, TURN, SOFT, GATE, PLACE, SCATTER = range(7)
    STAGES = 7
    with ExitStack() as ctx:
        pl = Place(nc, ctx, "rou")
        sb, sem = pl.sb, pl.sem
        idn = sb("ident", [P, P])
        bef = sb("before", [HALF, HALF])
        ones = sb("ones", [HALF, HALF])
        iota = sb("iota", [P, E])
        wr_sb = sb("wr", [D, E])
        gb = sb("gb", [P, 2])
        eps = sb("eps", [P, TILES])
        minus_half = sb("minus_half", [P, TILES])

        def two(name, shape, dt=F32):
            return [sb(f"{name}{b}", shape, dt) for b in range(2)]

        nm = Norm(pl, TILES, HALF)
        sh = Shift(pl, TILES, HALF)
        kept = two("kept", [HALF, TILES, D])
        going = two("going", [HALF, TILES, D])
        xT = two("xT", [D, N])
        best = two("best", [HALF, TILES])
        ex = two("ex", [HALF, TILES, E])
        total = two("total", [HALF, TILES])
        prob = two("prob", [HALF, TILES, E])
        top = two("top", [HALF, TILES, 8])
        at = two("at", [HALF, TILES, 8], U32)
        atf = two("atf", [HALF, 2, TILES])
        hot = two("hot", [HALF, 2, TILES, E])
        both = two("both", [HALF, TILES, E])
        count = two("count", [HALF, TILES, E])
        share = two("share", [HALF, TILES])
        gate = two("gate", [HALF, 2, TILES])
        mine = two("mine", [HALF, 2, TILES, E])
        pos = two("pos", [HALF, 2, TILES])
        late = two("late", [HALF, 2, TILES])
        base = two("base", [HALF, 2, TILES])
        near = two("near", [HALF, 2, TILES])
        row = two("row", [HALF, 2, TILES])
        row_u = two("row_u", [HALF, 2, TILES], U32)
        read_f = two("read_f", [HALF, 2, TILES])
        read_u = two("read_u", [HALF, 2, TILES], U32)
        gated = two("gated", [HALF, 2, TILES])

        ps_turn, ps_logit, ps_pos = pl.banks("x", 3)
        logit = ps_logit[0:HALF, 0:TILES * E].rearrange("p (t e) -> p t e", e=E)
        place = ps_pos[0:HALF, 0:TILES * E].rearrange("p (t e) -> p t e", e=E)

        weights_in = sem("weights_in")
        WEIGHTS = 6
        constants_set = sem("constants_set")
        counts_set = sem("counts_set")
        dve_passed, pool_passed = sem("dve_passed"), sem("pool_passed")
        x_in = [Landed(sem(f"x_in{b}"), 2) for b in range(2)]
        scattered = [Landed(sem(f"scattered{b}"), 2 * TILES, ahead=0) for b in range(2)]
        scatter_over = Signal(sem("scatter_over"))
        noted = [Landed(sem(f"noted{b}"), 2) for b in range(2)]
        turned = Signal(sem("turned"))
        xT_ready = Signal(sem("xT_ready"))
        kept_ready = Signal(sem("kept_ready"))
        going_ready = Signal(sem("going_ready"))
        logit_done = Signal(sem("logit_done"))
        best_ready = Signal(sem("best_ready"))
        shifted = Signal(sem("shifted"))
        ex_ready = Signal(sem("ex_ready"))
        total_ready = Signal(sem("total_ready"))
        inv_ready = Signal(sem("inv_ready"))
        prob_ready = Signal(sem("prob_ready"))
        top_ready = Signal(sem("top_ready"))
        at_ready = Signal(sem("at_ready"))
        atf_ready = Signal(sem("atf_ready"))
        hot_ready = Signal(sem("hot_ready"))
        both_ready = Signal(sem("both_ready"))
        share_ready = Signal(sem("share_ready"))
        share_inv = Signal(sem("share_inv"))
        gate_ready = Signal(sem("gate_ready"))
        count_ready = Signal(sem("count_ready"), TILES)
        place_done = Signal(sem("place_done"))
        mine_ready = Signal(sem("mine_ready"))
        pos_ready = Signal(sem("pos_ready"))
        late_ready = Signal(sem("late_ready"))
        row_ready = Signal(sem("row_ready"))
        row_u_ready = Signal(sem("row_u_ready"))
        notes_ready = Signal(sem("notes_ready"))

        with nc.Block() as block:

            @block.sync
            def _(sp):
                for dst, src in ((idn[:, :], ident), (bef[:, :], before), (iota[:, :], iota64), (wr_sb[:, :], wr),
                                 (gb[:, 0:1], g_col), (gb[:, 1:2], b_col)):
                    sp.dma_start(dst, src).then_inc(weights_in, 16)
                for b in range(2):
                    x_in[b].opened(sp)
                    noted[b].opened(sp)
                scatter_over.opened(sp)

                def body(n, par):
                    if n[LOAD] is not None:
                        u, b = n[LOAD], par[LOAD]
                        sp.wait_ge(nm.ready.sem, nm.ready.count(u, back=2))
                        load_rows(sp, nm.x[b], x_in_dram, u, x_in[b])
                    if n[SCATTER] is not None:
                        u, b = n[SCATTER], par[SCATTER]
                        sp.wait_ge(scattered[b].sem, scattered[b].count(u, b))
                        sp.sem_inc(scatter_over.sem, 1)
                    if n[PLACE] is not None:
                        u, b = n[PLACE], par[PLACE]
                        sp.wait_ge(notes_ready.sem, notes_ready.count(u))
                        sp.dma_start(slot_dram[bass.ds(u, 1), :, :].rearrange("u p x -> (u p) x"),
                                     read_u[b][:, :, :].rearrange("p k t -> p (k t)")).then_inc(noted[b].sem, 16)
                        sp.dma_start(gate_dram[bass.ds(u, 1), :, :].rearrange("u p x -> (u p) x"),
                                     gated[b][:, :, :].rearrange("p k t -> p (k t)")).then_inc(noted[b].sem, 16)

                in_lanes(sp, UNITS, STAGES, body)
                for b in range(2):
                    sp.wait_ge(noted[b].sem, noted[b].final(UNITS))
                    sp.wait_ge(scattered[b].sem, scattered[b].final(UNITS))

            @block.tensor
            def _(pe):
                for x in (turned, logit_done, place_done):
                    x.opened(pe)
                pe.wait_ge(weights_in, 16 * WEIGHTS)
                pe.wait_ge(counts_set, 3)

                def body(n, par):
                    if n[SOFT] is not None:
                        u, b = n[SOFT], par[SOFT]
                        pe.wait_ge(xT_ready.sem, xT_ready.count(u))
                        pe.wait_ge(shifted.sem, shifted.count(u, back=1))
                        for t in range(TILES):
                            last = nc.tensor.matmul(logit[:, t, :], xT[b][:, t * HALF:(t + 1) * HALF], wr_sb[:, :], start=True, stop=True)
                        last.then_inc(logit_done.sem, 1)
                    if n[PLACE] is not None:
                        u, b = n[PLACE], par[PLACE]
                        pe.wait_ge(count_ready.sem, count_ready.count(u))
                        pe.wait_ge(mine_ready.sem, mine_ready.count(u, back=1))
                        nc.tensor.matmul(place, bef[:, :], both[b][:, :, :], start=True, stop=False)
                        nc.tensor.matmul(place, ones[:, :], count[b][:, :, :], start=False, stop=True).then_inc(place_done.sem, 1)
                    if n[TURN] is not None:
                        u, b = n[TURN], par[TURN]
                        pe.wait_ge(nm.ready.sem, nm.ready.count(u))
                        pe.wait_ge(xT_ready.sem, xT_ready.count(u, back=1))
                        for t in range(TILES):
                            last = nc.tensor.transpose(ps_turn[:, t * HALF:(t + 1) * HALF], nm.y[b][:, t, :], idn[0:HALF, 0:HALF])
                        last.then_inc(turned.sem, 1)

                in_lanes(pe, UNITS, STAGES, body)

            @block.scalar
            def _(act):
                for x in (nm.ready, xT_ready, kept_ready, going_ready, ex_ready):
                    x.opened(act)
                act.wait_ge(weights_in, 16 * WEIGHTS)

                def body(n, par):
                    if n[TURN] is not None:
                        u, b = n[TURN], par[TURN]
                        act.wait_ge(kept_ready.sem, kept_ready.count(u, back=2))
                        norm_rows_scalar(nc, act, nm, sh, u, b, turned)
                    if n[PLACE] is not None:
                        u, b = n[PLACE], par[PLACE]
                        act.wait_ge(kept_ready.sem, kept_ready.count(u))
                        act.wait_ge(scatter_over.sem, scatter_over.count(u, back=2))
                        nc.scalar.copy(going[b][:, :, :], kept[b][:, :, :]).then_inc(going_ready.sem, 1)
                    if n[SOFT] is not None:
                        u, b = n[SOFT], par[SOFT]
                        act.wait_ge(going_ready.sem, going_ready.count(u, back=2))
                        act.wait_ge(nm.ready.sem, nm.ready.count(u))
                        nc.scalar.copy(kept[b][:, :, :], nm.y[b][:, :, :]).then_inc(kept_ready.sem, 1)
                    if n[SOFT] is not None:
                        u, b = n[SOFT], par[SOFT]
                        act.wait_ge(shifted.sem, shifted.count(u))
                        nc.scalar.activation(ex[b][:, :, :], ex[b][:, :, :], ACT.Exp).then_inc(ex_ready.sem, 1)
                    if n[TURN] is not None:
                        u, b = n[TURN], par[TURN]
                        act.wait_ge(turned.sem, turned.count(u))
                        act.wait_ge(logit_done.sem, logit_done.count(u, back=2))
                        nc.scalar.activation(xT[b][:, :], ps_turn[:, 0:N], ACT.Identity, bias=gb[:, 1:2], scale=gb[:, 0:1]).then_inc(xT_ready.sem, 1)

                in_lanes(act, UNITS, STAGES, body)

            @block.vector
            def _(dve):
                for x in (nm.stats, nm.moments, best_ready, shifted, total_ready, inv_ready, prob_ready, top_ready, at_ready,
                          atf_ready, hot_ready, both_ready, share_ready, share_inv, gate_ready, count_ready, mine_ready,
                          pos_ready, late_ready, row_ready, row_u_ready, notes_ready):
                    x.opened(dve)
                nc.vector.memset(ones[:, :], 1.0).then_inc(counts_set, 1)
                nc.vector.memset(both[1][:, :, :], 0.0).then_inc(counts_set, 1)
                nc.vector.memset(count[1][:, :, :], 0.0).then_inc(counts_set, 1)
                dve.wait_ge(counts_set, 3)
                dve.wait_ge(weights_in, 16 * WEIGHTS)

                def body(n, par):
                    if n[PLACE] is not None:
                        u, b = n[PLACE], par[PLACE]
                        dve.wait_ge(both_ready.sem, both_ready.count(u))
                        dve.wait_ge(place_done.sem, place_done.count(u, back=2))
                        for t in range(TILES):
                            if t > 0:
                                dve.wait_ge(count_ready.sem, count_ready.count(u, t))
                                nc.vector.tensor_tensor(count[b][:, t, :], count[b][:, t - 1, :], both[b][:, t - 1, :], ALU.add).then_inc(count_ready.sem, 1)
                            else:
                                dve.wait_ge(count_ready.sem, count_ready.count(u, back=1))
                                nc.vector.tensor_tensor(count[b][:, 0, :], count[1 - b][:, TILES - 1, :], both[1 - b][:, TILES - 1, :],
                                                        ALU.add).then_inc(count_ready.sem, 1)
                    if n[NORM] is not None:
                        u, b = n[NORM], par[NORM]
                        dve.wait_ge(x_in[b].sem, x_in[b].count(u, b))
                        dve.wait_ge(nm.ready.sem, nm.ready.count(u, back=2))
                        for t in range(TILES):
                            norm_moments(nc, dve, nm, u, b, t, dve_passed)
                    if n[SOFT] is not None:
                        u, b = n[SOFT], par[SOFT]
                        dve.wait_ge(logit_done.sem, logit_done.count(u))
                        nc.vector.tensor_reduce(best[b][:, :], logit, AX.X, ALU.max).then_inc(best_ready.sem, 1)
                        dve.wait_ge(best_ready.sem, best_ready.count(u))
                        dve.wait_ge(prob_ready.sem, prob_ready.count(u, back=2))
                        nc.vector.tensor_tensor(ex[b][:, :, :], logit, wide(best[b][:, :], E), ALU.subtract).then_inc(shifted.sem, 1)
                    if n[GATE] is not None:
                        u, b = n[GATE], par[GATE]
                        dve.wait_ge(ex_ready.sem, ex_ready.count(u))
                        nc.vector.tensor_reduce(total[b][:, :], ex[b][:, :, :], AX.X, ALU.add).then_inc(total_ready.sem, 1)
                        dve.wait_ge(total_ready.sem, total_ready.count(u))
                        nc.vector.reciprocal(total[b][:, :], total[b][:, :]).then_inc(inv_ready.sem, 1)
                        dve.wait_ge(inv_ready.sem, inv_ready.count(u))
                        nc.vector.tensor_tensor(prob[b][:, :, :], ex[b][:, :, :], wide(total[b][:, :], E), ALU.mult).then_inc(prob_ready.sem, 1)
                        dve.wait_ge(prob_ready.sem, prob_ready.count(u))
                        dve.sem_inc(dve_passed, 1)
                        for t in range(TILES):
                            last = nc.vector.max(top[b][:, t, :], prob[b][:, t, :])
                        last.then_inc(top_ready.sem, 1)
                        dve.wait_ge(top_ready.sem, top_ready.count(u))
                        nc.vector.tensor_tensor(share[b][:, :], top[b][:, :, 0], top[b][:, :, 1], ALU.add).then_inc(share_ready.sem, 1)
                        for t in range(TILES):
                            last = nc.vector.max_index(at[b][:, t, :], top[b][:, t, :], prob[b][:, t, :])
                        last.then_inc(at_ready.sem, 1)
                        dve.wait_ge(share_ready.sem, share_ready.count(u))
                        nc.vector.reciprocal(share[b][:, :], share[b][:, :]).then_inc(share_inv.sem, 1)
                        dve.wait_ge(at_ready.sem, at_ready.count(u))
                        nc.vector.tensor_copy(atf[b][:, :, :], at[b][:, :, 0:2].rearrange("p t k -> p k t")).then_inc(atf_ready.sem, 1)
                        dve.wait_ge(share_inv.sem, share_inv.count(u))
                        nc.vector.tensor_tensor(gate[b][:, :, :], top[b][:, :, 0:2].rearrange("p t k -> p k t"), over(share[b][:, :], 2),
                                                ALU.mult).then_inc(gate_ready.sem, 1)
                        dve.wait_ge(atf_ready.sem, atf_ready.count(u))
                        for k in range(2):
                            last = nc.vector.tensor_tensor(hot[b][:, k, :, :], over(iota[0:HALF, :], TILES), wide(atf[b][:, k, :], E), ALU.is_equal)
                        last.then_inc(hot_ready.sem, 1)
                        dve.wait_ge(hot_ready.sem, hot_ready.count(u))
                        nc.vector.tensor_tensor(both[b][:, :, :], hot[b][:, 0, :, :], hot[b][:, 1, :, :], ALU.add).then_inc(both_ready.sem, 1)
                    if n[PLACE] is not None:
                        u, b = n[PLACE], par[PLACE]
                        dve.wait_ge(place_done.sem, place_done.count(u))
                        for k in range(2):
                            last = nc.vector.tensor_tensor(mine[b][:, k, :, :], hot[b][:, k, :, :], place, ALU.mult)
                        last.then_inc(mine_ready.sem, 1)
                        dve.wait_ge(mine_ready.sem, mine_ready.count(u))
                        nc.vector.tensor_reduce(pos[b][:, :, :], mine[b][:, :, :, :], AX.X, ALU.add).then_inc(pos_ready.sem, 1)
                        dve.wait_ge(pos_ready.sem, pos_ready.count(u))
                        dve.wait_ge(noted[b].sem, noted[b].count(u, b, back=1))
                        nc.vector.tensor_scalar(late[b][:, :, :], pos[b][:, :, :], float(CAP), float(FAR), ALU.is_ge, ALU.mult)
                        nc.vector.tensor_scalar(base[b][:, :, :], atf[b][:, :, :], float(CAP), None, ALU.mult)
                        nc.vector.tensor_scalar(near[b][:, :, :], pos[b][:, :, :], float(CAP - 1), None, ALU.min)
                        nc.vector.scalar_tensor_tensor(gated[b][:, :, :], pos[b][:, :, :], float(CAP), gate[b][:, :, :], ALU.is_lt, ALU.mult).then_inc(late_ready.sem, 1)
                        dve.wait_ge(late_ready.sem, late_ready.count(u))
                        nc.vector.tensor_tensor(row[b][:, :, :], base[b][:, :, :], pos[b][:, :, :], ALU.add)
                        nc.vector.tensor_tensor(read_f[b][:, :, :], base[b][:, :, :], near[b][:, :, :], ALU.add).then_inc(row_ready.sem, 1)
                        dve.wait_ge(row_ready.sem, row_ready.count(u))
                        dve.wait_ge(scatter_over.sem, scatter_over.count(u, back=2))
                        nc.vector.tensor_tensor(row_u[b][:, :, :], row[b][:, :, :], late[b][:, :, :], ALU.add).then_inc(row_u_ready.sem, 1)
                        nc.vector.tensor_copy(read_u[b][:, :, :], read_f[b][:, :, :]).then_inc(notes_ready.sem, 1)

                in_lanes(dve, UNITS, STAGES, body)

            @block.gpsimd
            def _(pool):
                for x in (nm.var_eps, nm.rstd_ready, sh.product, sh.ready):
                    x.opened(pool)
                nc.gpsimd.memset(eps[:, :], EPS)
                nc.gpsimd.memset(minus_half[:, :], -0.5).then_inc(constants_set, 1)
                pool.wait_ge(constants_set, 1)

                def body(n, par):
                    if n[SCATTER] is not None:
                        u, b = n[SCATTER], par[SCATTER]
                        pool.wait_ge(going_ready.sem, going_ready.count(u))
                        pool.wait_ge(row_u_ready.sem, row_u_ready.count(u))
                        pool.sem_inc(pool_passed, 1)
                        for k in range(2):
                            for t in range(TILES):
                                nc.gpsimd.indirect_dma_start(
                                    out=slots, out_offset=bass.IndirectOffsetOnAxis(ap=row_u[b][:, k, t:t + 1], axis=0),
                                    in_=going[b][:, t, :], in_offset=None, bounds_check=EXP1 * CAP - 1,
                                    oob_is_err=False).then_inc(scattered[b].sem, 16)
                    if n[NORM] is not None:
                        u, b = n[NORM], par[NORM]
                        norm_scales(nc, pool, nm, sh, u, b, eps, minus_half, pool_passed)

                in_lanes(pool, UNITS, STAGES, body)

        pl.close()


def phase_experts64(nc, slots, ident, g_col, b_col, w1, b1, w2, b2, y_dram):
    TILES = CAP // HALF
    N = CAP // 2
    CH = FF1 // P
    LOAD, TURN, HID, OUT = range(4)
    STAGES = 4
    HIGH, LOW = range(2)
    PARTS = ((HIGH, LOW), (LOW, HIGH), (HIGH, HIGH))
    with ExitStack() as ctx:
        pl = Place(nc, ctx, "exp")
        sb, sem = pl.sb, pl.sem
        idn = sb("ident", [P, P])
        gb = sb("gb", [P, 2])

        def two(name, shape, dt=F32):
            return [sb(f"{name}{b}", shape, dt) for b in range(2)]

        def parts(name, shape):
            return [[sb(f"{name}_{part}{b}", shape, F32R) for part in ("high", "low")] for b in range(2)]

        x = two("x", [HALF, TILES, D])
        xT = sb("xT", [D, CAP])
        xs = parts("xs", [D, CAP])
        w1_sb = two("w1", [D, FF1])
        w1s = parts("w1s", [D, FF1])
        b1_sb = two("b1", [P, CH])
        w2_sb = two("w2", [P, CH, D])
        b2_sb = two("b2", [P, D])
        hid = two("hid", [P, CH, CAP])
        y = two("y", [HALF, TILES, D])
        ps_turn = pl.banks("turn", 2)
        ps_hid = pl.banks("hid", 2)
        ps_out = pl.banks("out", 2)

        weights_in = sem("weights_in")
        pool_passed = sem("pool_passed")
        x_in = [Landed(sem(f"x_in{b}"), 1) for b in range(2)]
        w1_in = [Landed(sem(f"w1_in{b}"), 1) for b in range(2)]
        b1_in = [Landed(sem(f"b1_in{b}"), 1) for b in range(2)]
        w2_in = [Landed(sem(f"w2_in{b}"), 1) for b in range(2)]
        b2_in = [Landed(sem(f"b2_in{b}"), 1) for b in range(2)]
        stored = [Landed(sem(f"stored{b}"), 1) for b in range(2)]
        turned = Signal(sem("turned"), 2)
        xT_ready = Signal(sem("xT_ready"), 2)
        x_high = Signal(sem("x_high"))
        x_low = Signal(sem("x_low"))
        w1_high = Signal(sem("w1_high"))
        w1_low = Signal(sem("w1_low"))
        hid_done = Signal(sem("hid_done"), 2 * CH)
        hid_ready = Signal(sem("hid_ready"), 2 * CH)
        out_done = Signal(sem("out_done"), TILES)
        y_ready = Signal(sem("y_ready"), TILES)

        with nc.Block() as block:

            @block.sync
            def _(sp):
                for dst, src in ((idn[:, :], ident), (gb[:, 0:1], g_col), (gb[:, 1:2], b_col)):
                    sp.dma_start(dst, src).then_inc(weights_in, 16)
                for s in x_in + w1_in + b1_in + w2_in + b2_in + stored:
                    s.opened(sp)

                def body(n, par):
                    if n[LOAD] is not None:
                        u, b = n[LOAD], par[LOAD]
                        sp.wait_ge(turned.sem, turned.count(u, back=2))
                        sp.dma_start(x[b][:, :, :], slots[bass.ds(u * CAP, CAP), :].rearrange("(p t) d -> p t d", t=TILES)).then_inc(x_in[b].sem, 16)
                        sp.wait_ge(w1_low.sem, w1_low.count(u, back=2))
                        sp.dma_start(w1_sb[b][:, :], w1[bass.ds(u, 1), :, :].rearrange("e d f -> (e d) f")).then_inc(w1_in[b].sem, 16)
                    if n[TURN] is not None:
                        u, b = n[TURN], par[TURN]
                        sp.wait_ge(hid_ready.sem, hid_ready.count(u, back=2))
                        sp.dma_start(b1_sb[b][:, :], b1[bass.ds(u, 1), :, :].rearrange("e p c -> (e p) c")).then_inc(b1_in[b].sem, 16)
                    if n[HID] is not None:
                        u, b = n[HID], par[HID]
                        sp.wait_ge(y_ready.sem, y_ready.count(u, back=2))
                        sp.dma_start(w2_sb[b][:, :, :], w2[bass.ds(u, 1), :, :].rearrange("e (c p) d -> p (e c) d", p=P)).then_inc(w2_in[b].sem, 16)
                        sp.dma_start(b2_sb[b][:, :], b2[bass.ds(u, 1), :].to_broadcast([P, D])).then_inc(b2_in[b].sem, 16)
                    if n[OUT] is not None:
                        u, b = n[OUT], par[OUT]
                        sp.wait_ge(y_ready.sem, y_ready.count(u))
                        sp.dma_start(y_dram[bass.ds(u * CAP, CAP), :].rearrange("(p t) d -> p t d", t=TILES), y[b][:, :, :]).then_inc(stored[b].sem, 16)

                in_lanes(sp, EXP1, STAGES, body)
                for b in range(2):
                    sp.wait_ge(stored[b].sem, stored[b].final(EXP1))

            @block.tensor
            def _(pe):
                for s in (turned, hid_done, out_done):
                    s.opened(pe)
                pe.wait_ge(weights_in, 48)

                def body(n, par):
                    for r in range(TILES):
                        if n[HID] is not None:
                            u, b = n[HID], par[HID]
                            half, c = r // CH, r % CH
                            if r == 0:
                                for s in (w1_high, w1_low, x_high, x_low):
                                    pe.wait_ge(s.sem, s.count(u))
                            pe.wait_ge(hid_ready.sem, hid_ready.count(u, r - 1))
                            for i, (wp, xp) in enumerate(PARTS):
                                last = nc.tensor.matmul(ps_hid[r % 2][:, 0:N], w1s[b][wp][:, c * P:(c + 1) * P], xs[b][xp][:, half * N:(half + 1) * N],
                                                        start=i == 0, stop=i == 2)
                            last.then_inc(hid_done.sem, 1)
                        if n[OUT] is not None:
                            u, b = n[OUT], par[OUT]
                            if r == 0:
                                pe.wait_ge(w2_in[b].sem, w2_in[b].count(u, b))
                                pe.wait_ge(hid_ready.sem, hid_ready.count(u))
                            pe.wait_ge(y_ready.sem, y_ready.count(u, r - 1))
                            for c in range(CH):
                                last = nc.tensor.matmul(ps_out[r % 2][0:HALF, 0:D], hid[b][:, c, r * HALF:(r + 1) * HALF], w2_sb[b][:, c, :],
                                                        start=c == 0, stop=c == CH - 1)
                            last.then_inc(out_done.sem, 1)
                        if n[TURN] is not None and r in (0, 1):
                            u, b, half = n[TURN], par[TURN], r
                            if half == 0:
                                pe.wait_ge(x_in[b].sem, x_in[b].count(u, b))
                            pe.wait_ge(xT_ready.sem, xT_ready.count(u, half + 1, back=1))
                            for t in range(TILES // 2):
                                last = nc.tensor.transpose(ps_turn[half][:, t * HALF:(t + 1) * HALF], x[b][:, half * TILES // 2 + t, :], idn[0:HALF, 0:HALF])
                            last.then_inc(turned.sem, 1)

                in_lanes(pe, EXP1, STAGES, body)

            @block.scalar
            def _(act):
                for s in (xT_ready, hid_ready):
                    s.opened(act)
                act.wait_ge(weights_in, 48)

                def body(n, par):
                    for r in range(TILES):
                        if n[HID] is not None:
                            u, b = n[HID], par[HID]
                            half, c = r // CH, r % CH
                            if r == 0:
                                act.wait_ge(b1_in[b].sem, b1_in[b].count(u, b))
                                act.wait_ge(out_done.sem, out_done.count(u, back=2))
                            act.wait_ge(hid_done.sem, hid_done.count(u, r + 1))
                            nc.scalar.activation(hid[b][:, c, half * N:(half + 1) * N], ps_hid[r % 2][:, 0:N], ACT.Gelu_apprx_tanh,
                                                 bias=b1_sb[b][:, c:c + 1]).then_inc(hid_ready.sem, 1)
                        if n[TURN] is not None and r in (1, 2):
                            u, half = n[TURN], r - 1
                            act.wait_ge(turned.sem, turned.count(u, half + 1))
                            act.wait_ge(x_low.sem, x_low.count(u, back=1))
                            nc.scalar.activation(xT[:, half * N:(half + 1) * N], ps_turn[half][:, 0:N], ACT.Identity,
                                                 bias=gb[:, 1:2], scale=gb[:, 0:1]).then_inc(xT_ready.sem, 1)

                in_lanes(act, EXP1, STAGES, body)

            @block.vector
            def _(dve):
                for s in (w1_low, x_low, y_ready):
                    s.opened(dve)

                def body(n, par):
                    for r in range(TILES):
                        if n[OUT] is not None:
                            u, b = n[OUT], par[OUT]
                            if r == 0:
                                dve.wait_ge(b2_in[b].sem, b2_in[b].count(u, b))
                                dve.wait_ge(stored[b].sem, stored[b].count(u, b, back=1))
                            dve.wait_ge(out_done.sem, out_done.count(u, r + 1))
                            nc.vector.tensor_tensor(y[b][:, r, :], ps_out[r % 2][0:HALF, 0:D], b2_sb[b][0:HALF, :], ALU.add).then_inc(y_ready.sem, 1)
                        if n[TURN] is not None and r == 1:
                            u, b = n[TURN], par[TURN]
                            dve.wait_ge(w1_high.sem, w1_high.count(u))
                            dve.wait_ge(hid_done.sem, hid_done.count(u, back=2))
                            nc.vector.tensor_tensor(w1s[b][LOW][:, :], w1_sb[b][:, :], w1s[b][HIGH][:, :], ALU.subtract).then_inc(w1_low.sem, 1)
                        if n[TURN] is not None and r == 6:
                            u, b = n[TURN], par[TURN]
                            dve.wait_ge(x_high.sem, x_high.count(u))
                            nc.vector.tensor_tensor(xs[b][LOW][:, :], xT[:, :], xs[b][HIGH][:, :], ALU.subtract).then_inc(x_low.sem, 1)

                in_lanes(dve, EXP1, STAGES, body)

            @block.gpsimd
            def _(pool):
                for s in (w1_high, x_high):
                    s.opened(pool)

                def body(n, par):
                    if n[TURN] is not None:
                        u, b = n[TURN], par[TURN]
                        pool.wait_ge(w1_in[b].sem, w1_in[b].count(u, b))
                        pool.wait_ge(hid_done.sem, hid_done.count(u, back=2))
                        pool.sem_inc(pool_passed, 1)
                        nc.gpsimd.tensor_copy(w1s[b][HIGH][:, :], w1_sb[b][:, :]).then_inc(w1_high.sem, 1)
                    if n[TURN] is not None:
                        u, b = n[TURN], par[TURN]
                        pool.wait_ge(xT_ready.sem, xT_ready.count(u))
                        pool.sem_inc(pool_passed, 1)
                        nc.gpsimd.tensor_copy(xs[b][HIGH][:, :], xT[:, :]).then_inc(x_high.sem, 1)

                in_lanes(pool, EXP1, STAGES, body)

        pl.close()


def phase_combine(nc, h_dram, x_dram, y_dram, slot_dram, gate_dram, out_dram):
    UNITS = BATCH // 2
    TILES = 4
    LOAD, GATHER, SUM = range(3)
    STAGES = 3
    with ExitStack() as ctx:
        pl = Place(nc, ctx, "com")
        sb, sem = pl.sb, pl.sem

        def two(name, shape, dt=F32):
            return [sb(f"{name}{b}", shape, dt) for b in range(2)]

        slot = two("slot", [HALF, 2 * TILES], U32)
        gate = two("gate", [HALF, 2 * TILES])
        h = two("h", [HALF, TILES, D])
        x = two("x", [HALF, TILES, D])
        y = two("y", [HALF, 2, TILES, D])
        acc = two("acc", [HALF, TILES, D])
        pool_passed = sem("pool_passed")
        slot_in = [Landed(sem(f"slot_in{b}"), 2) for b in range(2)]
        rows_in = [Landed(sem(f"rows_in{b}"), 4) for b in range(2)]
        gathered = [Landed(sem(f"gathered{b}"), 2 * TILES, ahead=0) for b in range(2)]
        stored = [Landed(sem(f"stored{b}"), 2) for b in range(2)]
        base_ready = Signal(sem("base_ready"))
        acc_ready = Signal(sem("acc_ready"), 2)

        with nc.Block() as block:

            @block.sync
            def _(sp):
                for s in slot_in + rows_in + stored:
                    s.opened(sp)

                def body(n, par):
                    if n[LOAD] is not None:
                        u, b = n[LOAD], par[LOAD]
                        sp.wait_ge(acc_ready.sem, acc_ready.count(u, back=2))
                        sp.dma_start(slot[b][:, :], slot_dram[bass.ds(u, 1), :, :].rearrange("u p x -> (u p) x")).then_inc(slot_in[b].sem, 16)
                        sp.dma_start(gate[b][:, :], gate_dram[bass.ds(u, 1), :, :].rearrange("u p x -> (u p) x")).then_inc(slot_in[b].sem, 16)
                        load_rows(sp, h[b], h_dram, u, rows_in[b])
                        load_rows(sp, x[b], x_dram, u, rows_in[b])
                    if n[SUM] is not None:
                        u, b = n[SUM], par[SUM]
                        sp.wait_ge(acc_ready.sem, acc_ready.count(u))
                        store_rows(sp, out_dram, acc[b], u, stored[b])

                in_lanes(sp, UNITS, STAGES, body)
                for b in range(2):
                    sp.wait_ge(stored[b].sem, stored[b].final(UNITS))

            @block.gpsimd
            def _(pool):
                def body(n, par):
                    if n[GATHER] is not None:
                        u, b = n[GATHER], par[GATHER]
                        pool.wait_ge(acc_ready.sem, acc_ready.count(u, back=2))
                        pool.wait_ge(slot_in[b].sem, slot_in[b].count(u, b))
                        pool.sem_inc(pool_passed, 1)
                        for k in range(2):
                            for t in range(TILES):
                                nc.gpsimd.indirect_dma_start(
                                    out=y[b][:, k, t, :], out_offset=None, in_=y_dram,
                                    in_offset=bass.IndirectOffsetOnAxis(ap=slot[b][:, k * TILES + t:k * TILES + t + 1], axis=0),
                                    ).then_inc(gathered[b].sem, 16)

                in_lanes(pool, UNITS, STAGES, body)

            @block.vector
            def _(dve):
                for s in (base_ready, acc_ready):
                    s.opened(dve)

                def body(n, par):
                    if n[SUM] is not None:
                        u, b = n[SUM], par[SUM]
                        dve.wait_ge(rows_in[b].sem, rows_in[b].count(u, b))
                        dve.wait_ge(stored[b].sem, stored[b].count(u, b, back=1))
                        nc.vector.tensor_tensor(acc[b][:, :, :], h[b][:, :, :], x[b][:, :, :], ALU.add).then_inc(base_ready.sem, 1)
                        dve.wait_ge(base_ready.sem, base_ready.count(u))
                        dve.wait_ge(gathered[b].sem, gathered[b].count(u, b))
                        for k in range(2):
                            if k == 1:
                                dve.wait_ge(acc_ready.sem, acc_ready.count(u, 1))
                            for t in range(TILES):
                                last = nc.vector.scalar_tensor_tensor(acc[b][:, t, :], y[b][:, k, t, :], gate[b][:, k * TILES + t:k * TILES + t + 1],
                                                                      acc[b][:, t, :], ALU.mult, ALU.add)
                            last.then_inc(acc_ready.sem, 1)

                in_lanes(dve, UNITS, STAGES, body)

        pl.close()


def audio_tower(nc, a, out):
    def scratch(name, shape, dt=F32):
        return nc.dram_tensor(name, shape, dt, kind="Internal").ap()

    h0 = scratch("h0", [POS_PAD, BATCH, D])
    h1 = scratch("h1", [BATCH, POS_PAD, D])
    h2 = scratch("h2", [BATCH, SEQ, D])
    h3 = scratch("h3", [BATCH, SEQ, D])
    y4 = scratch("y4", [BATCH, SEQ, D])
    x5 = scratch("x5", [BATCH, SEQ, D])
    slots = scratch("slots", [EXP1 * CAP, D])
    y_slots = scratch("y_slots", [EXP1 * CAP, D])
    slot_of = scratch("slot_of", [BATCH // 2, HALF, 8], U32)
    gate_of = scratch("gate_of", [BATCH // 2, HALF, 8])

    phase_token_mixer(nc, a["x"], a["ident"], a["tok_w_compress"], a["tok_w_main"], a["tok_w_expand"], a["tok_w_ff1"],
                      a["tok_w_ff2"], a["tok_b_compress"], a["tok_b_main"], a["tok_b_ff1"], a["tok_g1_col"],
                      a["tok_b1_col"], a["tok_g2_col"], a["tok_b2_col"], a["tok_b_expand"], a["tok_g1_row"],
                      a["tok_b1_row"], a["tok_b_ff2"], h0, slots)
    phase_batch_attention(nc, h0, a["ident"], a["bat_mask"], a["bat_wq"], a["bat_wk"], a["bat_wv"], a["bat_wo"], h1)
    phase_experts8(nc, h1, a["ident"], a["mix_iota"], a["mix_wg"], a["mix_w1"], a["mix_b1"], a["mix_w2"], a["mix_b2"],
                   a["mix_gamma"], a["mix_beta"], h2)
    phase_linear_attention(nc, h2, a["ident"], a["lin_mask"], a["lin_blocks"], a["head_mask"], a["lin_index"], a["lin_wq"], a["lin_wk"],
                           a["lin_wv"], a["lin_bqk"], a["lin_bv"], a["lin_decay"], a["lin_wo"], a["lin_bo"], a["lin_g"],
                           a["lin_b"], h3)
    phase_attention(nc, h3, a["ident"], a["head_mask"], a["att_wq"], a["att_wk"], a["att_wv"], a["att_wo"],
                    a["att_g"], a["att_b"], y4, x5)
    phase_router(nc, x5, a["ident"], a["rou_before"], a["rou_iota"], a["rou_wr"], a["exp_g"], a["exp_b"], slots,
                 slot_of, gate_of)
    phase_experts64(nc, slots, a["ident"], a["exp_g"], a["exp_b"], a["exp_w1"], a["exp_b1"], a["exp_w2"], a["exp_b2"],
                    y_slots)
    phase_combine(nc, h3, x5, y_slots, slot_of, gate_of, out)


def layouts(inputs, np):
    tok = {n[7:]: w for n, w in inputs.items() if n.startswith("L0_tok_")}
    bat = {n[8:]: w for n, w in inputs.items() if n.startswith("L0_attn_")}
    mix = {n[7:]: w for n, w in inputs.items() if n.startswith("L0_ffn_")}
    lin = {n[8:]: w for n, w in inputs.items() if n.startswith("L1_attn_")}
    ffn = {n[7:]: w for n, w in inputs.items() if n.startswith("L1_ffn_")}

    f32 = np.float32
    at = np.arange(HALF)
    upto = (at[None, :] >= at[:, None]).astype(f32)
    width = N_HEAD * D_HEAD
    return {
        "x": inputs["x"],
        "ident": np.eye(P, dtype=f32),
        "head_mask": np.repeat(np.eye(N_HEAD, dtype=f32), E_HEAD, axis=0),
        "tok_w_compress": tok["w_compress"][:, :, 0].T, "tok_w_main": tok["w_main"].transpose(1, 2, 0),
        "tok_w_expand": tok["w_expand"][:, :, 0].T, "tok_w_ff1": tok["w_ff1"].T, "tok_w_ff2": tok["w_ff2"].T,
        "tok_b_compress": tok["b_compress"][:, None], "tok_b_main": tok["b_main"][:, None],
        "tok_b_ff1": tok["b_ff1"][:, None], "tok_g1_col": tok["g_conv_norm"][:, None],
        "tok_b1_col": tok["b_conv_norm"][:, None], "tok_g2_col": tok["g_ff_norm"][:, None],
        "tok_b2_col": tok["b_ff_norm"][:, None], "tok_b_expand": tok["b_expand"], "tok_g1_row": tok["g_conv_norm"],
        "tok_b1_row": tok["b_conv_norm"], "tok_b_ff2": tok["b_ff2"],
        "bat_mask": np.where(np.arange(4 * P)[None, :] % BATCH > np.arange(P)[:, None] % BATCH, f32(-1e6), f32(0)),
        "bat_wq": bat["Wq"].T, "bat_wk": bat["Wkv"][:width].T, "bat_wv": bat["Wkv"][width:].T, "bat_wo": bat["Wo"].T,
        "mix_iota": np.tile(np.arange(EXP0, dtype=f32), (P, 1)), "mix_wg": mix["Wg"], "mix_w1": mix["W1"],
        "mix_b1": mix["b1"].T, "mix_w2": mix["W2"], "mix_b2": mix["b2"].reshape(-1),
        "mix_gamma": mix["gamma"].reshape(-1), "mix_beta": mix["beta"],
        "lin_mask": np.concatenate([upto, np.ones((HALF, HALF), f32)], 1),
        "lin_blocks": np.kron(np.eye(N_HEAD, dtype=f32), np.ones((E_HEAD, E_HEAD), f32)),
        "lin_index": np.tile(np.arange(P, dtype=f32), (P, 1)),
        "lin_wq": lin["W_qkv"][:, :D], "lin_wk": lin["W_qkv"][:, D:2 * D], "lin_wv": lin["W_qkv"][:, 2 * D:],
        "lin_bqk": lin["b_qkv"][:2 * D].reshape(2, D).T, "lin_bv": lin["b_qkv"][2 * D:],
        "lin_decay": np.repeat(lin["decay_logits"], E_HEAD)[:, None], "lin_wo": lin["W_out"],
        "lin_bo": lin["b_out"], "lin_g": lin["ln_g"], "lin_b": lin["ln_b"],
        "att_wq": ffn["wq"], "att_wk": ffn["wk"],
        "att_wv": ffn["wv"], "att_wo": ffn["wo"], "att_g": ffn["ln1_g"][:, None], "att_b": ffn["ln1_b"][:, None],
        "rou_before": (at[:, None] < at[None, :]).astype(f32), "rou_iota": np.tile(np.arange(EXP1, dtype=f32), (P, 1)),
        "rou_wr": ffn["wr"], "exp_g": ffn["ln2_g"][:, None], "exp_b": ffn["ln2_b"][:, None], "exp_w1": ffn["w1"],
        "exp_b1": ffn["b1"].reshape(EXP1, 4, P).transpose(0, 2, 1), "exp_w2": ffn["w2"], "exp_b2": ffn["b2"],
    }


def kernel(**inputs):
    import numpy as np
    import concourse.bacc as bacc
    from concourse.bass_utils import run_bass_kernel_spmd

    nc = bacc.Bacc("TRN2", target_bir_lowering=False, num_devices=1)
    arrays = {n: np.ascontiguousarray(a) for n, a in layouts({n: np.asarray(a) for n, a in inputs.items()}, np).items()}
    args = {n: nc.dram_tensor(n, a.shape, mybir.dt.from_np(a.dtype), kind="ExternalInput").ap() for n, a in arrays.items()}
    out = nc.dram_tensor("out", [BATCH, SEQ, D], F32, kind="ExternalOutput").ap()
    audio_tower(nc, args, out)
    return run_bass_kernel_spmd(nc, [arrays], core_ids=[0]).results[0]["out"]
```
